# Optimizing a Trainium2 kernel written in Bass

```python
import numpy as np
import jax
import jax.numpy as jnp

def _softmax(x, axis=-1):
    return jax.nn.softmax(x, axis=axis)

def _gelu(x):
    return jax.nn.gelu(x, approximate=True)

def _silu(x):
    return jax.nn.silu(x)

def _sigmoid(x):
    return jax.nn.sigmoid(x)

def _layernorm(x, axis=-1, eps=1e-05):
    m = jnp.mean(x, axis=axis, keepdims=True)
    v = jnp.var(x, axis=axis, keepdims=True)
    return (x - m) / jnp.sqrt(v + eps)

def _scatter_add(tgt, idx, src, axis=0):
    return tgt.at[idx].add(src)

def _segment_sum(src, seg, n):
    return jax.ops.segment_sum(src, seg, n)
kernel_name = 'mk_early_fusion_d4_tok_img1024_r4_4bd99d'

def setup_inputs(seed: int=0):
    np.random.seed(seed)
    _w = jnp.asarray

    def _rec_inputs():
        import jax
        import jax.numpy as jnp
        _rk = jax.random.key(seed)
        x = -0.00016672 + 0.999947 * jax.random.normal(jax.random.fold_in(_rk, 1), (32, 3, 96, 96), jnp.float32)
        txt = -1.58432e-05 + 1.00006 * jax.random.normal(jax.random.fold_in(_rk, 2), (32, 77, 256), jnp.float32)
        return (x, txt)
    x, txt = _rec_inputs()

    def _L0_tok_setup():
        import jax, jax.numpy as jnp
        import numpy as np
        PATCH = 16
        key = jax.random.key(seed)
        k1, k2, k3 = jax.random.split(key, 3)
        B, C, H, Wd = (64, 3, 96, 96)
        patch_dim = C * PATCH * PATCH
        embed_dim = 256
        x = jax.random.normal(k1, (B, C, H, Wd), dtype=jnp.float32)
        W = jax.random.normal(k2, (embed_dim, patch_dim), dtype=jnp.float32) * patch_dim ** (-0.5)
        b = jax.random.normal(k3, (embed_dim,), dtype=jnp.float32) * 0.01
        return {'x': x, 'W': W, 'b': b}
    _L0_tok_all = _L0_tok_setup()
    _L0_tok_in = {k: v for k, v in _L0_tok_all.items() if k in ('W', 'b')}
    del _L0_tok_all

    def _L0_attn_setup():
        import jax, jax.numpy as jnp
        import numpy as np
        H = 16
        GRID = 16
        TOK_PER_FRAME = GRID * GRID

        def _rope(x, pos, dim):
            half = dim // 2
            omega = jnp.arange(half, dtype=x.dtype) / (dim / 2.0)
            inv = 1.0 / 10000.0 ** omega
            freq = pos.astype(x.dtype)[:, None] * inv
            sin = jnp.concatenate([jnp.sin(freq), jnp.sin(freq)], axis=-1)
            cos = jnp.concatenate([jnp.cos(freq), jnp.cos(freq)], axis=-1)
            y = x.reshape(*x.shape[:-1], half, 2)
            y1, y2 = (y[..., 0], y[..., 1])
            rot = jnp.stack((-y2, y1), axis=-1).reshape(x.shape)
            return x * cos + rot * sin

        def _apply_3d_rope(qk, f_ids, h_ids, w_ids, d_dim):
            s = 0
            parts = []
            for pos in (f_ids, h_ids, w_ids):
                parts.append(_rope(qk[..., s:s + d_dim], pos, d_dim))
                s += d_dim
            if s < qk.shape[-1]:
                parts.append(qk[..., s:])
            return jnp.concatenate(parts, axis=-1)
        key = jax.random.key(seed)
        ks = jax.random.split(key, 5)
        D = 256
        B, N = (4, 512)
        sc = 0.02
        return {'hidden_states': jax.random.normal(ks[0], (B, N, D), jnp.float32), 'Wq': jax.random.normal(ks[1], (D, D), jnp.float32) * sc, 'bq': jnp.zeros((D,), jnp.float32), 'Wk': jax.random.normal(ks[2], (D, D), jnp.float32) * sc, 'bk': jnp.zeros((D,), jnp.float32), 'Wv': jax.random.normal(ks[3], (D, D), jnp.float32) * sc, 'bv': jnp.zeros((D,), jnp.float32), 'Wo': jax.random.normal(ks[4], (D, D), jnp.float32) * sc, 'bo': jnp.zeros((D,), jnp.float32)}
    _L0_attn_all = _L0_attn_setup()
    _L0_attn_in = {k: v for k, v in _L0_attn_all.items() if k in ('Wq', 'bq', 'Wk', 'bk', 'Wv', 'bv', 'Wo', 'bo')}
    del _L0_attn_all

    def _L0_ffn_setup():
        import jax, jax.numpy as jnp
        import numpy as np
        B, S, D = (1, 512, 256)
        F = 352
        E = 16
        K = 2
        CAP_FACTOR = 1.25

        def _mlp(h, wg, wu, wd):
            return jax.nn.silu(h @ wg) * (h @ wu) @ wd
        key = jax.random.key(seed)
        ks = jax.random.split(key, 10)
        sd = 0.02
        return {'x': jax.random.normal(ks[0], (B, S, D), jnp.float32), 'router_w': jax.random.normal(ks[1], (D, E), jnp.float32) * sd, 'router_b': jnp.zeros((E,), jnp.float32), 'w_gate': jax.random.normal(ks[2], (E, D, F), jnp.float32) * sd, 'w_up': jax.random.normal(ks[3], (E, D, F), jnp.float32) * sd, 'w_down': jax.random.normal(ks[4], (E, F, D), jnp.float32) * sd, 'sw_gate': jax.random.normal(ks[5], (D, F), jnp.float32) * sd, 'sw_up': jax.random.normal(ks[6], (D, F), jnp.float32) * sd, 'sw_down': jax.random.normal(ks[7], (F, D), jnp.float32) * sd}
    _L0_ffn_all = _L0_ffn_setup()
    _L0_ffn_in = {k: v for k, v in _L0_ffn_all.items() if k in ('router_w', 'router_b', 'w_gate', 'w_up', 'w_down', 'sw_gate', 'sw_up', 'sw_down')}
    del _L0_ffn_all

    def _L1_attn_setup():
        import jax, jax.numpy as jnp
        import numpy as np
        D_MODEL = 256
        D_STATE = 16
        D_CONV = 4
        EXPAND = 2
        D_INNER = EXPAND * D_MODEL
        DT_RANK = (D_MODEL + 15) // 16
        BATCH = 2
        SEQ = 256

        def _mamba(x, in_w, conv_w, conv_b, xproj_w, dt_w, dt_b, A_log, D_param, out_w):
            Bsz, L, _ = x.shape
            xz = x @ in_w.T
            xh, z = jnp.split(xz, 2, axis=-1)
            xp = jnp.pad(xh, ((0, 0), (D_CONV - 1, 0), (0, 0)))
            xc = conv_b + sum((xp[:, k:k + L, :] * conv_w[:, k] for k in range(D_CONV)))
            xc = jax.nn.silu(xc)
            proj = xc @ xproj_w.T
            dt = proj[..., :DT_RANK]
            Bm = proj[..., DT_RANK:DT_RANK + D_STATE]
            Cm = proj[..., DT_RANK + D_STATE:]
            delta = jax.nn.softplus(dt @ dt_w.T + dt_b)
            A = -jnp.exp(A_log)
            deltaA = jnp.exp(jnp.einsum('bld,dn->bldn', delta, A))
            deltaBu = jnp.einsum('bld,bln->bldn', delta * xc, Bm)

            def step(h, inp):
                dA, dBu, c = inp
                h = dA * h + dBu
                y = jnp.einsum('bdn,bn->bd', h, c)
                return (h, y)
            h0 = jnp.zeros((Bsz, D_INNER, D_STATE), x.dtype)
            _, ys = jax.lax.scan(step, h0, (deltaA.transpose(1, 0, 2, 3), deltaBu.transpose(1, 0, 2, 3), Cm.transpose(1, 0, 2)))
            y = ys.transpose(1, 0, 2) + xc * D_param
            y = y * jax.nn.silu(z)
            return y @ out_w.T
        key = jax.random.key(seed)
        ks = jax.random.split(key, 20)
        s = 0.02

        def mk(i, shape):
            return jax.random.normal(ks[i], shape, jnp.float32) * s
        A_log = jnp.log(jnp.arange(1, D_STATE + 1, dtype=jnp.float32))[None, :].repeat(D_INNER, 0)
        inp = {'x': jax.random.normal(ks[0], (BATCH, SEQ, D_MODEL), jnp.float32)}
        for p, base in (('f', 1), ('b', 10)):
            inp[f'{p}_in_w'] = mk(base + 0, (2 * D_INNER, D_MODEL))
            inp[f'{p}_conv_w'] = mk(base + 1, (D_INNER, D_CONV))
            inp[f'{p}_conv_b'] = jnp.zeros((D_INNER,), jnp.float32)
            inp[f'{p}_xproj_w'] = mk(base + 2, (DT_RANK + 2 * D_STATE, D_INNER))
            inp[f'{p}_dt_w'] = mk(base + 3, (D_INNER, DT_RANK))
            inp[f'{p}_dt_b'] = mk(base + 4, (D_INNER,))
            inp[f'{p}_A_log'] = A_log
            inp[f'{p}_D'] = jnp.ones((D_INNER,), jnp.float32)
            inp[f'{p}_out_w'] = mk(base + 5, (D_MODEL, D_INNER))
        return inp
    _L1_attn_all = _L1_attn_setup()
    _L1_attn_in = {k: v for k, v in _L1_attn_all.items() if k in ('f_in_w', 'f_conv_w', 'f_conv_b', 'f_xproj_w', 'f_dt_w', 'f_dt_b', 'f_A_log', 'f_D', 'f_out_w', 'b_in_w', 'b_conv_w', 'b_conv_b', 'b_xproj_w', 'b_dt_w', 'b_dt_b', 'b_A_log', 'b_D', 'b_out_w')}
    del _L1_attn_all

    def _L1_ffn_setup():
        import jax, jax.numpy as jnp
        import numpy as np

        def _bitlinear(x, w_latent):
            scale = jax.lax.stop_gradient(jnp.clip(jnp.mean(jnp.abs(w_latent), axis=1, keepdims=True), 1e-05, None))
            tern = jnp.clip(jnp.round(w_latent / scale), -1.0, 1.0)
            w = w_latent + jax.lax.stop_gradient(tern - w_latent)
            return x @ (w * scale).T
        key = jax.random.key(seed)
        ks = jax.random.split(key, 6)
        dim, hidden, rank = (256, 1024, 16)
        B, S = (4, 1024)
        x = jax.random.normal(ks[0], (B, S, dim), dtype=jnp.float32)
        w_fc = 0.02 * jax.random.normal(ks[1], (hidden, dim), dtype=jnp.float32)
        w_proj = 0.02 * jax.random.normal(ks[2], (dim, hidden), dtype=jnp.float32)
        u = 0.02 * jax.random.normal(ks[3], (hidden, rank), dtype=jnp.float32)
        v = 0.02 * jax.random.normal(ks[4], (rank, dim), dtype=jnp.float32)
        fast_b = jax.random.normal(ks[5], (rank, rank), dtype=jnp.float32)
        gate = jnp.float32(0.05)
        return {'x': x, 'fast_b': fast_b, 'w_fc': w_fc, 'w_proj': w_proj, 'u': u, 'v': v, 'gate': gate}
    _L1_ffn_all = _L1_ffn_setup()
    _L1_ffn_in = {k: v for k, v in _L1_ffn_all.items() if k in ('fast_b', 'w_fc', 'w_proj', 'u', 'v', 'gate')}
    del _L1_ffn_all

    def _L2_attn_setup():
        import jax, jax.numpy as jnp
        import numpy as np
        B, S, D = (4, 512, 256)

        def _xavier(key, shape):
            bound = float(np.sqrt(6.0 / (shape[0] + shape[1])))
            return jax.random.uniform(key, shape, dtype=jnp.float32, minval=-bound, maxval=bound)
        key = jax.random.key(seed)
        k0, k1, k2, k3 = jax.random.split(key, 4)
        return {'embeddings': jax.random.normal(k0, (B, S, D), dtype=jnp.float32), 'W_Q': _xavier(k1, (D, D)), 'W_K': _xavier(k2, (D, D)), 'W_V': _xavier(k3, (D, D))}
    _L2_attn_all = _L2_attn_setup()
    _L2_attn_in = {k: v for k, v in _L2_attn_all.items() if k in ('W_Q', 'W_K', 'W_V')}
    del _L2_attn_all

    def _L2_ffn_setup():
        import jax, jax.numpy as jnp
        import numpy as np
        D_MODEL = 256
        D_FF = 1024
        NUM_EXPERTS = 8
        B, N = (16, 256)
        key = jax.random.key(seed)
        ks = jax.random.split(key, 7)
        s_in = 1.0 / np.sqrt(D_MODEL)
        s_ff = 1.0 / np.sqrt(D_FF)
        return {'x': jax.random.normal(ks[0], (B, N, D_MODEL), dtype=jnp.float32), 'Wr': jax.random.uniform(ks[1], (D_MODEL, NUM_EXPERTS), jnp.float32, -s_in, s_in), 'br': jax.random.uniform(ks[2], (NUM_EXPERTS,), jnp.float32, -s_in, s_in), 'W1': jax.random.uniform(ks[3], (NUM_EXPERTS, D_MODEL, D_FF), jnp.float32, -s_in, s_in), 'b1': jax.random.uniform(ks[4], (NUM_EXPERTS, D_FF), jnp.float32, -s_in, s_in), 'W2': jax.random.uniform(ks[5], (NUM_EXPERTS, D_FF, D_MODEL), jnp.float32, -s_ff, s_ff), 'b2': jax.random.uniform(ks[6], (NUM_EXPERTS, D_MODEL), jnp.float32, -s_ff, s_ff)}
    _L2_ffn_all = _L2_ffn_setup()
    _L2_ffn_in = {k: v for k, v in _L2_ffn_all.items() if k in ('Wr', 'br', 'W1', 'b1', 'W2', 'b2')}
    del _L2_ffn_all

    def _L3_attn_setup():
        import jax, jax.numpy as jnp
        import numpy as np
        LN_EPS = 1e-05
        NEG_INF = -1e+38

        def _layer_norm(x, g, b):
            mu = x.mean(-1, keepdims=True)
            var = ((x - mu) ** 2).mean(-1, keepdims=True)
            return (x - mu) * jax.lax.rsqrt(var + LN_EPS) * g + b

        def _wkv(w, u, k, v):
            B, T, C = k.shape
            kt = jnp.swapaxes(k, 0, 1)
            vt = jnp.swapaxes(v, 0, 1)
            aa0 = jnp.zeros((B, C), k.dtype)
            bb0 = jnp.zeros((B, C), k.dtype)
            pp0 = jnp.full((B, C), NEG_INF, k.dtype)

            def step(carry, inp):
                aa, bb, pp = carry
                kk, vv = inp
                p = jnp.maximum(pp, u + kk)
                e1 = jnp.exp(pp - p)
                e2 = jnp.exp(u + kk - p)
                y = (e1 * aa + e2 * vv) / (e1 + e2)
                p2 = jnp.maximum(pp + w, w + kk)
                e1u = jnp.exp(pp + w - p2)
                e2u = jnp.exp(w + kk - p2)
                aa2 = e1u * aa + e2u * vv
                bb2 = e1u + e2u
                pp2 = p2 + jnp.log(bb2)
                return ((aa2, bb2, pp2), y)
            _, ys = jax.lax.scan(step, (aa0, bb0, pp0), (kt, vt))
            return jnp.swapaxes(ys, 0, 1)

        def _shift(h):
            return jnp.pad(h[:, :-1, :], ((0, 0), (1, 0), (0, 0)))
        key = jax.random.key(seed)
        B, T, C = (8, 512, 256)
        ks = jax.random.split(key, 12)
        s = 0.02
        return {'x': jax.random.normal(ks[0], (B, T, C), jnp.float32), 'time_decay': jax.random.normal(ks[1], (C,), jnp.float32) * 0.01, 'time_first': jax.random.normal(ks[2], (C,), jnp.float32) * 0.01, 'w_tk': jax.random.normal(ks[3], (C, C), jnp.float32) * s, 'w_tv': jax.random.normal(ks[4], (C, C), jnp.float32) * s, 'w_tr': jax.random.normal(ks[5], (C, C), jnp.float32) * s, 'w_ck': jax.random.normal(ks[6], (C, 4 * C), jnp.float32) * s, 'w_cv': jax.random.normal(ks[7], (4 * C, C), jnp.float32) * s, 'w_cr': jax.random.normal(ks[8], (C, C), jnp.float32) * s, 'ln1_g': jnp.ones((C,), jnp.float32), 'ln1_b': jnp.zeros((C,), jnp.float32), 'ln2_g': jnp.ones((C,), jnp.float32), 'ln2_b': jnp.zeros((C,), jnp.float32), 'mix_k': jnp.ones((1, 1, C), jnp.float32), 'mix_v': jnp.ones((1, 1, C), jnp.float32), 'mix_r': jnp.ones((1, 1, C), jnp.float32), 'cmix_k': jnp.ones((1, 1, C), jnp.float32), 'cmix_r': jnp.ones((1, 1, C), jnp.float32)}
    _L3_attn_all = _L3_attn_setup()
    _L3_attn_in = {k: v for k, v in _L3_attn_all.items() if k in ('time_decay', 'time_first', 'w_tk', 'w_tv', 'w_tr', 'w_ck', 'w_cv', 'w_cr', 'ln1_g', 'ln1_b', 'ln2_g', 'ln2_b', 'mix_k', 'mix_v', 'mix_r', 'cmix_k', 'cmix_r')}
    del _L3_attn_all

    def _L3_ffn_setup():
        import jax, jax.numpy as jnp
        import numpy as np
        B, T, D = (2, 256, 256)
        H, DK, K = (8, 128, 8)
        NKEYS = 64
        NEXP = NKEYS * NKEYS

        def _rmsnorm(x, w, eps=1e-06):
            inv = jax.lax.rsqrt(jnp.mean(x * x, axis=-1, keepdims=True) + eps)
            return x * inv * w
        key = jax.random.key(seed)
        ks = jax.random.split(key, 5)
        return {'x': jax.random.normal(ks[0], (B, T, D), jnp.float32), 'w_q': jax.random.normal(ks[1], (H * 2 * DK, D), jnp.float32) * 0.02, 'keys': jax.random.normal(ks[2], (H, NKEYS, 2, DK), jnp.float32) * 0.02, 'expert_down': jax.random.normal(ks[3], (NEXP, D), jnp.float32) * 0.02, 'expert_up': jax.random.normal(ks[4], (NEXP, D), jnp.float32) * 0.02, 'norm_w': jnp.ones((D,), jnp.float32)}
    _L3_ffn_all = _L3_ffn_setup()
    _L3_ffn_in = {k: v for k, v in _L3_ffn_all.items() if k in ('w_q', 'keys', 'expert_down', 'expert_up', 'norm_w')}
    del _L3_ffn_all
    return {'x': x, 'txt': txt, 'L0_tok_W': _L0_tok_in['W'], 'L0_tok_b': _L0_tok_in['b'], 'L0_attn_Wq': _L0_attn_in['Wq'], 'L0_attn_bq': _L0_attn_in['bq'], 'L0_attn_Wk': _L0_attn_in['Wk'], 'L0_attn_bk': _L0_attn_in['bk'], 'L0_attn_Wv': _L0_attn_in['Wv'], 'L0_attn_bv': _L0_attn_in['bv'], 'L0_attn_Wo': _L0_attn_in['Wo'], 'L0_attn_bo': _L0_attn_in['bo'], 'L0_ffn_router_w': _L0_ffn_in['router_w'], 'L0_ffn_router_b': _L0_ffn_in['router_b'], 'L0_ffn_w_gate': _L0_ffn_in['w_gate'], 'L0_ffn_w_up': _L0_ffn_in['w_up'], 'L0_ffn_w_down': _L0_ffn_in['w_down'], 'L0_ffn_sw_gate': _L0_ffn_in['sw_gate'], 'L0_ffn_sw_up': _L0_ffn_in['sw_up'], 'L0_ffn_sw_down': _L0_ffn_in['sw_down'], 'L1_attn_f_in_w': _L1_attn_in['f_in_w'], 'L1_attn_f_conv_w': _L1_attn_in['f_conv_w'], 'L1_attn_f_conv_b': _L1_attn_in['f_conv_b'], 'L1_attn_f_xproj_w': _L1_attn_in['f_xproj_w'], 'L1_attn_f_dt_w': _L1_attn_in['f_dt_w'], 'L1_attn_f_dt_b': _L1_attn_in['f_dt_b'], 'L1_attn_f_A_log': _L1_attn_in['f_A_log'], 'L1_attn_f_D': _L1_attn_in['f_D'], 'L1_attn_f_out_w': _L1_attn_in['f_out_w'], 'L1_attn_b_in_w': _L1_attn_in['b_in_w'], 'L1_attn_b_conv_w': _L1_attn_in['b_conv_w'], 'L1_attn_b_conv_b': _L1_attn_in['b_conv_b'], 'L1_attn_b_xproj_w': _L1_attn_in['b_xproj_w'], 'L1_attn_b_dt_w': _L1_attn_in['b_dt_w'], 'L1_attn_b_dt_b': _L1_attn_in['b_dt_b'], 'L1_attn_b_A_log': _L1_attn_in['b_A_log'], 'L1_attn_b_D': _L1_attn_in['b_D'], 'L1_attn_b_out_w': _L1_attn_in['b_out_w'], 'L1_ffn_fast_b': _L1_ffn_in['fast_b'], 'L1_ffn_w_fc': _L1_ffn_in['w_fc'], 'L1_ffn_w_proj': _L1_ffn_in['w_proj'], 'L1_ffn_u': _L1_ffn_in['u'], 'L1_ffn_v': _L1_ffn_in['v'], 'L1_ffn_gate': _L1_ffn_in['gate'], 'L2_attn_W_Q': _L2_attn_in['W_Q'], 'L2_attn_W_K': _L2_attn_in['W_K'], 'L2_attn_W_V': _L2_attn_in['W_V'], 'L2_ffn_Wr': _L2_ffn_in['Wr'], 'L2_ffn_br': _L2_ffn_in['br'], 'L2_ffn_W1': _L2_ffn_in['W1'], 'L2_ffn_b1': _L2_ffn_in['b1'], 'L2_ffn_W2': _L2_ffn_in['W2'], 'L2_ffn_b2': _L2_ffn_in['b2'], 'L3_attn_time_decay': _L3_attn_in['time_decay'], 'L3_attn_time_first': _L3_attn_in['time_first'], 'L3_attn_w_tk': _L3_attn_in['w_tk'], 'L3_attn_w_tv': _L3_attn_in['w_tv'], 'L3_attn_w_tr': _L3_attn_in['w_tr'], 'L3_attn_w_ck': _L3_attn_in['w_ck'], 'L3_attn_w_cv': _L3_attn_in['w_cv'], 'L3_attn_w_cr': _L3_attn_in['w_cr'], 'L3_attn_ln1_g': _L3_attn_in['ln1_g'], 'L3_attn_ln1_b': _L3_attn_in['ln1_b'], 'L3_attn_ln2_g': _L3_attn_in['ln2_g'], 'L3_attn_ln2_b': _L3_attn_in['ln2_b'], 'L3_attn_mix_k': _L3_attn_in['mix_k'], 'L3_attn_mix_v': _L3_attn_in['mix_v'], 'L3_attn_mix_r': _L3_attn_in['mix_r'], 'L3_attn_cmix_k': _L3_attn_in['cmix_k'], 'L3_attn_cmix_r': _L3_attn_in['cmix_r'], 'L3_ffn_w_q': _L3_ffn_in['w_q'], 'L3_ffn_keys': _L3_ffn_in['keys'], 'L3_ffn_expert_down': _L3_ffn_in['expert_down'], 'L3_ffn_expert_up': _L3_ffn_in['expert_up'], 'L3_ffn_norm_w': _L3_ffn_in['norm_w']}

def reference(x, txt, L0_tok_W, L0_tok_b, L0_attn_Wq, L0_attn_bq, L0_attn_Wk, L0_attn_bk, L0_attn_Wv, L0_attn_bv, L0_attn_Wo, L0_attn_bo, L0_ffn_router_w, L0_ffn_router_b, L0_ffn_w_gate, L0_ffn_w_up, L0_ffn_w_down, L0_ffn_sw_gate, L0_ffn_sw_up, L0_ffn_sw_down, L1_attn_f_in_w, L1_attn_f_conv_w, L1_attn_f_conv_b, L1_attn_f_xproj_w, L1_attn_f_dt_w, L1_attn_f_dt_b, L1_attn_f_A_log, L1_attn_f_D, L1_attn_f_out_w, L1_attn_b_in_w, L1_attn_b_conv_w, L1_attn_b_conv_b, L1_attn_b_xproj_w, L1_attn_b_dt_w, L1_attn_b_dt_b, L1_attn_b_A_log, L1_attn_b_D, L1_attn_b_out_w, L1_ffn_fast_b, L1_ffn_w_fc, L1_ffn_w_proj, L1_ffn_u, L1_ffn_v, L1_ffn_gate, L2_attn_W_Q, L2_attn_W_K, L2_attn_W_V, L2_ffn_Wr, L2_ffn_br, L2_ffn_W1, L2_ffn_b1, L2_ffn_W2, L2_ffn_b2, L3_attn_time_decay, L3_attn_time_first, L3_attn_w_tk, L3_attn_w_tv, L3_attn_w_tr, L3_attn_w_ck, L3_attn_w_cv, L3_attn_w_cr, L3_attn_ln1_g, L3_attn_ln1_b, L3_attn_ln2_g, L3_attn_ln2_b, L3_attn_mix_k, L3_attn_mix_v, L3_attn_mix_r, L3_attn_cmix_k, L3_attn_cmix_r, L3_ffn_w_q, L3_ffn_keys, L3_ffn_expert_down, L3_ffn_expert_up, L3_ffn_norm_w):
    import jax
    import jax.numpy as jnp

    def _L0_tok_ref(x, W, b):
        import jax, jax.numpy as jnp
        import numpy as np
        PATCH = 16
        B, C, H, Wd = x.shape
        ph = pw = PATCH
        gh, gw = (H // ph, Wd // pw)
        patches = x.reshape(B, C, gh, ph, gw, pw)
        patches = patches.transpose(0, 2, 4, 1, 3, 5).reshape(B, gh * gw, C * ph * pw)
        out = jnp.einsum('bnp,dp->bnd', patches, W) + b
        return out

    def _L0_attn_ref(hidden_states, Wq, bq, Wk, bk, Wv, bv, Wo, bo):
        import jax, jax.numpy as jnp
        import numpy as np
        H = 16
        GRID = 16
        TOK_PER_FRAME = GRID * GRID

        def _rope(x, pos, dim):
            half = dim // 2
            omega = jnp.arange(half, dtype=x.dtype) / (dim / 2.0)
            inv = 1.0 / 10000.0 ** omega
            freq = pos.astype(x.dtype)[:, None] * inv
            sin = jnp.concatenate([jnp.sin(freq), jnp.sin(freq)], axis=-1)
            cos = jnp.concatenate([jnp.cos(freq), jnp.cos(freq)], axis=-1)
            y = x.reshape(*x.shape[:-1], half, 2)
            y1, y2 = (y[..., 0], y[..., 1])
            rot = jnp.stack((-y2, y1), axis=-1).reshape(x.shape)
            return x * cos + rot * sin

        def _apply_3d_rope(qk, f_ids, h_ids, w_ids, d_dim):
            s = 0
            parts = []
            for pos in (f_ids, h_ids, w_ids):
                parts.append(_rope(qk[..., s:s + d_dim], pos, d_dim))
                s += d_dim
            if s < qk.shape[-1]:
                parts.append(qk[..., s:])
            return jnp.concatenate(parts, axis=-1)
        B, N, D = hidden_states.shape
        hd = D // H
        d_dim = 2 * (hd // 3 // 2)

        def heads(x):
            return x.reshape(B, N, H, hd).transpose(0, 2, 1, 3)
        q = heads(hidden_states @ Wq + bq)
        k = heads(hidden_states @ Wk + bk)
        v = heads(hidden_states @ Wv + bv)
        ids = jnp.arange(N)
        f_ids = ids // TOK_PER_FRAME
        rem = ids - TOK_PER_FRAME * f_ids
        h_ids = rem // GRID
        w_ids = rem - GRID * h_ids
        q = _apply_3d_rope(q, f_ids, h_ids, w_ids, d_dim)
        k = _apply_3d_rope(k, f_ids, h_ids, w_ids, d_dim)
        scale = hd ** (-0.5)
        attn = jnp.einsum('bhqd,bhkd->bhqk', q, k) * scale
        attn = jax.nn.softmax(attn.astype(jnp.float32), axis=-1).astype(q.dtype)
        ctx = jnp.einsum('bhqk,bhkd->bhqd', attn, v)
        ctx = ctx.transpose(0, 2, 1, 3).reshape(B, N, D)
        return ctx @ Wo + bo

    def _L0_ffn_ref(x, router_w, router_b, w_gate, w_up, w_down, sw_gate, sw_up, sw_down):
        import jax, jax.numpy as jnp
        import numpy as np
        B, S, D = (1, 512, 256)
        F = 352
        E = 16
        K = 2
        CAP_FACTOR = 1.25

        def _mlp(h, wg, wu, wd):
            return jax.nn.silu(h @ wg) * (h @ wu) @ wd
        b, s, d = x.shape
        N = b * s
        NK = N * K
        C = int(np.ceil(CAP_FACTOR * NK / E))
        x_tokens = x.reshape(N, d)
        logits = x_tokens @ router_w + router_b
        probs = jax.nn.softmax(logits, axis=-1)
        vals, idx = jax.lax.top_k(probs, K)
        vals = vals / (jnp.sum(vals, axis=-1, keepdims=True) + 1e-09)
        idx_flat = idx.reshape(NK)
        vals_flat = vals.reshape(NK)
        oh_e = jax.nn.one_hot(idx_flat, E, dtype=x.dtype)
        pos = (jnp.cumsum(oh_e, axis=0) * oh_e).sum(axis=1) - 1
        within = (pos < C).astype(x.dtype)
        pos_c = jnp.clip(pos, 0, C - 1).astype(jnp.int32)
        token_ids = jnp.arange(NK) // K
        x_pair = x_tokens[token_ids] * within[:, None]
        expert_inputs = jnp.zeros((E, C, d), x.dtype).at[idx_flat, pos_c].add(x_pair)
        expert_outputs = jax.vmap(_mlp)(expert_inputs, w_gate, w_up, w_down)
        gathered = expert_outputs[idx_flat, pos_c] * (vals_flat * within)[:, None]
        output_tokens = gathered.reshape(N, K, d).sum(axis=1)
        return x + _mlp(x, sw_gate, sw_up, sw_down) + output_tokens.reshape(b, s, d)

    def _L1_attn_ref(x, f_in_w, f_conv_w, f_conv_b, f_xproj_w, f_dt_w, f_dt_b, f_A_log, f_D, f_out_w, b_in_w, b_conv_w, b_conv_b, b_xproj_w, b_dt_w, b_dt_b, b_A_log, b_D, b_out_w):
        import jax, jax.numpy as jnp
        import numpy as np
        D_MODEL = 256
        D_STATE = 16
        D_CONV = 4
        EXPAND = 2
        D_INNER = EXPAND * D_MODEL
        DT_RANK = (D_MODEL + 15) // 16
        BATCH = 2
        SEQ = 256

        def _mamba(x, in_w, conv_w, conv_b, xproj_w, dt_w, dt_b, A_log, D_param, out_w):
            Bsz, L, _ = x.shape
            xz = x @ in_w.T
            xh, z = jnp.split(xz, 2, axis=-1)
            xp = jnp.pad(xh, ((0, 0), (D_CONV - 1, 0), (0, 0)))
            xc = conv_b + sum((xp[:, k:k + L, :] * conv_w[:, k] for k in range(D_CONV)))
            xc = jax.nn.silu(xc)
            proj = xc @ xproj_w.T
            dt = proj[..., :DT_RANK]
            Bm = proj[..., DT_RANK:DT_RANK + D_STATE]
            Cm = proj[..., DT_RANK + D_STATE:]
            delta = jax.nn.softplus(dt @ dt_w.T + dt_b)
            A = -jnp.exp(A_log)
            deltaA = jnp.exp(jnp.einsum('bld,dn->bldn', delta, A))
            deltaBu = jnp.einsum('bld,bln->bldn', delta * xc, Bm)

            def step(h, inp):
                dA, dBu, c = inp
                h = dA * h + dBu
                y = jnp.einsum('bdn,bn->bd', h, c)
                return (h, y)
            h0 = jnp.zeros((Bsz, D_INNER, D_STATE), x.dtype)
            _, ys = jax.lax.scan(step, h0, (deltaA.transpose(1, 0, 2, 3), deltaBu.transpose(1, 0, 2, 3), Cm.transpose(1, 0, 2)))
            y = ys.transpose(1, 0, 2) + xc * D_param
            y = y * jax.nn.silu(z)
            return y @ out_w.T
        y_fwd = _mamba(x, f_in_w, f_conv_w, f_conv_b, f_xproj_w, f_dt_w, f_dt_b, f_A_log, f_D, f_out_w)
        y_bwd = jnp.flip(_mamba(jnp.flip(x, 1), b_in_w, b_conv_w, b_conv_b, b_xproj_w, b_dt_w, b_dt_b, b_A_log, b_D, b_out_w), 1)
        return y_fwd + y_bwd

    def _L1_ffn_ref(x, fast_b, w_fc, w_proj, u, v, gate):
        import jax, jax.numpy as jnp
        import numpy as np

        def _bitlinear(x, w_latent):
            scale = jax.lax.stop_gradient(jnp.clip(jnp.mean(jnp.abs(w_latent), axis=1, keepdims=True), 1e-05, None))
            tern = jnp.clip(jnp.round(w_latent / scale), -1.0, 1.0)
            w = w_latent + jax.lax.stop_gradient(tern - w_latent)
            return x @ (w * scale).T
        h = _bitlinear(x, w_fc) + gate * (x @ v.T @ fast_b.T @ u.T)
        r = jnp.maximum(h, 0.0)
        return _bitlinear(r * r, w_proj)

    def _L2_attn_ref(embeddings, W_Q, W_K, W_V):
        import jax, jax.numpy as jnp
        import numpy as np
        B, S, D = (4, 512, 256)

        def _xavier(key, shape):
            bound = float(np.sqrt(6.0 / (shape[0] + shape[1])))
            return jax.random.uniform(key, shape, dtype=jnp.float32, minval=-bound, maxval=bound)
        _, seq_len, d = embeddings.shape
        Q = embeddings @ W_Q
        K = embeddings @ W_K
        V = embeddings @ W_V
        scale = 1.0 / jnp.sqrt(jnp.float32(d))
        scores = jnp.einsum('bqd,bkd->bqk', Q, K) * scale
        causal = jnp.tril(jnp.ones((seq_len, seq_len), dtype=bool))
        scores = jnp.where(causal[None, :, :], scores, -jnp.inf)
        probs = jax.nn.softmax(scores, axis=-1)
        return jnp.einsum('bqk,bkd->bqd', probs, V)

    def _L2_ffn_ref(x, Wr, br, W1, b1, W2, b2):
        import jax, jax.numpy as jnp
        import numpy as np
        D_MODEL = 256
        D_FF = 1024
        NUM_EXPERTS = 8
        B, N = (16, 256)
        scores = jnp.einsum('bh,he->be', x.mean(axis=1), Wr) + br
        top1 = jnp.argmax(scores, axis=-1)
        w1 = W1[top1]
        c1 = b1[top1]
        w2 = W2[top1]
        c2 = b2[top1]
        h = jax.nn.relu(jnp.einsum('bnh,bhf->bnf', x, w1) + c1[:, None, :])
        out = jnp.einsum('bnf,bfh->bnh', h, w2) + c2[:, None, :]
        return out

    def _L3_attn_ref(x, time_decay, time_first, w_tk, w_tv, w_tr, w_ck, w_cv, w_cr, ln1_g, ln1_b, ln2_g, ln2_b, mix_k, mix_v, mix_r, cmix_k, cmix_r):
        import jax, jax.numpy as jnp
        import numpy as np
        LN_EPS = 1e-05
        NEG_INF = -1e+38

        def _layer_norm(x, g, b):
            mu = x.mean(-1, keepdims=True)
            var = ((x - mu) ** 2).mean(-1, keepdims=True)
            return (x - mu) * jax.lax.rsqrt(var + LN_EPS) * g + b

        def _wkv(w, u, k, v):
            B, T, C = k.shape
            kt = jnp.swapaxes(k, 0, 1)
            vt = jnp.swapaxes(v, 0, 1)
            aa0 = jnp.zeros((B, C), k.dtype)
            bb0 = jnp.zeros((B, C), k.dtype)
            pp0 = jnp.full((B, C), NEG_INF, k.dtype)

            def step(carry, inp):
                aa, bb, pp = carry
                kk, vv = inp
                p = jnp.maximum(pp, u + kk)
                e1 = jnp.exp(pp - p)
                e2 = jnp.exp(u + kk - p)
                y = (e1 * aa + e2 * vv) / (e1 + e2)
                p2 = jnp.maximum(pp + w, w + kk)
                e1u = jnp.exp(pp + w - p2)
                e2u = jnp.exp(w + kk - p2)
                aa2 = e1u * aa + e2u * vv
                bb2 = e1u + e2u
                pp2 = p2 + jnp.log(bb2)
                return ((aa2, bb2, pp2), y)
            _, ys = jax.lax.scan(step, (aa0, bb0, pp0), (kt, vt))
            return jnp.swapaxes(ys, 0, 1)

        def _shift(h):
            return jnp.pad(h[:, :-1, :], ((0, 0), (1, 0), (0, 0)))
        h = _layer_norm(x, ln1_g, ln1_b)
        hp = _shift(h)
        xk = h * mix_k + hp * (1.0 - mix_k)
        xv = h * mix_v + hp * (1.0 - mix_v)
        xr = h * mix_r + hp * (1.0 - mix_r)
        k = xk @ w_tk
        v = xv @ w_tv
        r = jax.nn.sigmoid(xr @ w_tr)
        y = _wkv(time_decay, time_first, k, v)
        x = x + r * y
        h2 = _layer_norm(x, ln2_g, ln2_b)
        hp2 = _shift(h2)
        ck = h2 * cmix_k + hp2 * (1.0 - cmix_k)
        cr = h2 * cmix_r + hp2 * (1.0 - cmix_r)
        kk = jnp.square(jax.nn.relu(ck @ w_ck))
        x = x + jax.nn.sigmoid(cr @ w_cr) * (kk @ w_cv)
        return x

    def _L3_ffn_ref(x, w_q, keys, expert_down, expert_up, norm_w):
        import jax, jax.numpy as jnp
        import numpy as np
        B, T, D = (2, 256, 256)
        H, DK, K = (8, 128, 8)
        NKEYS = 64
        NEXP = NKEYS * NKEYS

        def _rmsnorm(x, w, eps=1e-06):
            inv = jax.lax.rsqrt(jnp.mean(x * x, axis=-1, keepdims=True) + eps)
            return x * inv * w
        b, t, d = x.shape
        xn = _rmsnorm(x, norm_w)
        q = (xn @ w_q.T).reshape(b, t, H, 2, DK)
        sim1 = jnp.einsum('bthd,hkd->bthk', q[..., 0, :], keys[:, :, 0, :])
        sim2 = jnp.einsum('bthd,hkd->bthk', q[..., 1, :], keys[:, :, 1, :])
        s1, i1 = jax.lax.top_k(sim1, K)
        s2, i2 = jax.lax.top_k(sim2, K)
        all_idx = (i1[..., :, None] * NKEYS + i2[..., None, :]).reshape(b, t, H, K * K)
        all_sc = (s1[..., :, None] + s2[..., None, :]).reshape(b, t, H, K * K)
        fs, pk = jax.lax.top_k(all_sc, K)
        fi = jnp.take_along_axis(all_idx, pk, axis=-1)
        wd = expert_down[fi]
        wu = expert_up[fi]
        hidden = jax.nn.gelu(jnp.einsum('btd,bthkd->bthk', xn, wd), approximate=False)
        hidden = hidden * jax.nn.relu(fs)
        return jnp.einsum('bthk,bthkd->btd', hidden, wu)
    h = _L0_tok_ref(x, L0_tok_W, L0_tok_b)
    h = jnp.concatenate([h, txt], axis=1)
    h = h + _L0_attn_ref(_layernorm(h, axis=-1), L0_attn_Wq, L0_attn_bq, L0_attn_Wk, L0_attn_bk, L0_attn_Wv, L0_attn_bv, L0_attn_Wo, L0_attn_bo)
    h = h + _L0_ffn_ref(_layernorm(h, axis=-1), L0_ffn_router_w, L0_ffn_router_b, L0_ffn_w_gate, L0_ffn_w_up, L0_ffn_w_down, L0_ffn_sw_gate, L0_ffn_sw_up, L0_ffn_sw_down)
    h = h + _L1_attn_ref(_layernorm(h, axis=-1), L1_attn_f_in_w, L1_attn_f_conv_w, L1_attn_f_conv_b, L1_attn_f_xproj_w, L1_attn_f_dt_w, L1_attn_f_dt_b, L1_attn_f_A_log, L1_attn_f_D, L1_attn_f_out_w, L1_attn_b_in_w, L1_attn_b_conv_w, L1_attn_b_conv_b, L1_attn_b_xproj_w, L1_attn_b_dt_w, L1_attn_b_dt_b, L1_attn_b_A_log, L1_attn_b_D, L1_attn_b_out_w)
    h = h + _L1_ffn_ref(_layernorm(h, axis=-1), L1_ffn_fast_b, L1_ffn_w_fc, L1_ffn_w_proj, L1_ffn_u, L1_ffn_v, L1_ffn_gate)
    h = h + _L2_attn_ref(_layernorm(h, axis=-1), L2_attn_W_Q, L2_attn_W_K, L2_attn_W_V)
    h = h + _L2_ffn_ref(_layernorm(h, axis=-1), L2_ffn_Wr, L2_ffn_br, L2_ffn_W1, L2_ffn_b1, L2_ffn_W2, L2_ffn_b2)
    h = h + _L3_attn_ref(_layernorm(h, axis=-1), L3_attn_time_decay, L3_attn_time_first, L3_attn_w_tk, L3_attn_w_tv, L3_attn_w_tr, L3_attn_w_ck, L3_attn_w_cv, L3_attn_w_cr, L3_attn_ln1_g, L3_attn_ln1_b, L3_attn_ln2_g, L3_attn_ln2_b, L3_attn_mix_k, L3_attn_mix_v, L3_attn_mix_r, L3_attn_cmix_k, L3_attn_cmix_r)
    h = h + _L3_ffn_ref(_layernorm(h, axis=-1), L3_ffn_w_q, L3_ffn_keys, L3_ffn_expert_down, L3_ffn_expert_up, L3_ffn_norm_w)
    return h

_drawn_inputs = setup_inputs


def setup_inputs(seed=0):
    import zlib

    import numpy as np

    out = dict(_drawn_inputs(seed))
    spreads = {'L0_attn_bq': (0.0, 0.8),
     'L0_attn_bk': (0.0, 0.8),
     'L0_attn_bv': (0.0, 0.1),
     'L0_attn_bo': (0.0, 0.1),
     'L0_ffn_router_b': (0.0, 0.8),
     'L1_attn_f_conv_b': (0.0, 0.8),
     'L1_attn_f_D': (1.0, 0.6),
     'L1_attn_b_conv_b': (0.0, 0.8),
     'L1_attn_b_D': (1.0, 0.6),
     'L3_attn_ln1_g': (1.0, 0.6),
     'L3_attn_ln1_b': (0.0, 0.294),
     'L3_attn_ln2_g': (1.0, 0.6),
     'L3_attn_ln2_b': (0.0, 0.8),
     'L3_attn_mix_k': (1.0, 0.6),
     'L3_attn_mix_v': (1.0, 0.6),
     'L3_attn_mix_r': (1.0, 0.6),
     'L3_attn_cmix_k': (1.0, 0.6),
     'L3_attn_cmix_r': (1.0, 0.6),
     'L3_ffn_norm_w': (1.0, 0.6)}
    factors = {'L0_tok_b': 7.814,
     'L0_attn_Wq': 8.0,
     'L0_attn_Wk': 8.0,
     'L0_ffn_router_w': 8.0,
     'L0_ffn_w_gate': 8.0,
     'L0_ffn_w_up': 8.0,
     'L0_ffn_w_down': 8.0,
     'L0_ffn_sw_gate': 5.722,
     'L0_ffn_sw_up': 5.662,
     'L0_ffn_sw_down': 5.668,
     'L1_attn_f_in_w': 8.0,
     'L1_attn_f_conv_w': 8.0,
     'L1_attn_f_xproj_w': 8.0,
     'L1_attn_f_dt_w': 8.0,
     'L1_attn_f_dt_b': 8.0,
     'L1_attn_f_A_log': 8.0,
     'L1_attn_f_out_w': 8.0,
     'L1_attn_b_in_w': 8.0,
     'L1_attn_b_conv_w': 8.0,
     'L1_attn_b_xproj_w': 8.0,
     'L1_attn_b_dt_w': 8.0,
     'L1_attn_b_dt_b': 8.0,
     'L1_attn_b_A_log': 8.0,
     'L1_attn_b_out_w': 8.0,
     'L1_ffn_fast_b': 8.0,
     'L1_ffn_w_fc': 5.202,
     'L1_ffn_w_proj': 4.732,
     'L1_ffn_u': 8.0,
     'L1_ffn_v': 8.0,
     'L2_ffn_b1': 23.515,
     'L2_ffn_b2': 18.206,
     'L3_attn_time_decay': 8.0,
     'L3_attn_time_first': 27.484,
     'L3_attn_w_tr': 3.35,
     'L3_attn_w_ck': 3.928,
     'L3_attn_w_cv': 3.601,
     'L3_attn_w_cr': 8.0,
     'L3_ffn_w_q': 8.0,
     'L3_ffn_keys': 8.0,
     'L3_ffn_expert_down': 8.0,
     'L3_ffn_expert_up': 8.0,
     'L2_ffn_br': 2.696}
    for name, (base, spread) in spreads.items():
        noise = np.random.default_rng([zlib.crc32(name.encode()), seed]).standard_normal(out[name].shape)
        drawn = base * np.exp(spread * noise) if base else spread * noise
        out[name] = jnp.asarray(drawn.astype(out[name].dtype))
    for name, factor in factors.items():
        out[name] = (out[name] * factor).astype(out[name].dtype)
    return out
```

```python
from contextlib import ExitStack


import numpy as np
import concourse.bass as bass
from concourse import mybir

F32 = mybir.dt.float32
U32 = mybir.dt.uint32
I32 = mybir.dt.int32
ALU = mybir.AluOpType
ACT = mybir.ActivationFunctionType
AX = mybir.AxisListType

P = 128
B = 32
GRID = 6
IMG = GRID * GRID
TXT = 77
N = IMG + TXT
T = B * N
D = 256
DK = D // P
GB = 4
GT = GB * N
GROUPS = B // GB
LN_EPS = 1e-5


EXP_LN = "natural_log_exp_and_others"


class Stage:

    def __init__(self, nc, name):
        self.nc, self.name, self.stack, self.sems = nc, name, ExitStack(), []

    def __enter__(self):
        return self

    def __exit__(self, *exc):
        self.stack.close()

    def sbuf(self, name, shape, dt=F32):
        return self.stack.enter_context(self.nc.sbuf_tensor(f"{self.name}_{name}", shape, dt))

    def psum(self, name, shape=(P, 512), dt=F32):
        return self.stack.enter_context(self.nc.psum_tensor(f"{self.name}_{name}", list(shape), dt))

    def sem(self, name):
        s = self.stack.enter_context(self.nc.semaphore(f"{self.name}_{name}"))
        self.sems.append(s)
        return s

    def clear(self, pool_dmas=False):
        def zero(eng):
            at = 0
            while at < len(self.sems):
                last = at
                while last + 1 < len(self.sems) and self.sems[last + 1].num == self.sems[last].num + 1:
                    last += 1
                numbers = range(self.sems[at].num, self.sems[last].num + 1)
                if pool_dmas:
                    eng.dma_reset(numbers)
                eng.sem_clear(numbers)
                at = last + 1

        with self.nc.Block(no_gpsimd_drain=True) as block:
            if pool_dmas:
                block.gpsimd(zero)
            else:
                block.sync(zero)


def group_cols(g):
    return bass.ds(g * GT, GT)


class Norm:

    def __init__(self, st, mean_ps, var_ps, name="ln", width=GT):
        self.mean_ps, self.var_ps, self.width = mean_ps, var_ps, width
        self.centred = st.sbuf(f"{name}_centred", [P, DK, width])
        self.square = st.sbuf(f"{name}_square", [P, DK, width])
        self.log_var = st.sbuf(f"{name}_log_var", [P, width])
        self.rstd = st.sbuf(f"{name}_rstd", [P, width])
        self.out = st.sbuf(f"{name}_out", [P, DK, width])
        self.mean_ready = st.sem(f"{name}_mean_ready")
        self.centred_ready = st.sem(f"{name}_centred_ready")
        self.square_ready = st.sem(f"{name}_square_ready")
        self.var_ready = st.sem(f"{name}_var_ready")
        self.log_ready = st.sem(f"{name}_log_ready")
        self.rstd_ready = st.sem(f"{name}_rstd_ready")
        self.ready = st.sem(f"{name}_ready")

    def tensor_mean(self, nc, pe, ones, x):
        for k in range(DK):
            mm = nc.tensor.matmul(self.mean_ps[:, 0:self.width], ones[:, :], x(k), start=(k == 0), stop=(k == DK - 1))
        mm.then_inc(self.mean_ready, 1)

    def tensor_var(self, nc, pe, ones):
        pe.wait_ge(self.square_ready, 1)
        for k in range(DK):
            mm = nc.tensor.matmul(self.var_ps[:, 0:self.width], ones[:, :], self.square[:, k, :],
                                  start=(k == 0), stop=(k == DK - 1))
        mm.then_inc(self.var_ready, 1)

    def scalar(self, nc, act, eps_col):
        act.wait_ge(self.centred_ready, 1)
        nc.scalar.activation(self.square[:, :, :], self.centred[:, :, :], ACT.Square).then_inc(self.square_ready, 1)
        act.wait_ge(self.var_ready, 1)
        nc.scalar.activation(self.log_var[:, :], self.var_ps[:, 0:self.width], ACT.Ln, bias=eps_col[:, 0:1])\
            .then_inc(self.log_ready, 1)
        act.wait_ge(self.log_ready, 1)
        nc.scalar.activation(self.rstd[:, :], self.log_var[:, :], ACT.Exp, scale=-0.5).then_inc(self.rstd_ready, 1)

    def vector(self, nc, dve, x_all):
        dve.wait_ge(self.mean_ready, 1)
        nc.vector.tensor_tensor(self.centred[:, :, :], x_all,
                                self.mean_ps[:, 0:self.width].unsqueeze(1).to_broadcast([P, DK, self.width]),
                                ALU.subtract).then_inc(self.centred_ready, 1)
        dve.wait_ge(self.rstd_ready, 1)
        dve.wait_ge(self.centred_ready, 1)
        nc.vector.tensor_tensor(self.out[:, :, :], self.centred[:, :, :],
                                self.rstd[:, :].unsqueeze(1).to_broadcast([P, DK, self.width]),
                                ALU.mult).then_inc(self.ready, 1)


def constants(nc, c):
    with Stage(nc, "const") as st:
        zero_done, done = st.sem("zero"), st.sem("done")
        with nc.Block() as block:
            @block.gpsimd
            def _(pool):
                nc.gpsimd.memset(c["ones"][:, :], 1.0 / D).then_inc(done, 1)
                nc.gpsimd.memset(c["eps"][:, :], LN_EPS).then_inc(done, 1)
                nc.gpsimd.memset(c["ident"][:, :], 0.0).then_inc(zero_done, 1)
                pool.wait_ge(zero_done, 1)
                nc.gpsimd.affine_select(out=c["ident"][:, :], in_=c["ident"][:, :], compare_op=ALU.not_equal, fill=1.0,
                                        base=0, pattern=[[-1, P]], channel_multiplier=1).then_inc(done, 1)
                pool.wait_ge(done, 3)
        st.clear()


def tok(nc, h, c, h_text, patches, w_t, bias):
    KB = patches.shape[1]
    CB = 8
    with Stage(nc, "tok") as st:
        px = st.sbuf("px", [P, KB, B * IMG])
        w = st.sbuf("w", [P, KB, D])
        b = st.sbuf("b", [P, DK])
        ps = [st.psum(f"ps{i}") for i in range(8)]
        text_in, w_in, mm_done, tok_done = (st.sem(x) for x in ("text_in", "w_in", "mm_done", "tok_done"))
        px_in = [st.sem(f"px_in{i}") for i in range(B // CB)]
        with nc.Block() as block:
            @block.sync
            def _(sp):
                sp.dma_start(w[:, :, :], w_t).then_inc(w_in, 16)
                sp.dma_start(b[:, :], bias).then_inc(w_in, 16)
                for i in range(B // CB):
                    sp.dma_start(px[:, :, i * CB * IMG:(i + 1) * CB * IMG], patches[:, :, i * CB * IMG:(i + 1) * CB * IMG])\
                        .then_inc(px_in[i], 16)

            @block.tensor
            def _(pe):
                pe.wait_ge(w_in, 32)
                for i in range(B // CB):
                    pe.wait_ge(px_in[i], 16)
                    for m in range(DK):
                        for k in range(KB):
                            mm = nc.tensor.matmul(ps[2 * i + m][:, 0:CB * IMG], w[:, k, m * P:(m + 1) * P],
                                                  px[:, k, i * CB * IMG:(i + 1) * CB * IMG], start=(k == 0), stop=(k == KB - 1))
                        mm.then_inc(mm_done, 1)

            @block.scalar
            def _(act):
                act.dma_start(h[:, :, :], h_text).then_inc(text_in, 16)
                nc.scalar.preload_act_table_set(EXP_LN)
                act.wait_ge(text_in, 16)
                act.wait_ge(w_in, 32)
                for i in range(B // CB):
                    for m in range(DK):
                        act.wait_ge(mm_done, 2 * i + m + 1)
                        dst = h[:, m, :].rearrange("p (b n) -> p b n", n=N)[:, i * CB:(i + 1) * CB, 0:IMG]
                        nc.scalar.activation(dst, ps[2 * i + m][:, 0:CB * IMG].rearrange("p (b n) -> p b n", n=IMG),
                                             ACT.Identity, bias=b[:, m:m + 1]).then_inc(tok_done, 1)
        st.clear()


def l0_attn(nc, h, c, wq, wq_rot, wk, wk_rot, wv, wo, biases, cos, sin, even):
    H, HD = 16, 16
    UNITS = GB * 4
    with Stage(nc, "at0") as st:
        W = {x: st.sbuf(x, [P, DK, D]) for x in ("wq", "wqr", "wk", "wkr", "wv", "wo")}
        bs = st.sbuf("bs", [P, 6, DK])
        cs = st.sbuf("cos", [P, DK, N])
        sn = st.sbuf("sin", [P, DK, N])
        ev = st.sbuf("even", [P, 2])
        ps = [st.psum(f"ps{i}") for i in range(8)]
        norm = Norm(st, ps[0], ps[1])
        rot_a = st.sbuf("rot_a", [P, 4, GT])
        rot_b = st.sbuf("rot_b", [P, 4, GT])
        q = st.sbuf("q", [P, DK, GT])
        kk = st.sbuf("k", [P, DK, GT])
        kpar = [st.sbuf("k_even", [P, DK, GT]), st.sbuf("k_odd", [P, DK, GT])]
        v = st.sbuf("v", [N, GB, H, HD + 1])
        NE = 3
        low = st.sbuf("shifted", [N, NE, 4 * N])
        ex = st.sbuf("ex", [N, NE, 4 * N])
        exT = st.sbuf("exT", [N, NE, 4 * N])
        mx = st.sbuf("mx", [N, UNITS, 4])
        rs = st.sbuf("rs", [N, GB, H])
        cn = st.sbuf("cn", [N, GB, D])
        ctxT = st.sbuf("ctxT", [P, DK, GT])
        (w_in, ones_set, proj_done, a_done, b_done, q_done, k_done, kpar_done, v_mm, v_done, s_done, mx_done, low_done,
         ex_done, t_done, exT_done, av_done, rs_done, cn_done, ct_done, ctx_done, o_done, res_done) = (
            st.sem(x) for x in ("w_in", "ones_set", "proj_done", "a_done", "b_done", "q_done", "k_done", "kpar_done", "v_mm",
                                "v_done", "s_done", "mx_done", "low_done", "ex_done", "t_done", "exT_done", "av_done",
                                "rs_done", "cn_done", "ct_done", "ctx_done", "o_done", "res_done"))
        with nc.Block() as block:
            @block.sync
            def _(sp):
                for x, src in (("wq", wq), ("wqr", wq_rot), ("wk", wk), ("wkr", wk_rot), ("wv", wv), ("wo", wo)):
                    sp.dma_start(W[x][:, :, :], src.rearrange("(k p) n -> p k n", p=P)).then_inc(w_in, 16)
                sp.dma_start(bs[:, :, :], biases).then_inc(w_in, 16)
                sp.dma_start(cs[:, :, :], cos).then_inc(w_in, 16)
                sp.dma_start(sn[:, :, :], sin).then_inc(w_in, 16)
                sp.dma_start(ev[:, :], even).then_inc(w_in, 16)
                sp.wait_ge(w_in, 160)

            @block.gpsimd
            def _(pool):
                nc.gpsimd.memset(v[:, :, :, :], 1.0).then_inc(ones_set, 1)

            @block.scalar
            def _(act):
                nc.scalar.preload_act_table_set(EXP_LN)
        st.clear()
        S_BANK, T_BANK, C_BANK, CT_BANK = (0, 1, 2), (3, 4), (5, 6), 7

        def head(r, j):
            return 8 * (j // 2) + 2 * r + j % 2

        with nc.Fori(0, GROUPS) as g:
            with nc.Block(no_gpsimd_drain=True) as block:
                @block.tensor
                def _(pe):
                    norm.tensor_mean(nc, pe, c["ones"], lambda k: h[:, k, group_cols(g)])
                    norm.tensor_var(nc, pe, c["ones"])
                    pe.wait_ge(norm.ready, 1)
                    for i, x in enumerate(("wq", "wqr", "wk", "wkr")):
                        for m in range(DK):
                            for k in range(DK):
                                mm = nc.tensor.matmul(ps[2 * i + m][:, 0:GT], W[x][:, k, m * P:(m + 1) * P],
                                                      norm.out[:, k, :], start=(k == 0), stop=(k == DK - 1))
                            mm.then_inc(proj_done, 1)
                    for b in range(GB):
                        if b % 2 == 0:
                            pe.wait_ge(b_done if b else a_done, 2)
                        bank = ps[2 * (b // 2)]
                        for k in range(DK):
                            mm = nc.tensor.matmul(bank[0:N, (b % 2) * D:(b % 2 + 1) * D], norm.out[:, k, b * N:(b + 1) * N],
                                                  W["wv"][:, k, :], start=(k == 0), stop=(k == DK - 1))
                        if b % 2:
                            mm.then_inc(v_mm, 1)

                    def scores(u):
                        b, r = u // 4, u % 4
                        if u < 3:
                            pe.wait_ge(v_done, GB // 2)
                            pe.wait_ge(b_done, 4)
                            pe.wait_ge(q_done, 2)
                            pe.wait_ge(kpar_done, 4)
                        else:
                            pe.wait_ge(low_done, u - 2)
                        for j in range(4):
                            m = j // 2
                            mm = nc.tensor.matmul(ps[S_BANK[u % 3]][0:N, j * N:(j + 1) * N],
                                                  q[32 * r:32 * r + 32, m, b * N:(b + 1) * N],
                                                  kpar[j % 2][32 * r:32 * r + 32, m, b * N:(b + 1) * N], start=True, stop=True)
                        mm.then_inc(s_done, 1)

                    def turn(u):
                        pe.wait_ge(ex_done, u + 1)
                        if u >= 2:
                            pe.wait_ge(exT_done, u - 1)
                        for j in range(4):
                            mm = nc.tensor.transpose(ps[T_BANK[u % 2]][0:N, j * N:(j + 1) * N],
                                                     ex[:, u % NE, j * N:(j + 1) * N], c["ident"][0:N, 0:N])
                        mm.then_inc(t_done, 1)

                    def values(u):
                        b, r = u // 4, u % 4
                        pe.wait_ge(exT_done, u + 1)
                        if r == 0 and b >= 2:
                            pe.wait_ge(cn_done, b - 1)
                        for j in range(4):
                            hd = head(r, j)
                            mm = nc.tensor.matmul(ps[C_BANK[b % 2]][0:N, hd * (HD + 1):(hd + 1) * (HD + 1)],
                                                  exT[:, u % NE, j * N:(j + 1) * N], v[:, b, hd, :], start=True, stop=True)
                        mm.then_inc(av_done, 1)

                    def turn_context(b):
                        pe.wait_ge(cn_done, b + 1)
                        if b >= 1:
                            pe.wait_ge(ctx_done, 2 * b)
                        for m in range(DK):
                            mm = nc.tensor.transpose(ps[CT_BANK][:, m * N:(m + 1) * N], cn[:, b, m * P:(m + 1) * P],
                                                     c["ident"][0:N, 0:N])
                        mm.then_inc(ct_done, 1)

                    for u in range(UNITS + 3):
                        if u < UNITS:
                            scores(u)
                        if 1 <= u <= UNITS:
                            turn(u - 1)
                        if 2 <= u <= UNITS + 1:
                            values(u - 2)
                        if u >= 6 and (u - 6) % 4 == 0:
                            turn_context((u - 6) // 4)
                    pe.wait_ge(ctx_done, 2 * GB)
                    pe.wait_ge(low_done, UNITS)
                    for m in range(DK):
                        for k in range(DK):
                            mm = nc.tensor.matmul(ps[m][:, 0:GT], W["wo"][:, k, m * P:(m + 1) * P], ctxT[:, k, :],
                                                  start=(k == 0), stop=(k == DK - 1))
                        mm.then_inc(o_done, 1)

                @block.scalar
                def _(act):
                    norm.scalar(nc, act, c["eps"])
                    for b in range(0, GB, 2):
                        act.wait_ge(v_mm, b // 2 + 1)
                        nc.scalar.activation(v[:, b:b + 2, :, 0:HD],
                                             ps[b][0:N, :].rearrange("p (b h e) -> p b h e", b=2, e=HD),
                                             ACT.Copy).then_inc(v_done, 1)
                    for u in range(UNITS + 1):
                        if u < UNITS:
                            act.wait_ge(low_done, u + 1)
                            if u >= NE:
                                act.wait_ge(t_done, u - NE + 1)
                            nc.scalar.activation(ex[:, u % NE, :], low[:, u % NE, :], ACT.Exp, scale=HD ** -0.5)\
                                .then_inc(ex_done, 1)
                        if u >= 1:
                            act.wait_ge(t_done, u)
                            if u - 1 >= NE:
                                act.wait_ge(av_done, u - NE)
                            nc.scalar.activation(exT[:, (u - 1) % NE, :], ps[T_BANK[(u - 1) % 2]][0:N, 0:4 * N], ACT.Copy)\
                                .then_inc(exT_done, 1)
                        if u >= 7 and (u - 7) % 4 == 0 or u == UNITS:
                            b = (u - 7) // 4 if u < UNITS else GB - 1
                            act.wait_ge(ct_done, b + 1)
                            for m in range(DK):
                                nc.scalar.activation(ctxT[:, m, b * N:(b + 1) * N], ps[CT_BANK][:, m * N:(m + 1) * N],
                                                     ACT.Identity, bias=bs[:, 4, m:m + 1]).then_inc(ctx_done, 1)

                @block.vector
                def _(dve):
                    norm.vector(nc, dve, h[:, :, group_cols(g)])

                    def table(t, m):
                        return t[:, m, :].unsqueeze(1).to_broadcast([P, GB, N])

                    def rows(ap):
                        return ap.rearrange("p (b n) -> p b n", n=N)

                    for i in range(2):
                        for m in range(DK):
                            j = 2 * i + m
                            dve.wait_ge(proj_done, 4 * i + m + 1)
                            nc.vector.scalar_tensor_tensor(out=rows(rot_a[:, j, :]), in0=rows(ps[4 * i + m][:, 0:GT]),
                                                           scalar=bs[:, 2 * i, m:m + 1], in1=table(cs, m),
                                                           op0=ALU.add, op1=ALU.mult).then_inc(a_done, 1)
                        for m in range(DK):
                            j = 2 * i + m
                            dve.wait_ge(proj_done, 4 * i + 2 + m + 1)
                            nc.vector.scalar_tensor_tensor(out=rows(rot_b[:, j, :]), in0=rows(ps[4 * i + 2 + m][:, 0:GT]),
                                                           scalar=bs[:, 2 * i + 1, m:m + 1], in1=table(sn, m),
                                                           op0=ALU.add, op1=ALU.mult).then_inc(b_done, 1)
                        for m in range(DK):
                            j = 2 * i + m
                            dve.wait_ge(b_done, j + 1)
                            dve.wait_ge(a_done, j + 1)
                            dst, done = ((q, q_done), (kk, k_done))[i]
                            nc.vector.tensor_tensor(dst[:, m, :], rot_a[:, j, :], rot_b[:, j, :], ALU.add).then_inc(done, 1)
                    dve.wait_ge(k_done, 2)
                    for par in range(2):
                        for m in range(DK):
                            nc.vector.tensor_scalar(kpar[par][:, m, :], kk[:, m, :], ev[:, par:par + 1], None, ALU.mult)\
                                .then_inc(kpar_done, 1)

                    def shift(u):
                        s = ps[S_BANK[u % 3]][0:N, 0:4 * N].rearrange("p (j n) -> p j n", n=N)
                        dve.wait_ge(s_done, u + 1)
                        nc.vector.tensor_reduce(mx[:, u, :], s, AX.X, ALU.max).then_inc(mx_done, 1)
                        dve.wait_ge(mx_done, u + 1)
                        if u >= NE:
                            dve.wait_ge(ex_done, u - NE + 1)
                        nc.vector.tensor_tensor(low[:, u % NE, :].rearrange("p (j n) -> p j n", n=N), s,
                                                mx[:, u, :].unsqueeze(2).to_broadcast([N, 4, N]), ALU.subtract)\
                            .then_inc(low_done, 1)

                    def context(b):
                        dve.wait_ge(av_done, 4 * (b + 1))
                        cx = ps[C_BANK[b % 2]][0:N, 0:H * (HD + 1)].rearrange("p (h e) -> p h e", e=HD + 1)
                        nc.vector.reciprocal(rs[:, b, :], cx[:, :, HD]).then_inc(rs_done, 1)
                        dve.wait_ge(rs_done, b + 1)
                        nc.vector.tensor_tensor(cn[:, b, :].rearrange("p (h e) -> p h e", e=HD), cx[:, :, 0:HD],
                                                rs[:, b, :].unsqueeze(2).to_broadcast([N, H, HD]), ALU.mult).then_inc(cn_done, 1)

                    for u in range(UNITS):
                        shift(u)
                        if u >= 6 and (u - 6) % 4 == 0:
                            context((u - 6) // 4)
                    context(GB - 1)
                    for m in range(DK):
                        dve.wait_ge(o_done, m + 1)
                        nc.vector.scalar_tensor_tensor(out=h[:, m, group_cols(g)], in0=ps[m][:, 0:GT],
                                                       scalar=bs[:, 5, m:m + 1], in1=h[:, m, group_cols(g)],
                                                       op0=ALU.add, op1=ALU.add).then_inc(res_done, 1)
            st.clear()


def l2_attn(nc, h, c, wq, wk, wv):
    MASKED = -1e30
    with Stage(nc, "at2") as st:
        W = {x: st.sbuf(x, [P, DK, D]) for x in ("wq", "wk", "wv")}
        mask = st.sbuf("mask", [N, N])
        ps = [st.psum(f"ps{i}") for i in range(8)]
        norm = Norm(st, ps[0], ps[1])
        q = st.sbuf("q", [P, DK, GT])
        kk = st.sbuf("k", [P, DK, GT])
        v = st.sbuf("v", [N, GB, D])
        sc = st.sbuf("sc", [N, GB, N])
        low = st.sbuf("low", [N, GB, N])
        ex = st.sbuf("ex", [N, GB, N])
        pr = st.sbuf("pr", [N, GB, N])
        prT = st.sbuf("prT", [N, GB, N])
        mx, sm, rs = (st.sbuf(x, [N, GB]) for x in ("mx", "sm", "rs"))
        (w_in, zero, masked, proj_done, qk_done, v_mm, v_done, s_done, sc_done, mx_done, low_done, ex_done, sm_done, rs_done,
         pr_done, t_done, prT_done, o_done, res_done) = (
            st.sem(x) for x in ("w_in", "zero", "masked", "proj_done", "qk_done", "v_mm", "v_done", "s_done", "sc_done",
                                "mx_done", "low_done", "ex_done", "sm_done", "rs_done", "pr_done", "t_done", "prT_done",
                                "o_done", "res_done"))
        with nc.Block() as block:
            @block.sync
            def _(sp):
                for x, src in (("wq", wq), ("wk", wk), ("wv", wv)):
                    sp.dma_start(W[x][:, :, :], src.rearrange("(k p) n -> p k n", p=P)).then_inc(w_in, 16)
                sp.wait_ge(w_in, 48)

            @block.gpsimd
            def _(pool):
                nc.gpsimd.memset(mask[:, :], 0.0).then_inc(zero, 1)
                pool.wait_ge(zero, 1)
                nc.gpsimd.affine_select(out=mask[:, :], in_=mask[:, :], compare_op=ALU.is_ge, fill=MASKED,
                                        base=0, pattern=[[-1, N]], channel_multiplier=1).then_inc(masked, 1)

            @block.scalar
            def _(act):
                nc.scalar.preload_act_table_set(EXP_LN)
        st.clear()
        with nc.Fori(0, GROUPS) as g:
            with nc.Block(no_gpsimd_drain=True) as block:
                @block.tensor
                def _(pe):
                    norm.tensor_mean(nc, pe, c["ones"], lambda k: h[:, k, group_cols(g)])
                    norm.tensor_var(nc, pe, c["ones"])
                    pe.wait_ge(norm.ready, 1)
                    for i, x in enumerate(("wq", "wk")):
                        for m in range(DK):
                            for k in range(DK):
                                mm = nc.tensor.matmul(ps[2 + 2 * i + m][:, 0:GT], W[x][:, k, m * P:(m + 1) * P],
                                                      norm.out[:, k, :], start=(k == 0), stop=(k == DK - 1))
                            mm.then_inc(proj_done, 1)
                    for b in range(GB):
                        for k in range(DK):
                            mm = nc.tensor.matmul(ps[6 + b // 2][0:N, (b % 2) * D:(b % 2 + 1) * D],
                                                  norm.out[:, k, b * N:(b + 1) * N], W["wv"][:, k, :],
                                                  start=(k == 0), stop=(k == DK - 1))
                        if b % 2:
                            mm.then_inc(v_mm, 1)
                    pe.wait_ge(qk_done, 4)
                    for b in range(GB):
                        for k in range(DK):
                            mm = nc.tensor.matmul(ps[0][0:N, b * N:(b + 1) * N], q[:, k, b * N:(b + 1) * N],
                                                  kk[:, k, b * N:(b + 1) * N], start=(k == 0), stop=(k == DK - 1))
                    mm.then_inc(s_done, 1)
                    pe.wait_ge(pr_done, 1)
                    for b in range(GB):
                        mm = nc.tensor.transpose(ps[1][0:N, b * N:(b + 1) * N], pr[:, b, :], c["ident"][0:N, 0:N])
                    mm.then_inc(t_done, 1)
                    pe.wait_ge(prT_done, 1)
                    pe.wait_ge(v_done, GB // 2)
                    for m in range(DK):
                        for b in range(GB):
                            mm = nc.tensor.matmul(ps[2 + m][:, b * N:(b + 1) * N], v[:, b, m * P:(m + 1) * P], prT[:, b, :],
                                                  start=True, stop=True)
                        mm.then_inc(o_done, 1)

                @block.scalar
                def _(act):
                    norm.scalar(nc, act, c["eps"])
                    for i in range(4):
                        act.wait_ge(proj_done, i + 1)
                        dst = (q, kk)[i // 2]
                        nc.scalar.activation(dst[:, i % 2, :], ps[2 + i][:, 0:GT], ACT.Copy).then_inc(qk_done, 1)
                    for b in range(0, GB, 2):
                        act.wait_ge(v_mm, b // 2 + 1)
                        nc.scalar.activation(v[:, b:b + 2, :], ps[6 + b // 2][0:N, :].rearrange("p (b d) -> p b d", b=2),
                                             ACT.Copy).then_inc(v_done, 1)
                    act.wait_ge(low_done, 1)
                    nc.scalar.activation(ex[:, :, :], low[:, :, :], ACT.Exp).then_inc(ex_done, 1)
                    act.wait_ge(t_done, 1)
                    nc.scalar.activation(prT[:, :, :], ps[1][0:N, 0:GT].rearrange("p (b n) -> p b n", n=N), ACT.Copy)\
                        .then_inc(prT_done, 1)

                @block.vector
                def _(dve):
                    norm.vector(nc, dve, h[:, :, group_cols(g)])
                    dve.wait_ge(s_done, 1)
                    nc.vector.scalar_tensor_tensor(out=sc[:, :, :], in0=ps[0][0:N, 0:GT].rearrange("p (b n) -> p b n", n=N),
                                                   scalar=D ** -0.5, in1=mask[:, :].unsqueeze(1).to_broadcast([N, GB, N]),
                                                   op0=ALU.mult, op1=ALU.add).then_inc(sc_done, 1)
                    dve.wait_ge(sc_done, 1)
                    nc.vector.tensor_reduce(mx[:, :], sc[:, :, :], AX.X, ALU.max).then_inc(mx_done, 1)
                    dve.wait_ge(mx_done, 1)
                    nc.vector.tensor_tensor(low[:, :, :], sc[:, :, :], mx[:, :].unsqueeze(2).to_broadcast([N, GB, N]),
                                            ALU.subtract).then_inc(low_done, 1)
                    dve.wait_ge(ex_done, 1)
                    nc.vector.tensor_reduce(sm[:, :], ex[:, :, :], AX.X, ALU.add).then_inc(sm_done, 1)
                    dve.wait_ge(sm_done, 1)
                    nc.vector.reciprocal(rs[:, :], sm[:, :]).then_inc(rs_done, 1)
                    dve.wait_ge(rs_done, 1)
                    nc.vector.tensor_tensor(pr[:, :, :], ex[:, :, :], rs[:, :].unsqueeze(2).to_broadcast([N, GB, N]),
                                            ALU.mult).then_inc(pr_done, 1)
                    for m in range(DK):
                        dve.wait_ge(o_done, m + 1)
                        nc.vector.tensor_tensor(h[:, m, group_cols(g)], ps[2 + m][:, 0:GT], h[:, m, group_cols(g)],
                                                ALU.add).then_inc(res_done, 1)
            st.clear()


def moe(nc, h, c, router_w, router_b, gate_up, down, slots_in, slots_out):
    E = router_w.shape[1]
    TOPK = 2
    F = gate_up.shape[4]
    FB = [(f, min(P, F - f)) for f in range(0, F, P)]
    C = -(-5 * T * TOPK // (4 * E))
    STRIDE = slots_in.shape[0] // (E + 1)
    TILES = [(t, min(P, C - t)) for t in range(0, C, P)]
    HALVES = [(0, (C + 1) // 2), ((C + 1) // 2, C // 2)]
    NOWHERE = 1 << 20
    NT = len(TILES)
    with Stage(nc, "moe") as st:
        ps = [st.psum(f"ps{i}") for i in range(8)]
        normed = st.sbuf("normed", [P, DK, T])
        share = st.sbuf("share", [N, B, TOPK])
        to_slot = st.sbuf("to_slot", [P, B, TOPK], U32)
        from_slot = st.sbuf("from_slot", [P, B, TOPK], U32)

        with Stage(nc, "rt") as sr:
            token_rows = sr.sbuf("token_rows", [P, B, D])
            logits = sr.sbuf("logits", [N, B, E])
            w_r = sr.sbuf("w_r", [P, DK, E])
            b_r = sr.sbuf("b_r", [N, E])
            zeros = sr.sbuf("zeros", [P, STRIDE // P, D])
            scattered = sr.sem("scattered")
            with Stage(nc, "rn") as sn:
                norm = Norm(sn, ps[0], ps[1])
                loaded, zeroed, filled, kept, score_mm, score_done, turned, rows_done = (
                    sn.sem(x) for x in ("loaded", "zeroed", "filled", "kept", "score_mm", "score_done", "turned", "rows_done"))
                with nc.Block() as block:
                    @block.sync
                    def _(sp):
                        sp.dma_start(w_r[:, :, :], router_w.rearrange("(k p) e -> p k e", p=P)).then_inc(loaded, 16)
                        sp.dma_start(b_r[:, :], router_b.to_broadcast([N, E])).then_inc(loaded, 16)
                        sp.wait_ge(loaded, 32)
                        sp.wait_ge(zeroed, 1)
                        for e in range(E + 1):
                            sp.dma_start(slots_in[e * STRIDE:(e + 1) * STRIDE, :].rearrange("(a p) d -> p a d", p=P),
                                         zeros[:, :, :]).then_inc(filled, 16)
                        sp.wait_ge(filled, 16 * (E + 1))

                    @block.gpsimd
                    def _(pool):
                        nc.gpsimd.memset(zeros[:, :, :], 0.0).then_inc(zeroed, 1)
                        nc.gpsimd.memset(token_rows[:, :, :], 0.0)

                    @block.scalar
                    def _(act):
                        nc.scalar.preload_act_table_set(EXP_LN)
                sn.clear()
                with nc.Fori(0, GROUPS) as g:
                    with nc.Block(no_gpsimd_drain=True) as block:
                        @block.tensor
                        def _(pe):
                            norm.tensor_mean(nc, pe, c["ones"], lambda k: h[:, k, group_cols(g)])
                            norm.tensor_var(nc, pe, c["ones"])
                            pe.wait_ge(norm.ready, 1)
                            for b in range(GB):
                                for k in range(DK):
                                    mm = nc.tensor.matmul(ps[2][0:N, b * E:(b + 1) * E], norm.out[:, k, b * N:(b + 1) * N],
                                                          w_r[:, k, :], start=(k == 0), stop=(k == DK - 1))
                            mm.then_inc(score_mm, 1)
                            for b in range(GB):
                                for k in range(DK):
                                    mm = nc.tensor.transpose(ps[3 + b // 2][0:N, (b % 2 * DK + k) * P:(b % 2 * DK + k + 1) * P],
                                                             norm.out[:, k, b * N:(b + 1) * N], c["ident"][:, :])
                                if b % 2:
                                    mm.then_inc(turned, 1)

                        @block.scalar
                        def _(act):
                            norm.scalar(nc, act, c["eps"])
                            act.wait_ge(norm.ready, 1)
                            nc.scalar.activation(normed[:, :, group_cols(g)], norm.out[:, :, :], ACT.Copy).then_inc(kept, 1)
                            for i in range(GB // 2):
                                act.wait_ge(turned, i + 1)
                                nc.scalar.activation(token_rows[0:N, bass.ds(g * GB + 2 * i, 2), :],
                                                     ps[3 + i][0:N, :].rearrange("p (b d) -> p b d", b=2), ACT.Copy)\
                                    .then_inc(rows_done, 1)

                        @block.vector
                        def _(dve):
                            norm.vector(nc, dve, h[:, :, group_cols(g)])
                            dve.wait_ge(score_mm, 1)
                            nc.vector.tensor_tensor(logits[:, bass.ds(g * GB, GB), :],
                                                    ps[2][0:N, 0:GB * E].rearrange("p (b e) -> p b e", e=E),
                                                    b_r[:, :].unsqueeze(1).to_broadcast([N, GB, E]), ALU.add)\
                                .then_inc(score_done, 1)
                    sn.clear()

            with Stage(nc, "ch") as sc:
                tile = lambda x, shape=(N, B, E), dt=F32: sc.sbuf(x, list(shape), dt)
                small = lambda x: sc.sbuf(x, [N, B])
                ramp, shifted, ex, probs = tile("ramp", (N, E)), tile("shifted"), tile("ex"), tile("probs")
                top, idx = tile("top", (N, B, 8)), tile("idx", (N, B, 8), U32)
                hot = [tile("hot0"), tile("hot1")]
                both_hot, totals = tile("both_hot"), tile("totals", (N, E, B))
                fresh, upto, before = tile("fresh", (N, E, B)), tile("upto", (N, E, B)), tile("before", (N, E, B))
                place, hit = tile("place"), [tile("hit0"), tile("hit1")]
                earlier, every = sc.sbuf("earlier", [N, N]), sc.sbuf("every", [N, N])
                mx, sm, rs, wsum, wr_ = small("mx"), small("sm"), small("rs"), small("wsum"), small("wr")
                pos, base, inside, low, gat, far, sca, wk_ = ([small(f"{x}{k}") for k in range(TOPK)] for x in
                                                             ("pos", "base", "inside", "low", "gat", "far", "sca", "wk"))
                made, step, counted, spread_ready = (sc.sem(x) for x in ("made", "step", "counted", "spread_ready"))
                with nc.Block() as block:
                    @block.gpsimd
                    def _(pool):
                        nc.gpsimd.iota(ramp[:, :], pattern=[[1, E]], base=0, channel_multiplier=0,
                                       allow_small_or_imprecise_dtypes=True)
                        nc.gpsimd.memset(every[:, :], 1.0)
                        nc.gpsimd.memset(fresh[:, :, :], 1.0)
                        nc.gpsimd.memset(to_slot[:, :, :], NOWHERE)
                        nc.gpsimd.memset(from_slot[:, :, :], NOWHERE)
                        nc.gpsimd.memset(earlier[:, :], 1.0).then_inc(made, 1)
                        pool.wait_ge(made, 1)
                        nc.gpsimd.memset(fresh[:, :, 0:1], 0.0)
                        nc.gpsimd.affine_select(out=earlier[:, :], in_=earlier[:, :], compare_op=ALU.is_gt, fill=0.0,
                                                base=0, pattern=[[1, N]], channel_multiplier=-1).then_inc(made, 1)
                        pool.wait_ge(spread_ready, TOPK)
                        for b in range(B):
                            for k in range(TOPK):
                                nc.gpsimd.indirect_dma_start(
                                    out=slots_in[:, :], out_offset=bass.IndirectOffsetOnAxis(ap=to_slot[:, b, k:k + 1], axis=0),
                                    in_=token_rows[:, b, :], in_offset=None, bounds_check=(E + 1) * STRIDE - 1,
                                    oob_is_err=False).then_inc(scattered, 16)
                        pool.wait_ge(scattered, 16 * B * TOPK)

                    @block.scalar
                    def _(act):
                        act.wait_ge(step, 2)
                        nc.scalar.activation(ex[:, :, :], shifted[:, :, :], ACT.Exp).then_inc(counted, 1)

                    @block.tensor
                    def _(pe):
                        pe.wait_ge(made, 2)
                        pe.wait_ge(step, 11 + 2 * B)
                        flat = both_hot[:, :, :].rearrange("p b e -> p (b e)")
                        nc.tensor.matmul(ps[0][0:N, :], earlier[:, :], flat, start=True, stop=True).then_inc(counted, 1)
                        nc.tensor.matmul(ps[1][0:N, :], every[:, :], flat, start=True, stop=True).then_inc(counted, 1)

                    @block.vector
                    def _(dve):
                        n = [0]

                        def after(ins):
                            n[0] += 1
                            ins.then_inc(step, 1)
                            dve.wait_ge(step, n[0])

                        def wide(x):
                            return x[:, :].unsqueeze(2).to_broadcast([N, B, E])

                        V = nc.vector
                        after(V.tensor_reduce(mx[:, :], logits[:, :, :], AX.X, ALU.max))
                        after(V.tensor_tensor(shifted[:, :, :], logits[:, :, :], wide(mx), ALU.subtract))
                        dve.wait_ge(counted, 1)
                        after(V.tensor_reduce(sm[:, :], ex[:, :, :], AX.X, ALU.add))
                        after(V.reciprocal(rs[:, :], sm[:, :]))
                        after(V.tensor_tensor(probs[:, :, :], ex[:, :, :], wide(rs), ALU.mult))
                        for b in range(B):
                            after(V.max(top[:, b, :], probs[:, b, :]))
                        for b in range(B):
                            after(V.max_index(idx[:, b, :], top[:, b, :], probs[:, b, :]))
                        dve.wait_ge(made, 2)
                        after(V.tensor_tensor(wsum[:, :], top[:, :, 0], top[:, :, 1], ALU.add))
                        after(V.tensor_scalar(wsum[:, :], wsum[:, :], 1e-9, None, ALU.add))
                        after(V.reciprocal(wr_[:, :], wsum[:, :]))
                        for k in range(TOPK):
                            after(V.tensor_tensor(hot[k][:, :, :], ramp[:, :].unsqueeze(1).to_broadcast([N, B, E]),
                                                  idx[:, :, k:k + 1].to_broadcast([N, B, E]), ALU.is_equal))
                        after(V.tensor_tensor(both_hot[:, :, :], hot[0][:, :, :], hot[1][:, :, :], ALU.add))
                        dve.wait_ge(counted, 3)
                        after(V.tensor_copy(totals[:, :, :], ps[1][0:N, :].rearrange("p (b e) -> p e b", e=E)))
                        line = lambda x: x[:, :, :].rearrange("p e b -> p (e b)")
                        after(V.tensor_tensor_scan(line(upto), line(fresh), line(totals), 0.0, ALU.mult, ALU.add))
                        after(V.tensor_tensor(before[:, :, :], upto[:, :, :], totals[:, :, :], ALU.subtract))
                        after(V.tensor_tensor(place[:, :, :], ps[0][0:N, :].rearrange("p (b e) -> p b e", e=E),
                                              before[:, :, :].rearrange("p e b -> p b e"), ALU.add))
                        for k in range(TOPK):
                            after(V.tensor_tensor(hit[k][:, :, :], hot[k][:, :, :], place[:, :, :], ALU.mult))
                            after(V.tensor_reduce(pos[k][:, :], hit[k][:, :, :], AX.X, ALU.add))
                            after(V.tensor_scalar(base[k][:, :], idx[:, :, k], float(STRIDE), None, ALU.mult))
                            after(V.tensor_scalar(inside[k][:, :], pos[k][:, :], float(C), None, ALU.is_lt))
                            after(V.tensor_scalar(low[k][:, :], pos[k][:, :], float(C - 1), None, ALU.min))
                            after(V.scalar_tensor_tensor(out=gat[k][:, :], in0=idx[:, :, k], scalar=float(C), in1=low[k][:, :],
                                                         op0=ALU.mult, op1=ALU.add))
                            after(V.tensor_copy(from_slot[0:N, :, k], gat[k][:, :]))
                            after(V.tensor_tensor(low[k][:, :], low[k][:, :], base[k][:, :], ALU.add))
                            after(V.tensor_scalar(far[k][:, :], inside[k][:, :], -float(NOWHERE), float(NOWHERE), ALU.mult, ALU.add))
                            after(V.tensor_tensor(sca[k][:, :], far[k][:, :], low[k][:, :], ALU.add))
                            after(V.tensor_copy(to_slot[0:N, :, k], sca[k][:, :]))
                            after(V.tensor_tensor(wk_[k][:, :], top[:, :, k], wr_[:, :], ALU.mult))
                            V.tensor_tensor(share[:, :, k], wk_[k][:, :], inside[k][:, :], ALU.mult).then_inc(spread_ready, 1)
                sr.clear(pool_dmas=True)
                sc.clear()

        w_gu = [st.sbuf(f"w_gu{i}", [P, DK, 2, F]) for i in range(2)]
        w_dn = [st.sbuf(f"w_dn{i}", [P, len(FB), D]) for i in range(2)]

        def fetch_weights(sp, e, i, done):
            sp.dma_start(w_gu[i][:, :, :, :], gate_up[bass.ds(e, 1), :, :, :, :].rearrange("e p k g f -> (e p) k g f"))\
                .then_inc(done, 16)
            sp.dma_start(w_dn[i][:, :, :], down[bass.ds(e, 1), :, :, :].rearrange("e p k n -> (e p) k n")).then_inc(done, 16)

        with Stage(nc, "xp") as sx:
            rows_in = [sx.sbuf(f"rows_in{i}", [P, NT, D]) for i in range(2)]
            xT = [sx.sbuf(f"xT{i}", [P, DK, C]) for i in range(2)]
            silu = sx.sbuf("silu", [P, 2, HALVES[0][1]])
            hid = [sx.sbuf(f"hid{i}", [P, len(FB), C]) for i in range(2)]
            rows_out = [sx.sbuf(f"rows_out{i}", [P, NT, D]) for i in range(2)]
            landed = [sx.sem(f"landed{i}") for i in range(2)]
            turned, xT_done, gate_mm, up_mm, silu_done, hid_done, down_mm, out_done, stored = (
                sx.sem(x) for x in ("turned", "xT_done", "gate_mm", "up_mm", "silu_done", "hid_done", "down_mm", "out_done", "stored"))
            NF = len(FB)
            FULL = NT - 1
            LAST = TILES[-1][1]

            def fetch(sp, e, i):
                fetch_weights(sp, e, i, landed[i])
                sp.dma_start(rows_in[i][:, 0:FULL, :], slots_in[bass.ds(e * STRIDE, FULL * P), :].rearrange("(a p) d -> p a d", p=P))\
                    .then_inc(landed[i], 16)
                sp.dma_start(rows_in[i][0:LAST, FULL, :], slots_in[bass.ds(e * STRIDE + FULL * P, LAST), :]).then_inc(landed[i], 16)

            with nc.Block() as block:
                @block.sync
                def _(sp):
                    fetch(sp, 0, 0)
                    sp.wait_ge(landed[0], 64)
            sx.clear()
            with nc.Fori(0, E // 2) as g:
                with nc.Block(no_gpsimd_drain=True) as block:
                    @block.sync
                    def _(sp):
                        fetch(sp, g * 2 + 1, 1)
                        sp.wait_ge(down_mm, 3)
                        fetch(sp, g * 2 + 2, 0)
                        sp.wait_ge(landed[0], 64)

                    @block.tensor
                    def _(pe):
                        for i in range(2):
                            if i:
                                pe.wait_ge(landed[1], 64)
                            if i:
                                pe.wait_ge(xT_done, 3)
                            for t in range(NT):
                                for k in range(DK):
                                    r = TILES[t][1]
                                    dst = ps[k][:, t * P:(t + 1) * P] if t < FULL else ps[2][:, k * LAST:(k + 1) * LAST]
                                    mm = nc.tensor.transpose(dst, rows_in[i][0:r, t, k * P:(k + 1) * P], c["ident"][0:r, 0:r])
                            mm.then_inc(turned, 1)
                            pe.wait_ge(xT_done, 3 * i + 3)
                            for hf, (c0, cn) in enumerate(HALVES):
                                for f, (f0, fn) in enumerate(FB):
                                    u = (i * 2 + hf) * NF + f
                                    if u >= 2:
                                        pe.wait_ge(silu_done, u - 1)
                                    for k in range(DK):
                                        mm = nc.tensor.matmul(ps[3 + u % 2][0:fn, 0:cn], w_gu[i][:, k, 0, f0:f0 + fn],
                                                              xT[i][:, k, c0:c0 + cn], start=(k == 0), stop=(k == DK - 1))
                                    mm.then_inc(gate_mm, 1)
                                    if u >= 2:
                                        pe.wait_ge(hid_done, u - 1)
                                    for k in range(DK):
                                        mm = nc.tensor.matmul(ps[5 + u % 2][0:fn, 0:cn], w_gu[i][:, k, 1, f0:f0 + fn],
                                                              xT[i][:, k, c0:c0 + cn], start=(k == 0), stop=(k == DK - 1))
                                    mm.then_inc(up_mm, 1)
                            pe.wait_ge(hid_done, (i + 1) * 2 * NF)
                            for t, (t0, r) in enumerate(TILES):
                                q = 3 * i + t // 2
                                if q >= 1 and t % 2 == 0:
                                    pe.wait_ge(out_done, q)
                                for f, (f0, fn) in enumerate(FB):
                                    mm = nc.tensor.matmul(ps[7][0:r, (t % 2) * D:(t % 2 + 1) * D], hid[i][0:fn, f, t0:t0 + r],
                                                          w_dn[i][0:fn, f, :], start=(f == 0), stop=(f == NF - 1))
                                if t % 2 or t == NT - 1:
                                    mm.then_inc(down_mm, 1)

                    @block.scalar
                    def _(act):
                        for i in range(2):
                            act.wait_ge(turned, i + 1)
                            for k in range(DK):
                                nc.scalar.activation(xT[i][:, k, 0:FULL * P], ps[k][:, :], ACT.Copy).then_inc(xT_done, 1)
                            nc.scalar.activation(xT[i][:, :, FULL * P:C], ps[2][:, 0:DK * LAST].rearrange("p (k r) -> p k r", k=DK),
                                                 ACT.Copy).then_inc(xT_done, 1)
                            for u in range(2 * NF * i, 2 * NF * (i + 1)):
                                hf, f = u // NF % 2, u % NF
                                cn, fn = HALVES[hf][1], FB[f][1]
                                act.wait_ge(gate_mm, u + 1)
                                if u >= 2:
                                    act.wait_ge(hid_done, u - 1)
                                nc.scalar.activation(silu[0:fn, u % 2, 0:cn], ps[3 + u % 2][0:fn, 0:cn], ACT.Silu).then_inc(silu_done, 1)
                        for i in range(2):
                            act.wait_ge(out_done, 3 * i + 3)
                            e = g * 2 + i
                            act.dma_start(slots_out[bass.ds(e * C, FULL * P), :].rearrange("(a p) d -> p a d", p=P),
                                          rows_out[i][:, 0:FULL, :]).then_inc(stored, 16)
                            act.dma_start(slots_out[bass.ds(e * C + FULL * P, LAST), :], rows_out[i][0:LAST, FULL, :])\
                                .then_inc(stored, 16)
                        act.wait_ge(stored, 64)

                    @block.vector
                    def _(dve):
                        for i in range(2):
                            for u in range(2 * NF * i, 2 * NF * (i + 1)):
                                hf, f = u // NF % 2, u % NF
                                (c0, cn), fn = HALVES[hf], FB[f][1]
                                dve.wait_ge(silu_done, u + 1)
                                dve.wait_ge(up_mm, u + 1)
                                nc.vector.tensor_tensor(hid[i][0:fn, f, c0:c0 + cn], silu[0:fn, u % 2, 0:cn],
                                                        ps[5 + u % 2][0:fn, 0:cn], ALU.mult).then_inc(hid_done, 1)
                            for q in range(3):
                                r = P if q < 2 else LAST
                                tiles = 2 if q < 2 else 1
                                dve.wait_ge(down_mm, 3 * i + q + 1)
                                nc.vector.tensor_copy(rows_out[i][0:r, 2 * q:2 * q + tiles, :],
                                                      ps[7][0:r, 0:tiles * D].rearrange("p (t d) -> p t d", d=D)).then_inc(out_done, 1)
                sx.clear()

        with Stage(nc, "sh") as ss:
            now_slot = ss.sbuf("now_slot", [P, GB * TOPK], U32)
            now_share = ss.sbuf("now_share", [N, GB * TOPK])
            got = [[ss.sbuf(f"got{b}{k}", [P, D]) for k in range(TOPK)] for b in range(GB)]
            part = ss.sbuf("part", [N, GB, D])
            mixed = ss.sbuf("mixed", [N, GB, D])
            x_in = ss.sbuf("x_in", [P, DK, GT])
            silu = ss.sbuf("silu", [P, 2, GT])
            hid = ss.sbuf("hid", [P, len(FB), GT])
            hn = ss.sbuf("hn", [P, DK, GT])
            NF = len(FB)
            gathered = [ss.sem(f"gathered{b}") for b in range(GB)]
            slot_done, share_done, x_done, part_done, mixed_done, gate_mm, up_mm, silu_done, hid_done, sum_mm, hn_done, res_done = (
                ss.sem(x) for x in ("slot_done", "share_done", "x_done", "part_done", "mixed_done", "gate_mm", "up_mm", "silu_done",
                                    "hid_done", "sum_mm", "hn_done", "res_done"))
            with nc.Fori(0, GROUPS) as g:
                with nc.Block(no_gpsimd_drain=True) as block:
                    @block.gpsimd
                    def _(pool):
                        pool.wait_ge(slot_done, 1)
                        for b in range(GB):
                            for k in range(TOPK):
                                nc.gpsimd.indirect_dma_start(
                                    out=got[b][k][:, :], out_offset=None, in_=slots_out[:, :],
                                    in_offset=bass.IndirectOffsetOnAxis(ap=now_slot[:, b * TOPK + k:b * TOPK + k + 1], axis=0),
                                    bounds_check=E * C - 1, oob_is_err=False).then_inc(gathered[b], 16)
                        for b in range(GB):
                            pool.wait_ge(gathered[b], 16 * TOPK)

                    @block.scalar
                    def _(act):
                        nc.scalar.activation(x_in[:, :, :], normed[:, :, group_cols(g)], ACT.Copy).then_inc(x_done, 1)
                        for f, (f0, fn) in enumerate(FB):
                            act.wait_ge(gate_mm, f + 1)
                            if f >= 2:
                                act.wait_ge(hid_done, f - 1)
                            nc.scalar.activation(silu[0:fn, f % 2, :], ps[f][0:fn, 0:GT], ACT.Silu).then_inc(silu_done, 1)

                    @block.tensor
                    def _(pe):
                        pe.wait_ge(x_done, 1)
                        for f, (f0, fn) in enumerate(FB):
                            for k in range(DK):
                                mm = nc.tensor.matmul(ps[f][0:fn, 0:GT], w_gu[0][:, k, 0, f0:f0 + fn], x_in[:, k, :],
                                                      start=(k == 0), stop=(k == DK - 1))
                            mm.then_inc(gate_mm, 1)
                            for k in range(DK):
                                mm = nc.tensor.matmul(ps[3 + f][0:fn, 0:GT], w_gu[0][:, k, 1, f0:f0 + fn], x_in[:, k, :],
                                                      start=(k == 0), stop=(k == DK - 1))
                            mm.then_inc(up_mm, 1)
                        for m in range(DK):
                            for f, (f0, fn) in enumerate(FB):
                                pe.wait_ge(hid_done, f + 1)
                                nc.tensor.matmul(ps[6 + m][:, 0:GT], w_dn[0][0:fn, f, m * P:(m + 1) * P], hid[0:fn, f, :],
                                                 start=(f == 0), stop=False, skip_group_check=True)
                            for b in range(GB):
                                pe.wait_ge(mixed_done, b + 1)
                                mm = nc.tensor.matmul(ps[6 + m][:, b * N:(b + 1) * N], mixed[:, b, m * P:(m + 1) * P],
                                                      c["ident"][0:N, 0:N], start=False, stop=(b == GB - 1), skip_group_check=True)
                            mm.then_inc(sum_mm, 1)

                    @block.vector
                    def _(dve):
                        nc.vector.tensor_copy(now_slot[:, :], from_slot[:, bass.ds(g * GB, GB), :].rearrange("p b k -> p (b k)"))\
                            .then_inc(slot_done, 1)
                        nc.vector.tensor_copy(now_share[:, :], share[:, bass.ds(g * GB, GB), :].rearrange("p b k -> p (b k)"))\
                            .then_inc(share_done, 1)
                        nc.vector.tensor_tensor(hn[:, :, :], h[:, :, group_cols(g)], normed[:, :, group_cols(g)], ALU.add)\
                            .then_inc(hn_done, 1)
                        for f, (f0, fn) in enumerate(FB):
                            dve.wait_ge(silu_done, f + 1)
                            dve.wait_ge(up_mm, f + 1)
                            nc.vector.tensor_tensor(hid[0:fn, f, :], silu[0:fn, f % 2, :], ps[3 + f][0:fn, 0:GT], ALU.mult)\
                                .then_inc(hid_done, 1)
                        dve.wait_ge(share_done, 1)
                        for b in range(GB):
                            dve.wait_ge(gathered[b], 16 * TOPK)
                            nc.vector.tensor_scalar(part[:, b, :], got[b][0][0:N, :], now_share[:, 2 * b:2 * b + 1], None, ALU.mult)\
                                .then_inc(part_done, 1)
                            dve.wait_ge(part_done, b + 1)
                            nc.vector.scalar_tensor_tensor(out=mixed[:, b, :], in0=got[b][1][0:N, :],
                                                           scalar=now_share[:, 2 * b + 1:2 * b + 2], in1=part[:, b, :],
                                                           op0=ALU.mult, op1=ALU.add).then_inc(mixed_done, 1)
                        for m in range(DK):
                            dve.wait_ge(sum_mm, m + 1)
                            dve.wait_ge(hn_done, 1)
                            nc.vector.tensor_tensor(h[:, m, group_cols(g)], ps[6 + m][:, 0:GT], hn[:, m, :], ALU.add)\
                                .then_inc(res_done, 1)
                ss.clear(pool_dmas=True)


def mamba(nc, h, c, params):
    INNER = params[0]["in_t"].shape[1] // 2
    IB = INNER // P
    S = params[0]["a_log"].shape[2]
    R = params[0]["dt_t"].shape[0]
    TAPS = params[0]["conv_w"].shape[2]
    XP = R + 2 * S
    STEPS = S * IB
    NB = 4
    POOL_EVERY = 2
    with Stage(nc, "ssm") as st:
        w_in = [st.sbuf(f"w_in{d}", [P, DK, 2 * INNER]) for d in range(2)]
        w_xp = [st.sbuf(f"w_xp{d}", [P, IB, XP]) for d in range(2)]
        w_dt = [st.sbuf(f"w_dt{d}", [R, INNER]) for d in range(2)]
        w_out = [st.sbuf(f"w_out{d}", [P, IB, D]) for d in range(2)]
        conv_w = [st.sbuf(f"conv_w{d}", [P, IB, TAPS]) for d in range(2)]
        conv_b, dt_b, skip = ([st.sbuf(f"{x}{d}", [P, IB]) for d in range(2)] for x in ("conv_b", "dt_b", "skip"))
        decay = [st.sbuf(f"decay{d}", [P, IB, S]) for d in range(2)]
        expo = [st.sbuf(f"expo{d}", [P, IB, S]) for d in range(2)]
        pick = st.sbuf("pick", [XP, 2 * S, P])
        dA = [st.sbuf(f"dA{d}", [P, NB, GT]) for d in range(2)]
        one = st.sbuf("one", [P, 1])
        ps = [st.psum(f"ps{i}") for i in range(8)]
        norm = Norm(st, ps[0], ps[1])
        conv = st.sbuf("conv", [P, IB, GT])
        xc = st.sbuf("xc", [P, IB, GT])
        z = st.sbuf("z", [P, IB, GT])
        proj = st.sbuf("proj", [XP, GT])
        mag = st.sbuf("mag", [P, 2, GT])
        pos = st.sbuf("pos", [P, 2, GT])
        step = st.sbuf("step", [P, IB, GT])
        du = st.sbuf("du", [P, IB, GT])
        bc = st.sbuf("bc", [P, 2, GT])
        dBu = st.sbuf("dBu", [P, NB, GT])
        hs = st.sbuf("hs", [P, NB, GT])
        hc = st.sbuf("hc", [P, NB, GT])
        y = st.sbuf("y", [P, IB, GT])
        yz = st.sbuf("yz", [P, IB, GT])
        names = ("w_loaded", "zeros", "picked", "expd", "decay_done",
                 "xz_done", "conv_step", "xc_done", "z_done", "xp_done", "proj_done", "dt_done", "mag_done", "pos_done",
                 "ea_done", "step_done", "sp_done", "du_done", "b_mm", "c_mm", "bc_done", "dA_done", "dbu_dve", "dbu_pool",
                 "scan_done", "hc_done", "y_mm", "y_done", "yz_done", "o_done", "res_done")
        s = {x: st.sem(x) for x in names}
        with nc.Block() as block:
            @block.sync
            def _(sp):
                n = 0
                for d in range(2):
                    for dst, src in ((w_in[d][:, :, :], params[d]["in_t"].rearrange("(k p) n -> p k n", p=P)),
                                     (w_xp[d][:, :, :], params[d]["xproj_t"].rearrange("(k p) n -> p k n", p=P)),
                                     (w_dt[d][:, :], params[d]["dt_t"]),
                                     (w_out[d][:, :, :], params[d]["out_t"].rearrange("(k p) n -> p k n", p=P)),
                                     (conv_w[d][:, :, :], params[d]["conv_w"]), (conv_b[d][:, :], params[d]["conv_b"]),
                                     (dt_b[d][:, :], params[d]["dt_b"]), (skip[d][:, :], params[d]["d"]),
                                     (expo[d][:, :, :], params[d]["a_log"])):
                        sp.dma_start(dst, src).then_inc(s["w_loaded"], 16)
                        n += 16
                sp.wait_ge(s["w_loaded"], n)

            @block.gpsimd
            def _(pool):
                nc.gpsimd.memset(dA[0][:, :, :], 0.0)
                nc.gpsimd.memset(dA[1][:, :, :], 0.0)
                nc.gpsimd.memset(one[:, :], 1.0)
                nc.gpsimd.memset(pick[:, :, :], 0.0).then_inc(s["zeros"], 1)
                pool.wait_ge(s["zeros"], 1)
                nc.gpsimd.affine_select(out=pick[:, :, :], in_=pick[:, :, :], compare_op=ALU.not_equal, fill=1.0,
                                        base=-R, pattern=[[-1, 2 * S], [0, P]], channel_multiplier=1).then_inc(s["picked"], 1)

            @block.scalar
            def _(act):
                nc.scalar.preload_act_table_set(EXP_LN)
                act.wait_ge(s["w_loaded"], 18 * 16)
                for d in range(2):
                    nc.scalar.activation(decay[d][:, :, :], expo[d][:, :, :], ACT.Exp).then_inc(s["expd"], 1)

            @block.vector
            def _(dve):
                dve.wait_ge(s["expd"], 2)
                for d in range(2):
                    nc.vector.tensor_scalar(decay[d][:, :, :], decay[d][:, :, :], -1.0, None, ALU.mult)\
                        .then_inc(s["decay_done"], 1)
        st.clear()

        def rows(ap):
            return ap.rearrange("p (b n) -> p b n", n=N)

        def flow(ap, d):
            return ap if d == 0 else ap[:, ::-1]

        def by_pool(i):
            return i % POOL_EVERY == POOL_EVERY - 1

        pool_upto = [sum(by_pool(j) for j in range(i + 1)) for i in range(STEPS)]
        dve_upto = [i + 1 - pool_upto[i] for i in range(STEPS)]

        def delta(dve, d, m):
            i = IB * d + m
            dve.wait_ge(s["sp_done"], i + 1)
            dve.wait_ge(s["pos_done"], i + 1)
            nc.vector.tensor_tensor(step[:, m, :], step[:, m, :], pos[:, m % 2, :], ALU.add).then_inc(s["step_done"], 1)
            dve.wait_ge(s["step_done"], i + 1)
            nc.vector.tensor_tensor(du[:, m, :], step[:, m, :], xc[:, m, :], ALU.mult).then_inc(s["du_done"], 1)

        def recur(dve, d, i):
            n, j = i // IB, i % IB
            if not by_pool(i):
                if n == 0:
                    dve.wait_ge(s["du_done"], IB * d + j + 1)
                dve.wait_ge(s["bc_done"], S * d + n + 1)
                if i >= NB:
                    dve.wait_ge(s["scan_done"], STEPS * d + i - NB + 1)
                nc.vector.tensor_tensor(dBu[:, i % NB, :], du[:, j, :], ps[4 + n % 2][:, 0:GT], ALU.mult)\
                    .then_inc(s["dbu_dve"], 1)
                dve.wait_ge(s["dbu_dve"], d * dve_upto[-1] + dve_upto[i])
            else:
                dve.wait_ge(s["dbu_pool"], d * pool_upto[-1] + pool_upto[i])
            dve.wait_ge(s["dA_done"], STEPS * d + i + 1)
            if STEPS * d + i >= NB:
                dve.wait_ge(s["hc_done"], STEPS * d + i - NB + 1)
            nc.vector.tensor_tensor_scan(flow(hs[:, i % NB, :], d), flow(dA[d][:, i % NB, :], d),
                                         flow(dBu[:, i % NB, :], d), 0.0, ALU.mult, ALU.add).then_inc(s["scan_done"], 1)
            dve.wait_ge(s["scan_done"], STEPS * d + i + 1)
            dve.wait_ge(s["c_mm"], S * d + n + 1)
            if STEPS * d + i >= NB:
                dve.wait_ge(s["y_mm"], STEPS * d + i - NB + 1)
            nc.vector.tensor_tensor(hc[:, i % NB, :], hs[:, i % NB, :], ps[6 + n % 2][:, 0:GT], ALU.mult)\
                .then_inc(s["hc_done"], 1)

        with nc.Fori(0, GROUPS) as g:
            with nc.Block(no_gpsimd_drain=True) as block:
                @block.tensor
                def _(pe):
                    norm.tensor_mean(nc, pe, c["ones"], lambda k: h[:, k, group_cols(g)])
                    norm.tensor_var(nc, pe, c["ones"])
                    pe.wait_ge(norm.ready, 1)
                    for d in range(2):
                        if d:
                            pe.wait_ge(s["res_done"], DK)
                            pe.wait_ge(s["y_done"], IB)
                        for m in range(2 * IB):
                            for k in range(DK):
                                mm = nc.tensor.matmul(ps[m][:, 0:GT], w_in[d][:, k, m * P:(m + 1) * P], norm.out[:, k, :],
                                                      start=(k == 0), stop=(k == DK - 1))
                            mm.then_inc(s["xz_done"], 1)
                        pe.wait_ge(s["z_done"], IB * (d + 1))
                        for k in range(IB):
                            pe.wait_ge(s["xc_done"], IB * d + k + 1)
                            mm = nc.tensor.matmul(ps[4][0:XP, 0:GT], w_xp[d][:, k, :], xc[:, k, :],
                                                  start=(k == 0), stop=(k == IB - 1))
                        mm.then_inc(s["xp_done"], 1)
                        pe.wait_ge(s["proj_done"], d + 1)
                        for m in range(IB):
                            nc.tensor.matmul(ps[m][:, 0:GT], w_dt[d][:, m * P:(m + 1) * P], proj[0:R, :],
                                             start=True, stop=True).then_inc(s["dt_done"], 1)

                        def spread(n):
                            if n >= 2:
                                pe.wait_ge(s["bc_done"], S * d + n - 1)
                                pe.wait_ge(s["dbu_dve"], d * dve_upto[-1] + dve_upto[IB * (n - 1) - 1])
                            elif n == 1 and d == 0:
                                pass
                            nc.tensor.matmul(ps[4 + n % 2][:, 0:GT], pick[:, n, :], proj[:, :], start=True, stop=True)\
                                .then_inc(s["b_mm"], 1)
                            if n >= 2:
                                pe.wait_ge(s["hc_done"], STEPS * d + IB * (n - 1))
                            nc.tensor.matmul(ps[6 + n % 2][:, 0:GT], pick[:, S + n, :], proj[:, :], start=True, stop=True)\
                                .then_inc(s["c_mm"], 1)

                        spread(0)
                        spread(1)
                        pe.wait_ge(s["mag_done"], IB * (d + 1))
                        pe.wait_ge(s["pos_done"], IB * (d + 1))
                        for n in range(S):
                            for j in range(IB):
                                i = n * IB + j
                                pe.wait_ge(s["hc_done"], STEPS * d + i + 1)
                                nc.tensor.matmul(ps[j][:, 0:GT], c["ident"][:, :], hc[:, i % NB, :],
                                                 start=(n == 0), stop=(n == S - 1)).then_inc(s["y_mm"], 1)
                            if n + 2 < S:
                                spread(n + 2)
                        pe.wait_ge(s["bc_done"], S * (d + 1))
                        pe.wait_ge(s["dbu_dve"], (d + 1) * dve_upto[-1])
                        for m in range(DK):
                            for k in range(IB):
                                pe.wait_ge(s["yz_done"], IB * d + k + 1)
                                mm = nc.tensor.matmul(ps[4 + m][:, 0:GT], w_out[d][:, k, m * P:(m + 1) * P], yz[:, k, :],
                                                      start=(k == 0), stop=(k == IB - 1))
                            mm.then_inc(s["o_done"], 1)

                @block.scalar
                def _(act):
                    nc.scalar.preload_act_table_set(EXP_LN)
                    norm.scalar(nc, act, c["eps"])
                    for d in range(2):
                        if d:
                            act.wait_ge(s["yz_done"], IB)
                        for m in range(IB):
                            act.wait_ge(s["xz_done"], 2 * IB * d + IB + m + 1)
                            nc.scalar.activation(z[:, m, :], ps[IB + m][:, 0:GT], ACT.Silu).then_inc(s["z_done"], 1)
                        for m in range(IB):
                            act.wait_ge(s["conv_step"], TAPS * (IB * d + m + 1))
                            nc.scalar.activation(xc[:, m, :], conv[:, m, :], ACT.Silu).then_inc(s["xc_done"], 1)
                        nc.scalar.preload_act_table_set(EXP_LN)
                        act.wait_ge(s["xp_done"], d + 1)
                        nc.scalar.activation(proj[:, :], ps[4][0:XP, 0:GT], ACT.Copy).then_inc(s["proj_done"], 1)
                        for m in range(IB):
                            i = IB * d + m
                            act.wait_ge(s["pos_done"], i + 1)
                            nc.scalar.activation(mag[:, m % 2, :], ps[m][:, 0:GT], ACT.Abs, bias=dt_b[d][:, m:m + 1])\
                                .then_inc(s["mag_done"], 1)
                            act.wait_ge(s["mag_done"], i + 1)
                            nc.scalar.activation(mag[:, m % 2, :], mag[:, m % 2, :], ACT.Exp, scale=-1.0).then_inc(s["ea_done"], 1)
                            act.wait_ge(s["ea_done"], i + 1)
                            nc.scalar.activation(step[:, m, :], mag[:, m % 2, :], ACT.Ln, bias=one[:, 0:1]).then_inc(s["sp_done"], 1)
                        for n in range(S):
                            act.wait_ge(s["b_mm"], S * d + n + 1)
                            if n >= 2:
                                act.wait_ge(s["dbu_pool"], d * pool_upto[-1] + pool_upto[IB * (n - 1) - 1])
                            nc.scalar.activation(bc[:, n % 2, :], ps[4 + n % 2][:, 0:GT], ACT.Copy).then_inc(s["bc_done"], 1)
                            for j in range(IB):
                                i = n * IB + j
                                if n == 0:
                                    act.wait_ge(s["step_done"], IB * d + j + 1)
                                if i >= NB:
                                    act.wait_ge(s["scan_done"], STEPS * d + i - NB + 1)
                                lo = 1 if d == 0 else 0
                                nc.scalar.activation(rows(dA[d][:, i % NB, :])[:, :, lo:lo + N - 1],
                                                     rows(step[:, j, :])[:, :, lo:lo + N - 1], ACT.Exp,
                                                     scale=decay[d][:, j, n:n + 1]).then_inc(s["dA_done"], 1)

                @block.gpsimd
                def _(pool):
                    for d in range(2):
                        for i in range(STEPS):
                            n, j = i // IB, i % IB
                            if not by_pool(i):
                                continue
                            pool.wait_ge(s["bc_done"], S * d + n + 1)
                            if n == 0:
                                pool.wait_ge(s["du_done"], IB * d + j + 1)
                            if i >= NB:
                                pool.wait_ge(s["scan_done"], STEPS * d + i - NB + 1)
                            elif d:
                                pool.wait_ge(s["scan_done"], STEPS)
                            nc.gpsimd.tensor_tensor(dBu[:, i % NB, :], du[:, j, :], bc[:, n % 2, :], ALU.mult)\
                                .then_inc(s["dbu_pool"], 1)

                @block.vector
                def _(dve):
                    norm.vector(nc, dve, h[:, :, group_cols(g)])
                    for d in range(2):
                        for m in range(IB):
                            dve.wait_ge(s["xz_done"], 2 * IB * d + m + 1)
                            n0 = TAPS * (IB * d + m)
                            if d:
                                dve.wait_ge(s["xc_done"], IB)
                            nc.vector.tensor_scalar(conv[:, m, :], ps[m][:, 0:GT], conv_w[d][:, m, TAPS - 1:TAPS],
                                                    conv_b[d][:, m:m + 1], ALU.mult, ALU.add).then_inc(s["conv_step"], 1)
                            for t in range(1, TAPS):
                                src = rows(ps[m][:, 0:GT])
                                dst = rows(conv[:, m, :])
                                src, dst = ((src[:, :, 0:N - t], dst[:, :, t:N]) if d == 0 else
                                            (src[:, :, t:N], dst[:, :, 0:N - t]))
                                dve.wait_ge(s["conv_step"], n0 + t)
                                nc.vector.scalar_tensor_tensor(out=dst, in0=src, scalar=conv_w[d][:, m, TAPS - 1 - t:TAPS - t],
                                                               in1=dst, op0=ALU.mult, op1=ALU.add).then_inc(s["conv_step"], 1)
                        for m in range(IB):
                            i = IB * d + m
                            dve.wait_ge(s["dt_done"], i + 1)
                            if m >= 2:
                                dve.wait_ge(s["step_done"], i - 1)
                            nc.vector.tensor_scalar(pos[:, m % 2, :], ps[m][:, 0:GT], dt_b[d][:, m:m + 1], 0.0, ALU.add, ALU.max)\
                                .then_inc(s["pos_done"], 1)
                            if m >= 1:
                                delta(dve, d, m - 1)
                        delta(dve, d, IB - 1)
                        for i in range(STEPS):
                            recur(dve, d, i)
                        for j in range(IB):
                            dve.wait_ge(s["y_mm"], STEPS * d + STEPS - IB + j + 1)
                            nc.vector.scalar_tensor_tensor(out=y[:, j, :], in0=xc[:, j, :], scalar=skip[d][:, j:j + 1],
                                                           in1=ps[j][:, 0:GT], op0=ALU.mult, op1=ALU.add).then_inc(s["y_done"], 1)
                            dve.wait_ge(s["y_done"], IB * d + j + 1)
                            nc.vector.tensor_tensor(yz[:, j, :], y[:, j, :], z[:, j, :], ALU.mult).then_inc(s["yz_done"], 1)
                        for m in range(DK):
                            dve.wait_ge(s["o_done"], DK * d + m + 1)
                            nc.vector.tensor_tensor(h[:, m, group_cols(g)], ps[4 + m][:, 0:GT], h[:, m, group_cols(g)],
                                                    ALU.add).then_inc(s["res_done"], 1)

            st.clear()


def l1_ffn(nc, h, c, w_fc, w_proj, u_t, v, fast_b, gate):
    HID, RANK = w_fc.shape[0], v.shape[0]
    HB = HID // P
    with Stage(nc, "l1f") as st:
        ps = [st.psum(f"ps{i}") for i in range(8)]
        wfcT = st.sbuf("wfcT", [P, DK, HID])
        wprojT = st.sbuf("wprojT", [P, HB, D])
        with Stage(nc, "l1w") as sw:
            raw = {"fc": sw.sbuf("raw_fc", [P, HB, D]), "proj": sw.sbuf("raw_proj", [P, DK, HID])}
            mag = {"fc": sw.sbuf("mag_fc", [P, HB]), "proj": sw.sbuf("mag_proj", [P, DK])}
            pos = sw.sbuf("pos", [P, HB * D])
            neg = sw.sbuf("neg", [P, HB * D])
            uT = sw.sbuf("uT", [RANK, HID])
            vs = sw.sbuf("vs", [RANK, D])
            fb = sw.sbuf("fb", [RANK, RANK])
            gt = sw.sbuf("gt", [RANK, 1])
            low = sw.sbuf("low", [RANK, HID])
            thr = {"fc": sw.sbuf("thr_fc", [P, HB]), "proj": sw.sbuf("thr_proj", [P, DK])}
            loaded, step, low_mm, low_ready, tern, turned, copied = (
                sw.sem(x) for x in ("loaded", "step", "low_mm", "low_ready", "tern", "turned", "copied"))
            with nc.Block() as block:
                @block.sync
                def _(sp):
                    sp.dma_start(raw["fc"][:, :, :], w_fc.rearrange("(m p) d -> p m d", p=P)).then_inc(loaded, 16)
                    sp.dma_start(raw["proj"][:, :, :], w_proj.rearrange("(m p) d -> p m d", p=P)).then_inc(loaded, 16)
                    sp.dma_start(uT[:, :], u_t).then_inc(loaded, 16)
                    sp.dma_start(vs[:, :], v).then_inc(loaded, 16)
                    sp.dma_start(fb[:, :], fast_b).then_inc(loaded, 16)
                    sp.dma_start(gt[:, :], gate.to_broadcast([RANK, 1])).then_inc(loaded, 16)

                @block.vector
                def _(dve):
                    dve.wait_ge(loaded, 96)
                    n = 0
                    for w, rows, cols in (("fc", HB, D), ("proj", DK, HID)):
                        W, pv = raw[w], pos[:, 0:rows * cols].rearrange("p (m d) -> p m d", m=rows)
                        nv = neg[:, 0:rows * cols].rearrange("p (m d) -> p m d", m=rows)
                        nc.vector.scalar_tensor_tensor(out=pv, in0=W[:, :, :], scalar=-1.0, in1=W[:, :, :],
                                                       op0=ALU.mult, op1=ALU.max).then_inc(step, 1)
                        dve.wait_ge(step, n + 1)
                        nc.vector.tensor_reduce(thr[w][:, :], pv, AX.X, ALU.add).then_inc(step, 1)
                        dve.wait_ge(step, n + 2)
                        nc.vector.tensor_scalar(mag[w][:, :], thr[w][:, :], 1.0 / cols, 1e-5, ALU.mult, ALU.max)\
                            .then_inc(step, 1)
                        dve.wait_ge(step, n + 3)
                        nc.vector.tensor_scalar(thr[w][:, :], mag[w][:, :], 0.5, None, ALU.mult).then_inc(step, 1)
                        dve.wait_ge(step, n + 4)
                        wide = thr[w][:, :].unsqueeze(2).to_broadcast([P, rows, cols])
                        nc.vector.tensor_tensor(pv, W[:, :, :], wide, ALU.is_gt).then_inc(step, 1)
                        nc.vector.scalar_tensor_tensor(out=nv, in0=W[:, :, :], scalar=-1.0, in1=wide,
                                                       op0=ALU.mult, op1=ALU.is_gt).then_inc(step, 1)
                        dve.wait_ge(step, n + 6)
                        nc.vector.tensor_tensor(pv, pv, nv, ALU.subtract).then_inc(step, 1)
                        dve.wait_ge(step, n + 7)
                        nc.vector.tensor_tensor(nv, pv, W[:, :, :], ALU.subtract).then_inc(step, 1)
                        dve.wait_ge(step, n + 8)
                        nc.vector.tensor_tensor(nv, W[:, :, :], nv, ALU.add).then_inc(step, 1)
                        dve.wait_ge(step, n + 9)
                        nc.vector.tensor_tensor(W[:, :, :], nv, mag[w][:, :].unsqueeze(2).to_broadcast([P, rows, cols]),
                                                ALU.mult).then_inc(tern, 1)
                        dve.wait_ge(tern, 1 if w == "fc" else 2)
                        n += 9
                    for j in range(2):
                        dve.wait_ge(low_mm, j + 1)
                        nc.vector.tensor_scalar(low[:, j * 512:(j + 1) * 512], ps[j][0:RANK, :], gt[:, 0:1], None,
                                                ALU.mult).then_inc(low_ready, 1)
                    for i in range(HB + DK * HB // 4):
                        dve.wait_ge(turned, i + 1)
                        bank = ps[2 + i % 6]
                        if i < HB:
                            dst = wfcT[:, i // 4, (i % 4) * 256:(i % 4) * 256 + 256]
                            nc.vector.tensor_copy(dst, bank[:, 0:256]).then_inc(copied, 1)
                        else:
                            m = i - HB
                            nc.vector.tensor_copy(wprojT[:, 2 * m:2 * m + 2, :].rearrange("p a d -> p (a d)"),
                                                  bank[:, :]).then_inc(copied, 1)

                @block.tensor
                def _(pe):
                    pe.wait_ge(loaded, 96)
                    for j in range(2):
                        nc.tensor.matmul(ps[j][0:RANK, :], fb[:, :], uT[:, j * 512:(j + 1) * 512],
                                         start=True, stop=True).then_inc(low_mm, 1)
                    pe.wait_ge(low_ready, 2)
                    pe.wait_ge(tern, 1)
                    for i in range(HB):
                        if i >= 6:
                            pe.wait_ge(copied, i - 5)
                        k, q = i // 4, i % 4
                        for j in range(2):
                            m = 2 * q + j
                            out = ps[2 + i % 6][:, j * P:(j + 1) * P]
                            nc.tensor.matmul(out, raw["fc"][:, m, k * P:(k + 1) * P], c["ident"][:, :], start=True, stop=False)
                            mm = nc.tensor.matmul(out, vs[:, k * P:(k + 1) * P], low[:, m * P:(m + 1) * P],
                                                  start=False, stop=True)
                        mm.then_inc(turned, 1)
                    pe.wait_ge(tern, 2)
                    for i in range(HB, HB + DK * HB // 4):
                        pe.wait_ge(copied, i - 5)
                        for j in range(4):
                            kb, m = 2 * (i - HB) + j // 2, j % 2
                            mm = nc.tensor.matmul(ps[2 + i % 6][:, j * P:(j + 1) * P], raw["proj"][:, m, kb * P:(kb + 1) * P],
                                                  c["ident"][:, :], start=True, stop=True)
                        mm.then_inc(turned, 1)
            sw.clear()

        norm = Norm(st, ps[0], ps[1])
        relu = st.sbuf("relu", [P, HB, GT])
        act2 = st.sbuf("act2", [P, HB, GT])
        fc_done, relu_done, sq_done, proj_done, res_done = (
            st.sem(x) for x in ("fc_done", "relu_done", "sq_done", "proj_done", "res_done"))
        with nc.Fori(0, GROUPS) as g:
            with nc.Block(no_gpsimd_drain=True) as block:
                @block.tensor
                def _(pe):
                    norm.tensor_mean(nc, pe, c["ones"], lambda k: h[:, k, group_cols(g)])
                    norm.tensor_var(nc, pe, c["ones"])
                    pe.wait_ge(norm.ready, 1)
                    for m in range(HB):
                        if m >= 4:
                            pe.wait_ge(relu_done, m - 3)
                        for k in range(DK):
                            mm = nc.tensor.matmul(ps[2 + m % 4][:, 0:GT], wfcT[:, k, m * P:(m + 1) * P], norm.out[:, k, :],
                                                  start=(k == 0), stop=(k == DK - 1))
                        mm.then_inc(fc_done, 1)
                    for j in range(DK):
                        for m in range(HB):
                            if j == 0:
                                pe.wait_ge(sq_done, m + 1)
                            mm = nc.tensor.matmul(ps[6 + j][:, 0:GT], wprojT[:, m, j * P:(j + 1) * P], act2[:, m, :],
                                                  start=(m == 0), stop=(m == HB - 1))
                        mm.then_inc(proj_done, 1)

                @block.scalar
                def _(act):
                    norm.scalar(nc, act, c["eps"])
                    for m in range(HB):
                        act.wait_ge(fc_done, m + 1)
                        nc.scalar.activation(relu[:, m, :], ps[2 + m % 4][:, 0:GT], ACT.Relu).then_inc(relu_done, 1)

                @block.vector
                def _(dve):
                    norm.vector(nc, dve, h[:, :, group_cols(g)])
                    for m in range(HB):
                        dve.wait_ge(relu_done, m + 1)
                        nc.vector.tensor_tensor(act2[:, m, :], relu[:, m, :], relu[:, m, :], ALU.mult).then_inc(sq_done, 1)
                    for j in range(DK):
                        dve.wait_ge(proj_done, j + 1)
                        nc.vector.tensor_tensor(h[:, j, group_cols(g)], h[:, j, group_cols(g)], ps[6 + j][:, 0:GT],
                                                ALU.add).then_inc(res_done, 1)
            st.clear()


def l2_ffn(nc, h, c, wr, br, w1, b1, w2, b2, row_expert):
    E = wr.shape[1]
    HID = w1.shape[3]
    HB = HID // P
    with Stage(nc, "ex2") as st:
        ps = [st.psum(f"ps{i}") for i in range(8)]
        normed = st.sbuf("normed", [P, DK, T])
        means = st.sbuf("means", [P, DK, B])
        with Stage(nc, "rt2") as sr:
            norm = Norm(sr, ps[0], ps[1])
            kept, summed = sr.sem("kept"), sr.sem("summed")
            with nc.Fori(0, GROUPS) as g:
                with nc.Block(no_gpsimd_drain=True) as block:
                    @block.tensor
                    def _(pe):
                        norm.tensor_mean(nc, pe, c["ones"], lambda k: h[:, k, group_cols(g)])
                        norm.tensor_var(nc, pe, c["ones"])

                    @block.scalar
                    def _(act):
                        nc.scalar.preload_act_table_set(EXP_LN)
                        norm.scalar(nc, act, c["eps"])
                        act.wait_ge(norm.ready, 1)
                        nc.scalar.activation(normed[:, :, group_cols(g)], norm.out[:, :, :], ACT.Copy).then_inc(kept, 1)

                    @block.vector
                    def _(dve):
                        norm.vector(nc, dve, h[:, :, group_cols(g)])
                        dve.wait_ge(norm.ready, 1)
                        nc.vector.tensor_reduce(means[:, :, bass.ds(g * GB, GB)],
                                                norm.out[:, :, :].rearrange("p k (b n) -> p k b n", n=N), AX.X, ALU.add)\
                            .then_inc(summed, 1)
                sr.clear()
            w_r = sr.sbuf("w_r", [P, DK, E])
            b_r = sr.sbuf("b_r", [B, E])
            score = sr.sbuf("score", [B, E])
            top = sr.sbuf("top", [B, 8])
            best = sr.sbuf("best", [B, 8], U32)
            loaded, mean_ready, score_mm, score_done, top_done, best_done, sent = (
                sr.sem(x) for x in ("loaded", "mean_ready", "score_mm", "score_done", "top_done", "best_done", "sent"))
            with nc.Block() as block:
                @block.sync
                def _(sp):
                    sp.dma_start(w_r[:, :, :], wr.rearrange("(k p) e -> p k e", p=P)).then_inc(loaded, 16)
                    sp.dma_start(b_r[:, :], br.to_broadcast([B, E])).then_inc(loaded, 16)
                    sp.wait_ge(best_done, 1)
                    sp.dma_start(row_expert, best[:, 0:1]).then_inc(sent, 16)
                    sp.wait_ge(sent, 16)

                @block.vector
                def _(dve):
                    nc.vector.tensor_scalar(means[:, :, :], means[:, :, :], 1.0 / N, None, ALU.mult).then_inc(mean_ready, 1)
                    dve.wait_ge(score_mm, 1)
                    dve.wait_ge(loaded, 32)
                    nc.vector.tensor_tensor(score[:, :], ps[0][0:B, 0:E], b_r[:, :], ALU.add).then_inc(score_done, 1)
                    dve.wait_ge(score_done, 1)
                    nc.vector.max(top[:, :], score[:, :]).then_inc(top_done, 1)
                    dve.wait_ge(top_done, 1)
                    nc.vector.max_index(best[:, :], top[:, :], score[:, :]).then_inc(best_done, 1)

                @block.tensor
                def _(pe):
                    pe.wait_ge(loaded, 32)
                    pe.wait_ge(mean_ready, 1)
                    for k in range(DK):
                        mm = nc.tensor.matmul(ps[0][0:B, 0:E], means[:, k, :], w_r[:, k, :], start=(k == 0), stop=(k == DK - 1))
                    mm.then_inc(score_mm, 1)
            sr.clear()

        WB = GB
        W1 = [st.sbuf(f"w1_{i}", [P, DK, HID]) for i in range(WB)]
        W2 = [st.sbuf(f"w2_{i}", [P, HB, D]) for i in range(WB)]
        B1 = [st.sbuf(f"b1_{i}", [P, HB]) for i in range(WB)]
        B2 = [st.sbuf(f"b2_{i}", [P, DK]) for i in range(WB)]
        ids = st.sbuf("ids", [1, B + 1], U32)
        hid = st.sbuf("hid", [P, 2, HB, N])
        x_in = st.sbuf("x_in", [P, DK, GT])
        id_in = st.sem("id_in")
        landed = [st.sem(f"landed{i}") for i in range(WB)]
        x_done, up_done, relu_done, down_done, res_done = (
            st.sem(x) for x in ("x_done", "up_done", "relu_done", "down_done", "res_done"))

        def fetch(sp, row, i):
            e = nc.sync.value_load(ids[0:1, bass.ds(row, 1)], min_val=0, max_val=E - 1)
            for dst, src in ((W1[i][:, :, :], w1[bass.ds(e, 1), :, :, :]), (W2[i][:, :, :], w2[bass.ds(e, 1), :, :, :]),
                             (B1[i][:, :], b1[bass.ds(e, 1), :, :]), (B2[i][:, :], b2[bass.ds(e, 1), :, :])):
                names = "e p k n -> (e p) k n" if len(src.shape) == 4 else "e p n -> (e p) n"
                sp.dma_start(dst, src.rearrange(names)).then_inc(landed[i], 16)

        with nc.Block() as block:
            @block.sync
            def _(sp):
                sp.dma_start(ids[0:1, 0:B], row_expert.rearrange("b a -> a b")).then_inc(id_in, 16)
                sp.dma_start(ids[0:1, B:B + 1], row_expert[0:1, :]).then_inc(id_in, 16)
                sp.wait_ge(id_in, 32)
                fetch(sp, 0, 0)
                sp.wait_ge(landed[0], 64)
        st.clear()
        with nc.Fori(0, GROUPS) as g:
            with nc.Block(no_gpsimd_drain=True) as block:
                @block.sync
                def _(sp):
                    for i in range(1, WB):
                        fetch(sp, g * GB + i, i)
                    sp.wait_ge(down_done, DK)
                    sp.wait_ge(res_done, DK)
                    fetch(sp, g * GB + GB, 0)
                    sp.wait_ge(landed[0], 64)

                @block.tensor
                def _(pe):
                    pe.wait_ge(x_done, 1)
                    for i in range(GB):
                        if i:
                            pe.wait_ge(landed[i], 64)
                        for m in range(HB):
                            bank = ps[2 * (i % 2) + m // 4]
                            if m % 4 == 0 and i >= 2:
                                pe.wait_ge(relu_done, HB * (i - 2) + m + 4)
                            for k in range(DK):
                                mm = nc.tensor.matmul(bank[:, (m % 4) * N:(m % 4 + 1) * N], W1[i][:, k, m * P:(m + 1) * P],
                                                      x_in[:, k, i * N:(i + 1) * N], start=(k == 0), stop=(k == DK - 1))
                            if m % 4 == 3:
                                mm.then_inc(up_done, 1)
                        for j in range(DK):
                            if i >= 2:
                                pe.wait_ge(res_done, DK * (i - 2) + j + 1)
                            for m in range(HB):
                                if j == 0:
                                    pe.wait_ge(relu_done, HB * i + m + 1)
                                mm = nc.tensor.matmul(ps[4 + 2 * (i % 2) + j][:, 0:N], W2[i][:, m, j * P:(j + 1) * P],
                                                      hid[:, i % 2, m, :], start=(m == 0), stop=(m == HB - 1))
                            mm.then_inc(down_done, 1)

                @block.scalar
                def _(act):
                    nc.scalar.activation(x_in[:, :, :], normed[:, :, group_cols(g)], ACT.Copy).then_inc(x_done, 1)
                    for i in range(GB):
                        if i:
                            act.wait_ge(landed[i], 64)
                        if i >= 2:
                            act.wait_ge(down_done, DK * (i - 1))
                        for m in range(HB):
                            act.wait_ge(up_done, 2 * i + m // 4 + 1)
                            nc.scalar.activation(hid[:, i % 2, m, :], ps[2 * (i % 2) + m // 4][:, (m % 4) * N:(m % 4 + 1) * N],
                                                 ACT.Relu, bias=B1[i][:, m:m + 1]).then_inc(relu_done, 1)

                @block.vector
                def _(dve):
                    for i in range(GB):
                        if i:
                            dve.wait_ge(landed[i], 64)
                        for j in range(DK):
                            at = h[:, j, bass.ds(g * GT + i * N, N)]
                            dve.wait_ge(down_done, DK * i + j + 1)
                            nc.vector.scalar_tensor_tensor(out=at, in0=ps[4 + 2 * (i % 2) + j][:, 0:N], scalar=B2[i][:, j:j + 1],
                                                           in1=at, op0=ALU.add, op1=ALU.add).then_inc(res_done, 1)
            st.clear()


FAR = -1e38


def rwkv(nc, h, c, wk, wv, wr, ck, cv, cr, cols):
    HID = ck.shape[1]
    HB = HID // P
    NC = 11
    DECAY, FIRST, G1, B1, G2, B2, MK, MV, MR, CK, CR = range(NC)
    MIXES = (MK, MV, MR, CK, CR)
    with Stage(nc, "rw") as st:
        W = {x: st.sbuf(x, [P, DK, D]) for x in ("wk", "wv", "wr", "cr")}
        w_ck = st.sbuf("ck", [P, DK, HID])
        w_cv = st.sbuf("cv", [P, HB, D])
        col = st.sbuf("cols", [P, NC, DK])
        rest = st.sbuf("rest", [P, NC, DK])
        first_neg = st.sbuf("first_neg", [P, DK])
        ps = [st.psum(f"ps{i}") for i in range(8)]
        norms = [Norm(st, ps[0], ps[1], f"ln{i}") for i in range(3)]
        h1 = st.sbuf("h1", [P, DK, GT])
        back = st.sbuf("back", [P, 5, DK, GT])
        mixed = st.sbuf("mixed", [P, 5, DK, GT])
        drift = st.sbuf("drift", [P, DK, GB, N + 1])
        kp = st.sbuf("kp", [P, DK, GB, N + 1])
        v = st.sbuf("v", [P, DK, GT])
        Mp = st.sbuf("Mp", [P, DK, GB, N + 1])
        PPp = st.sbuf("PPp", [P, DK, GB, N + 1])
        AAp = st.sbuf("AAp", [P, DK, GB, N + 1])
        d1 = st.sbuf("d1", [P, DK, GT])
        d2 = st.sbuf("d2", [P, DK, GT])
        s_ = st.sbuf("s", [P, DK, GT])
        gate = st.sbuf("gate", [P, DK, GT])
        rg = st.sbuf("rg", [P, DK, GT])
        aa = st.sbuf("aa", [P, DK, GT])
        x2 = st.sbuf("x2", [P, DK, GT])
        relu = st.sbuf("relu", [P, 2, GT])
        act2 = st.sbuf("act2", [P, HB, GT])
        names = ("loaded", "set", "rested", "h1_done", "back_done", "mix_done", "k_mm", "v_mm", "r_mm", "k_done", "v_done",
                 "M_done", "d1_done", "d2_done", "a_done", "s_done", "ln_done", "pp_done", "dl_done", "min_done", "e_done",
                 "ev_done", "aa_done", "aap_done", "diff_done", "gate_done", "rg_done", "gd_done", "y_done", "ry_done", "x2_done", "h2_done",
                 "c_mm", "relu_done", "sq_done", "cr_mm", "cv_mm", "sig_done", "sk_done", "x3_done", "res_done")
        s = {x: st.sem(x) for x in names}
        with nc.Block() as block:
            @block.sync
            def _(sp):
                for dst, src in ((W["wk"], wk), (W["wv"], wv), (W["wr"], wr), (W["cr"], cr), (w_ck, ck), (w_cv, cv)):
                    sp.dma_start(dst[:, :, :], src.rearrange("(k p) n -> p k n", p=P)).then_inc(s["loaded"], 16)
                sp.dma_start(col[:, :, :], cols).then_inc(s["loaded"], 16)
                sp.wait_ge(s["loaded"], 112)

            @block.gpsimd
            def _(pool):
                nc.gpsimd.memset(back[:, :, :, :], 0.0)
                nc.gpsimd.memset(kp[:, :, :, :], 0.0)
                nc.gpsimd.memset(PPp[:, :, :, :], FAR)
                nc.gpsimd.memset(AAp[:, :, :, :], 0.0)
                nc.gpsimd.memset(drift[:, :, :, :], 0.0).then_inc(s["set"], 1)

            @block.vector
            def _(dve):
                dve.wait_ge(s["loaded"], 112)
                nc.vector.tensor_scalar(rest[:, :, :], col[:, :, :], -1.0, 1.0, ALU.mult, ALU.add).then_inc(s["rested"], 1)
                nc.vector.tensor_scalar(first_neg[:, :], col[:, FIRST, :], -1.0, None, ALU.mult).then_inc(s["rested"], 1)
                dve.wait_ge(s["set"], 1)
                for k in range(DK):
                    nc.vector.tensor_scalar(drift[:, k, :, 1:N + 1], drift[:, k, :, 1:N + 1], col[:, DECAY, k:k + 1], None,
                                            ALU.add).then_inc(s["rested"], 1)
                nc.vector.memset(drift[:, :, :, 0:1], FAR).then_inc(s["rested"], 1)

            @block.scalar
            def _(act):
                nc.scalar.preload_act_table_set(EXP_LN)
        st.clear()

        def rows(ap):
            return ap.rearrange("p (b n) -> p b n", n=N)

        def both(ap):
            return ap.rearrange("p k (b n) -> p k b n", n=N)

        with nc.Fori(0, GROUPS) as g:
            with nc.Block(no_gpsimd_drain=True) as block:
                @block.tensor
                def _(pe):
                    norms[0].tensor_mean(nc, pe, c["ones"], lambda k: h[:, k, group_cols(g)])
                    norms[0].tensor_var(nc, pe, c["ones"])
                    pe.wait_ge(norms[0].ready, 1)
                    norms[1].tensor_mean(nc, pe, c["ones"], lambda k: norms[0].out[:, k, :])
                    norms[1].tensor_var(nc, pe, c["ones"])
                    for i, (x, done) in enumerate((("wk", s["k_mm"]), ("wv", s["v_mm"]), ("wr", s["r_mm"]))):
                        pe.wait_ge(s["mix_done"], DK * (i + 1))
                        for m in range(DK):
                            for k in range(DK):
                                mm = nc.tensor.matmul(ps[2 + 2 * i + m][:, 0:GT], W[x][:, k, m * P:(m + 1) * P],
                                                      mixed[:, i, k, :], start=(k == 0), stop=(k == DK - 1))
                            mm.then_inc(done, 1)
                    pe.wait_ge(s["x2_done"], 1)
                    norms[2].tensor_mean(nc, pe, c["ones"], lambda k: x2[:, k, :])
                    norms[2].tensor_var(nc, pe, c["ones"])
                    pe.wait_ge(s["mix_done"], DK * 4)
                    pe.wait_ge(s["k_done"], DK)
                    pe.wait_ge(s["v_done"], DK)
                    for m in range(HB):
                        if m >= 4:
                            pe.wait_ge(s["relu_done"], m - 3)
                        for k in range(DK):
                            mm = nc.tensor.matmul(ps[2 + m % 4][:, 0:GT], w_ck[:, k, m * P:(m + 1) * P], mixed[:, 3, k, :],
                                                  start=(k == 0), stop=(k == DK - 1))
                        mm.then_inc(s["c_mm"], 1)
                    pe.wait_ge(s["mix_done"], DK * 5)
                    pe.wait_ge(s["rg_done"], DK)
                    for m in range(DK):
                        for k in range(DK):
                            mm = nc.tensor.matmul(ps[6 + m][:, 0:GT], W["cr"][:, k, m * P:(m + 1) * P], mixed[:, 4, k, :],
                                                  start=(k == 0), stop=(k == DK - 1))
                        mm.then_inc(s["cr_mm"], 1)
                    pe.wait_ge(norms[2].ready, 1)
                    for j in range(DK):
                        for m in range(HB):
                            pe.wait_ge(s["sq_done"], m + 1)
                            mm = nc.tensor.matmul(ps[j][:, 0:GT], w_cv[:, m, j * P:(j + 1) * P], act2[:, m, :],
                                                  start=(m == 0), stop=(m == HB - 1))
                        mm.then_inc(s["cv_mm"], 1)

                @block.scalar
                def _(act):
                    nc.scalar.preload_act_table_set(EXP_LN)
                    norms[0].scalar(nc, act, c["eps"])
                    norms[1].scalar(nc, act, c["eps"])

                    def shifted(i, mix, ready):
                        act.wait_ge(s["h1_done"] if i < 3 else s["h2_done"], ready)
                        for k in range(DK):
                            nc.scalar.activation(rows(back[:, i, k, :])[:, :, 1:N], rows(h1[:, k, :])[:, :, 0:N - 1],
                                                 ACT.Copy, scale=rest[:, mix, k:k + 1]).then_inc(s["back_done"], 1)

                    for i in range(3):
                        shifted(i, MIXES[i], DK)
                    for k in range(DK):
                        act.wait_ge(s["k_mm"], k + 1)
                        nc.scalar.activation(kp[:, k, :, 1:N + 1], rows(ps[2 + k][:, 0:GT]), ACT.Copy).then_inc(s["k_done"], 1)
                    for k in range(DK):
                        act.wait_ge(s["v_mm"], k + 1)
                        nc.scalar.activation(v[:, k, :], ps[4 + k][:, 0:GT], ACT.Copy).then_inc(s["v_done"], 1)
                    act.wait_ge(s["d1_done"], DK)
                    nc.scalar.activation(d1[:, :, :], d1[:, :, :], ACT.Exp).then_inc(s["a_done"], 1)
                    act.wait_ge(s["d2_done"], DK)
                    nc.scalar.activation(d2[:, :, :], d2[:, :, :], ACT.Exp).then_inc(s["a_done"], 1)
                    act.wait_ge(s["s_done"], DK)
                    nc.scalar.activation(aa[:, :, :], s_[:, :, :], ACT.Ln).then_inc(s["ln_done"], 1)
                    act.wait_ge(s["min_done"], 1)
                    nc.scalar.activation(d1[:, :, :], d1[:, :, :], ACT.Exp).then_inc(s["e_done"], 1)
                    act.wait_ge(s["min_done"], 2)
                    nc.scalar.activation(d2[:, :, :], d2[:, :, :], ACT.Exp).then_inc(s["e_done"], 1)
                    for k in range(DK):
                        act.wait_ge(s["r_mm"], k + 1)
                        nc.scalar.activation(rg[:, k, :], ps[6 + k][:, 0:GT], ACT.Sigmoid).then_inc(s["rg_done"], 1)
                    for k in range(DK):
                        nc.scalar.activation(gate[:, k, :], s_[:, k, :], ACT.Sigmoid, bias=first_neg[:, k:k + 1])\
                            .then_inc(s["gate_done"], 1)
                    nc.scalar.preload_act_table_set(EXP_LN)
                    norms[2].scalar(nc, act, c["eps"])
                    for i in range(3, 5):
                        shifted(i, MIXES[i], DK)
                    for m in range(HB):
                        act.wait_ge(s["c_mm"], m + 1)
                        if m >= 2:
                            act.wait_ge(s["sq_done"], m - 1)
                        nc.scalar.activation(relu[:, m % 2, :], ps[2 + m % 4][:, 0:GT], ACT.Relu).then_inc(s["relu_done"], 1)
                    for k in range(DK):
                        act.wait_ge(s["cr_mm"], k + 1)
                        nc.scalar.activation(rg[:, k, :], ps[6 + k][:, 0:GT], ACT.Sigmoid).then_inc(s["sig_done"], 1)

                @block.vector
                def _(dve):
                    x = norms[0].out
                    norms[0].vector(nc, dve, h[:, :, group_cols(g)])
                    dve.wait_ge(norms[0].ready, 1)
                    norms[1].vector(nc, dve, x[:, :, :])

                    def scaled(norm, gain, bias, done):
                        dve.wait_ge(norm.ready, 1)
                        for k in range(DK):
                            nc.vector.tensor_scalar(h1[:, k, :], norm.out[:, k, :], col[:, gain, k:k + 1],
                                                    col[:, bias, k:k + 1], ALU.mult, ALU.add).then_inc(done, 1)
                        dve.wait_ge(done, DK)

                    def mix(i):
                        for k in range(DK):
                            dve.wait_ge(s["back_done"], DK * i + k + 1)
                            nc.vector.scalar_tensor_tensor(out=mixed[:, i, k, :], in0=h1[:, k, :],
                                                           scalar=col[:, MIXES[i], k:k + 1], in1=back[:, i, k, :],
                                                           op0=ALU.mult, op1=ALU.add).then_inc(s["mix_done"], 1)

                    scaled(norms[1], G1, B1, s["h1_done"])
                    for i in range(3):
                        mix(i)
                    for k in range(DK):
                        dve.wait_ge(s["k_done"], k + 1)
                        nc.vector.tensor_tensor_scan(Mp[:, k, :, :].rearrange("p b n -> p (b n)"),
                                                     kp[:, k, :, :].rearrange("p b n -> p (b n)"),
                                                     drift[:, k, :, :].rearrange("p b n -> p (b n)"), FAR, ALU.max, ALU.add)\
                            .then_inc(s["M_done"], 1)
                    for k in range(DK):
                        dve.wait_ge(s["M_done"], k + 1)
                        nc.vector.scalar_tensor_tensor(out=rows(d1[:, k, :]), in0=Mp[:, k, :, 0:N], scalar=col[:, DECAY, k:k + 1],
                                                       in1=Mp[:, k, :, 1:N + 1], op0=ALU.add, op1=ALU.subtract)\
                            .then_inc(s["d1_done"], 1)
                        nc.vector.scalar_tensor_tensor(out=rows(d2[:, k, :]), in0=kp[:, k, :, 1:N + 1],
                                                       scalar=col[:, DECAY, k:k + 1],
                                                       in1=Mp[:, k, :, 1:N + 1], op0=ALU.add, op1=ALU.subtract)\
                            .then_inc(s["d2_done"], 1)
                    dve.wait_ge(s["a_done"], 2)
                    for k in range(DK):
                        nc.vector.tensor_tensor_scan(s_[:, k, :], d1[:, k, :], d2[:, k, :], 0.0, ALU.mult, ALU.add)\
                            .then_inc(s["s_done"], 1)
                    dve.wait_ge(s["ln_done"], 1)
                    nc.vector.tensor_tensor(PPp[:, 0, :, 1:N + 1], Mp[:, 0, :, 1:N + 1], rows(aa[:, 0, :]), ALU.add)\
                        .then_inc(s["pp_done"], 1)
                    nc.vector.tensor_tensor(PPp[:, 1, :, 1:N + 1], Mp[:, 1, :, 1:N + 1], rows(aa[:, 1, :]), ALU.add)\
                        .then_inc(s["pp_done"], 1)
                    for k in range(DK):
                        dve.wait_ge(s["pp_done"], k + 1)
                        nc.vector.tensor_tensor(rows(s_[:, k, :]), PPp[:, k, :, 0:N], kp[:, k, :, 1:N + 1], ALU.subtract)\
                            .then_inc(s["dl_done"], 1)
                    dve.wait_ge(s["dl_done"], DK)
                    nc.vector.tensor_scalar(d1[:, :, :], s_[:, :, :], 0.0, None, ALU.min).then_inc(s["min_done"], 1)
                    nc.vector.tensor_scalar(d2[:, :, :], s_[:, :, :], -1.0, 0.0, ALU.mult, ALU.min).then_inc(s["min_done"], 1)
                    dve.wait_ge(s["e_done"], 2)
                    dve.wait_ge(s["v_done"], DK)
                    nc.vector.tensor_tensor(d2[:, :, :], d2[:, :, :], v[:, :, :], ALU.mult).then_inc(s["ev_done"], 1)
                    dve.wait_ge(s["ev_done"], 1)
                    for k in range(DK):
                        nc.vector.tensor_tensor_scan(aa[:, k, :], d1[:, k, :], d2[:, k, :], 0.0, ALU.mult, ALU.add)\
                            .then_inc(s["aa_done"], 1)
                    for k in range(DK):
                        dve.wait_ge(s["aa_done"], k + 1)
                        nc.vector.tensor_copy(AAp[:, k, :, 1:N + 1], rows(aa[:, k, :])).then_inc(s["aap_done"], 1)
                    for k in range(DK):
                        dve.wait_ge(s["aap_done"], k + 1)
                        dve.wait_ge(s["aa_done"], DK)
                        nc.vector.tensor_tensor(rows(d1[:, k, :]), AAp[:, k, :, 0:N], rows(v[:, k, :]), ALU.subtract)\
                            .then_inc(s["diff_done"], 1)
                    dve.wait_ge(s["diff_done"], DK)
                    dve.wait_ge(s["gate_done"], DK)
                    nc.vector.tensor_tensor(d1[:, :, :], d1[:, :, :], gate[:, :, :], ALU.mult).then_inc(s["gd_done"], 1)
                    dve.wait_ge(s["gd_done"], 1)
                    nc.vector.tensor_tensor(d1[:, :, :], d1[:, :, :], v[:, :, :], ALU.add).then_inc(s["y_done"], 1)
                    dve.wait_ge(s["y_done"], 1)
                    dve.wait_ge(s["rg_done"], DK)
                    nc.vector.tensor_tensor(d1[:, :, :], d1[:, :, :], rg[:, :, :], ALU.mult).then_inc(s["ry_done"], 1)
                    dve.wait_ge(s["ry_done"], 1)
                    nc.vector.tensor_tensor(x2[:, :, :], d1[:, :, :], x[:, :, :], ALU.add).then_inc(s["x2_done"], 1)
                    dve.wait_ge(s["x2_done"], 1)
                    norms[2].vector(nc, dve, x2[:, :, :])
                    scaled(norms[2], G2, B2, s["h2_done"])
                    mix(3)
                    mix(4)
                    for m in range(HB):
                        dve.wait_ge(s["relu_done"], m + 1)
                        nc.vector.tensor_tensor(act2[:, m, :], relu[:, m % 2, :], relu[:, m % 2, :], ALU.mult)\
                            .then_inc(s["sq_done"], 1)
                    nc.vector.tensor_tensor(x2[:, :, :], x2[:, :, :], h[:, :, group_cols(g)], ALU.add).then_inc(s["x3_done"], 1)
                    for k in range(DK):
                        dve.wait_ge(s["sig_done"], k + 1)
                        dve.wait_ge(s["cv_mm"], k + 1)
                        nc.vector.tensor_tensor(d2[:, k, :], rg[:, k, :], ps[k][:, 0:GT], ALU.mult).then_inc(s["sk_done"], 1)
                        dve.wait_ge(s["sk_done"], k + 1)
                        dve.wait_ge(s["x3_done"], 1)
                        nc.vector.tensor_tensor(h[:, k, group_cols(g)], x2[:, k, :], d2[:, k, :], ALU.add).then_inc(s["res_done"], 1)
            st.clear()


def peer(nc, h, c, wq, keys_t, down_t, up, norm_w, out):
    HEADS, KEYS, TOP = keys_t.shape[1] // 2, keys_t.shape[2], 8
    CH = HEADS * TOP
    EB = KEYS // 2
    PB = 2
    PT = PB * N
    CHUNK = 512 // (PB * EB)
    CHUNKS = [(t, min(CHUNK, N - t)) for t in range(0, N, CHUNK)]
    SETS = 2 * HEADS
    STEPS = B // PB
    with Stage(nc, "peer_out") as so, Stage(nc, "peer") as st:
        out_sent = so.sem("out_sent")
        ps = [st.psum(f"ps{i}") for i in range(8)]
        kq = st.sbuf("kq", [P, DK, SETS * KEYS])
        down = st.sbuf("down", [P, DK, EB, P])
        w_up = st.sbuf("up", [P, EB, D])
        nw = st.sbuf("nw", [P, DK])
        ramp = st.sbuf("ramp", [P, P])
        eps6 = st.sbuf("eps6", [P, 1])
        with Stage(nc, "pkq") as sk:
            w_q = sk.sbuf("w_q", [P, SETS, D])
            keys = sk.sbuf("keys", [P, SETS, KEYS])
            loaded, set_, big_in, kq_mm, kq_done = (sk.sem(x) for x in ("loaded", "set", "big_in", "kq_mm", "kq_done"))
            with nc.Block() as block:
                @block.sync
                def _(sp):
                    sp.dma_start(w_q[:, :, :], wq.rearrange("(s p) d -> p s d", p=P)).then_inc(loaded, 16)
                    sp.dma_start(keys[:, :, :], keys_t).then_inc(loaded, 16)
                    sp.dma_start(nw[:, :], norm_w).then_inc(big_in, 16)
                    sp.dma_start(down[:, :, :, :], down_t).then_inc(big_in, 16)
                    sp.dma_start(w_up[:, :, :], up).then_inc(big_in, 16)
                    sp.wait_ge(big_in, 48)

                @block.gpsimd
                def _(pool):
                    nc.gpsimd.iota(ramp[:, :], pattern=[[1, P]], base=0, channel_multiplier=0,
                                   allow_small_or_imprecise_dtypes=True).then_inc(set_, 1)
                    nc.gpsimd.memset(eps6[:, :], 1e-6).then_inc(set_, 1)

                @block.tensor
                def _(pe):
                    pe.wait_ge(loaded, 32)
                    for m in range(DK):
                        for half in range(2):
                            for j in range(SETS // 2):
                                i = half * SETS // 2 + j
                                mm = nc.tensor.matmul(ps[2 * m + half][:, j * KEYS:(j + 1) * KEYS],
                                                      w_q[:, i, m * P:(m + 1) * P], keys[:, i, :], start=True, stop=True)
                            mm.then_inc(kq_mm, 1)

                @block.vector
                def _(dve):
                    for m in range(DK):
                        for half in range(2):
                            dve.wait_ge(kq_mm, 2 * m + half + 1)
                            nc.vector.tensor_copy(kq[:, m, half * 512:(half + 1) * 512], ps[2 * m + half][:, :])\
                                .then_inc(kq_done, 1)
            sk.clear()

        norm = Norm(st, ps[0], ps[0], "ln", PT)
        log2, rms = norm.log_var, norm.rstd
        xn = st.sbuf("xn", [P, DK, PT])
        hid = st.sbuf("hid", [P, EB, PT])
        weight = st.sbuf("weight", [P, EB, PB, N])
        top = st.sbuf("top", [N, PB, SETS, TOP])
        idx = st.sbuf("idx", [N, PB, SETS, TOP], U32)
        pair = st.sbuf("pair", [N, PB, HEADS, TOP, TOP])
        best = st.sbuf("best", [N, PB, HEADS, TOP])
        at = st.sbuf("at", [N, PB, HEADS, TOP], U32)
        at_hi = st.sbuf("at_hi", [N, PB * HEADS, TOP], U32)
        at_lo = st.sbuf("at_lo", [N, PB * HEADS, TOP], U32)
        hit1 = st.sbuf("hit1", [N, PB * HEADS, TOP, TOP])
        hit2 = st.sbuf("hit2", [N, PB * HEADS, TOP, TOP])
        i1 = st.sbuf("i1", [N, PB * HEADS, TOP])
        i2 = st.sbuf("i2", [N, PB * HEADS, TOP])
        i2u, odd = (st.sbuf(x, [N, PB * CH], U32) for x in ("i2u", "odd"))
        half_ = st.sbuf("half", [N, PB * CH], U32)
        codes = st.sbuf("codes", [N, 3, PB * CH])
        codesT = st.sbuf("codesT", [P, 3, N])
        HB = 3
        hot_rows = st.sbuf("hot_rows", [P, HB, CHUNK, P])
        hot_cols = st.sbuf("hot_cols", [P, HB, CHUNK, PB * EB])
        names = ("sq2", "ms_mm", "log2_done", "rms_done", "xn_done", "sim_mm", "top_done", "idx_done", "pair_done", "best_done", "at_done",
                 "split_done", "hit_done", "mul_done", "sel_done", "u_done", "bits_done", "code_done", "t_done", "ct_done",
                 "hid_mm", "gelu_done", "rows_done", "hot_done", "cols_done", "g_mm", "evac_done", "wgt_done", "up_mm", "res_done")
        s = {x: st.sem(x) for x in names}
        J = 2
        HU = EB // J
        NC = len(CHUNKS)

        def best_experts(dve):
            for b in range(PB):
                for i in range(SETS):
                    if i % HEADS == 0:
                        dve.wait_ge(s["sim_mm"], 2 * b + i // HEADS + 1)
                    nc.vector.max(top[:, b, i, :], ps[1 + 2 * b + i // HEADS][0:N, (i % HEADS) * KEYS:(i % HEADS + 1) * KEYS])\
                        .then_inc(s["top_done"], 1)
                for i in range(SETS):
                    dve.wait_ge(s["top_done"], SETS * b + i + 1)
                    nc.vector.max_index(idx[:, b, i, :], top[:, b, i, :],
                                        ps[1 + 2 * b + i // HEADS][0:N, (i % HEADS) * KEYS:(i % HEADS + 1) * KEYS])\
                        .then_inc(s["idx_done"], 1)
                sets = top[:, b, :, :].rearrange("p (h s) k -> p h s k", s=2)
                nc.vector.tensor_tensor(pair[:, b, :, :, :], sets[:, :, 0, :].unsqueeze(3).to_broadcast([N, HEADS, TOP, TOP]),
                                        sets[:, :, 1, :].unsqueeze(2).to_broadcast([N, HEADS, TOP, TOP]), ALU.add)\
                    .then_inc(s["pair_done"], 1)
                dve.wait_ge(s["pair_done"], b + 1)
                for i in range(HEADS):
                    nc.vector.max(best[:, b, i, :], pair[:, b, i, :, :].rearrange("p a k -> p (a k)")).then_inc(s["best_done"], 1)
                for i in range(HEADS):
                    dve.wait_ge(s["best_done"], HEADS * b + i + 1)
                    nc.vector.max_index(at[:, b, i, :], best[:, b, i, :], pair[:, b, i, :, :].rearrange("p a k -> p (a k)"))\
                        .then_inc(s["at_done"], 1)
            dve.wait_ge(s["at_done"], PB * HEADS)
            dve.wait_ge(s["idx_done"], PB * SETS)
            flat = at[:, :, :, :].rearrange("p b h k -> p (b h) k")
            nc.vector.tensor_scalar(at_hi[:, :, :], flat, 3, None, ALU.logical_shift_right).then_inc(s["split_done"], 1)
            nc.vector.tensor_scalar(at_lo[:, :, :], flat, 7, None, ALU.bitwise_and).then_inc(s["split_done"], 1)
            dve.wait_ge(s["split_done"], 2)
            shape = [N, PB * HEADS, TOP, TOP]
            ids = idx[:, :, :, :].rearrange("p b (h s) k -> p (b h) s k", s=2)
            steps = ramp[0:N, 0:TOP].unsqueeze(1).unsqueeze(1).to_broadcast(shape)
            for i, (hit, place) in enumerate(((hit1, at_hi), (hit2, at_lo))):
                nc.vector.tensor_tensor(hit[:, :, :, :], steps, place[:, :, :].unsqueeze(3).to_broadcast(shape), ALU.is_equal)\
                    .then_inc(s["hit_done"], 1)
            for i, hit in enumerate((hit1, hit2)):
                dve.wait_ge(s["hit_done"], i + 1)
                nc.vector.tensor_tensor(hit[:, :, :, :], hit[:, :, :, :], ids[:, :, i, :].unsqueeze(2).to_broadcast(shape),
                                        ALU.mult).then_inc(s["mul_done"], 1)
            for i, (hit, sel) in enumerate(((hit1, i1), (hit2, i2))):
                dve.wait_ge(s["mul_done"], i + 1)
                nc.vector.tensor_reduce(sel[:, :, :], hit[:, :, :, :], AX.X, ALU.add).then_inc(s["sel_done"], 1)
            dve.wait_ge(s["sel_done"], 2)
            nc.vector.tensor_copy(i2u[:, :], i2[:, :, :].rearrange("p h k -> p (h k)")).then_inc(s["u_done"], 1)
            dve.wait_ge(s["u_done"], 1)
            nc.vector.tensor_scalar(odd[:, :], i2u[:, :], 1, None, ALU.bitwise_and).then_inc(s["bits_done"], 1)
            nc.vector.tensor_scalar(half_[:, :], i2u[:, :], 1, None, ALU.logical_shift_right).then_inc(s["bits_done"], 1)
            dve.wait_ge(s["bits_done"], 2)
            nc.vector.scalar_tensor_tensor(out=codes[:, 0, :], in0=odd[:, :], scalar=float(KEYS),
                                           in1=i1[:, :, :].rearrange("p h k -> p (h k)"), op0=ALU.mult, op1=ALU.add)\
                .then_inc(s["code_done"], 1)
            for b in range(PB):
                nc.vector.tensor_scalar(codes[:, 1, b * CH:(b + 1) * CH], half_[:, b * CH:(b + 1) * CH], float(b * EB), None, ALU.add)\
                    .then_inc(s["code_done"], 1)
            nc.vector.tensor_scalar(codes[:, 2, :], best[:, :, :, :].rearrange("p b h k -> p (b h k)"), 0.0, None, ALU.max)\
                .then_inc(s["code_done"], 1)

        def step(front, back):
            with nc.Block(no_gpsimd_drain=True) as block:
                @block.sync
                def _(sp):
                    if back is not None:
                        sp.wait_ge(s["res_done"], DK)
                        sp.dma_start(out[:, :, back], h[:, :, back]).then_inc(out_sent, 16)

                @block.tensor
                def _(pe):
                    def hidden(i):
                        if i >= 3:
                            pe.wait_ge(s["gelu_done"], i - 2)
                        for jj in range(J):
                            for k in range(DK):
                                mm = nc.tensor.matmul(ps[1 + i % 3][:, jj * PT:(jj + 1) * PT], down[:, k, i * J + jj, :],
                                                      xn[:, k, :], start=(k == 0), stop=(k == DK - 1))
                        mm.then_inc(s["hid_mm"], 1)

                    def weights(ch):
                        pe.wait_ge(s["rows_done"], ch + 1)
                        pe.wait_ge(s["cols_done"], ch + 1)
                        if ch >= HB:
                            pe.wait_ge(s["evac_done"], ch - HB + 1)
                        for t in range(CHUNKS[ch][1]):
                            mm = nc.tensor.matmul(ps[4 + ch % HB][:, t * PB * EB:(t + 1) * PB * EB], hot_rows[:, ch % HB, t, :],
                                                  hot_cols[:, ch % HB, t, :], start=True, stop=True)
                        mm.then_inc(s["g_mm"], 1)

                    if front is not None:
                        norm.tensor_mean(nc, pe, c["ones"], lambda k: h[:, k, front])
                    if back is not None:
                        hidden(0)
                    if front is not None:
                        norm.tensor_var(nc, pe, c["ones"])
                    if back is not None:
                        hidden(1)
                        weights(0)
                    if front is not None:
                        pe.wait_ge(s["sq2"], 1)
                        for k in range(DK):
                            mm = nc.tensor.matmul(ps[0][:, 0:PT], c["ones"][:, :], norm.square[:, k, :],
                                                  start=(k == 0), stop=(k == DK - 1))
                        mm.then_inc(s["ms_mm"], 1)
                    if back is not None:
                        for i in range(2, HU):
                            hidden(i)
                            if i - 1 < NC:
                                weights(i - 1)
                        for ch in range(HU - 1, NC):
                            weights(ch)
                        pe.wait_ge(s["gelu_done"], HU)
                        pe.wait_ge(s["evac_done"], NC)
                    if front is not None:
                        pe.wait_ge(s["xn_done"], DK)
                        for b in range(PB):
                            for half in range(2):
                                for k in range(DK):
                                    mm = nc.tensor.matmul(ps[1 + 2 * b + half][0:N, :], xn[:, k, b * N:(b + 1) * N],
                                                          kq[:, k, half * 512:(half + 1) * 512], start=(k == 0), stop=(k == DK - 1))
                                mm.then_inc(s["sim_mm"], 1)
                    if back is not None:
                        for m in range(DK):
                            for j in range(EB):
                                if m == 0 and j % J == 0:
                                    pe.wait_ge(s["wgt_done"], j // J + 1)
                                mm = nc.tensor.matmul(ps[5 + m][:, 0:PT], w_up[:, j, m * P:(m + 1) * P], hid[:, j, :],
                                                      start=(j == 0), stop=(j == EB - 1))
                            mm.then_inc(s["up_mm"], 1)
                    if front is not None:
                        pe.wait_ge(s["code_done"], 4)
                        for i in range(3):
                            mm = nc.tensor.transpose(ps[7][:, i * N:(i + 1) * N], codes[:, i, :], c["ident"][0:N, 0:N])
                        mm.then_inc(s["t_done"], 1)

                @block.scalar
                def _(act):
                    if front is not None:
                        nc.scalar.preload_act_table_set(EXP_LN)
                        norm.scalar(nc, act, c["eps"])
                        act.wait_ge(norm.ready, 1)
                        nc.scalar.activation(norm.square[:, :, :], norm.out[:, :, :], ACT.Square).then_inc(s["sq2"], 1)
                        act.wait_ge(s["ms_mm"], 1)
                        nc.scalar.activation(log2[:, :], ps[0][:, 0:PT], ACT.Ln, bias=eps6[:, 0:1]).then_inc(s["log2_done"], 1)
                        act.wait_ge(s["log2_done"], 1)
                        nc.scalar.activation(rms[:, :], log2[:, :], ACT.Exp, scale=-0.5).then_inc(s["rms_done"], 1)
                    if back is not None:
                        for i in range(max(HU, NC)):
                            if i < HU:
                                act.wait_ge(s["hid_mm"], i + 1)
                                nc.scalar.activation(hid[:, i * J:(i + 1) * J, :].rearrange("p j n -> p (j n)"),
                                                     ps[1 + i % 3][:, 0:J * PT], ACT.Gelu).then_inc(s["gelu_done"], 1)
                            if i < NC:
                                t0, n = CHUNKS[i]
                                act.wait_ge(s["g_mm"], i + 1)
                                nc.scalar.activation(weight[:, :, :, t0:t0 + n],
                                                     ps[4 + i % HB][:, 0:n * PB * EB].rearrange("p (t b j) -> p j b t", b=PB, j=EB),
                                                     ACT.Copy).then_inc(s["evac_done"], 1)
                    if front is not None:
                        act.wait_ge(s["t_done"], 1)
                        if back is not None:
                            act.wait_ge(s["rows_done"], NC)
                            act.wait_ge(s["cols_done"], NC)
                        nc.scalar.activation(codesT[:, :, :].rearrange("p a n -> p (a n)"), ps[7][:, 0:3 * N], ACT.Copy)\
                            .then_inc(s["ct_done"], 1)

                @block.gpsimd
                def _(pool):
                    if back is not None:
                        for ch, (t0, n) in enumerate(CHUNKS):
                            shape = [P, n, PB * EB]
                            pool.wait_ge(s["hot_done"], ch + 1)
                            nc.gpsimd.tensor_tensor(hot_cols[:, ch % HB, 0:n, :], hot_cols[:, ch % HB, 0:n, :],
                                                    codesT[:, 2, t0:t0 + n].unsqueeze(2).to_broadcast(shape), ALU.mult)\
                                .then_inc(s["cols_done"], 1)

                @block.vector
                def _(dve):
                    def one_hot(ch):
                        t0, n = CHUNKS[ch]
                        if ch >= HB:
                            dve.wait_ge(s["g_mm"], ch - HB + 1)
                        nc.vector.tensor_tensor(hot_rows[:, ch % HB, 0:n, :], ramp[:, :].unsqueeze(1).to_broadcast([P, n, P]),
                                                codesT[:, 0, t0:t0 + n].unsqueeze(2).to_broadcast([P, n, P]), ALU.is_equal)\
                            .then_inc(s["rows_done"], 1)
                        nc.vector.tensor_tensor(hot_cols[:, ch % HB, 0:n, :], ramp[:, 0:PB * EB].unsqueeze(1).to_broadcast([P, n, PB * EB]),
                                                codesT[:, 1, t0:t0 + n].unsqueeze(2).to_broadcast([P, n, PB * EB]), ALU.is_equal)\
                            .then_inc(s["hot_done"], 1)

                    if back is not None:
                        one_hot(0)
                    if front is not None:
                        norm.vector(nc, dve, h[:, :, front])
                    if back is not None:
                        for ch in range(1, NC):
                            one_hot(ch)
                    if front is not None:
                        dve.wait_ge(norm.ready, 1)
                        dve.wait_ge(s["rms_done"], 1)
                        if back is not None:
                            dve.wait_ge(s["hid_mm"], HU)
                        for k in range(DK):
                            nc.vector.scalar_tensor_tensor(out=xn[:, k, :], in0=norm.out[:, k, :], scalar=nw[:, k:k + 1],
                                                           in1=rms[:, :], op0=ALU.mult, op1=ALU.mult).then_inc(s["xn_done"], 1)
                    if back is not None:
                        dve.wait_ge(s["gelu_done"], HU)
                        dve.wait_ge(s["evac_done"], NC)
                        for i in range(HU):
                            block_ = hid[:, i * J:(i + 1) * J, :]
                            nc.vector.tensor_tensor(block_, block_, weight[:, i * J:(i + 1) * J, :, :].rearrange("p j b n -> p j (b n)"),
                                                    ALU.mult).then_inc(s["wgt_done"], 1)
                    if front is not None:
                        best_experts(dve)
                    if back is not None:
                        for m in range(DK):
                            dve.wait_ge(s["up_mm"], m + 1)
                            nc.vector.tensor_tensor(h[:, m, back], h[:, m, back], ps[5 + m][:, 0:PT], ALU.add).then_inc(s["res_done"], 1)
            st.clear()

        def pair_cols(g):
            return bass.ds(g * PT, PT)

        step(pair_cols(0), None)
        with nc.Fori(0, STEPS - 1) as g:
            step(pair_cols(g + 1), pair_cols(g))
        step(None, pair_cols(STEPS - 1))
        with nc.Block() as block:
            @block.sync
            def _(sp):
                sp.wait_ge(out_sent, 16 * STEPS)
        so.clear()


def early_fusion(nc, a, out):
    with Stage(nc, "net") as st:
        h = st.sbuf("h", [P, DK, T])
        c = dict(ones=st.sbuf("ones", [P, P]), ident=st.sbuf("ident", [P, P]), eps=st.sbuf("eps", [P, 1]))
        slots_in = nc.dram_tensor("slots_in", [17 * 640, D], F32).ap()
        slots_out = nc.dram_tensor("slots_out", [16 * 565, D], F32).ap()
        row_expert = nc.dram_tensor("row_expert", [B, 1], U32).ap()
        constants(nc, c)
        tok(nc, h, c, **a["tok"])
        l0_attn(nc, h, c, **a["l0_attn"])
        moe(nc, h, c, slots_in=slots_in, slots_out=slots_out, **a["moe"])
        mamba(nc, h, c, [a["mamba_f"], a["mamba_b"]])
        l1_ffn(nc, h, c, **a["l1_ffn"])
        l2_attn(nc, h, c, **a["l2_attn"])
        l2_ffn(nc, h, c, row_expert=row_expert, **a["l2_ffn"])
        rwkv(nc, h, c, **a["rwkv"])
        peer(nc, h, c, out=out, **a["peer"])



def feature_cols(v):
    return v.reshape(-1, P).T


def feature_blocks(w):
    return w.reshape(-1, P, w.shape[1]).transpose(1, 0, 2)


def rope_tables():
    n = np.arange(N)
    places = (n // 256, n % 256 // 16, n % 16)
    rate = (1.0 / 10000.0 ** (np.arange(2, dtype=np.float32) / 2.0)).astype(np.float32)
    cos, sin = np.ones((D, N), np.float32), np.zeros((D, N), np.float32)
    for i in range(D):
        f = i % 16
        if f < 12:
            angle = (places[f // 4].astype(np.float32) * rate[f % 2]).astype(np.float32)
            cos[i] = np.cos(angle)
            sin[i] = np.sin(angle) * (-1 if f % 2 == 0 else 1)
    head = np.arange(P) // 16 % 2
    even = np.stack([head == 0, head == 1], 1).astype(np.float32)
    table = lambda t: t.reshape(DK, P, N).transpose(1, 0, 2)
    return table(cos), table(sin), even


def layout(I):
    out = {}
    x = I["x"]
    text = np.zeros((B, N, D), np.float32)
    text[:, IMG:] = I["txt"]
    px = x.reshape(B, 3, GRID, 16, GRID, 16).transpose(1, 3, 5, 0, 2, 4).reshape(6, P, B * IMG).transpose(1, 0, 2)
    out["tok"] = dict(h_text=text.reshape(T, DK, P).transpose(2, 1, 0), patches=px, w_t=feature_blocks(I["L0_tok_W"].T),
                      bias=feature_cols(I["L0_tok_b"]))

    w = lambda n: I[f"L0_attn_{n}"]
    turn = np.arange(D) ^ 1
    cos, sin, even = rope_tables()
    biases = np.stack([feature_cols(v) for v in (w("bq"), w("bq")[turn], w("bk"), w("bk")[turn], w("bv"), w("bo"))], 1)
    out["l0_attn"] = dict(wq=w("Wq"), wq_rot=w("Wq")[:, turn], wk=w("Wk"), wk_rot=w("Wk")[:, turn], wv=w("Wv"), wo=w("Wo"),
                          biases=biases, cos=cos, sin=sin, even=even)

    w = lambda n: I[f"L0_ffn_{n}"]
    gate = np.concatenate([w("w_gate"), w("sw_gate")[None]])
    up = np.concatenate([w("w_up"), w("sw_up")[None]])
    down = np.concatenate([w("w_down"), w("sw_down")[None]])
    gate_up = np.stack([gate, up], 2).reshape(17, DK, P, 2, 352).transpose(0, 2, 1, 3, 4)
    padded = np.zeros((17, 3 * P, D), np.float32)
    padded[:, :352] = down
    out["moe"] = dict(router_w=w("router_w"), router_b=w("router_b").reshape(1, 16), gate_up=gate_up,
                      down=padded.reshape(17, 3, P, D).transpose(0, 2, 1, 3))

    for p in "fb":
        w = lambda n: I[f"L1_attn_{p}_{n}"]
        out[f"mamba_{p}"] = dict(in_t=w("in_w").T, xproj_t=w("xproj_w").T, dt_t=w("dt_w").T, out_t=w("out_w").T,
                                 conv_w=feature_blocks(w("conv_w")), conv_b=feature_cols(w("conv_b")),
                                 dt_b=feature_cols(w("dt_b")), a_log=feature_blocks(w("A_log")), d=feature_cols(w("D")))

    w = lambda n: I[f"L1_ffn_{n}"]
    out["l1_ffn"] = dict(w_fc=w("w_fc"), w_proj=w("w_proj"), u_t=w("u").T, v=w("v"), fast_b=w("fast_b"),
                         gate=np.asarray(w("gate")).reshape(1, 1))
    w = lambda n: I[f"L2_attn_{n}"]
    out["l2_attn"] = dict(wq=w("W_Q"), wk=w("W_K"), wv=w("W_V"))

    w = lambda n: I[f"L2_ffn_{n}"]
    out["l2_ffn"] = dict(wr=w("Wr"), br=w("br").reshape(1, 8), w1=w("W1").reshape(8, DK, P, 1024).transpose(0, 2, 1, 3),
                         b1=w("b1").reshape(8, 8, P).transpose(0, 2, 1), w2=w("W2").reshape(8, 8, P, D).transpose(0, 2, 1, 3),
                         b2=w("b2").reshape(8, DK, P).transpose(0, 2, 1))

    w = lambda n: I[f"L3_attn_{n}"]
    cols = np.stack([feature_cols(w(n).reshape(-1)) for n in
                     ("time_decay", "time_first", "ln1_g", "ln1_b", "ln2_g", "ln2_b", "mix_k", "mix_v", "mix_r", "cmix_k",
                      "cmix_r")], 1)
    out["rwkv"] = dict(wk=w("w_tk"), wv=w("w_tv"), wr=w("w_tr"), ck=w("w_ck"), cv=w("w_cv"), cr=w("w_cr"), cols=cols)

    w = lambda n: I[f"L3_ffn_{n}"]
    keys = w("keys").transpose(3, 0, 2, 1).reshape(P, 16, 64)
    order = np.arange(4096).reshape(64, 32, 2).transpose(1, 2, 0).reshape(32, P)
    out["peer"] = dict(wq=w("w_q"), keys_t=keys,
                       down_t=w("expert_down")[order].transpose(2, 0, 1).reshape(DK, P, 32, P).transpose(1, 0, 2, 3),
                       up=w("expert_up")[order].transpose(1, 0, 2), norm_w=feature_cols(w("norm_w")))
    return out


def kernel(**inputs):
    import concourse.bacc as _bacc
    from concourse.bass_utils import run_bass_kernel_spmd as _run

    nc = _bacc.Bacc("TRN2", target_bir_lowering=False, num_devices=1)
    arrays, aps = {}, {}
    for stage, parts in layout({k: np.asarray(v) for k, v in inputs.items()}).items():
        aps[stage] = {}
        for name, value in parts.items():
            value = np.ascontiguousarray(value)
            arrays[f"in_{stage}_{name}"] = value
            aps[stage][name] = nc.dram_tensor(f"in_{stage}_{name}", value.shape, mybir.dt.from_np(value.dtype),
                                              kind="ExternalInput").ap()
    out = nc.dram_tensor("out", [P, DK, T], F32, kind="ExternalOutput").ap()
    early_fusion(nc, aps, out)
    result = _run(nc, [arrays], core_ids=[0]).results[0]["out"]
    return np.ascontiguousarray(result.transpose(2, 1, 0).reshape(B, N, D))
```

```python
from contextlib import ExitStack


import numpy as np
import concourse.bass as bass
from concourse import mybir

F32 = mybir.dt.float32
BF16 = mybir.dt.bfloat16
U32 = mybir.dt.uint32
I32 = mybir.dt.int32
ALU = mybir.AluOpType
ACT = mybir.ActivationFunctionType
AX = mybir.AxisListType

P = 128
B = 32
GRID = 6
IMG = GRID * GRID
TXT = 77
N = IMG + TXT
T = B * N
D = 256
DK = D // P
GB = 4
GT = GB * N
GROUPS = B // GB
LN_EPS = 1e-5


EXP_LN = "natural_log_exp_and_others"


class Stage:

    def __init__(self, nc, name):
        self.nc, self.name, self.stack, self.sems = nc, name, ExitStack(), []

    def __enter__(self):
        return self

    def __exit__(self, *exc):
        self.stack.close()

    def sbuf(self, name, shape, dt=F32):
        return self.stack.enter_context(self.nc.sbuf_tensor(f"{self.name}_{name}", shape, dt))

    def psum(self, name, shape=(P, 512), dt=F32):
        return self.stack.enter_context(self.nc.psum_tensor(f"{self.name}_{name}", list(shape), dt))

    def sem(self, name):
        s = self.stack.enter_context(self.nc.semaphore(f"{self.name}_{name}"))
        self.sems.append(s)
        return s

    def clear(self, pool_dmas=False):
        def zero(eng):
            at = 0
            while at < len(self.sems):
                last = at
                while last + 1 < len(self.sems) and self.sems[last + 1].num == self.sems[last].num + 1:
                    last += 1
                numbers = range(self.sems[at].num, self.sems[last].num + 1)
                if pool_dmas:
                    eng.dma_reset(numbers)
                eng.sem_clear(numbers)
                at = last + 1

        with self.nc.Block(no_gpsimd_drain=True) as block:
            if pool_dmas:
                block.gpsimd(zero)
            else:
                block.sync(zero)


def group_cols(g):
    return bass.ds(g * GT, GT)


class Norm:

    def __init__(self, st, mean_ps, var_ps, name="ln", width=GT):
        self.mean_ps, self.var_ps, self.width = mean_ps, var_ps, width
        self.centred = st.sbuf(f"{name}_centred", [P, DK, width])
        self.square = st.sbuf(f"{name}_square", [P, DK, width])
        self.log_var = st.sbuf(f"{name}_log_var", [P, width])
        self.rstd = st.sbuf(f"{name}_rstd", [P, width])
        self.out = st.sbuf(f"{name}_out", [P, DK, width])
        self.mean_ready = st.sem(f"{name}_mean_ready")
        self.centred_ready = st.sem(f"{name}_centred_ready")
        self.square_ready = st.sem(f"{name}_square_ready")
        self.var_ready = st.sem(f"{name}_var_ready")
        self.log_ready = st.sem(f"{name}_log_ready")
        self.rstd_ready = st.sem(f"{name}_rstd_ready")
        self.ready = st.sem(f"{name}_ready")

    def tensor_mean(self, nc, pe, ones, x):
        for k in range(DK):
            mm = nc.tensor.matmul(self.mean_ps[:, 0:self.width], ones[:, :], x(k), start=(k == 0), stop=(k == DK - 1))
        mm.then_inc(self.mean_ready, 1)

    def tensor_var(self, nc, pe, ones):
        pe.wait_ge(self.square_ready, 1)
        for k in range(DK):
            mm = nc.tensor.matmul(self.var_ps[:, 0:self.width], ones[:, :], self.square[:, k, :],
                                  start=(k == 0), stop=(k == DK - 1))
        mm.then_inc(self.var_ready, 1)

    def scalar(self, nc, act, eps_col):
        act.wait_ge(self.centred_ready, 1)
        nc.scalar.activation(self.square[:, :, :], self.centred[:, :, :], ACT.Square).then_inc(self.square_ready, 1)
        act.wait_ge(self.var_ready, 1)
        nc.scalar.activation(self.log_var[:, :], self.var_ps[:, 0:self.width], ACT.Ln, bias=eps_col[:, 0:1])\
            .then_inc(self.log_ready, 1)
        act.wait_ge(self.log_ready, 1)
        nc.scalar.activation(self.rstd[:, :], self.log_var[:, :], ACT.Exp, scale=-0.5).then_inc(self.rstd_ready, 1)

    def vector(self, nc, dve, x_all):
        dve.wait_ge(self.mean_ready, 1)
        nc.vector.tensor_tensor(self.centred[:, :, :], x_all,
                                self.mean_ps[:, 0:self.width].unsqueeze(1).to_broadcast([P, DK, self.width]),
                                ALU.subtract).then_inc(self.centred_ready, 1)
        dve.wait_ge(self.rstd_ready, 1)
        dve.wait_ge(self.centred_ready, 1)
        nc.vector.tensor_tensor(self.out[:, :, :], self.centred[:, :, :],
                                self.rstd[:, :].unsqueeze(1).to_broadcast([P, DK, self.width]),
                                ALU.mult).then_inc(self.ready, 1)


def constants(nc, c):
    with Stage(nc, "const") as st:
        zero_done, done = st.sem("zero"), st.sem("done")
        with nc.Block() as block:
            @block.gpsimd
            def _(pool):
                nc.gpsimd.memset(c["ones"][:, :], 1.0 / D).then_inc(done, 1)
                nc.gpsimd.memset(c["eps"][:, :], LN_EPS).then_inc(done, 1)
                nc.gpsimd.memset(c["ident"][:, :], 0.0).then_inc(zero_done, 1)
                pool.wait_ge(zero_done, 1)
                nc.gpsimd.affine_select(out=c["ident"][:, :], in_=c["ident"][:, :], compare_op=ALU.not_equal, fill=1.0,
                                        base=0, pattern=[[-1, P]], channel_multiplier=1).then_inc(done, 1)
                pool.wait_ge(done, 3)
        st.clear()


def tok(nc, h, c, h_text, patches, w_t, bias):
    KB = patches.shape[1]
    CB = 8
    with Stage(nc, "tok") as st:
        px = st.sbuf("px", [P, KB, B * IMG])
        w = st.sbuf("w", [P, KB, D])
        b = st.sbuf("b", [P, DK])
        ps = [st.psum(f"ps{i}") for i in range(8)]
        text_in, w_in, mm_done, tok_done = (st.sem(x) for x in ("text_in", "w_in", "mm_done", "tok_done"))
        px_in = [st.sem(f"px_in{i}") for i in range(B // CB)]
        with nc.Block() as block:
            @block.sync
            def _(sp):
                sp.dma_start(w[:, :, :], w_t).then_inc(w_in, 16)
                sp.dma_start(b[:, :], bias).then_inc(w_in, 16)
                for i in range(B // CB):
                    sp.dma_start(px[:, :, i * CB * IMG:(i + 1) * CB * IMG], patches[:, :, i * CB * IMG:(i + 1) * CB * IMG])\
                        .then_inc(px_in[i], 16)

            @block.tensor
            def _(pe):
                pe.wait_ge(w_in, 32)
                for i in range(B // CB):
                    pe.wait_ge(px_in[i], 16)
                    for m in range(DK):
                        for k in range(KB):
                            mm = nc.tensor.matmul(ps[2 * i + m][:, 0:CB * IMG], w[:, k, m * P:(m + 1) * P],
                                                  px[:, k, i * CB * IMG:(i + 1) * CB * IMG], start=(k == 0), stop=(k == KB - 1))
                        mm.then_inc(mm_done, 1)

            @block.scalar
            def _(act):
                act.dma_start(h[:, :, :], h_text).then_inc(text_in, 16)
                nc.scalar.preload_act_table_set(EXP_LN)
                act.wait_ge(text_in, 16)
                act.wait_ge(w_in, 32)
                for i in range(B // CB):
                    for m in range(DK):
                        act.wait_ge(mm_done, 2 * i + m + 1)
                        dst = h[:, m, :].rearrange("p (b n) -> p b n", n=N)[:, i * CB:(i + 1) * CB, 0:IMG]
                        nc.scalar.activation(dst, ps[2 * i + m][:, 0:CB * IMG].rearrange("p (b n) -> p b n", n=IMG),
                                             ACT.Identity, bias=b[:, m:m + 1]).then_inc(tok_done, 1)
        st.clear()


def l0_attn(nc, h, c, wq, wq_rot, wk, wk_rot, wv, wo, biases, cos, sin, even):
    H, HD = 16, 16
    UNITS = GB * 4
    with Stage(nc, "at0") as st:
        W = {x: st.sbuf(x, [P, DK, D]) for x in ("wq", "wqr", "wk", "wkr", "wv", "wo")}
        bs = st.sbuf("bs", [P, 6, DK])
        cs = st.sbuf("cos", [P, DK, N])
        sn = st.sbuf("sin", [P, DK, N])
        ev = st.sbuf("even", [P, 2])
        ps = [st.psum(f"ps{i}") for i in range(8)]
        norm = Norm(st, ps[0], ps[1])
        rot_a = st.sbuf("rot_a", [P, 4, GT])
        rot_b = st.sbuf("rot_b", [P, 4, GT])
        q = st.sbuf("q", [P, DK, GT])
        kk = st.sbuf("k", [P, DK, GT])
        kpar = [st.sbuf("k_even", [P, DK, GT]), st.sbuf("k_odd", [P, DK, GT])]
        v = st.sbuf("v", [N, GB, H, HD + 1])
        NE = 3
        low = st.sbuf("shifted", [N, NE, 4 * N])
        ex = st.sbuf("ex", [N, NE, 4 * N])
        exT = st.sbuf("exT", [N, NE, 4 * N])
        mx = st.sbuf("mx", [N, UNITS, 4])
        rs = st.sbuf("rs", [N, GB, H])
        cn = st.sbuf("cn", [N, GB, D])
        ctxT = st.sbuf("ctxT", [P, DK, GT])
        (w_in, ones_set, proj_done, a_done, b_done, q_done, k_done, kpar_done, v_mm, v_done, s_done, mx_done, low_done,
         ex_done, t_done, exT_done, av_done, rs_done, cn_done, ct_done, ctx_done, o_done, res_done) = (
            st.sem(x) for x in ("w_in", "ones_set", "proj_done", "a_done", "b_done", "q_done", "k_done", "kpar_done", "v_mm",
                                "v_done", "s_done", "mx_done", "low_done", "ex_done", "t_done", "exT_done", "av_done",
                                "rs_done", "cn_done", "ct_done", "ctx_done", "o_done", "res_done"))
        with nc.Block() as block:
            @block.sync
            def _(sp):
                for x, src in (("wq", wq), ("wqr", wq_rot), ("wk", wk), ("wkr", wk_rot), ("wv", wv), ("wo", wo)):
                    sp.dma_start(W[x][:, :, :], src.rearrange("(k p) n -> p k n", p=P)).then_inc(w_in, 16)
                sp.dma_start(bs[:, :, :], biases).then_inc(w_in, 16)
                sp.dma_start(cs[:, :, :], cos).then_inc(w_in, 16)
                sp.dma_start(sn[:, :, :], sin).then_inc(w_in, 16)
                sp.dma_start(ev[:, :], even).then_inc(w_in, 16)
                sp.wait_ge(w_in, 160)

            @block.gpsimd
            def _(pool):
                nc.gpsimd.memset(v[:, :, :, :], 1.0).then_inc(ones_set, 1)

            @block.scalar
            def _(act):
                nc.scalar.preload_act_table_set(EXP_LN)
        st.clear()
        S_BANK, T_BANK, C_BANK, CT_BANK = (0, 1, 2), (3, 4), (5, 6), 7

        def head(r, j):
            return 8 * (j // 2) + 2 * r + j % 2

        with nc.Fori(0, GROUPS) as g:
            with nc.Block(no_gpsimd_drain=True) as block:
                @block.tensor
                def _(pe):
                    norm.tensor_mean(nc, pe, c["ones"], lambda k: h[:, k, group_cols(g)])
                    norm.tensor_var(nc, pe, c["ones"])
                    pe.wait_ge(norm.ready, 1)
                    for i, x in enumerate(("wq", "wqr", "wk", "wkr")):
                        for m in range(DK):
                            for k in range(DK):
                                mm = nc.tensor.matmul(ps[2 * i + m][:, 0:GT], W[x][:, k, m * P:(m + 1) * P],
                                                      norm.out[:, k, :], start=(k == 0), stop=(k == DK - 1))
                            mm.then_inc(proj_done, 1)
                    for b in range(GB):
                        if b % 2 == 0:
                            pe.wait_ge(b_done if b else a_done, 2)
                        bank = ps[2 * (b // 2)]
                        for k in range(DK):
                            mm = nc.tensor.matmul(bank[0:N, (b % 2) * D:(b % 2 + 1) * D], norm.out[:, k, b * N:(b + 1) * N],
                                                  W["wv"][:, k, :], start=(k == 0), stop=(k == DK - 1))
                        if b % 2:
                            mm.then_inc(v_mm, 1)

                    def scores(u):
                        b, r = u // 4, u % 4
                        if u < 3:
                            pe.wait_ge(v_done, GB // 2)
                            pe.wait_ge(b_done, 4)
                            pe.wait_ge(q_done, 2)
                            pe.wait_ge(kpar_done, 4)
                        else:
                            pe.wait_ge(low_done, u - 2)
                        for j in range(4):
                            m = j // 2
                            mm = nc.tensor.matmul(ps[S_BANK[u % 3]][0:N, j * N:(j + 1) * N],
                                                  q[32 * r:32 * r + 32, m, b * N:(b + 1) * N],
                                                  kpar[j % 2][32 * r:32 * r + 32, m, b * N:(b + 1) * N], start=True, stop=True)
                        mm.then_inc(s_done, 1)

                    def turn(u):
                        pe.wait_ge(ex_done, u + 1)
                        if u >= 2:
                            pe.wait_ge(exT_done, u - 1)
                        for j in range(4):
                            mm = nc.tensor.transpose(ps[T_BANK[u % 2]][0:N, j * N:(j + 1) * N],
                                                     ex[:, u % NE, j * N:(j + 1) * N], c["ident"][0:N, 0:N])
                        mm.then_inc(t_done, 1)

                    def values(u):
                        b, r = u // 4, u % 4
                        pe.wait_ge(exT_done, u + 1)
                        if r == 0 and b >= 2:
                            pe.wait_ge(cn_done, b - 1)
                        for j in range(4):
                            hd = head(r, j)
                            mm = nc.tensor.matmul(ps[C_BANK[b % 2]][0:N, hd * (HD + 1):(hd + 1) * (HD + 1)],
                                                  exT[:, u % NE, j * N:(j + 1) * N], v[:, b, hd, :], start=True, stop=True)
                        mm.then_inc(av_done, 1)

                    def turn_context(b):
                        pe.wait_ge(cn_done, b + 1)
                        if b >= 1:
                            pe.wait_ge(ctx_done, 2 * b)
                        for m in range(DK):
                            mm = nc.tensor.transpose(ps[CT_BANK][:, m * N:(m + 1) * N], cn[:, b, m * P:(m + 1) * P],
                                                     c["ident"][0:N, 0:N])
                        mm.then_inc(ct_done, 1)

                    for u in range(UNITS + 3):
                        if u < UNITS:
                            scores(u)
                        if 1 <= u <= UNITS:
                            turn(u - 1)
                        if 2 <= u <= UNITS + 1:
                            values(u - 2)
                        if u >= 6 and (u - 6) % 4 == 0:
                            turn_context((u - 6) // 4)
                    pe.wait_ge(ctx_done, 2 * GB)
                    pe.wait_ge(low_done, UNITS)
                    for m in range(DK):
                        for k in range(DK):
                            mm = nc.tensor.matmul(ps[m][:, 0:GT], W["wo"][:, k, m * P:(m + 1) * P], ctxT[:, k, :],
                                                  start=(k == 0), stop=(k == DK - 1))
                        mm.then_inc(o_done, 1)

                @block.scalar
                def _(act):
                    norm.scalar(nc, act, c["eps"])
                    for b in range(0, GB, 2):
                        act.wait_ge(v_mm, b // 2 + 1)
                        nc.scalar.activation(v[:, b:b + 2, :, 0:HD],
                                             ps[b][0:N, :].rearrange("p (b h e) -> p b h e", b=2, e=HD),
                                             ACT.Copy).then_inc(v_done, 1)
                    for u in range(UNITS + 1):
                        if u < UNITS:
                            act.wait_ge(low_done, u + 1)
                            if u >= NE:
                                act.wait_ge(t_done, u - NE + 1)
                            nc.scalar.activation(ex[:, u % NE, :], low[:, u % NE, :], ACT.Exp, scale=HD ** -0.5)\
                                .then_inc(ex_done, 1)
                        if u >= 1:
                            act.wait_ge(t_done, u)
                            if u - 1 >= NE:
                                act.wait_ge(av_done, u - NE)
                            nc.scalar.activation(exT[:, (u - 1) % NE, :], ps[T_BANK[(u - 1) % 2]][0:N, 0:4 * N], ACT.Copy)\
                                .then_inc(exT_done, 1)
                        if u >= 7 and (u - 7) % 4 == 0 or u == UNITS:
                            b = (u - 7) // 4 if u < UNITS else GB - 1
                            act.wait_ge(ct_done, b + 1)
                            for m in range(DK):
                                nc.scalar.activation(ctxT[:, m, b * N:(b + 1) * N], ps[CT_BANK][:, m * N:(m + 1) * N],
                                                     ACT.Identity, bias=bs[:, 4, m:m + 1]).then_inc(ctx_done, 1)

                @block.vector
                def _(dve):
                    norm.vector(nc, dve, h[:, :, group_cols(g)])

                    def table(t, m):
                        return t[:, m, :].unsqueeze(1).to_broadcast([P, GB, N])

                    def rows(ap):
                        return ap.rearrange("p (b n) -> p b n", n=N)

                    for i in range(2):
                        for m in range(DK):
                            j = 2 * i + m
                            dve.wait_ge(proj_done, 4 * i + m + 1)
                            nc.vector.scalar_tensor_tensor(out=rows(rot_a[:, j, :]), in0=rows(ps[4 * i + m][:, 0:GT]),
                                                           scalar=bs[:, 2 * i, m:m + 1], in1=table(cs, m),
                                                           op0=ALU.add, op1=ALU.mult).then_inc(a_done, 1)
                        for m in range(DK):
                            j = 2 * i + m
                            dve.wait_ge(proj_done, 4 * i + 2 + m + 1)
                            nc.vector.scalar_tensor_tensor(out=rows(rot_b[:, j, :]), in0=rows(ps[4 * i + 2 + m][:, 0:GT]),
                                                           scalar=bs[:, 2 * i + 1, m:m + 1], in1=table(sn, m),
                                                           op0=ALU.add, op1=ALU.mult).then_inc(b_done, 1)
                        for m in range(DK):
                            j = 2 * i + m
                            dve.wait_ge(b_done, j + 1)
                            dve.wait_ge(a_done, j + 1)
                            dst, done = ((q, q_done), (kk, k_done))[i]
                            nc.vector.tensor_tensor(dst[:, m, :], rot_a[:, j, :], rot_b[:, j, :], ALU.add).then_inc(done, 1)
                    dve.wait_ge(k_done, 2)
                    for par in range(2):
                        for m in range(DK):
                            nc.vector.tensor_scalar(kpar[par][:, m, :], kk[:, m, :], ev[:, par:par + 1], None, ALU.mult)\
                                .then_inc(kpar_done, 1)

                    def shift(u):
                        s = ps[S_BANK[u % 3]][0:N, 0:4 * N].rearrange("p (j n) -> p j n", n=N)
                        dve.wait_ge(s_done, u + 1)
                        nc.vector.tensor_reduce(mx[:, u, :], s, AX.X, ALU.max).then_inc(mx_done, 1)
                        dve.wait_ge(mx_done, u + 1)
                        if u >= NE:
                            dve.wait_ge(ex_done, u - NE + 1)
                        nc.vector.tensor_tensor(low[:, u % NE, :].rearrange("p (j n) -> p j n", n=N), s,
                                                mx[:, u, :].unsqueeze(2).to_broadcast([N, 4, N]), ALU.subtract)\
                            .then_inc(low_done, 1)

                    def context(b):
                        dve.wait_ge(av_done, 4 * (b + 1))
                        cx = ps[C_BANK[b % 2]][0:N, 0:H * (HD + 1)].rearrange("p (h e) -> p h e", e=HD + 1)
                        nc.vector.reciprocal(rs[:, b, :], cx[:, :, HD]).then_inc(rs_done, 1)
                        dve.wait_ge(rs_done, b + 1)
                        nc.vector.tensor_tensor(cn[:, b, :].rearrange("p (h e) -> p h e", e=HD), cx[:, :, 0:HD],
                                                rs[:, b, :].unsqueeze(2).to_broadcast([N, H, HD]), ALU.mult).then_inc(cn_done, 1)

                    for u in range(UNITS):
                        shift(u)
                        if u >= 6 and (u - 6) % 4 == 0:
                            context((u - 6) // 4)
                    context(GB - 1)
                    for m in range(DK):
                        dve.wait_ge(o_done, m + 1)
                        nc.vector.scalar_tensor_tensor(out=h[:, m, group_cols(g)], in0=ps[m][:, 0:GT],
                                                       scalar=bs[:, 5, m:m + 1], in1=h[:, m, group_cols(g)],
                                                       op0=ALU.add, op1=ALU.add).then_inc(res_done, 1)
            st.clear()


def l2_attn(nc, h, c, wq, wk, wv):
    MASKED = -1e30
    with Stage(nc, "at2") as st:
        W = {x: st.sbuf(x, [P, DK, D]) for x in ("wq", "wk", "wv")}
        mask = st.sbuf("mask", [N, N])
        ps = [st.psum(f"ps{i}") for i in range(8)]
        norm = Norm(st, ps[0], ps[1])
        q = st.sbuf("q", [P, DK, GT])
        kk = st.sbuf("k", [P, DK, GT])
        v = st.sbuf("v", [N, GB, D])
        sc = st.sbuf("sc", [N, GB, N])
        low = st.sbuf("low", [N, GB, N])
        ex = st.sbuf("ex", [N, GB, N])
        pr = st.sbuf("pr", [N, GB, N])
        prT = st.sbuf("prT", [N, GB, N])
        mx, sm, rs = (st.sbuf(x, [N, GB]) for x in ("mx", "sm", "rs"))
        (w_in, zero, masked, proj_done, qk_done, v_mm, v_done, s_done, sc_done, mx_done, low_done, ex_done, sm_done, rs_done,
         pr_done, t_done, prT_done, o_done, res_done) = (
            st.sem(x) for x in ("w_in", "zero", "masked", "proj_done", "qk_done", "v_mm", "v_done", "s_done", "sc_done",
                                "mx_done", "low_done", "ex_done", "sm_done", "rs_done", "pr_done", "t_done", "prT_done",
                                "o_done", "res_done"))
        with nc.Block() as block:
            @block.sync
            def _(sp):
                for x, src in (("wq", wq), ("wk", wk), ("wv", wv)):
                    sp.dma_start(W[x][:, :, :], src.rearrange("(k p) n -> p k n", p=P)).then_inc(w_in, 16)
                sp.wait_ge(w_in, 48)

            @block.gpsimd
            def _(pool):
                nc.gpsimd.memset(mask[:, :], 0.0).then_inc(zero, 1)
                pool.wait_ge(zero, 1)
                nc.gpsimd.affine_select(out=mask[:, :], in_=mask[:, :], compare_op=ALU.is_ge, fill=MASKED,
                                        base=0, pattern=[[-1, N]], channel_multiplier=1).then_inc(masked, 1)

            @block.scalar
            def _(act):
                nc.scalar.preload_act_table_set(EXP_LN)
        st.clear()
        with nc.Fori(0, GROUPS) as g:
            with nc.Block(no_gpsimd_drain=True) as block:
                @block.tensor
                def _(pe):
                    norm.tensor_mean(nc, pe, c["ones"], lambda k: h[:, k, group_cols(g)])
                    norm.tensor_var(nc, pe, c["ones"])
                    pe.wait_ge(norm.ready, 1)
                    for i, x in enumerate(("wq", "wk")):
                        for m in range(DK):
                            for k in range(DK):
                                mm = nc.tensor.matmul(ps[2 + 2 * i + m][:, 0:GT], W[x][:, k, m * P:(m + 1) * P],
                                                      norm.out[:, k, :], start=(k == 0), stop=(k == DK - 1))
                            mm.then_inc(proj_done, 1)
                    for b in range(GB):
                        for k in range(DK):
                            mm = nc.tensor.matmul(ps[6 + b // 2][0:N, (b % 2) * D:(b % 2 + 1) * D],
                                                  norm.out[:, k, b * N:(b + 1) * N], W["wv"][:, k, :],
                                                  start=(k == 0), stop=(k == DK - 1))
                        if b % 2:
                            mm.then_inc(v_mm, 1)
                    pe.wait_ge(qk_done, 4)
                    for b in range(GB):
                        for k in range(DK):
                            mm = nc.tensor.matmul(ps[0][0:N, b * N:(b + 1) * N], q[:, k, b * N:(b + 1) * N],
                                                  kk[:, k, b * N:(b + 1) * N], start=(k == 0), stop=(k == DK - 1))
                    mm.then_inc(s_done, 1)
                    pe.wait_ge(pr_done, 1)
                    for b in range(GB):
                        mm = nc.tensor.transpose(ps[1][0:N, b * N:(b + 1) * N], pr[:, b, :], c["ident"][0:N, 0:N])
                    mm.then_inc(t_done, 1)
                    pe.wait_ge(prT_done, 1)
                    pe.wait_ge(v_done, GB // 2)
                    for m in range(DK):
                        for b in range(GB):
                            mm = nc.tensor.matmul(ps[2 + m][:, b * N:(b + 1) * N], v[:, b, m * P:(m + 1) * P], prT[:, b, :],
                                                  start=True, stop=True)
                        mm.then_inc(o_done, 1)

                @block.scalar
                def _(act):
                    norm.scalar(nc, act, c["eps"])
                    for i in range(4):
                        act.wait_ge(proj_done, i + 1)
                        dst = (q, kk)[i // 2]
                        nc.scalar.activation(dst[:, i % 2, :], ps[2 + i][:, 0:GT], ACT.Copy).then_inc(qk_done, 1)
                    for b in range(0, GB, 2):
                        act.wait_ge(v_mm, b // 2 + 1)
                        nc.scalar.activation(v[:, b:b + 2, :], ps[6 + b // 2][0:N, :].rearrange("p (b d) -> p b d", b=2),
                                             ACT.Copy).then_inc(v_done, 1)
                    act.wait_ge(low_done, 1)
                    nc.scalar.activation(ex[:, :, :], low[:, :, :], ACT.Exp).then_inc(ex_done, 1)
                    act.wait_ge(t_done, 1)
                    nc.scalar.activation(prT[:, :, :], ps[1][0:N, 0:GT].rearrange("p (b n) -> p b n", n=N), ACT.Copy)\
                        .then_inc(prT_done, 1)

                @block.vector
                def _(dve):
                    norm.vector(nc, dve, h[:, :, group_cols(g)])
                    dve.wait_ge(s_done, 1)
                    nc.vector.scalar_tensor_tensor(out=sc[:, :, :], in0=ps[0][0:N, 0:GT].rearrange("p (b n) -> p b n", n=N),
                                                   scalar=D ** -0.5, in1=mask[:, :].unsqueeze(1).to_broadcast([N, GB, N]),
                                                   op0=ALU.mult, op1=ALU.add).then_inc(sc_done, 1)
                    dve.wait_ge(sc_done, 1)
                    nc.vector.tensor_reduce(mx[:, :], sc[:, :, :], AX.X, ALU.max).then_inc(mx_done, 1)
                    dve.wait_ge(mx_done, 1)
                    nc.vector.tensor_tensor(low[:, :, :], sc[:, :, :], mx[:, :].unsqueeze(2).to_broadcast([N, GB, N]),
                                            ALU.subtract).then_inc(low_done, 1)
                    dve.wait_ge(ex_done, 1)
                    nc.vector.tensor_reduce(sm[:, :], ex[:, :, :], AX.X, ALU.add).then_inc(sm_done, 1)
                    dve.wait_ge(sm_done, 1)
                    nc.vector.reciprocal(rs[:, :], sm[:, :]).then_inc(rs_done, 1)
                    dve.wait_ge(rs_done, 1)
                    nc.vector.tensor_tensor(pr[:, :, :], ex[:, :, :], rs[:, :].unsqueeze(2).to_broadcast([N, GB, N]),
                                            ALU.mult).then_inc(pr_done, 1)
                    for m in range(DK):
                        dve.wait_ge(o_done, m + 1)
                        nc.vector.tensor_tensor(h[:, m, group_cols(g)], ps[2 + m][:, 0:GT], h[:, m, group_cols(g)],
                                                ALU.add).then_inc(res_done, 1)
            st.clear()


def moe(nc, h, c, router_w, router_b, gate_up, down, slots_in, slots_out):
    E = router_w.shape[1]
    TOPK = 2
    F = gate_up.shape[4]
    FB = [(f, min(P, F - f)) for f in range(0, F, P)]
    C = -(-5 * T * TOPK // (4 * E))
    STRIDE = slots_in.shape[0] // (E + 1)
    TILES = [(t, min(P, C - t)) for t in range(0, C, P)]
    HALVES = [(0, (C + 1) // 2), ((C + 1) // 2, C // 2)]
    NOWHERE = 1 << 20
    NT = len(TILES)
    with Stage(nc, "moe") as st:
        ps = [st.psum(f"ps{i}") for i in range(8)]
        normed = st.sbuf("normed", [P, DK, T])
        share = st.sbuf("share", [N, B, TOPK])
        to_slot = st.sbuf("to_slot", [P, B, TOPK], U32)
        from_slot = st.sbuf("from_slot", [P, B, TOPK], U32)

        with Stage(nc, "rt") as sr:
            token_rows = sr.sbuf("token_rows", [P, B, D])
            logits = sr.sbuf("logits", [N, B, E])
            w_r = sr.sbuf("w_r", [P, DK, E])
            b_r = sr.sbuf("b_r", [N, E])
            zeros = sr.sbuf("zeros", [P, STRIDE // P, D])
            scattered = sr.sem("scattered")
            with Stage(nc, "rn") as sn:
                norm = Norm(sn, ps[0], ps[1])
                loaded, zeroed, filled, kept, score_mm, score_done, turned, rows_done = (
                    sn.sem(x) for x in ("loaded", "zeroed", "filled", "kept", "score_mm", "score_done", "turned", "rows_done"))
                with nc.Block() as block:
                    @block.sync
                    def _(sp):
                        sp.dma_start(w_r[:, :, :], router_w.rearrange("(k p) e -> p k e", p=P)).then_inc(loaded, 16)
                        sp.dma_start(b_r[:, :], router_b.to_broadcast([N, E])).then_inc(loaded, 16)
                        sp.wait_ge(loaded, 32)
                        sp.wait_ge(zeroed, 1)
                        for e in range(E + 1):
                            sp.dma_start(slots_in[e * STRIDE:(e + 1) * STRIDE, :].rearrange("(a p) d -> p a d", p=P),
                                         zeros[:, :, :]).then_inc(filled, 16)
                        sp.wait_ge(filled, 16 * (E + 1))

                    @block.gpsimd
                    def _(pool):
                        nc.gpsimd.memset(zeros[:, :, :], 0.0).then_inc(zeroed, 1)
                        nc.gpsimd.memset(token_rows[:, :, :], 0.0)

                    @block.scalar
                    def _(act):
                        nc.scalar.preload_act_table_set(EXP_LN)
                sn.clear()
                with nc.Fori(0, GROUPS) as g:
                    with nc.Block(no_gpsimd_drain=True) as block:
                        @block.tensor
                        def _(pe):
                            norm.tensor_mean(nc, pe, c["ones"], lambda k: h[:, k, group_cols(g)])
                            norm.tensor_var(nc, pe, c["ones"])
                            pe.wait_ge(norm.ready, 1)
                            for b in range(GB):
                                for k in range(DK):
                                    mm = nc.tensor.matmul(ps[2][0:N, b * E:(b + 1) * E], norm.out[:, k, b * N:(b + 1) * N],
                                                          w_r[:, k, :], start=(k == 0), stop=(k == DK - 1))
                            mm.then_inc(score_mm, 1)
                            for b in range(GB):
                                for k in range(DK):
                                    mm = nc.tensor.transpose(ps[3 + b // 2][0:N, (b % 2 * DK + k) * P:(b % 2 * DK + k + 1) * P],
                                                             norm.out[:, k, b * N:(b + 1) * N], c["ident"][:, :])
                                if b % 2:
                                    mm.then_inc(turned, 1)

                        @block.scalar
                        def _(act):
                            norm.scalar(nc, act, c["eps"])
                            act.wait_ge(norm.ready, 1)
                            nc.scalar.activation(normed[:, :, group_cols(g)], norm.out[:, :, :], ACT.Copy).then_inc(kept, 1)
                            for i in range(GB // 2):
                                act.wait_ge(turned, i + 1)
                                nc.scalar.activation(token_rows[0:N, bass.ds(g * GB + 2 * i, 2), :],
                                                     ps[3 + i][0:N, :].rearrange("p (b d) -> p b d", b=2), ACT.Copy)\
                                    .then_inc(rows_done, 1)

                        @block.vector
                        def _(dve):
                            norm.vector(nc, dve, h[:, :, group_cols(g)])
                            dve.wait_ge(score_mm, 1)
                            nc.vector.tensor_tensor(logits[:, bass.ds(g * GB, GB), :],
                                                    ps[2][0:N, 0:GB * E].rearrange("p (b e) -> p b e", e=E),
                                                    b_r[:, :].unsqueeze(1).to_broadcast([N, GB, E]), ALU.add)\
                                .then_inc(score_done, 1)
                    sn.clear()

            with Stage(nc, "ch") as sc:
                tile = lambda x, shape=(N, B, E), dt=F32: sc.sbuf(x, list(shape), dt)
                small = lambda x: sc.sbuf(x, [N, B])
                ramp, shifted, ex, probs = tile("ramp", (N, E)), tile("shifted"), tile("ex"), tile("probs")
                top, idx = tile("top", (N, B, 8)), tile("idx", (N, B, 8), U32)
                hot = [tile("hot0"), tile("hot1")]
                both_hot, totals = tile("both_hot"), tile("totals", (N, E, B))
                fresh, upto, before = tile("fresh", (N, E, B)), tile("upto", (N, E, B)), tile("before", (N, E, B))
                place, hit = tile("place"), [tile("hit0"), tile("hit1")]
                earlier, every = sc.sbuf("earlier", [N, N]), sc.sbuf("every", [N, N])
                mx, sm, rs, wsum, wr_ = small("mx"), small("sm"), small("rs"), small("wsum"), small("wr")
                pos, base, inside, low, gat, far, sca, wk_ = ([small(f"{x}{k}") for k in range(TOPK)] for x in
                                                             ("pos", "base", "inside", "low", "gat", "far", "sca", "wk"))
                made, step, counted, spread_ready = (sc.sem(x) for x in ("made", "step", "counted", "spread_ready"))
                with nc.Block() as block:
                    @block.gpsimd
                    def _(pool):
                        nc.gpsimd.iota(ramp[:, :], pattern=[[1, E]], base=0, channel_multiplier=0,
                                       allow_small_or_imprecise_dtypes=True)
                        nc.gpsimd.memset(every[:, :], 1.0)
                        nc.gpsimd.memset(fresh[:, :, :], 1.0)
                        nc.gpsimd.memset(to_slot[:, :, :], NOWHERE)
                        nc.gpsimd.memset(from_slot[:, :, :], NOWHERE)
                        nc.gpsimd.memset(earlier[:, :], 1.0).then_inc(made, 1)
                        pool.wait_ge(made, 1)
                        nc.gpsimd.memset(fresh[:, :, 0:1], 0.0)
                        nc.gpsimd.affine_select(out=earlier[:, :], in_=earlier[:, :], compare_op=ALU.is_gt, fill=0.0,
                                                base=0, pattern=[[1, N]], channel_multiplier=-1).then_inc(made, 1)
                        pool.wait_ge(spread_ready, TOPK)
                        for b in range(B):
                            for k in range(TOPK):
                                nc.gpsimd.indirect_dma_start(
                                    out=slots_in[:, :], out_offset=bass.IndirectOffsetOnAxis(ap=to_slot[:, b, k:k + 1], axis=0),
                                    in_=token_rows[:, b, :], in_offset=None, bounds_check=(E + 1) * STRIDE - 1,
                                    oob_is_err=False).then_inc(scattered, 16)
                        pool.wait_ge(scattered, 16 * B * TOPK)

                    @block.scalar
                    def _(act):
                        act.wait_ge(step, 2)
                        nc.scalar.activation(ex[:, :, :], shifted[:, :, :], ACT.Exp).then_inc(counted, 1)

                    @block.tensor
                    def _(pe):
                        pe.wait_ge(made, 2)
                        pe.wait_ge(step, 11 + 2 * B)
                        flat = both_hot[:, :, :].rearrange("p b e -> p (b e)")
                        nc.tensor.matmul(ps[0][0:N, :], earlier[:, :], flat, start=True, stop=True).then_inc(counted, 1)
                        nc.tensor.matmul(ps[1][0:N, :], every[:, :], flat, start=True, stop=True).then_inc(counted, 1)

                    @block.vector
                    def _(dve):
                        n = [0]

                        def after(ins):
                            n[0] += 1
                            ins.then_inc(step, 1)
                            dve.wait_ge(step, n[0])

                        def wide(x):
                            return x[:, :].unsqueeze(2).to_broadcast([N, B, E])

                        V = nc.vector
                        after(V.tensor_reduce(mx[:, :], logits[:, :, :], AX.X, ALU.max))
                        after(V.tensor_tensor(shifted[:, :, :], logits[:, :, :], wide(mx), ALU.subtract))
                        dve.wait_ge(counted, 1)
                        after(V.tensor_reduce(sm[:, :], ex[:, :, :], AX.X, ALU.add))
                        after(V.reciprocal(rs[:, :], sm[:, :]))
                        after(V.tensor_tensor(probs[:, :, :], ex[:, :, :], wide(rs), ALU.mult))
                        for b in range(B):
                            after(V.max(top[:, b, :], probs[:, b, :]))
                        for b in range(B):
                            after(V.max_index(idx[:, b, :], top[:, b, :], probs[:, b, :]))
                        dve.wait_ge(made, 2)
                        after(V.tensor_tensor(wsum[:, :], top[:, :, 0], top[:, :, 1], ALU.add))
                        after(V.tensor_scalar(wsum[:, :], wsum[:, :], 1e-9, None, ALU.add))
                        after(V.reciprocal(wr_[:, :], wsum[:, :]))
                        for k in range(TOPK):
                            after(V.tensor_tensor(hot[k][:, :, :], ramp[:, :].unsqueeze(1).to_broadcast([N, B, E]),
                                                  idx[:, :, k:k + 1].to_broadcast([N, B, E]), ALU.is_equal))
                        after(V.tensor_tensor(both_hot[:, :, :], hot[0][:, :, :], hot[1][:, :, :], ALU.add))
                        dve.wait_ge(counted, 3)
                        after(V.tensor_copy(totals[:, :, :], ps[1][0:N, :].rearrange("p (b e) -> p e b", e=E)))
                        line = lambda x: x[:, :, :].rearrange("p e b -> p (e b)")
                        after(V.tensor_tensor_scan(line(upto), line(fresh), line(totals), 0.0, ALU.mult, ALU.add))
                        after(V.tensor_tensor(before[:, :, :], upto[:, :, :], totals[:, :, :], ALU.subtract))
                        after(V.tensor_tensor(place[:, :, :], ps[0][0:N, :].rearrange("p (b e) -> p b e", e=E),
                                              before[:, :, :].rearrange("p e b -> p b e"), ALU.add))
                        for k in range(TOPK):
                            after(V.tensor_tensor(hit[k][:, :, :], hot[k][:, :, :], place[:, :, :], ALU.mult))
                            after(V.tensor_reduce(pos[k][:, :], hit[k][:, :, :], AX.X, ALU.add))
                            after(V.tensor_scalar(base[k][:, :], idx[:, :, k], float(STRIDE), None, ALU.mult))
                            after(V.tensor_scalar(inside[k][:, :], pos[k][:, :], float(C), None, ALU.is_lt))
                            after(V.tensor_scalar(low[k][:, :], pos[k][:, :], float(C - 1), None, ALU.min))
                            after(V.scalar_tensor_tensor(out=gat[k][:, :], in0=idx[:, :, k], scalar=float(C), in1=low[k][:, :],
                                                         op0=ALU.mult, op1=ALU.add))
                            after(V.tensor_copy(from_slot[0:N, :, k], gat[k][:, :]))
                            after(V.tensor_tensor(low[k][:, :], low[k][:, :], base[k][:, :], ALU.add))
                            after(V.tensor_scalar(far[k][:, :], inside[k][:, :], -float(NOWHERE), float(NOWHERE), ALU.mult, ALU.add))
                            after(V.tensor_tensor(sca[k][:, :], far[k][:, :], low[k][:, :], ALU.add))
                            after(V.tensor_copy(to_slot[0:N, :, k], sca[k][:, :]))
                            after(V.tensor_tensor(wk_[k][:, :], top[:, :, k], wr_[:, :], ALU.mult))
                            V.tensor_tensor(share[:, :, k], wk_[k][:, :], inside[k][:, :], ALU.mult).then_inc(spread_ready, 1)
                sr.clear(pool_dmas=True)
                sc.clear()

        w_gu = [st.sbuf(f"w_gu{i}", [P, DK, 2, F]) for i in range(2)]
        w_dn = [st.sbuf(f"w_dn{i}", [P, len(FB), D]) for i in range(2)]

        def fetch_weights(sp, e, i, done):
            sp.dma_start(w_gu[i][:, :, :, :], gate_up[bass.ds(e, 1), :, :, :, :].rearrange("e p k g f -> (e p) k g f"))\
                .then_inc(done, 16)
            sp.dma_start(w_dn[i][:, :, :], down[bass.ds(e, 1), :, :, :].rearrange("e p k n -> (e p) k n")).then_inc(done, 16)

        with Stage(nc, "xp") as sx:
            rows_in = [sx.sbuf(f"rows_in{i}", [P, NT, D]) for i in range(2)]
            xT = [sx.sbuf(f"xT{i}", [P, DK, C]) for i in range(2)]
            silu = sx.sbuf("silu", [P, 2, HALVES[0][1]])
            hid = [sx.sbuf(f"hid{i}", [P, len(FB), C]) for i in range(2)]
            rows_out = [sx.sbuf(f"rows_out{i}", [P, NT, D]) for i in range(2)]
            landed = [sx.sem(f"landed{i}") for i in range(2)]
            turned, xT_done, gate_mm, up_mm, silu_done, hid_done, down_mm, out_done, stored = (
                sx.sem(x) for x in ("turned", "xT_done", "gate_mm", "up_mm", "silu_done", "hid_done", "down_mm", "out_done", "stored"))
            NF = len(FB)
            FULL = NT - 1
            LAST = TILES[-1][1]

            def fetch(sp, e, i):
                fetch_weights(sp, e, i, landed[i])
                sp.dma_start(rows_in[i][:, 0:FULL, :], slots_in[bass.ds(e * STRIDE, FULL * P), :].rearrange("(a p) d -> p a d", p=P))\
                    .then_inc(landed[i], 16)
                sp.dma_start(rows_in[i][0:LAST, FULL, :], slots_in[bass.ds(e * STRIDE + FULL * P, LAST), :]).then_inc(landed[i], 16)

            with nc.Block() as block:
                @block.sync
                def _(sp):
                    fetch(sp, 0, 0)
                    sp.wait_ge(landed[0], 64)
            sx.clear()
            with nc.Fori(0, E // 2) as g:
                with nc.Block(no_gpsimd_drain=True) as block:
                    @block.sync
                    def _(sp):
                        fetch(sp, g * 2 + 1, 1)
                        sp.wait_ge(down_mm, 3)
                        fetch(sp, g * 2 + 2, 0)
                        sp.wait_ge(landed[0], 64)

                    @block.tensor
                    def _(pe):
                        for i in range(2):
                            if i:
                                pe.wait_ge(landed[1], 64)
                            if i:
                                pe.wait_ge(xT_done, 3)
                            for t in range(NT):
                                for k in range(DK):
                                    r = TILES[t][1]
                                    dst = ps[k][:, t * P:(t + 1) * P] if t < FULL else ps[2][:, k * LAST:(k + 1) * LAST]
                                    mm = nc.tensor.transpose(dst, rows_in[i][0:r, t, k * P:(k + 1) * P], c["ident"][0:r, 0:r])
                            mm.then_inc(turned, 1)
                            pe.wait_ge(xT_done, 3 * i + 3)
                            for hf, (c0, cn) in enumerate(HALVES):
                                for f, (f0, fn) in enumerate(FB):
                                    u = (i * 2 + hf) * NF + f
                                    if u >= 2:
                                        pe.wait_ge(silu_done, u - 1)
                                    for k in range(DK):
                                        mm = nc.tensor.matmul(ps[3 + u % 2][0:fn, 0:cn], w_gu[i][:, k, 0, f0:f0 + fn],
                                                              xT[i][:, k, c0:c0 + cn], start=(k == 0), stop=(k == DK - 1))
                                    mm.then_inc(gate_mm, 1)
                                    if u >= 2:
                                        pe.wait_ge(hid_done, u - 1)
                                    for k in range(DK):
                                        mm = nc.tensor.matmul(ps[5 + u % 2][0:fn, 0:cn], w_gu[i][:, k, 1, f0:f0 + fn],
                                                              xT[i][:, k, c0:c0 + cn], start=(k == 0), stop=(k == DK - 1))
                                    mm.then_inc(up_mm, 1)
                            pe.wait_ge(hid_done, (i + 1) * 2 * NF)
                            for t, (t0, r) in enumerate(TILES):
                                q = 3 * i + t // 2
                                if q >= 1 and t % 2 == 0:
                                    pe.wait_ge(out_done, q)
                                for f, (f0, fn) in enumerate(FB):
                                    mm = nc.tensor.matmul(ps[7][0:r, (t % 2) * D:(t % 2 + 1) * D], hid[i][0:fn, f, t0:t0 + r],
                                                          w_dn[i][0:fn, f, :], start=(f == 0), stop=(f == NF - 1))
                                if t % 2 or t == NT - 1:
                                    mm.then_inc(down_mm, 1)

                    @block.scalar
                    def _(act):
                        for i in range(2):
                            act.wait_ge(turned, i + 1)
                            for k in range(DK):
                                nc.scalar.activation(xT[i][:, k, 0:FULL * P], ps[k][:, :], ACT.Copy).then_inc(xT_done, 1)
                            nc.scalar.activation(xT[i][:, :, FULL * P:C], ps[2][:, 0:DK * LAST].rearrange("p (k r) -> p k r", k=DK),
                                                 ACT.Copy).then_inc(xT_done, 1)
                            for u in range(2 * NF * i, 2 * NF * (i + 1)):
                                hf, f = u // NF % 2, u % NF
                                cn, fn = HALVES[hf][1], FB[f][1]
                                act.wait_ge(gate_mm, u + 1)
                                if u >= 2:
                                    act.wait_ge(hid_done, u - 1)
                                nc.scalar.activation(silu[0:fn, u % 2, 0:cn], ps[3 + u % 2][0:fn, 0:cn], ACT.Silu).then_inc(silu_done, 1)
                        for i in range(2):
                            act.wait_ge(out_done, 3 * i + 3)
                            e = g * 2 + i
                            act.dma_start(slots_out[bass.ds(e * C, FULL * P), :].rearrange("(a p) d -> p a d", p=P),
                                          rows_out[i][:, 0:FULL, :]).then_inc(stored, 16)
                            act.dma_start(slots_out[bass.ds(e * C + FULL * P, LAST), :], rows_out[i][0:LAST, FULL, :])\
                                .then_inc(stored, 16)
                        act.wait_ge(stored, 64)

                    @block.vector
                    def _(dve):
                        for i in range(2):
                            for u in range(2 * NF * i, 2 * NF * (i + 1)):
                                hf, f = u // NF % 2, u % NF
                                (c0, cn), fn = HALVES[hf], FB[f][1]
                                dve.wait_ge(silu_done, u + 1)
                                dve.wait_ge(up_mm, u + 1)
                                nc.vector.tensor_tensor(hid[i][0:fn, f, c0:c0 + cn], silu[0:fn, u % 2, 0:cn],
                                                        ps[5 + u % 2][0:fn, 0:cn], ALU.mult).then_inc(hid_done, 1)
                            for q in range(3):
                                r = P if q < 2 else LAST
                                tiles = 2 if q < 2 else 1
                                dve.wait_ge(down_mm, 3 * i + q + 1)
                                nc.vector.tensor_copy(rows_out[i][0:r, 2 * q:2 * q + tiles, :],
                                                      ps[7][0:r, 0:tiles * D].rearrange("p (t d) -> p t d", d=D)).then_inc(out_done, 1)
                sx.clear()

        with Stage(nc, "sh") as ss:
            now_slot = ss.sbuf("now_slot", [P, GB * TOPK], U32)
            now_share = ss.sbuf("now_share", [N, GB * TOPK])
            got = [[ss.sbuf(f"got{b}{k}", [P, D]) for k in range(TOPK)] for b in range(GB)]
            part = ss.sbuf("part", [N, GB, D])
            mixed = ss.sbuf("mixed", [N, GB, D])
            x_in = ss.sbuf("x_in", [P, DK, GT])
            silu = ss.sbuf("silu", [P, 2, GT])
            hid = ss.sbuf("hid", [P, len(FB), GT])
            hn = ss.sbuf("hn", [P, DK, GT])
            NF = len(FB)
            gathered = [ss.sem(f"gathered{b}") for b in range(GB)]
            slot_done, share_done, x_done, part_done, mixed_done, gate_mm, up_mm, silu_done, hid_done, sum_mm, hn_done, res_done = (
                ss.sem(x) for x in ("slot_done", "share_done", "x_done", "part_done", "mixed_done", "gate_mm", "up_mm", "silu_done",
                                    "hid_done", "sum_mm", "hn_done", "res_done"))
            with nc.Fori(0, GROUPS) as g:
                with nc.Block(no_gpsimd_drain=True) as block:
                    @block.gpsimd
                    def _(pool):
                        pool.wait_ge(slot_done, 1)
                        for b in range(GB):
                            for k in range(TOPK):
                                nc.gpsimd.indirect_dma_start(
                                    out=got[b][k][:, :], out_offset=None, in_=slots_out[:, :],
                                    in_offset=bass.IndirectOffsetOnAxis(ap=now_slot[:, b * TOPK + k:b * TOPK + k + 1], axis=0),
                                    bounds_check=E * C - 1, oob_is_err=False).then_inc(gathered[b], 16)
                        for b in range(GB):
                            pool.wait_ge(gathered[b], 16 * TOPK)

                    @block.scalar
                    def _(act):
                        nc.scalar.activation(x_in[:, :, :], normed[:, :, group_cols(g)], ACT.Copy).then_inc(x_done, 1)
                        for f, (f0, fn) in enumerate(FB):
                            act.wait_ge(gate_mm, f + 1)
                            if f >= 2:
                                act.wait_ge(hid_done, f - 1)
                            nc.scalar.activation(silu[0:fn, f % 2, :], ps[f][0:fn, 0:GT], ACT.Silu).then_inc(silu_done, 1)

                    @block.tensor
                    def _(pe):
                        pe.wait_ge(x_done, 1)
                        for f, (f0, fn) in enumerate(FB):
                            for k in range(DK):
                                mm = nc.tensor.matmul(ps[f][0:fn, 0:GT], w_gu[0][:, k, 0, f0:f0 + fn], x_in[:, k, :],
                                                      start=(k == 0), stop=(k == DK - 1))
                            mm.then_inc(gate_mm, 1)
                            for k in range(DK):
                                mm = nc.tensor.matmul(ps[3 + f][0:fn, 0:GT], w_gu[0][:, k, 1, f0:f0 + fn], x_in[:, k, :],
                                                      start=(k == 0), stop=(k == DK - 1))
                            mm.then_inc(up_mm, 1)
                        for m in range(DK):
                            for f, (f0, fn) in enumerate(FB):
                                pe.wait_ge(hid_done, f + 1)
                                nc.tensor.matmul(ps[6 + m][:, 0:GT], w_dn[0][0:fn, f, m * P:(m + 1) * P], hid[0:fn, f, :],
                                                 start=(f == 0), stop=False, skip_group_check=True)
                            for b in range(GB):
                                pe.wait_ge(mixed_done, b + 1)
                                mm = nc.tensor.matmul(ps[6 + m][:, b * N:(b + 1) * N], mixed[:, b, m * P:(m + 1) * P],
                                                      c["ident"][0:N, 0:N], start=False, stop=(b == GB - 1), skip_group_check=True)
                            mm.then_inc(sum_mm, 1)

                    @block.vector
                    def _(dve):
                        nc.vector.tensor_copy(now_slot[:, :], from_slot[:, bass.ds(g * GB, GB), :].rearrange("p b k -> p (b k)"))\
                            .then_inc(slot_done, 1)
                        nc.vector.tensor_copy(now_share[:, :], share[:, bass.ds(g * GB, GB), :].rearrange("p b k -> p (b k)"))\
                            .then_inc(share_done, 1)
                        nc.vector.tensor_tensor(hn[:, :, :], h[:, :, group_cols(g)], normed[:, :, group_cols(g)], ALU.add)\
                            .then_inc(hn_done, 1)
                        for f, (f0, fn) in enumerate(FB):
                            dve.wait_ge(silu_done, f + 1)
                            dve.wait_ge(up_mm, f + 1)
                            nc.vector.tensor_tensor(hid[0:fn, f, :], silu[0:fn, f % 2, :], ps[3 + f][0:fn, 0:GT], ALU.mult)\
                                .then_inc(hid_done, 1)
                        dve.wait_ge(share_done, 1)
                        for b in range(GB):
                            dve.wait_ge(gathered[b], 16 * TOPK)
                            nc.vector.tensor_scalar(part[:, b, :], got[b][0][0:N, :], now_share[:, 2 * b:2 * b + 1], None, ALU.mult)\
                                .then_inc(part_done, 1)
                            dve.wait_ge(part_done, b + 1)
                            nc.vector.scalar_tensor_tensor(out=mixed[:, b, :], in0=got[b][1][0:N, :],
                                                           scalar=now_share[:, 2 * b + 1:2 * b + 2], in1=part[:, b, :],
                                                           op0=ALU.mult, op1=ALU.add).then_inc(mixed_done, 1)
                        for m in range(DK):
                            dve.wait_ge(sum_mm, m + 1)
                            dve.wait_ge(hn_done, 1)
                            nc.vector.tensor_tensor(h[:, m, group_cols(g)], ps[6 + m][:, 0:GT], hn[:, m, :], ALU.add)\
                                .then_inc(res_done, 1)
                ss.clear(pool_dmas=True)


def mamba(nc, h, c, params):
    INNER = params[0]["in_t"].shape[1] // 2
    IB = INNER // P
    S = params[0]["a_log"].shape[2]
    R = params[0]["dt_t"].shape[0]
    TAPS = params[0]["conv_w"].shape[2]
    BC = 2 * S
    PARTS = 3
    DT0 = PARTS * BC
    JS = 2
    STEPS = S * IB
    NB = 4
    CB = 4

    with Stage(nc, "ssm") as st:
        w_in = [st.sbuf(f"w_in{d}", [P, DK, 2 * INNER]) for d in range(2)]
        w_xp = [st.sbuf(f"w_xp{d}", [P, IB, DT0 + R]) for d in range(2)]
        w_dt = [st.sbuf(f"w_dt{d}", [R + 1, INNER]) for d in range(2)]
        w_out = [st.sbuf(f"w_out{d}", [P, IB, D]) for d in range(2)]
        conv_w = [st.sbuf(f"conv_w{d}", [P, IB, TAPS]) for d in range(2)]
        conv_b, skip = ([st.sbuf(f"{x}{d}", [P, IB]) for d in range(2)] for x in ("conv_b", "skip"))
        decay = [st.sbuf(f"decay{d}", [P, IB, S]) for d in range(2)]
        pick = st.sbuf("pick", [DT0, BC, P], BF16)
        dA = [st.sbuf(f"dA{d}", [P, NB, GT]) for d in range(2)]
        one = st.sbuf("one", [P, 1])
        ps = [st.psum(f"ps{i}") for i in range(8)]
        Y_BANK, B_BANK, C_BANK, X_BANK, Z_BANK = ps[0:2], ps[2:4], ps[4:6], ps[6], ps[7]
        norm = Norm(st, X_BANK, X_BANK)
        conv = st.sbuf("conv", [P, IB, GT])
        y = st.sbuf("y", [P, JS, GT])
        xc, z, step, du = ([st.sbuf(f"{x}{d}", [P, IB, GT]) for d in range(2)] for x in ("xc", "z", "step", "du"))
        parts = [st.sbuf(f"parts{d}", [DT0, GT], BF16) for d in range(2)]
        rest = st.sbuf("rest", [DT0, GT])
        dt_in = st.sbuf("dt_in", [R + 1, GT])
        mag = norm.square
        bc = st.sbuf("bc", [P, CB, GT])
        dBu = st.sbuf("dBu", [P, NB, GT])
        hs = st.sbuf("hs", [P, NB, GT])
        hc = st.sbuf("hc", [P, NB, GT])
        yz = st.sbuf("yz", [P, IB, GT])
        names = ("w_loaded", "zeros", "picked", "expd", "decay_done",
                 "x_mm", "z_mm", "conv_step", "z_raw", "xc_done", "z_done", "xp_done", "hi_done", "dt_in_done", "rest_done",
                 "mid_done", "lo_done", "dt_mm", "mag_done", "ea_done", "sp_done", "step_done", "du_done",
                 "b_mm", "c_mm", "bc_done", "dA_done", "dbu_dve", "dbu_pool",
                 "scan_done", "hc_done", "y_mm", "y_done", "yz_done", "o_mm", "res_done")
        s = {x: st.sem(x) for x in names}
        with nc.Block() as block:
            @block.sync
            def _(sp):
                n = 0
                for d in range(2):
                    xproj = params[d]["xproj_t"].rearrange("(k p) n -> p k n", p=P)
                    for dst, src in ((w_in[d][:, :, :], params[d]["in_t"].rearrange("(k p) n -> p k n", p=P)),
                                     (w_xp[d][:, :, DT0:DT0 + R], xproj[:, :, 0:R]),
                                     (w_dt[d][0:R, :], params[d]["dt_t"]),
                                     (w_dt[d][R:R + 1, :], params[d]["dt_b"]),
                                     (w_out[d][:, :, :], params[d]["out_t"].rearrange("(k p) n -> p k n", p=P)),
                                     (conv_w[d][:, :, :], params[d]["conv_w"]), (conv_b[d][:, :], params[d]["conv_b"]),
                                     (skip[d][:, :], params[d]["d"]), (decay[d][:, :, :], params[d]["a_log"])):
                        sp.dma_start(dst, src).then_inc(s["w_loaded"], 16)
                        n += 16
                    for r in range(PARTS):
                        sp.dma_start(w_xp[d][:, :, r * BC:(r + 1) * BC], xproj[:, :, R:R + BC]).then_inc(s["w_loaded"], 16)
                        n += 16
                sp.wait_ge(s["w_loaded"], n)

            @block.gpsimd
            def _(pool):
                nc.gpsimd.memset(dA[0][:, :, :], 0.0)
                nc.gpsimd.memset(dA[1][:, :, :], 0.0)
                nc.gpsimd.memset(one[:, :], 1.0)
                nc.gpsimd.memset(dt_in[:, :], 1.0)
                nc.gpsimd.memset(pick[:, :, :], 0.0).then_inc(s["zeros"], 1)
                for r in range(PARTS):
                    pool.wait_ge(s["zeros"], r + 1)
                    nc.gpsimd.affine_select(out=pick[:, :, :], in_=pick[:, :, :], compare_op=ALU.not_equal, fill=1.0,
                                            base=-r * BC, pattern=[[-1, BC], [0, P]], channel_multiplier=1).then_inc(s["zeros"], 1)

            @block.scalar
            def _(act):
                nc.scalar.preload_act_table_set(EXP_LN)
                act.wait_ge(s["w_loaded"], 2 * (9 + PARTS) * 16)
                for d in range(2):
                    nc.scalar.activation(decay[d][:, :, :], decay[d][:, :, :], ACT.Exp).then_inc(s["expd"], 1)

            @block.vector
            def _(dve):
                dve.wait_ge(s["expd"], 2)
                for d in range(2):
                    nc.vector.tensor_scalar(decay[d][:, :, :], decay[d][:, :, :], -1.0, None, ALU.mult)\
                        .then_inc(s["decay_done"], 1)
        st.clear()

        def rows(ap):
            return ap.rearrange("p (b n) -> p b n", n=N)

        def flow(ap, d):
            return ap if d == 0 else ap[:, ::-1]

        def recurrence(i):
            q = i // JS
            return q, q % S, q // S * JS + i % JS

        def by_pool(i):
            return i % 4 != 0

        pool_upto = [sum(by_pool(j) for j in range(i + 1)) for i in range(STEPS)]
        dve_upto = [i + 1 - pool_upto[i] for i in range(STEPS)]

        MEAN, CENTRE, SQUARE, VAR, RSTD, SCALE = -1, 1, 4, 4, 9, 10
        OUT_MM, RES = (-1, 5), (3, 12)
        X_MM = [12 + 6 * m for m in range(IB)]
        Z_MM = [15 + 6 * m for m in range(IB)]
        CONV = [15 + 6 * m for m in range(IB)]
        Z_RAW = [20 + 6 * m for m in range(IB)]
        XC = (29, 40)
        XP_MM, HI, REST, MID, LO = 41, 47, 48, 52, 53
        DT_MM = (49, 50, 55, 57)
        SOFTPLUS = (53, 55, 59, 61)
        STEP = (54, 56, 60, 62)
        DU = (55, 57, 61, 63)
        Z_SILU = STEPS - 1

        def half(d, rec, front, norm_in, out_cols):
            f = 1 - d
            with nc.Block(no_gpsimd_drain=True) as block:
                @block.tensor
                def _(pe):
                    def spread_b(q):
                        if q >= 2:
                            pe.wait_ge(s["bc_done"], q - 1)
                        nc.tensor.matmul(B_BANK[q % 2][:, 0:GT], pick[:, q % S, :], parts[d][:, :], start=True, stop=True)\
                            .then_inc(s["b_mm"], 1)

                    def spread_c(q):
                        if q >= 2:
                            pe.wait_ge(s["hc_done"], JS * (q - 1))
                        nc.tensor.matmul(C_BANK[q % 2][:, 0:GT], pick[:, S + q % S, :], parts[d][:, :], start=True, stop=True)\
                            .then_inc(s["c_mm"], 1)

                    def beside(i):
                        if norm_in is not None and i == MEAN:
                            norm.tensor_mean(nc, pe, c["ones"], lambda k: h[:, k, norm_in])
                        if norm_in is not None and i == VAR:
                            norm.tensor_var(nc, pe, c["ones"])
                        if out_cols is not None and i in OUT_MM:
                            m = OUT_MM.index(i)
                            if m:
                                pe.wait_ge(s["res_done"], m)
                            for k in range(IB):
                                mm = nc.tensor.matmul(Z_BANK[:, 0:GT], w_out[f][:, k, m * P:(m + 1) * P], yz[:, k, :],
                                                      start=(k == 0), stop=(k == IB - 1))
                            mm.then_inc(s["o_mm"], 1)
                        if not front:
                            return
                        if i in X_MM:
                            m = X_MM.index(i)
                            if m:
                                pe.wait_ge(s["conv_step"], TAPS * m)
                            elif norm_in is not None:
                                pe.wait_ge(norm.ready, 1)
                            for k in range(DK):
                                mm = nc.tensor.matmul(X_BANK[:, 0:GT], w_in[f][:, k, m * P:(m + 1) * P], norm.out[:, k, :],
                                                      start=(k == 0), stop=(k == DK - 1))
                            mm.then_inc(s["x_mm"], 1)
                        if i in Z_MM:
                            m = Z_MM.index(i)
                            if m:
                                pe.wait_ge(s["z_raw"], m)
                            elif out_cols is not None:
                                pe.wait_ge(s["res_done"], DK)
                            for k in range(DK):
                                mm = nc.tensor.matmul(Z_BANK[:, 0:GT], w_in[f][:, k, INNER + m * P:INNER + (m + 1) * P],
                                                      norm.out[:, k, :], start=(k == 0), stop=(k == DK - 1))
                            mm.then_inc(s["z_mm"], 1)
                        if i == XP_MM:
                            pe.wait_ge(s["xc_done"], IB)
                            pe.wait_ge(s["conv_step"], TAPS * IB)
                            for k in range(IB):
                                mm = nc.tensor.matmul(X_BANK[0:DT0 + R, 0:GT], w_xp[f][:, k, :], xc[f][:, k, :],
                                                      start=(k == 0), stop=(k == IB - 1))
                            mm.then_inc(s["xp_done"], 1)
                        if i in DT_MM:
                            m = DT_MM.index(i)
                            if m == 0:
                                pe.wait_ge(s["dt_in_done"], 1)
                                pe.wait_ge(s["z_raw"], IB)
                            elif m == 1:
                                pe.wait_ge(s["rest_done"], 1)
                            else:
                                pe.wait_ge(s["step_done"], m - 1)
                            nc.tensor.matmul((Z_BANK, X_BANK)[m % 2][:, 0:GT], w_dt[f][:, m * P:(m + 1) * P], dt_in[:, :],
                                             start=True, stop=True).then_inc(s["dt_mm"], 1)

                    if rec:
                        spread_b(0)
                        spread_b(1)
                        spread_c(0)
                        spread_c(1)
                    beside(-1)
                    for i in range(STEPS):
                        q, n, j = recurrence(i)
                        if rec:
                            if q == 0:
                                spread_b(2 + i)
                            pe.wait_ge(s["hc_done"], i + 1)
                            if n == 0 and j >= JS:
                                pe.wait_ge(s["y_done"], j - JS + 1)
                            nc.tensor.matmul(Y_BANK[j % JS][:, 0:GT], c["ident"][:, :], hc[:, i % NB, :],
                                             start=(n == 0), stop=(n == S - 1)).then_inc(s["y_mm"], 1)
                            if i % JS == JS - 1:
                                if q + 4 < STEPS // JS:
                                    spread_b(q + 4)
                                if q + 2 < STEPS // JS:
                                    spread_c(q + 2)
                        beside(i)

                @block.scalar
                def _(act):
                    def input_row(q):
                        act.wait_ge(s["b_mm"], q + 1)
                        if q >= CB:
                            act.wait_ge(s["dbu_pool"], pool_upto[JS * (q - CB + 1) - 1])
                            act.wait_ge(s["dbu_dve"], dve_upto[JS * (q - CB + 1) - 1])
                        nc.scalar.activation(bc[:, q % CB, :], B_BANK[q % 2][:, 0:GT], ACT.Copy).then_inc(s["bc_done"], 1)

                    def beside(i):
                        if norm_in is not None and i == SQUARE:
                            act.wait_ge(norm.centred_ready, 1)
                            nc.scalar.activation(norm.square[:, :, :], norm.centred[:, :, :], ACT.Square)\
                                .then_inc(norm.square_ready, 1)
                        if norm_in is not None and i == RSTD:
                            act.wait_ge(norm.var_ready, 1)
                            nc.scalar.activation(norm.log_var[:, :], norm.var_ps[:, 0:GT], ACT.Ln, bias=c["eps"][:, 0:1])\
                                .then_inc(norm.log_ready, 1)
                            act.wait_ge(norm.log_ready, 1)
                            nc.scalar.activation(norm.rstd[:, :], norm.log_var[:, :], ACT.Exp, scale=-0.5)\
                                .then_inc(norm.rstd_ready, 1)
                        if not front:
                            return
                        if i in Z_RAW:
                            m = Z_RAW.index(i)
                            act.wait_ge(s["z_mm"], m + 1)
                            nc.scalar.activation(z[f][:, m, :], Z_BANK[:, 0:GT], ACT.Copy).then_inc(s["z_raw"], 1)
                        if i in XC:
                            m0 = XC.index(i) * IB // 2
                            act.wait_ge(s["conv_step"], TAPS * (m0 + IB // 2))
                            nc.scalar.activation(xc[f][:, m0:m0 + IB // 2, :], conv[:, m0:m0 + IB // 2, :], ACT.Silu)\
                                .then_inc(s["xc_done"], IB // 2)
                            nc.scalar.preload_act_table_set(EXP_LN)
                        if i == Z_SILU:
                            act.wait_ge(s["z_raw"], IB)
                            nc.scalar.activation(z[f][:, :, :], z[f][:, :, :], ACT.Silu).then_inc(s["z_done"], IB)
                            nc.scalar.preload_act_table_set(EXP_LN)
                        if i == HI:
                            act.wait_ge(s["xp_done"], 1)
                            nc.scalar.activation(dt_in[0:R, :], X_BANK[DT0:DT0 + R, 0:GT], ACT.Copy).then_inc(s["dt_in_done"], 1)
                            nc.scalar.activation(parts[f][:, :], X_BANK[0:DT0, 0:GT], ACT.Copy).then_inc(s["hi_done"], 1)
                        if i == MID:
                            act.wait_ge(s["rest_done"], 1)
                            nc.scalar.activation(parts[f][0:2 * BC, :], rest[0:2 * BC, :], ACT.Copy).then_inc(s["mid_done"], 1)
                        if i in SOFTPLUS:
                            m = SOFTPLUS.index(i)
                            act.wait_ge(s["dt_mm"], m + 1)
                            nc.scalar.activation(mag[:, m % 2, :], (Z_BANK, X_BANK)[m % 2][:, 0:GT], ACT.Abs).then_inc(s["mag_done"], 1)
                            act.wait_ge(s["mag_done"], m + 1)
                            nc.scalar.activation(mag[:, m % 2, :], mag[:, m % 2, :], ACT.Exp, scale=-1.0).then_inc(s["ea_done"], 1)
                            act.wait_ge(s["ea_done"], m + 1)
                            nc.scalar.activation(step[f][:, m, :], mag[:, m % 2, :], ACT.Ln, bias=one[:, 0:1]).then_inc(s["sp_done"], 1)

                    nc.scalar.preload_act_table_set(EXP_LN)
                    for i in range(STEPS):
                        q, n, j = recurrence(i)
                        if rec:
                            if i == 0:
                                input_row(0)
                            if i % JS == 0 and i // JS + 1 < STEPS // JS:
                                input_row(i // JS + 1)
                            if i >= NB:
                                act.wait_ge(s["scan_done"], i - NB + 1)
                            lo = 1 if d == 0 else 0
                            nc.scalar.activation(rows(dA[d][:, i % NB, :])[:, :, lo:lo + N - 1],
                                                 rows(step[d][:, j, :])[:, :, lo:lo + N - 1], ACT.Exp,
                                                 scale=decay[d][:, j, n:n + 1]).then_inc(s["dA_done"], 1)
                        beside(i)

                @block.gpsimd
                def _(pool):
                    for i in range(STEPS):
                        q, n, j = recurrence(i)
                        if rec and by_pool(i):
                            pool.wait_ge(s["bc_done"], q + 1)
                            if i >= NB:
                                pool.wait_ge(s["scan_done"], i - NB + 1)
                            nc.gpsimd.tensor_tensor(dBu[:, i % NB, :], du[d][:, j, :], bc[:, q % CB, :], ALU.mult)\
                                .then_inc(s["dbu_pool"], 1)

                @block.vector
                def _(dve):
                    def input_term(i):
                        q, n, j = recurrence(i)
                        dve.wait_ge(s["bc_done"], q + 1)
                        if i >= NB:
                            dve.wait_ge(s["scan_done"], i - NB + 1)
                        nc.vector.tensor_tensor(dBu[:, i % NB, :], du[d][:, j, :], bc[:, q % CB, :], ALU.mult)\
                            .then_inc(s["dbu_dve"], 1)

                    def recur(i):
                        if not by_pool(i):
                            dve.wait_ge(s["dbu_dve"], dve_upto[i])
                        else:
                            dve.wait_ge(s["dbu_pool"], pool_upto[i])
                        dve.wait_ge(s["dA_done"], i + 1)
                        if i >= NB:
                            dve.wait_ge(s["hc_done"], i - NB + 1)
                        nc.vector.tensor_tensor_scan(flow(hs[:, i % NB, :], d), flow(dA[d][:, i % NB, :], d),
                                                     flow(dBu[:, i % NB, :], d), 0.0, ALU.mult, ALU.add).then_inc(s["scan_done"], 1)

                    def output_term(i):
                        q, n, j = recurrence(i)
                        dve.wait_ge(s["scan_done"], i + 1)
                        dve.wait_ge(s["c_mm"], q + 1)
                        if i >= NB:
                            dve.wait_ge(s["y_mm"], i - NB + 1)
                        nc.vector.tensor_tensor(hc[:, i % NB, :], hs[:, i % NB, :], C_BANK[q % 2][:, 0:GT], ALU.mult)\
                            .then_inc(s["hc_done"], 1)

                    def tap(m, t):
                        if t == 0:
                            dve.wait_ge(s["x_mm"], m + 1)
                            nc.vector.tensor_scalar(conv[:, m, :], X_BANK[:, 0:GT], conv_w[f][:, m, TAPS - 1:TAPS],
                                                    conv_b[f][:, m:m + 1], ALU.mult, ALU.add).then_inc(s["conv_step"], 1)
                            return
                        src, dst = rows(X_BANK[:, 0:GT]), rows(conv[:, m, :])
                        src, dst = ((src[:, :, 0:N - t], dst[:, :, t:N]) if f == 0 else
                                    (src[:, :, t:N], dst[:, :, 0:N - t]))
                        dve.wait_ge(s["conv_step"], TAPS * m + t)
                        nc.vector.scalar_tensor_tensor(out=dst, in0=src, scalar=conv_w[f][:, m, TAPS - 1 - t:TAPS - t],
                                                       in1=dst, op0=ALU.mult, op1=ALU.add).then_inc(s["conv_step"], 1)

                    def beside(i):
                        if norm_in is not None and i == CENTRE:
                            dve.wait_ge(norm.mean_ready, 1)
                            nc.vector.tensor_tensor(norm.centred[:, :, :], h[:, :, norm_in],
                                                    norm.mean_ps[:, 0:GT].unsqueeze(1).to_broadcast([P, DK, GT]),
                                                    ALU.subtract).then_inc(norm.centred_ready, 1)
                        if norm_in is not None and i == SCALE:
                            dve.wait_ge(norm.rstd_ready, 1)
                            dve.wait_ge(norm.centred_ready, 1)
                            nc.vector.tensor_tensor(norm.out[:, :, :], norm.centred[:, :, :],
                                                    norm.rstd[:, :].unsqueeze(1).to_broadcast([P, DK, GT]),
                                                    ALU.mult).then_inc(norm.ready, 1)
                        if out_cols is not None and i in RES:
                            m = RES.index(i)
                            dve.wait_ge(s["o_mm"], m + 1)
                            nc.vector.tensor_tensor(h[:, m, out_cols], Z_BANK[:, 0:GT], h[:, m, out_cols], ALU.add)\
                                .then_inc(s["res_done"], 1)
                        if not front:
                            return
                        for m in range(IB):
                            if CONV[m] <= i < CONV[m] + TAPS:
                                tap(m, i - CONV[m])
                        if i == REST:
                            dve.wait_ge(s["hi_done"], 1)
                            nc.vector.tensor_tensor(rest[:, :], X_BANK[0:DT0, 0:GT], parts[f][:, :], ALU.subtract)\
                                .then_inc(s["rest_done"], 1)
                        if i == LO:
                            dve.wait_ge(s["mid_done"], 1)
                            nc.vector.tensor_tensor(parts[f][0:BC, :], rest[0:BC, :], parts[f][0:BC, :], ALU.subtract)\
                                .then_inc(s["lo_done"], 1)
                        if i in STEP:
                            m = STEP.index(i)
                            dve.wait_ge(s["sp_done"], m + 1)
                            nc.vector.scalar_tensor_tensor(out=step[f][:, m, :], in0=(Z_BANK, X_BANK)[m % 2][:, 0:GT], scalar=0.0,
                                                           in1=step[f][:, m, :], op0=ALU.max, op1=ALU.add).then_inc(s["step_done"], 1)
                        if i in DU:
                            m = DU.index(i)
                            dve.wait_ge(s["step_done"], m + 1)
                            dve.wait_ge(s["xc_done"], IB)
                            nc.vector.tensor_tensor(du[f][:, m, :], step[f][:, m, :], xc[f][:, m, :], ALU.mult)\
                                .then_inc(s["du_done"], 1)

                    def collect(j):
                        dve.wait_ge(s["y_mm"], STEPS // IB * JS * (j // JS + 1) - JS + j % JS + 1)
                        if j >= JS:
                            dve.wait_ge(s["yz_done"], j - JS + 1)
                        elif out_cols is not None:
                            dve.wait_ge(s["o_mm"], DK)
                        nc.vector.scalar_tensor_tensor(out=y[:, j % JS, :], in0=xc[d][:, j, :], scalar=skip[d][:, j:j + 1],
                                                       in1=Y_BANK[j % JS][:, 0:GT], op0=ALU.mult, op1=ALU.add).then_inc(s["y_done"], 1)

                    def gate(j):
                        dve.wait_ge(s["y_done"], j + 1)
                        nc.vector.tensor_tensor(yz[:, j, :], y[:, j % JS, :], z[d][:, j, :], ALU.mult).then_inc(s["yz_done"], 1)

                    if rec:
                        input_term(0)
                    for i in range(STEPS):
                        if rec:
                            recur(i)
                            if i + 1 < STEPS and not by_pool(i + 1):
                                input_term(i + 1)
                            if i:
                                output_term(i - 1)
                            for j in range(JS):
                                if i == STEPS // 2 + 1 + j:
                                    collect(j)
                                if i == STEPS // 2 + 2 + j:
                                    gate(j)
                        beside(i)
                    if rec:
                        output_term(STEPS - 1)
                        for j in range(JS, IB):
                            collect(j)
                        for j in range(JS, IB):
                            gate(j)

            st.clear()

        def both(g, before, after):
            half(0, True, True, None, group_cols(g - 1) if before else None)
            half(1, True, after, group_cols(g + 1) if after else None, group_cols(g))

        half(1, False, True, group_cols(0), None)
        both(0, False, True)
        with nc.Fori(1, GROUPS - 1) as g:
            both(g, True, True)
        both(GROUPS - 1, True, False)
        half(0, False, False, None, group_cols(GROUPS - 1))


def l1_ffn(nc, h, c, w_fc, w_proj, u_t, v, fast_b, gate):
    HID, RANK = w_fc.shape[0], v.shape[0]
    HB = HID // P
    with Stage(nc, "l1f") as st:
        ps = [st.psum(f"ps{i}") for i in range(8)]
        wfcT = st.sbuf("wfcT", [P, DK, HID])
        wprojT = st.sbuf("wprojT", [P, HB, D])
        with Stage(nc, "l1w") as sw:
            raw = {"fc": sw.sbuf("raw_fc", [P, HB, D]), "proj": sw.sbuf("raw_proj", [P, DK, HID])}
            mag = {"fc": sw.sbuf("mag_fc", [P, HB]), "proj": sw.sbuf("mag_proj", [P, DK])}
            pos = sw.sbuf("pos", [P, HB * D])
            neg = sw.sbuf("neg", [P, HB * D])
            uT = sw.sbuf("uT", [RANK, HID])
            vs = sw.sbuf("vs", [RANK, D])
            fb = sw.sbuf("fb", [RANK, RANK])
            gt = sw.sbuf("gt", [RANK, 1])
            low = sw.sbuf("low", [RANK, HID])
            thr = {"fc": sw.sbuf("thr_fc", [P, HB]), "proj": sw.sbuf("thr_proj", [P, DK])}
            loaded, step, low_mm, low_ready, tern, turned, copied = (
                sw.sem(x) for x in ("loaded", "step", "low_mm", "low_ready", "tern", "turned", "copied"))
            with nc.Block() as block:
                @block.sync
                def _(sp):
                    sp.dma_start(raw["fc"][:, :, :], w_fc.rearrange("(m p) d -> p m d", p=P)).then_inc(loaded, 16)
                    sp.dma_start(raw["proj"][:, :, :], w_proj.rearrange("(m p) d -> p m d", p=P)).then_inc(loaded, 16)
                    sp.dma_start(uT[:, :], u_t).then_inc(loaded, 16)
                    sp.dma_start(vs[:, :], v).then_inc(loaded, 16)
                    sp.dma_start(fb[:, :], fast_b).then_inc(loaded, 16)
                    sp.dma_start(gt[:, :], gate.to_broadcast([RANK, 1])).then_inc(loaded, 16)

                @block.vector
                def _(dve):
                    dve.wait_ge(loaded, 96)
                    n = 0
                    for w, rows, cols in (("fc", HB, D), ("proj", DK, HID)):
                        W, pv = raw[w], pos[:, 0:rows * cols].rearrange("p (m d) -> p m d", m=rows)
                        nv = neg[:, 0:rows * cols].rearrange("p (m d) -> p m d", m=rows)
                        nc.vector.scalar_tensor_tensor(out=pv, in0=W[:, :, :], scalar=-1.0, in1=W[:, :, :],
                                                       op0=ALU.mult, op1=ALU.max).then_inc(step, 1)
                        dve.wait_ge(step, n + 1)
                        nc.vector.tensor_reduce(thr[w][:, :], pv, AX.X, ALU.add).then_inc(step, 1)
                        dve.wait_ge(step, n + 2)
                        nc.vector.tensor_scalar(mag[w][:, :], thr[w][:, :], 1.0 / cols, 1e-5, ALU.mult, ALU.max)\
                            .then_inc(step, 1)
                        dve.wait_ge(step, n + 3)
                        nc.vector.tensor_scalar(thr[w][:, :], mag[w][:, :], 0.5, None, ALU.mult).then_inc(step, 1)
                        dve.wait_ge(step, n + 4)
                        wide = thr[w][:, :].unsqueeze(2).to_broadcast([P, rows, cols])
                        nc.vector.tensor_tensor(pv, W[:, :, :], wide, ALU.is_gt).then_inc(step, 1)
                        nc.vector.scalar_tensor_tensor(out=nv, in0=W[:, :, :], scalar=-1.0, in1=wide,
                                                       op0=ALU.mult, op1=ALU.is_gt).then_inc(step, 1)
                        dve.wait_ge(step, n + 6)
                        nc.vector.tensor_tensor(pv, pv, nv, ALU.subtract).then_inc(step, 1)
                        dve.wait_ge(step, n + 7)
                        nc.vector.tensor_tensor(nv, pv, W[:, :, :], ALU.subtract).then_inc(step, 1)
                        dve.wait_ge(step, n + 8)
                        nc.vector.tensor_tensor(nv, W[:, :, :], nv, ALU.add).then_inc(step, 1)
                        dve.wait_ge(step, n + 9)
                        nc.vector.tensor_tensor(W[:, :, :], nv, mag[w][:, :].unsqueeze(2).to_broadcast([P, rows, cols]),
                                                ALU.mult).then_inc(tern, 1)
                        dve.wait_ge(tern, 1 if w == "fc" else 2)
                        n += 9
                    for j in range(2):
                        dve.wait_ge(low_mm, j + 1)
                        nc.vector.tensor_scalar(low[:, j * 512:(j + 1) * 512], ps[j][0:RANK, :], gt[:, 0:1], None,
                                                ALU.mult).then_inc(low_ready, 1)
                    for i in range(HB + DK * HB // 4):
                        dve.wait_ge(turned, i + 1)
                        bank = ps[2 + i % 6]
                        if i < HB:
                            dst = wfcT[:, i // 4, (i % 4) * 256:(i % 4) * 256 + 256]
                            nc.vector.tensor_copy(dst, bank[:, 0:256]).then_inc(copied, 1)
                        else:
                            m = i - HB
                            nc.vector.tensor_copy(wprojT[:, 2 * m:2 * m + 2, :].rearrange("p a d -> p (a d)"),
                                                  bank[:, :]).then_inc(copied, 1)

                @block.tensor
                def _(pe):
                    pe.wait_ge(loaded, 96)
                    for j in range(2):
                        nc.tensor.matmul(ps[j][0:RANK, :], fb[:, :], uT[:, j * 512:(j + 1) * 512],
                                         start=True, stop=True).then_inc(low_mm, 1)
                    pe.wait_ge(low_ready, 2)
                    pe.wait_ge(tern, 1)
                    for i in range(HB):
                        if i >= 6:
                            pe.wait_ge(copied, i - 5)
                        k, q = i // 4, i % 4
                        for j in range(2):
                            m = 2 * q + j
                            out = ps[2 + i % 6][:, j * P:(j + 1) * P]
                            nc.tensor.matmul(out, raw["fc"][:, m, k * P:(k + 1) * P], c["ident"][:, :], start=True, stop=False)
                            mm = nc.tensor.matmul(out, vs[:, k * P:(k + 1) * P], low[:, m * P:(m + 1) * P],
                                                  start=False, stop=True)
                        mm.then_inc(turned, 1)
                    pe.wait_ge(tern, 2)
                    for i in range(HB, HB + DK * HB // 4):
                        pe.wait_ge(copied, i - 5)
                        for j in range(4):
                            kb, m = 2 * (i - HB) + j // 2, j % 2
                            mm = nc.tensor.matmul(ps[2 + i % 6][:, j * P:(j + 1) * P], raw["proj"][:, m, kb * P:(kb + 1) * P],
                                                  c["ident"][:, :], start=True, stop=True)
                        mm.then_inc(turned, 1)
            sw.clear()

        norm = Norm(st, ps[0], ps[1])
        relu = st.sbuf("relu", [P, HB, GT])
        act2 = st.sbuf("act2", [P, HB, GT])
        fc_done, relu_done, sq_done, proj_done, res_done = (
            st.sem(x) for x in ("fc_done", "relu_done", "sq_done", "proj_done", "res_done"))
        with nc.Fori(0, GROUPS) as g:
            with nc.Block(no_gpsimd_drain=True) as block:
                @block.tensor
                def _(pe):
                    norm.tensor_mean(nc, pe, c["ones"], lambda k: h[:, k, group_cols(g)])
                    norm.tensor_var(nc, pe, c["ones"])
                    pe.wait_ge(norm.ready, 1)
                    for m in range(HB):
                        if m >= 4:
                            pe.wait_ge(relu_done, m - 3)
                        for k in range(DK):
                            mm = nc.tensor.matmul(ps[2 + m % 4][:, 0:GT], wfcT[:, k, m * P:(m + 1) * P], norm.out[:, k, :],
                                                  start=(k == 0), stop=(k == DK - 1))
                        mm.then_inc(fc_done, 1)
                    for j in range(DK):
                        for m in range(HB):
                            if j == 0:
                                pe.wait_ge(sq_done, m + 1)
                            mm = nc.tensor.matmul(ps[6 + j][:, 0:GT], wprojT[:, m, j * P:(j + 1) * P], act2[:, m, :],
                                                  start=(m == 0), stop=(m == HB - 1))
                        mm.then_inc(proj_done, 1)

                @block.scalar
                def _(act):
                    norm.scalar(nc, act, c["eps"])
                    for m in range(HB):
                        act.wait_ge(fc_done, m + 1)
                        nc.scalar.activation(relu[:, m, :], ps[2 + m % 4][:, 0:GT], ACT.Relu).then_inc(relu_done, 1)

                @block.vector
                def _(dve):
                    norm.vector(nc, dve, h[:, :, group_cols(g)])
                    for m in range(HB):
                        dve.wait_ge(relu_done, m + 1)
                        nc.vector.tensor_tensor(act2[:, m, :], relu[:, m, :], relu[:, m, :], ALU.mult).then_inc(sq_done, 1)
                    for j in range(DK):
                        dve.wait_ge(proj_done, j + 1)
                        nc.vector.tensor_tensor(h[:, j, group_cols(g)], h[:, j, group_cols(g)], ps[6 + j][:, 0:GT],
                                                ALU.add).then_inc(res_done, 1)
            st.clear()


def l2_ffn(nc, h, c, wr, br, w1, b1, w2, b2, row_expert):
    E = wr.shape[1]
    HID = w1.shape[3]
    HB = HID // P
    with Stage(nc, "ex2") as st:
        ps = [st.psum(f"ps{i}") for i in range(8)]
        normed = st.sbuf("normed", [P, DK, T])
        means = st.sbuf("means", [P, DK, B])
        with Stage(nc, "rt2") as sr:
            norm = Norm(sr, ps[0], ps[1])
            kept, summed = sr.sem("kept"), sr.sem("summed")
            with nc.Fori(0, GROUPS) as g:
                with nc.Block(no_gpsimd_drain=True) as block:
                    @block.tensor
                    def _(pe):
                        norm.tensor_mean(nc, pe, c["ones"], lambda k: h[:, k, group_cols(g)])
                        norm.tensor_var(nc, pe, c["ones"])

                    @block.scalar
                    def _(act):
                        nc.scalar.preload_act_table_set(EXP_LN)
                        norm.scalar(nc, act, c["eps"])
                        act.wait_ge(norm.ready, 1)
                        nc.scalar.activation(normed[:, :, group_cols(g)], norm.out[:, :, :], ACT.Copy).then_inc(kept, 1)

                    @block.vector
                    def _(dve):
                        norm.vector(nc, dve, h[:, :, group_cols(g)])
                        dve.wait_ge(norm.ready, 1)
                        nc.vector.tensor_reduce(means[:, :, bass.ds(g * GB, GB)],
                                                norm.out[:, :, :].rearrange("p k (b n) -> p k b n", n=N), AX.X, ALU.add)\
                            .then_inc(summed, 1)
                sr.clear()
            w_r = sr.sbuf("w_r", [P, DK, E])
            b_r = sr.sbuf("b_r", [B, E])
            score = sr.sbuf("score", [B, E])
            top = sr.sbuf("top", [B, 8])
            best = sr.sbuf("best", [B, 8], U32)
            loaded, mean_ready, score_mm, score_done, top_done, best_done, sent = (
                sr.sem(x) for x in ("loaded", "mean_ready", "score_mm", "score_done", "top_done", "best_done", "sent"))
            with nc.Block() as block:
                @block.sync
                def _(sp):
                    sp.dma_start(w_r[:, :, :], wr.rearrange("(k p) e -> p k e", p=P)).then_inc(loaded, 16)
                    sp.dma_start(b_r[:, :], br.to_broadcast([B, E])).then_inc(loaded, 16)
                    sp.wait_ge(best_done, 1)
                    sp.dma_start(row_expert, best[:, 0:1]).then_inc(sent, 16)
                    sp.wait_ge(sent, 16)

                @block.vector
                def _(dve):
                    nc.vector.tensor_scalar(means[:, :, :], means[:, :, :], 1.0 / N, None, ALU.mult).then_inc(mean_ready, 1)
                    dve.wait_ge(score_mm, 1)
                    dve.wait_ge(loaded, 32)
                    nc.vector.tensor_tensor(score[:, :], ps[0][0:B, 0:E], b_r[:, :], ALU.add).then_inc(score_done, 1)
                    dve.wait_ge(score_done, 1)
                    nc.vector.max(top[:, :], score[:, :]).then_inc(top_done, 1)
                    dve.wait_ge(top_done, 1)
                    nc.vector.max_index(best[:, :], top[:, :], score[:, :]).then_inc(best_done, 1)

                @block.tensor
                def _(pe):
                    pe.wait_ge(loaded, 32)
                    pe.wait_ge(mean_ready, 1)
                    for k in range(DK):
                        mm = nc.tensor.matmul(ps[0][0:B, 0:E], means[:, k, :], w_r[:, k, :], start=(k == 0), stop=(k == DK - 1))
                    mm.then_inc(score_mm, 1)
            sr.clear()

        WB = GB
        W1 = [st.sbuf(f"w1_{i}", [P, DK, HID]) for i in range(WB)]
        W2 = [st.sbuf(f"w2_{i}", [P, HB, D]) for i in range(WB)]
        B1 = [st.sbuf(f"b1_{i}", [P, HB]) for i in range(WB)]
        B2 = [st.sbuf(f"b2_{i}", [P, DK]) for i in range(WB)]
        ids = st.sbuf("ids", [1, B + 1], U32)
        hid = st.sbuf("hid", [P, 2, HB, N])
        x_in = st.sbuf("x_in", [P, DK, GT])
        id_in = st.sem("id_in")
        landed = [st.sem(f"landed{i}") for i in range(WB)]
        x_done, up_done, relu_done, down_done, res_done = (
            st.sem(x) for x in ("x_done", "up_done", "relu_done", "down_done", "res_done"))

        def fetch(sp, row, i):
            e = nc.sync.value_load(ids[0:1, bass.ds(row, 1)], min_val=0, max_val=E - 1)
            for dst, src in ((W1[i][:, :, :], w1[bass.ds(e, 1), :, :, :]), (W2[i][:, :, :], w2[bass.ds(e, 1), :, :, :]),
                             (B1[i][:, :], b1[bass.ds(e, 1), :, :]), (B2[i][:, :], b2[bass.ds(e, 1), :, :])):
                names = "e p k n -> (e p) k n" if len(src.shape) == 4 else "e p n -> (e p) n"
                sp.dma_start(dst, src.rearrange(names)).then_inc(landed[i], 16)

        with nc.Block() as block:
            @block.sync
            def _(sp):
                sp.dma_start(ids[0:1, 0:B], row_expert.rearrange("b a -> a b")).then_inc(id_in, 16)
                sp.dma_start(ids[0:1, B:B + 1], row_expert[0:1, :]).then_inc(id_in, 16)
                sp.wait_ge(id_in, 32)
                fetch(sp, 0, 0)
                sp.wait_ge(landed[0], 64)
        st.clear()
        with nc.Fori(0, GROUPS) as g:
            with nc.Block(no_gpsimd_drain=True) as block:
                @block.sync
                def _(sp):
                    for i in range(1, WB):
                        fetch(sp, g * GB + i, i)
                    sp.wait_ge(down_done, DK)
                    sp.wait_ge(res_done, DK)
                    fetch(sp, g * GB + GB, 0)
                    sp.wait_ge(landed[0], 64)

                @block.tensor
                def _(pe):
                    pe.wait_ge(x_done, 1)
                    for i in range(GB):
                        if i:
                            pe.wait_ge(landed[i], 64)
                        for m in range(HB):
                            bank = ps[2 * (i % 2) + m // 4]
                            if m % 4 == 0 and i >= 2:
                                pe.wait_ge(relu_done, HB * (i - 2) + m + 4)
                            for k in range(DK):
                                mm = nc.tensor.matmul(bank[:, (m % 4) * N:(m % 4 + 1) * N], W1[i][:, k, m * P:(m + 1) * P],
                                                      x_in[:, k, i * N:(i + 1) * N], start=(k == 0), stop=(k == DK - 1))
                            if m % 4 == 3:
                                mm.then_inc(up_done, 1)
                        for j in range(DK):
                            if i >= 2:
                                pe.wait_ge(res_done, DK * (i - 2) + j + 1)
                            for m in range(HB):
                                if j == 0:
                                    pe.wait_ge(relu_done, HB * i + m + 1)
                                mm = nc.tensor.matmul(ps[4 + 2 * (i % 2) + j][:, 0:N], W2[i][:, m, j * P:(j + 1) * P],
                                                      hid[:, i % 2, m, :], start=(m == 0), stop=(m == HB - 1))
                            mm.then_inc(down_done, 1)

                @block.scalar
                def _(act):
                    nc.scalar.activation(x_in[:, :, :], normed[:, :, group_cols(g)], ACT.Copy).then_inc(x_done, 1)
                    for i in range(GB):
                        if i:
                            act.wait_ge(landed[i], 64)
                        if i >= 2:
                            act.wait_ge(down_done, DK * (i - 1))
                        for m in range(HB):
                            act.wait_ge(up_done, 2 * i + m // 4 + 1)
                            nc.scalar.activation(hid[:, i % 2, m, :], ps[2 * (i % 2) + m // 4][:, (m % 4) * N:(m % 4 + 1) * N],
                                                 ACT.Relu, bias=B1[i][:, m:m + 1]).then_inc(relu_done, 1)

                @block.vector
                def _(dve):
                    for i in range(GB):
                        if i:
                            dve.wait_ge(landed[i], 64)
                        for j in range(DK):
                            at = h[:, j, bass.ds(g * GT + i * N, N)]
                            dve.wait_ge(down_done, DK * i + j + 1)
                            nc.vector.scalar_tensor_tensor(out=at, in0=ps[4 + 2 * (i % 2) + j][:, 0:N], scalar=B2[i][:, j:j + 1],
                                                           in1=at, op0=ALU.add, op1=ALU.add).then_inc(res_done, 1)
            st.clear()


FAR = -1e38


def rwkv(nc, h, c, wk, wv, wr, ck, cv, cr, cols):
    HID = ck.shape[1]
    HB = HID // P
    NC = 11
    DECAY, FIRST, G1, B1, G2, B2, MK, MV, MR, CK, CR = range(NC)
    MIXES = (MK, MV, MR, CK, CR)
    with Stage(nc, "rw") as st:
        W = {x: st.sbuf(x, [P, DK, D]) for x in ("wk", "wv", "wr", "cr")}
        w_ck = st.sbuf("ck", [P, DK, HID])
        w_cv = st.sbuf("cv", [P, HB, D])
        col = st.sbuf("cols", [P, NC, DK])
        rest = st.sbuf("rest", [P, NC, DK])
        first_neg = st.sbuf("first_neg", [P, DK])
        ps = [st.psum(f"ps{i}") for i in range(8)]
        norms = [Norm(st, ps[0], ps[1], f"ln{i}") for i in range(3)]
        h1 = st.sbuf("h1", [P, DK, GT])
        back = st.sbuf("back", [P, 5, DK, GT])
        mixed = st.sbuf("mixed", [P, 5, DK, GT])
        drift = st.sbuf("drift", [P, DK, GB, N + 1])
        kp = st.sbuf("kp", [P, DK, GB, N + 1])
        v = st.sbuf("v", [P, DK, GT])
        Mp = st.sbuf("Mp", [P, DK, GB, N + 1])
        PPp = st.sbuf("PPp", [P, DK, GB, N + 1])
        AAp = st.sbuf("AAp", [P, DK, GB, N + 1])
        d1 = st.sbuf("d1", [P, DK, GT])
        d2 = st.sbuf("d2", [P, DK, GT])
        s_ = st.sbuf("s", [P, DK, GT])
        gate = st.sbuf("gate", [P, DK, GT])
        rg = st.sbuf("rg", [P, DK, GT])
        aa = st.sbuf("aa", [P, DK, GT])
        x2 = st.sbuf("x2", [P, DK, GT])
        relu = st.sbuf("relu", [P, 2, GT])
        act2 = st.sbuf("act2", [P, HB, GT])
        names = ("loaded", "set", "rested", "h1_done", "back_done", "mix_done", "k_mm", "v_mm", "r_mm", "k_done", "v_done",
                 "M_done", "d1_done", "d2_done", "a_done", "s_done", "ln_done", "pp_done", "dl_done", "min_done", "e_done",
                 "ev_done", "aa_done", "aap_done", "diff_done", "gate_done", "rg_done", "gd_done", "y_done", "ry_done", "x2_done", "h2_done",
                 "c_mm", "relu_done", "sq_done", "cr_mm", "cv_mm", "sig_done", "sk_done", "x3_done", "res_done")
        s = {x: st.sem(x) for x in names}
        with nc.Block() as block:
            @block.sync
            def _(sp):
                for dst, src in ((W["wk"], wk), (W["wv"], wv), (W["wr"], wr), (W["cr"], cr), (w_ck, ck), (w_cv, cv)):
                    sp.dma_start(dst[:, :, :], src.rearrange("(k p) n -> p k n", p=P)).then_inc(s["loaded"], 16)
                sp.dma_start(col[:, :, :], cols).then_inc(s["loaded"], 16)
                sp.wait_ge(s["loaded"], 112)

            @block.gpsimd
            def _(pool):
                nc.gpsimd.memset(back[:, :, :, :], 0.0)
                nc.gpsimd.memset(kp[:, :, :, :], 0.0)
                nc.gpsimd.memset(PPp[:, :, :, :], FAR)
                nc.gpsimd.memset(AAp[:, :, :, :], 0.0)
                nc.gpsimd.memset(drift[:, :, :, :], 0.0).then_inc(s["set"], 1)

            @block.vector
            def _(dve):
                dve.wait_ge(s["loaded"], 112)
                nc.vector.tensor_scalar(rest[:, :, :], col[:, :, :], -1.0, 1.0, ALU.mult, ALU.add).then_inc(s["rested"], 1)
                nc.vector.tensor_scalar(first_neg[:, :], col[:, FIRST, :], -1.0, None, ALU.mult).then_inc(s["rested"], 1)
                dve.wait_ge(s["set"], 1)
                for k in range(DK):
                    nc.vector.tensor_scalar(drift[:, k, :, 1:N + 1], drift[:, k, :, 1:N + 1], col[:, DECAY, k:k + 1], None,
                                            ALU.add).then_inc(s["rested"], 1)
                nc.vector.memset(drift[:, :, :, 0:1], FAR).then_inc(s["rested"], 1)

            @block.scalar
            def _(act):
                nc.scalar.preload_act_table_set(EXP_LN)
        st.clear()

        def rows(ap):
            return ap.rearrange("p (b n) -> p b n", n=N)

        def both(ap):
            return ap.rearrange("p k (b n) -> p k b n", n=N)

        with nc.Fori(0, GROUPS) as g:
            with nc.Block(no_gpsimd_drain=True) as block:
                @block.tensor
                def _(pe):
                    norms[0].tensor_mean(nc, pe, c["ones"], lambda k: h[:, k, group_cols(g)])
                    norms[0].tensor_var(nc, pe, c["ones"])
                    pe.wait_ge(norms[0].ready, 1)
                    norms[1].tensor_mean(nc, pe, c["ones"], lambda k: norms[0].out[:, k, :])
                    norms[1].tensor_var(nc, pe, c["ones"])
                    for i, (x, done) in enumerate((("wk", s["k_mm"]), ("wv", s["v_mm"]), ("wr", s["r_mm"]))):
                        pe.wait_ge(s["mix_done"], DK * (i + 1))
                        for m in range(DK):
                            for k in range(DK):
                                mm = nc.tensor.matmul(ps[2 + 2 * i + m][:, 0:GT], W[x][:, k, m * P:(m + 1) * P],
                                                      mixed[:, i, k, :], start=(k == 0), stop=(k == DK - 1))
                            mm.then_inc(done, 1)
                    pe.wait_ge(s["x2_done"], 1)
                    norms[2].tensor_mean(nc, pe, c["ones"], lambda k: x2[:, k, :])
                    norms[2].tensor_var(nc, pe, c["ones"])
                    pe.wait_ge(s["mix_done"], DK * 4)
                    pe.wait_ge(s["k_done"], DK)
                    pe.wait_ge(s["v_done"], DK)
                    for m in range(HB):
                        if m >= 4:
                            pe.wait_ge(s["relu_done"], m - 3)
                        for k in range(DK):
                            mm = nc.tensor.matmul(ps[2 + m % 4][:, 0:GT], w_ck[:, k, m * P:(m + 1) * P], mixed[:, 3, k, :],
                                                  start=(k == 0), stop=(k == DK - 1))
                        mm.then_inc(s["c_mm"], 1)
                    pe.wait_ge(s["mix_done"], DK * 5)
                    pe.wait_ge(s["rg_done"], DK)
                    for m in range(DK):
                        for k in range(DK):
                            mm = nc.tensor.matmul(ps[6 + m][:, 0:GT], W["cr"][:, k, m * P:(m + 1) * P], mixed[:, 4, k, :],
                                                  start=(k == 0), stop=(k == DK - 1))
                        mm.then_inc(s["cr_mm"], 1)
                    pe.wait_ge(norms[2].ready, 1)
                    for j in range(DK):
                        for m in range(HB):
                            pe.wait_ge(s["sq_done"], m + 1)
                            mm = nc.tensor.matmul(ps[j][:, 0:GT], w_cv[:, m, j * P:(j + 1) * P], act2[:, m, :],
                                                  start=(m == 0), stop=(m == HB - 1))
                        mm.then_inc(s["cv_mm"], 1)

                @block.scalar
                def _(act):
                    nc.scalar.preload_act_table_set(EXP_LN)
                    norms[0].scalar(nc, act, c["eps"])
                    norms[1].scalar(nc, act, c["eps"])

                    def shifted(i, mix, ready):
                        act.wait_ge(s["h1_done"] if i < 3 else s["h2_done"], ready)
                        for k in range(DK):
                            nc.scalar.activation(rows(back[:, i, k, :])[:, :, 1:N], rows(h1[:, k, :])[:, :, 0:N - 1],
                                                 ACT.Copy, scale=rest[:, mix, k:k + 1]).then_inc(s["back_done"], 1)

                    for i in range(3):
                        shifted(i, MIXES[i], DK)
                    for k in range(DK):
                        act.wait_ge(s["k_mm"], k + 1)
                        nc.scalar.activation(kp[:, k, :, 1:N + 1], rows(ps[2 + k][:, 0:GT]), ACT.Copy).then_inc(s["k_done"], 1)
                    for k in range(DK):
                        act.wait_ge(s["v_mm"], k + 1)
                        nc.scalar.activation(v[:, k, :], ps[4 + k][:, 0:GT], ACT.Copy).then_inc(s["v_done"], 1)
                    act.wait_ge(s["d1_done"], DK)
                    nc.scalar.activation(d1[:, :, :], d1[:, :, :], ACT.Exp).then_inc(s["a_done"], 1)
                    act.wait_ge(s["d2_done"], DK)
                    nc.scalar.activation(d2[:, :, :], d2[:, :, :], ACT.Exp).then_inc(s["a_done"], 1)
                    act.wait_ge(s["s_done"], DK)
                    nc.scalar.activation(aa[:, :, :], s_[:, :, :], ACT.Ln).then_inc(s["ln_done"], 1)
                    act.wait_ge(s["min_done"], 1)
                    nc.scalar.activation(d1[:, :, :], d1[:, :, :], ACT.Exp).then_inc(s["e_done"], 1)
                    act.wait_ge(s["min_done"], 2)
                    nc.scalar.activation(d2[:, :, :], d2[:, :, :], ACT.Exp).then_inc(s["e_done"], 1)
                    for k in range(DK):
                        act.wait_ge(s["r_mm"], k + 1)
                        nc.scalar.activation(rg[:, k, :], ps[6 + k][:, 0:GT], ACT.Sigmoid).then_inc(s["rg_done"], 1)
                    for k in range(DK):
                        nc.scalar.activation(gate[:, k, :], s_[:, k, :], ACT.Sigmoid, bias=first_neg[:, k:k + 1])\
                            .then_inc(s["gate_done"], 1)
                    nc.scalar.preload_act_table_set(EXP_LN)
                    norms[2].scalar(nc, act, c["eps"])
                    for i in range(3, 5):
                        shifted(i, MIXES[i], DK)
                    for m in range(HB):
                        act.wait_ge(s["c_mm"], m + 1)
                        if m >= 2:
                            act.wait_ge(s["sq_done"], m - 1)
                        nc.scalar.activation(relu[:, m % 2, :], ps[2 + m % 4][:, 0:GT], ACT.Relu).then_inc(s["relu_done"], 1)
                    for k in range(DK):
                        act.wait_ge(s["cr_mm"], k + 1)
                        nc.scalar.activation(rg[:, k, :], ps[6 + k][:, 0:GT], ACT.Sigmoid).then_inc(s["sig_done"], 1)

                @block.vector
                def _(dve):
                    x = norms[0].out
                    norms[0].vector(nc, dve, h[:, :, group_cols(g)])
                    dve.wait_ge(norms[0].ready, 1)
                    norms[1].vector(nc, dve, x[:, :, :])

                    def scaled(norm, gain, bias, done):
                        dve.wait_ge(norm.ready, 1)
                        for k in range(DK):
                            nc.vector.tensor_scalar(h1[:, k, :], norm.out[:, k, :], col[:, gain, k:k + 1],
                                                    col[:, bias, k:k + 1], ALU.mult, ALU.add).then_inc(done, 1)
                        dve.wait_ge(done, DK)

                    def mix(i):
                        for k in range(DK):
                            dve.wait_ge(s["back_done"], DK * i + k + 1)
                            nc.vector.scalar_tensor_tensor(out=mixed[:, i, k, :], in0=h1[:, k, :],
                                                           scalar=col[:, MIXES[i], k:k + 1], in1=back[:, i, k, :],
                                                           op0=ALU.mult, op1=ALU.add).then_inc(s["mix_done"], 1)

                    scaled(norms[1], G1, B1, s["h1_done"])
                    for i in range(3):
                        mix(i)
                    for k in range(DK):
                        dve.wait_ge(s["k_done"], k + 1)
                        nc.vector.tensor_tensor_scan(Mp[:, k, :, :].rearrange("p b n -> p (b n)"),
                                                     kp[:, k, :, :].rearrange("p b n -> p (b n)"),
                                                     drift[:, k, :, :].rearrange("p b n -> p (b n)"), FAR, ALU.max, ALU.add)\
                            .then_inc(s["M_done"], 1)
                    for k in range(DK):
                        dve.wait_ge(s["M_done"], k + 1)
                        nc.vector.scalar_tensor_tensor(out=rows(d1[:, k, :]), in0=Mp[:, k, :, 0:N], scalar=col[:, DECAY, k:k + 1],
                                                       in1=Mp[:, k, :, 1:N + 1], op0=ALU.add, op1=ALU.subtract)\
                            .then_inc(s["d1_done"], 1)
                        nc.vector.scalar_tensor_tensor(out=rows(d2[:, k, :]), in0=kp[:, k, :, 1:N + 1],
                                                       scalar=col[:, DECAY, k:k + 1],
                                                       in1=Mp[:, k, :, 1:N + 1], op0=ALU.add, op1=ALU.subtract)\
                            .then_inc(s["d2_done"], 1)
                    dve.wait_ge(s["a_done"], 2)
                    for k in range(DK):
                        nc.vector.tensor_tensor_scan(s_[:, k, :], d1[:, k, :], d2[:, k, :], 0.0, ALU.mult, ALU.add)\
                            .then_inc(s["s_done"], 1)
                    dve.wait_ge(s["ln_done"], 1)
                    nc.vector.tensor_tensor(PPp[:, 0, :, 1:N + 1], Mp[:, 0, :, 1:N + 1], rows(aa[:, 0, :]), ALU.add)\
                        .then_inc(s["pp_done"], 1)
                    nc.vector.tensor_tensor(PPp[:, 1, :, 1:N + 1], Mp[:, 1, :, 1:N + 1], rows(aa[:, 1, :]), ALU.add)\
                        .then_inc(s["pp_done"], 1)
                    for k in range(DK):
                        dve.wait_ge(s["pp_done"], k + 1)
                        nc.vector.tensor_tensor(rows(s_[:, k, :]), PPp[:, k, :, 0:N], kp[:, k, :, 1:N + 1], ALU.subtract)\
                            .then_inc(s["dl_done"], 1)
                    dve.wait_ge(s["dl_done"], DK)
                    nc.vector.tensor_scalar(d1[:, :, :], s_[:, :, :], 0.0, None, ALU.min).then_inc(s["min_done"], 1)
                    nc.vector.tensor_scalar(d2[:, :, :], s_[:, :, :], -1.0, 0.0, ALU.mult, ALU.min).then_inc(s["min_done"], 1)
                    dve.wait_ge(s["e_done"], 2)
                    dve.wait_ge(s["v_done"], DK)
                    nc.vector.tensor_tensor(d2[:, :, :], d2[:, :, :], v[:, :, :], ALU.mult).then_inc(s["ev_done"], 1)
                    dve.wait_ge(s["ev_done"], 1)
                    for k in range(DK):
                        nc.vector.tensor_tensor_scan(aa[:, k, :], d1[:, k, :], d2[:, k, :], 0.0, ALU.mult, ALU.add)\
                            .then_inc(s["aa_done"], 1)
                    for k in range(DK):
                        dve.wait_ge(s["aa_done"], k + 1)
                        nc.vector.tensor_copy(AAp[:, k, :, 1:N + 1], rows(aa[:, k, :])).then_inc(s["aap_done"], 1)
                    for k in range(DK):
                        dve.wait_ge(s["aap_done"], k + 1)
                        dve.wait_ge(s["aa_done"], DK)
                        nc.vector.tensor_tensor(rows(d1[:, k, :]), AAp[:, k, :, 0:N], rows(v[:, k, :]), ALU.subtract)\
                            .then_inc(s["diff_done"], 1)
                    dve.wait_ge(s["diff_done"], DK)
                    dve.wait_ge(s["gate_done"], DK)
                    nc.vector.tensor_tensor(d1[:, :, :], d1[:, :, :], gate[:, :, :], ALU.mult).then_inc(s["gd_done"], 1)
                    dve.wait_ge(s["gd_done"], 1)
                    nc.vector.tensor_tensor(d1[:, :, :], d1[:, :, :], v[:, :, :], ALU.add).then_inc(s["y_done"], 1)
                    dve.wait_ge(s["y_done"], 1)
                    dve.wait_ge(s["rg_done"], DK)
                    nc.vector.tensor_tensor(d1[:, :, :], d1[:, :, :], rg[:, :, :], ALU.mult).then_inc(s["ry_done"], 1)
                    dve.wait_ge(s["ry_done"], 1)
                    nc.vector.tensor_tensor(x2[:, :, :], d1[:, :, :], x[:, :, :], ALU.add).then_inc(s["x2_done"], 1)
                    dve.wait_ge(s["x2_done"], 1)
                    norms[2].vector(nc, dve, x2[:, :, :])
                    scaled(norms[2], G2, B2, s["h2_done"])
                    mix(3)
                    mix(4)
                    for m in range(HB):
                        dve.wait_ge(s["relu_done"], m + 1)
                        nc.vector.tensor_tensor(act2[:, m, :], relu[:, m % 2, :], relu[:, m % 2, :], ALU.mult)\
                            .then_inc(s["sq_done"], 1)
                    nc.vector.tensor_tensor(x2[:, :, :], x2[:, :, :], h[:, :, group_cols(g)], ALU.add).then_inc(s["x3_done"], 1)
                    for k in range(DK):
                        dve.wait_ge(s["sig_done"], k + 1)
                        dve.wait_ge(s["cv_mm"], k + 1)
                        nc.vector.tensor_tensor(d2[:, k, :], rg[:, k, :], ps[k][:, 0:GT], ALU.mult).then_inc(s["sk_done"], 1)
                        dve.wait_ge(s["sk_done"], k + 1)
                        dve.wait_ge(s["x3_done"], 1)
                        nc.vector.tensor_tensor(h[:, k, group_cols(g)], x2[:, k, :], d2[:, k, :], ALU.add).then_inc(s["res_done"], 1)
            st.clear()


def peer(nc, h, c, wq, keys_t, down_t, up, norm_w, out):
    HEADS, KEYS, TOP = keys_t.shape[1] // 2, keys_t.shape[2], 8
    CH = HEADS * TOP
    EB = KEYS // 2
    PB = 2
    PT = PB * N
    CHUNK = 512 // (PB * EB)
    CHUNKS = [(t, min(CHUNK, N - t)) for t in range(0, N, CHUNK)]
    SETS = 2 * HEADS
    STEPS = B // PB
    with Stage(nc, "peer_out") as so, Stage(nc, "peer") as st:
        out_sent = so.sem("out_sent")
        ps = [st.psum(f"ps{i}") for i in range(8)]
        kq = st.sbuf("kq", [P, DK, SETS * KEYS])
        down = st.sbuf("down", [P, DK, EB, P])
        w_up = st.sbuf("up", [P, EB, D])
        nw = st.sbuf("nw", [P, DK])
        ramp = st.sbuf("ramp", [P, P])
        eps6 = st.sbuf("eps6", [P, 1])
        with Stage(nc, "pkq") as sk:
            w_q = sk.sbuf("w_q", [P, SETS, D])
            keys = sk.sbuf("keys", [P, SETS, KEYS])
            loaded, set_, big_in, kq_mm, kq_done = (sk.sem(x) for x in ("loaded", "set", "big_in", "kq_mm", "kq_done"))
            with nc.Block() as block:
                @block.sync
                def _(sp):
                    sp.dma_start(w_q[:, :, :], wq.rearrange("(s p) d -> p s d", p=P)).then_inc(loaded, 16)
                    sp.dma_start(keys[:, :, :], keys_t).then_inc(loaded, 16)
                    sp.dma_start(nw[:, :], norm_w).then_inc(big_in, 16)
                    sp.dma_start(down[:, :, :, :], down_t).then_inc(big_in, 16)
                    sp.dma_start(w_up[:, :, :], up).then_inc(big_in, 16)
                    sp.wait_ge(big_in, 48)

                @block.gpsimd
                def _(pool):
                    nc.gpsimd.iota(ramp[:, :], pattern=[[1, P]], base=0, channel_multiplier=0,
                                   allow_small_or_imprecise_dtypes=True).then_inc(set_, 1)
                    nc.gpsimd.memset(eps6[:, :], 1e-6).then_inc(set_, 1)

                @block.tensor
                def _(pe):
                    pe.wait_ge(loaded, 32)
                    for m in range(DK):
                        for half in range(2):
                            for j in range(SETS // 2):
                                i = half * SETS // 2 + j
                                mm = nc.tensor.matmul(ps[2 * m + half][:, j * KEYS:(j + 1) * KEYS],
                                                      w_q[:, i, m * P:(m + 1) * P], keys[:, i, :], start=True, stop=True)
                            mm.then_inc(kq_mm, 1)

                @block.vector
                def _(dve):
                    for m in range(DK):
                        for half in range(2):
                            dve.wait_ge(kq_mm, 2 * m + half + 1)
                            nc.vector.tensor_copy(kq[:, m, half * 512:(half + 1) * 512], ps[2 * m + half][:, :])\
                                .then_inc(kq_done, 1)
            sk.clear()

        norm = Norm(st, ps[0], ps[0], "ln", PT)
        log2, rms = norm.log_var, norm.rstd
        xn = st.sbuf("xn", [P, DK, PT])
        hid = st.sbuf("hid", [P, EB, PT])
        weight = st.sbuf("weight", [P, EB, PB, N])
        top = st.sbuf("top", [N, PB, SETS, TOP])
        idx = st.sbuf("idx", [N, PB, SETS, TOP], U32)
        pair = st.sbuf("pair", [N, PB, HEADS, TOP, TOP])
        best = st.sbuf("best", [N, PB, HEADS, TOP])
        at = st.sbuf("at", [N, PB, HEADS, TOP], U32)
        at_hi = st.sbuf("at_hi", [N, PB * HEADS, TOP], U32)
        at_lo = st.sbuf("at_lo", [N, PB * HEADS, TOP], U32)
        hit1 = st.sbuf("hit1", [N, PB * HEADS, TOP, TOP])
        hit2 = st.sbuf("hit2", [N, PB * HEADS, TOP, TOP])
        i1 = st.sbuf("i1", [N, PB * HEADS, TOP])
        i2 = st.sbuf("i2", [N, PB * HEADS, TOP])
        i2u, odd = (st.sbuf(x, [N, PB * CH], U32) for x in ("i2u", "odd"))
        half_ = st.sbuf("half", [N, PB * CH], U32)
        codes = st.sbuf("codes", [N, 3, PB * CH])
        codesT = st.sbuf("codesT", [P, 3, N])
        HB = 3
        hot_rows = st.sbuf("hot_rows", [P, HB, CHUNK, P])
        hot_cols = st.sbuf("hot_cols", [P, HB, CHUNK, PB * EB])
        names = ("sq2", "ms_mm", "log2_done", "rms_done", "xn_done", "sim_mm", "top_done", "idx_done", "pair_done", "best_done", "at_done",
                 "split_done", "hit_done", "mul_done", "sel_done", "u_done", "bits_done", "code_done", "t_done", "ct_done",
                 "hid_mm", "gelu_done", "rows_done", "hot_done", "cols_done", "g_mm", "evac_done", "wgt_done", "up_mm", "res_done")
        s = {x: st.sem(x) for x in names}
        J = 2
        HU = EB // J
        NC = len(CHUNKS)

        def best_experts(dve):
            for b in range(PB):
                for i in range(SETS):
                    if i % HEADS == 0:
                        dve.wait_ge(s["sim_mm"], 2 * b + i // HEADS + 1)
                    nc.vector.max(top[:, b, i, :], ps[1 + 2 * b + i // HEADS][0:N, (i % HEADS) * KEYS:(i % HEADS + 1) * KEYS])\
                        .then_inc(s["top_done"], 1)
                for i in range(SETS):
                    dve.wait_ge(s["top_done"], SETS * b + i + 1)
                    nc.vector.max_index(idx[:, b, i, :], top[:, b, i, :],
                                        ps[1 + 2 * b + i // HEADS][0:N, (i % HEADS) * KEYS:(i % HEADS + 1) * KEYS])\
                        .then_inc(s["idx_done"], 1)
                sets = top[:, b, :, :].rearrange("p (h s) k -> p h s k", s=2)
                nc.vector.tensor_tensor(pair[:, b, :, :, :], sets[:, :, 0, :].unsqueeze(3).to_broadcast([N, HEADS, TOP, TOP]),
                                        sets[:, :, 1, :].unsqueeze(2).to_broadcast([N, HEADS, TOP, TOP]), ALU.add)\
                    .then_inc(s["pair_done"], 1)
                dve.wait_ge(s["pair_done"], b + 1)
                for i in range(HEADS):
                    nc.vector.max(best[:, b, i, :], pair[:, b, i, :, :].rearrange("p a k -> p (a k)")).then_inc(s["best_done"], 1)
                for i in range(HEADS):
                    dve.wait_ge(s["best_done"], HEADS * b + i + 1)
                    nc.vector.max_index(at[:, b, i, :], best[:, b, i, :], pair[:, b, i, :, :].rearrange("p a k -> p (a k)"))\
                        .then_inc(s["at_done"], 1)
            dve.wait_ge(s["at_done"], PB * HEADS)
            dve.wait_ge(s["idx_done"], PB * SETS)
            flat = at[:, :, :, :].rearrange("p b h k -> p (b h) k")
            nc.vector.tensor_scalar(at_hi[:, :, :], flat, 3, None, ALU.logical_shift_right).then_inc(s["split_done"], 1)
            nc.vector.tensor_scalar(at_lo[:, :, :], flat, 7, None, ALU.bitwise_and).then_inc(s["split_done"], 1)
            dve.wait_ge(s["split_done"], 2)
            shape = [N, PB * HEADS, TOP, TOP]
            ids = idx[:, :, :, :].rearrange("p b (h s) k -> p (b h) s k", s=2)
            steps = ramp[0:N, 0:TOP].unsqueeze(1).unsqueeze(1).to_broadcast(shape)
            for i, (hit, place) in enumerate(((hit1, at_hi), (hit2, at_lo))):
                nc.vector.tensor_tensor(hit[:, :, :, :], steps, place[:, :, :].unsqueeze(3).to_broadcast(shape), ALU.is_equal)\
                    .then_inc(s["hit_done"], 1)
            for i, hit in enumerate((hit1, hit2)):
                dve.wait_ge(s["hit_done"], i + 1)
                nc.vector.tensor_tensor(hit[:, :, :, :], hit[:, :, :, :], ids[:, :, i, :].unsqueeze(2).to_broadcast(shape),
                                        ALU.mult).then_inc(s["mul_done"], 1)
            for i, (hit, sel) in enumerate(((hit1, i1), (hit2, i2))):
                dve.wait_ge(s["mul_done"], i + 1)
                nc.vector.tensor_reduce(sel[:, :, :], hit[:, :, :, :], AX.X, ALU.add).then_inc(s["sel_done"], 1)
            dve.wait_ge(s["sel_done"], 2)
            nc.vector.tensor_copy(i2u[:, :], i2[:, :, :].rearrange("p h k -> p (h k)")).then_inc(s["u_done"], 1)
            dve.wait_ge(s["u_done"], 1)
            nc.vector.tensor_scalar(odd[:, :], i2u[:, :], 1, None, ALU.bitwise_and).then_inc(s["bits_done"], 1)
            nc.vector.tensor_scalar(half_[:, :], i2u[:, :], 1, None, ALU.logical_shift_right).then_inc(s["bits_done"], 1)
            dve.wait_ge(s["bits_done"], 2)
            nc.vector.scalar_tensor_tensor(out=codes[:, 0, :], in0=odd[:, :], scalar=float(KEYS),
                                           in1=i1[:, :, :].rearrange("p h k -> p (h k)"), op0=ALU.mult, op1=ALU.add)\
                .then_inc(s["code_done"], 1)
            for b in range(PB):
                nc.vector.tensor_scalar(codes[:, 1, b * CH:(b + 1) * CH], half_[:, b * CH:(b + 1) * CH], float(b * EB), None, ALU.add)\
                    .then_inc(s["code_done"], 1)
            nc.vector.tensor_scalar(codes[:, 2, :], best[:, :, :, :].rearrange("p b h k -> p (b h k)"), 0.0, None, ALU.max)\
                .then_inc(s["code_done"], 1)

        def step(front, back):
            with nc.Block(no_gpsimd_drain=True) as block:
                @block.sync
                def _(sp):
                    if back is not None:
                        sp.wait_ge(s["res_done"], DK)
                        sp.dma_start(out[:, :, back], h[:, :, back]).then_inc(out_sent, 16)

                @block.tensor
                def _(pe):
                    def hidden(i):
                        if i >= 3:
                            pe.wait_ge(s["gelu_done"], i - 2)
                        for jj in range(J):
                            for k in range(DK):
                                mm = nc.tensor.matmul(ps[1 + i % 3][:, jj * PT:(jj + 1) * PT], down[:, k, i * J + jj, :],
                                                      xn[:, k, :], start=(k == 0), stop=(k == DK - 1))
                        mm.then_inc(s["hid_mm"], 1)

                    def weights(ch):
                        pe.wait_ge(s["rows_done"], ch + 1)
                        pe.wait_ge(s["cols_done"], ch + 1)
                        if ch >= HB:
                            pe.wait_ge(s["evac_done"], ch - HB + 1)
                        for t in range(CHUNKS[ch][1]):
                            mm = nc.tensor.matmul(ps[4 + ch % HB][:, t * PB * EB:(t + 1) * PB * EB], hot_rows[:, ch % HB, t, :],
                                                  hot_cols[:, ch % HB, t, :], start=True, stop=True)
                        mm.then_inc(s["g_mm"], 1)

                    if front is not None:
                        norm.tensor_mean(nc, pe, c["ones"], lambda k: h[:, k, front])
                    if back is not None:
                        hidden(0)
                    if front is not None:
                        norm.tensor_var(nc, pe, c["ones"])
                    if back is not None:
                        hidden(1)
                        weights(0)
                    if front is not None:
                        pe.wait_ge(s["sq2"], 1)
                        for k in range(DK):
                            mm = nc.tensor.matmul(ps[0][:, 0:PT], c["ones"][:, :], norm.square[:, k, :],
                                                  start=(k == 0), stop=(k == DK - 1))
                        mm.then_inc(s["ms_mm"], 1)
                    if back is not None:
                        for i in range(2, HU):
                            hidden(i)
                            if i - 1 < NC:
                                weights(i - 1)
                        for ch in range(HU - 1, NC):
                            weights(ch)
                        pe.wait_ge(s["gelu_done"], HU)
                        pe.wait_ge(s["evac_done"], NC)
                    if front is not None:
                        pe.wait_ge(s["xn_done"], DK)
                        for b in range(PB):
                            for half in range(2):
                                for k in range(DK):
                                    mm = nc.tensor.matmul(ps[1 + 2 * b + half][0:N, :], xn[:, k, b * N:(b + 1) * N],
                                                          kq[:, k, half * 512:(half + 1) * 512], start=(k == 0), stop=(k == DK - 1))
                                mm.then_inc(s["sim_mm"], 1)
                    if back is not None:
                        for m in range(DK):
                            for j in range(EB):
                                if m == 0 and j % J == 0:
                                    pe.wait_ge(s["wgt_done"], j // J + 1)
                                mm = nc.tensor.matmul(ps[5 + m][:, 0:PT], w_up[:, j, m * P:(m + 1) * P], hid[:, j, :],
                                                      start=(j == 0), stop=(j == EB - 1))
                            mm.then_inc(s["up_mm"], 1)
                    if front is not None:
                        pe.wait_ge(s["code_done"], 4)
                        for i in range(3):
                            mm = nc.tensor.transpose(ps[7][:, i * N:(i + 1) * N], codes[:, i, :], c["ident"][0:N, 0:N])
                        mm.then_inc(s["t_done"], 1)

                @block.scalar
                def _(act):
                    if front is not None:
                        nc.scalar.preload_act_table_set(EXP_LN)
                        norm.scalar(nc, act, c["eps"])
                        act.wait_ge(norm.ready, 1)
                        nc.scalar.activation(norm.square[:, :, :], norm.out[:, :, :], ACT.Square).then_inc(s["sq2"], 1)
                        act.wait_ge(s["ms_mm"], 1)
                        nc.scalar.activation(log2[:, :], ps[0][:, 0:PT], ACT.Ln, bias=eps6[:, 0:1]).then_inc(s["log2_done"], 1)
                        act.wait_ge(s["log2_done"], 1)
                        nc.scalar.activation(rms[:, :], log2[:, :], ACT.Exp, scale=-0.5).then_inc(s["rms_done"], 1)
                    if back is not None:
                        for i in range(max(HU, NC)):
                            if i < HU:
                                act.wait_ge(s["hid_mm"], i + 1)
                                nc.scalar.activation(hid[:, i * J:(i + 1) * J, :].rearrange("p j n -> p (j n)"),
                                                     ps[1 + i % 3][:, 0:J * PT], ACT.Gelu).then_inc(s["gelu_done"], 1)
                            if i < NC:
                                t0, n = CHUNKS[i]
                                act.wait_ge(s["g_mm"], i + 1)
                                nc.scalar.activation(weight[:, :, :, t0:t0 + n],
                                                     ps[4 + i % HB][:, 0:n * PB * EB].rearrange("p (t b j) -> p j b t", b=PB, j=EB),
                                                     ACT.Copy).then_inc(s["evac_done"], 1)
                    if front is not None:
                        act.wait_ge(s["t_done"], 1)
                        if back is not None:
                            act.wait_ge(s["rows_done"], NC)
                            act.wait_ge(s["cols_done"], NC)
                        nc.scalar.activation(codesT[:, :, :].rearrange("p a n -> p (a n)"), ps[7][:, 0:3 * N], ACT.Copy)\
                            .then_inc(s["ct_done"], 1)

                @block.gpsimd
                def _(pool):
                    if back is not None:
                        for ch, (t0, n) in enumerate(CHUNKS):
                            shape = [P, n, PB * EB]
                            pool.wait_ge(s["hot_done"], ch + 1)
                            nc.gpsimd.tensor_tensor(hot_cols[:, ch % HB, 0:n, :], hot_cols[:, ch % HB, 0:n, :],
                                                    codesT[:, 2, t0:t0 + n].unsqueeze(2).to_broadcast(shape), ALU.mult)\
                                .then_inc(s["cols_done"], 1)

                @block.vector
                def _(dve):
                    def one_hot(ch):
                        t0, n = CHUNKS[ch]
                        if ch >= HB:
                            dve.wait_ge(s["g_mm"], ch - HB + 1)
                        nc.vector.tensor_tensor(hot_rows[:, ch % HB, 0:n, :], ramp[:, :].unsqueeze(1).to_broadcast([P, n, P]),
                                                codesT[:, 0, t0:t0 + n].unsqueeze(2).to_broadcast([P, n, P]), ALU.is_equal)\
                            .then_inc(s["rows_done"], 1)
                        nc.vector.tensor_tensor(hot_cols[:, ch % HB, 0:n, :], ramp[:, 0:PB * EB].unsqueeze(1).to_broadcast([P, n, PB * EB]),
                                                codesT[:, 1, t0:t0 + n].unsqueeze(2).to_broadcast([P, n, PB * EB]), ALU.is_equal)\
                            .then_inc(s["hot_done"], 1)

                    if back is not None:
                        one_hot(0)
                    if front is not None:
                        norm.vector(nc, dve, h[:, :, front])
                    if back is not None:
                        for ch in range(1, NC):
                            one_hot(ch)
                    if front is not None:
                        dve.wait_ge(norm.ready, 1)
                        dve.wait_ge(s["rms_done"], 1)
                        if back is not None:
                            dve.wait_ge(s["hid_mm"], HU)
                        for k in range(DK):
                            nc.vector.scalar_tensor_tensor(out=xn[:, k, :], in0=norm.out[:, k, :], scalar=nw[:, k:k + 1],
                                                           in1=rms[:, :], op0=ALU.mult, op1=ALU.mult).then_inc(s["xn_done"], 1)
                    if back is not None:
                        dve.wait_ge(s["gelu_done"], HU)
                        dve.wait_ge(s["evac_done"], NC)
                        for i in range(HU):
                            block_ = hid[:, i * J:(i + 1) * J, :]
                            nc.vector.tensor_tensor(block_, block_, weight[:, i * J:(i + 1) * J, :, :].rearrange("p j b n -> p j (b n)"),
                                                    ALU.mult).then_inc(s["wgt_done"], 1)
                    if front is not None:
                        best_experts(dve)
                    if back is not None:
                        for m in range(DK):
                            dve.wait_ge(s["up_mm"], m + 1)
                            nc.vector.tensor_tensor(h[:, m, back], h[:, m, back], ps[5 + m][:, 0:PT], ALU.add).then_inc(s["res_done"], 1)
            st.clear()

        def pair_cols(g):
            return bass.ds(g * PT, PT)

        step(pair_cols(0), None)
        with nc.Fori(0, STEPS - 1) as g:
            step(pair_cols(g + 1), pair_cols(g))
        step(None, pair_cols(STEPS - 1))
        with nc.Block() as block:
            @block.sync
            def _(sp):
                sp.wait_ge(out_sent, 16 * STEPS)
        so.clear()


def early_fusion(nc, a, out):
    with Stage(nc, "net") as st:
        h = st.sbuf("h", [P, DK, T])
        c = dict(ones=st.sbuf("ones", [P, P]), ident=st.sbuf("ident", [P, P]), eps=st.sbuf("eps", [P, 1]))
        slots_in = nc.dram_tensor("slots_in", [17 * 640, D], F32).ap()
        slots_out = nc.dram_tensor("slots_out", [16 * 565, D], F32).ap()
        row_expert = nc.dram_tensor("row_expert", [B, 1], U32).ap()
        constants(nc, c)
        tok(nc, h, c, **a["tok"])
        l0_attn(nc, h, c, **a["l0_attn"])
        moe(nc, h, c, slots_in=slots_in, slots_out=slots_out, **a["moe"])
        mamba(nc, h, c, [a["mamba_f"], a["mamba_b"]])
        l1_ffn(nc, h, c, **a["l1_ffn"])
        l2_attn(nc, h, c, **a["l2_attn"])
        l2_ffn(nc, h, c, row_expert=row_expert, **a["l2_ffn"])
        rwkv(nc, h, c, **a["rwkv"])
        peer(nc, h, c, out=out, **a["peer"])



def feature_cols(v):
    return v.reshape(-1, P).T


def feature_blocks(w):
    return w.reshape(-1, P, w.shape[1]).transpose(1, 0, 2)


def rope_tables():
    n = np.arange(N)
    places = (n // 256, n % 256 // 16, n % 16)
    rate = (1.0 / 10000.0 ** (np.arange(2, dtype=np.float32) / 2.0)).astype(np.float32)
    cos, sin = np.ones((D, N), np.float32), np.zeros((D, N), np.float32)
    for i in range(D):
        f = i % 16
        if f < 12:
            angle = (places[f // 4].astype(np.float32) * rate[f % 2]).astype(np.float32)
            cos[i] = np.cos(angle)
            sin[i] = np.sin(angle) * (-1 if f % 2 == 0 else 1)
    head = np.arange(P) // 16 % 2
    even = np.stack([head == 0, head == 1], 1).astype(np.float32)
    table = lambda t: t.reshape(DK, P, N).transpose(1, 0, 2)
    return table(cos), table(sin), even


def layout(I):
    out = {}
    x = I["x"]
    text = np.zeros((B, N, D), np.float32)
    text[:, IMG:] = I["txt"]
    px = x.reshape(B, 3, GRID, 16, GRID, 16).transpose(1, 3, 5, 0, 2, 4).reshape(6, P, B * IMG).transpose(1, 0, 2)
    out["tok"] = dict(h_text=text.reshape(T, DK, P).transpose(2, 1, 0), patches=px, w_t=feature_blocks(I["L0_tok_W"].T),
                      bias=feature_cols(I["L0_tok_b"]))

    w = lambda n: I[f"L0_attn_{n}"]
    turn = np.arange(D) ^ 1
    cos, sin, even = rope_tables()
    biases = np.stack([feature_cols(v) for v in (w("bq"), w("bq")[turn], w("bk"), w("bk")[turn], w("bv"), w("bo"))], 1)
    out["l0_attn"] = dict(wq=w("Wq"), wq_rot=w("Wq")[:, turn], wk=w("Wk"), wk_rot=w("Wk")[:, turn], wv=w("Wv"), wo=w("Wo"),
                          biases=biases, cos=cos, sin=sin, even=even)

    w = lambda n: I[f"L0_ffn_{n}"]
    gate = np.concatenate([w("w_gate"), w("sw_gate")[None]])
    up = np.concatenate([w("w_up"), w("sw_up")[None]])
    down = np.concatenate([w("w_down"), w("sw_down")[None]])
    gate_up = np.stack([gate, up], 2).reshape(17, DK, P, 2, 352).transpose(0, 2, 1, 3, 4)
    padded = np.zeros((17, 3 * P, D), np.float32)
    padded[:, :352] = down
    out["moe"] = dict(router_w=w("router_w"), router_b=w("router_b").reshape(1, 16), gate_up=gate_up,
                      down=padded.reshape(17, 3, P, D).transpose(0, 2, 1, 3))

    for p in "fb":
        w = lambda n: I[f"L1_attn_{p}_{n}"]
        out[f"mamba_{p}"] = dict(in_t=w("in_w").T, xproj_t=w("xproj_w").T, dt_t=w("dt_w").T, out_t=w("out_w").T,
                                 conv_w=feature_blocks(w("conv_w")), conv_b=feature_cols(w("conv_b")),
                                 dt_b=w("dt_b").reshape(1, -1), a_log=feature_blocks(w("A_log")), d=feature_cols(w("D")))

    w = lambda n: I[f"L1_ffn_{n}"]
    out["l1_ffn"] = dict(w_fc=w("w_fc"), w_proj=w("w_proj"), u_t=w("u").T, v=w("v"), fast_b=w("fast_b"),
                         gate=np.asarray(w("gate")).reshape(1, 1))
    w = lambda n: I[f"L2_attn_{n}"]
    out["l2_attn"] = dict(wq=w("W_Q"), wk=w("W_K"), wv=w("W_V"))

    w = lambda n: I[f"L2_ffn_{n}"]
    out["l2_ffn"] = dict(wr=w("Wr"), br=w("br").reshape(1, 8), w1=w("W1").reshape(8, DK, P, 1024).transpose(0, 2, 1, 3),
                         b1=w("b1").reshape(8, 8, P).transpose(0, 2, 1), w2=w("W2").reshape(8, 8, P, D).transpose(0, 2, 1, 3),
                         b2=w("b2").reshape(8, DK, P).transpose(0, 2, 1))

    w = lambda n: I[f"L3_attn_{n}"]
    cols = np.stack([feature_cols(w(n).reshape(-1)) for n in
                     ("time_decay", "time_first", "ln1_g", "ln1_b", "ln2_g", "ln2_b", "mix_k", "mix_v", "mix_r", "cmix_k",
                      "cmix_r")], 1)
    out["rwkv"] = dict(wk=w("w_tk"), wv=w("w_tv"), wr=w("w_tr"), ck=w("w_ck"), cv=w("w_cv"), cr=w("w_cr"), cols=cols)

    w = lambda n: I[f"L3_ffn_{n}"]
    keys = w("keys").transpose(3, 0, 2, 1).reshape(P, 16, 64)
    order = np.arange(4096).reshape(64, 32, 2).transpose(1, 2, 0).reshape(32, P)
    out["peer"] = dict(wq=w("w_q"), keys_t=keys,
                       down_t=w("expert_down")[order].transpose(2, 0, 1).reshape(DK, P, 32, P).transpose(1, 0, 2, 3),
                       up=w("expert_up")[order].transpose(1, 0, 2), norm_w=feature_cols(w("norm_w")))
    return out


def kernel(**inputs):
    import concourse.bacc as _bacc
    from concourse.bass_utils import run_bass_kernel_spmd as _run

    nc = _bacc.Bacc("TRN2", target_bir_lowering=False, num_devices=1)
    arrays, aps = {}, {}
    for stage, parts in layout({k: np.asarray(v) for k, v in inputs.items()}).items():
        aps[stage] = {}
        for name, value in parts.items():
            value = np.ascontiguousarray(value)
            arrays[f"in_{stage}_{name}"] = value
            aps[stage][name] = nc.dram_tensor(f"in_{stage}_{name}", value.shape, mybir.dt.from_np(value.dtype),
                                              kind="ExternalInput").ap()
    out = nc.dram_tensor("out", [P, DK, T], F32, kind="ExternalOutput").ap()
    early_fusion(nc, aps, out)
    result = _run(nc, [arrays], core_ids=[0]).results[0]["out"]
    return np.ascontiguousarray(result.transpose(2, 1, 0).reshape(B, N, D))
```

```python
from contextlib import ExitStack


import numpy as np
import concourse.bass as bass
from concourse import mybir

F32 = mybir.dt.float32
BF16 = mybir.dt.bfloat16
U32 = mybir.dt.uint32
I32 = mybir.dt.int32
ALU = mybir.AluOpType
ACT = mybir.ActivationFunctionType
AX = mybir.AxisListType

P = 128
B = 32
GRID = 6
IMG = GRID * GRID
TXT = 77
N = IMG + TXT
T = B * N
D = 256
DK = D // P
GB = 4
GT = GB * N
GROUPS = B // GB
LN_EPS = 1e-5


EXP_LN = "natural_log_exp_and_others"


class Stage:

    def __init__(self, nc, name):
        self.nc, self.name, self.stack, self.sems = nc, name, ExitStack(), []

    def __enter__(self):
        return self

    def __exit__(self, *exc):
        self.stack.close()

    def sbuf(self, name, shape, dt=F32):
        return self.stack.enter_context(self.nc.sbuf_tensor(f"{self.name}_{name}", shape, dt))

    def psum(self, name, shape=(P, 512), dt=F32):
        return self.stack.enter_context(self.nc.psum_tensor(f"{self.name}_{name}", list(shape), dt))

    def sem(self, name):
        s = self.stack.enter_context(self.nc.semaphore(f"{self.name}_{name}"))
        self.sems.append(s)
        return s

    def clear(self, pool_dmas=False):
        def zero(eng):
            at = 0
            while at < len(self.sems):
                last = at
                while last + 1 < len(self.sems) and self.sems[last + 1].num == self.sems[last].num + 1:
                    last += 1
                numbers = range(self.sems[at].num, self.sems[last].num + 1)
                if pool_dmas:
                    eng.dma_reset(numbers)
                eng.sem_clear(numbers)
                at = last + 1

        with self.nc.Block(no_gpsimd_drain=True) as block:
            if pool_dmas:
                block.gpsimd(zero)
            else:
                block.sync(zero)


def group_cols(g):
    return bass.ds(g * GT, GT)


class Norm:

    def __init__(self, st, mean_ps, var_ps, name="ln", width=GT):
        self.mean_ps, self.var_ps, self.width = mean_ps, var_ps, width
        self.centred = st.sbuf(f"{name}_centred", [P, DK, width])
        self.square = st.sbuf(f"{name}_square", [P, DK, width])
        self.log_var = st.sbuf(f"{name}_log_var", [P, width])
        self.rstd = st.sbuf(f"{name}_rstd", [P, width])
        self.out = st.sbuf(f"{name}_out", [P, DK, width])
        self.mean_ready = st.sem(f"{name}_mean_ready")
        self.centred_ready = st.sem(f"{name}_centred_ready")
        self.square_ready = st.sem(f"{name}_square_ready")
        self.var_ready = st.sem(f"{name}_var_ready")
        self.log_ready = st.sem(f"{name}_log_ready")
        self.rstd_ready = st.sem(f"{name}_rstd_ready")
        self.ready = st.sem(f"{name}_ready")

    def tensor_mean(self, nc, pe, ones, x):
        for k in range(DK):
            mm = nc.tensor.matmul(self.mean_ps[:, 0:self.width], ones[:, :], x(k), start=(k == 0), stop=(k == DK - 1))
        mm.then_inc(self.mean_ready, 1)

    def tensor_var(self, nc, pe, ones):
        pe.wait_ge(self.square_ready, 1)
        for k in range(DK):
            mm = nc.tensor.matmul(self.var_ps[:, 0:self.width], ones[:, :], self.square[:, k, :],
                                  start=(k == 0), stop=(k == DK - 1))
        mm.then_inc(self.var_ready, 1)

    def scalar(self, nc, act, eps_col):
        act.wait_ge(self.centred_ready, 1)
        nc.scalar.activation(self.square[:, :, :], self.centred[:, :, :], ACT.Square).then_inc(self.square_ready, 1)
        self.scalar_root(nc, act, eps_col)

    def scalar_root(self, nc, act, eps_col):
        act.wait_ge(self.var_ready, 1)
        nc.scalar.activation(self.log_var[:, :], self.var_ps[:, 0:self.width], ACT.Ln, bias=eps_col[:, 0:1])\
            .then_inc(self.log_ready, 1)
        act.wait_ge(self.log_ready, 1)
        nc.scalar.activation(self.rstd[:, :], self.log_var[:, :], ACT.Exp, scale=-0.5).then_inc(self.rstd_ready, 1)

    def vector(self, nc, dve, x_all):
        self.vector_centre(nc, dve, x_all)
        self.vector_scale(nc, dve)

    def vector_centre(self, nc, dve, x_all):
        dve.wait_ge(self.mean_ready, 1)
        nc.vector.tensor_tensor(self.centred[:, :, :], x_all,
                                self.mean_ps[:, 0:self.width].unsqueeze(1).to_broadcast([P, DK, self.width]),
                                ALU.subtract).then_inc(self.centred_ready, 1)

    def vector_scale(self, nc, dve):
        dve.wait_ge(self.rstd_ready, 1)
        dve.wait_ge(self.centred_ready, 1)
        nc.vector.tensor_tensor(self.out[:, :, :], self.centred[:, :, :],
                                self.rstd[:, :].unsqueeze(1).to_broadcast([P, DK, self.width]),
                                ALU.mult).then_inc(self.ready, 1)


def constants(nc, c):
    with Stage(nc, "const") as st:
        zero_done, done = st.sem("zero"), st.sem("done")
        with nc.Block() as block:
            @block.gpsimd
            def _(pool):
                nc.gpsimd.memset(c["ones"][:, :], 1.0 / D).then_inc(done, 1)
                nc.gpsimd.memset(c["eps"][:, :], LN_EPS).then_inc(done, 1)
                nc.gpsimd.memset(c["ident"][:, :], 0.0).then_inc(zero_done, 1)
                pool.wait_ge(zero_done, 1)
                nc.gpsimd.affine_select(out=c["ident"][:, :], in_=c["ident"][:, :], compare_op=ALU.not_equal, fill=1.0,
                                        base=0, pattern=[[-1, P]], channel_multiplier=1).then_inc(done, 1)
                pool.wait_ge(done, 3)
        st.clear()


def tok(nc, h, c, h_text, patches, w_t, bias):
    KB = patches.shape[1]
    CB = 8
    with Stage(nc, "tok") as st:
        px = st.sbuf("px", [P, KB, B * IMG])
        w = st.sbuf("w", [P, KB, D])
        b = st.sbuf("b", [P, DK])
        ps = [st.psum(f"ps{i}") for i in range(8)]
        text_in, w_in, mm_done, tok_done = (st.sem(x) for x in ("text_in", "w_in", "mm_done", "tok_done"))
        px_in = [st.sem(f"px_in{i}") for i in range(B // CB)]
        with nc.Block() as block:
            @block.sync
            def _(sp):
                sp.dma_start(w[:, :, :], w_t).then_inc(w_in, 16)
                sp.dma_start(b[:, :], bias).then_inc(w_in, 16)
                for i in range(B // CB):
                    sp.dma_start(px[:, :, i * CB * IMG:(i + 1) * CB * IMG], patches[:, :, i * CB * IMG:(i + 1) * CB * IMG])\
                        .then_inc(px_in[i], 16)

            @block.tensor
            def _(pe):
                pe.wait_ge(w_in, 32)
                for i in range(B // CB):
                    pe.wait_ge(px_in[i], 16)
                    for m in range(DK):
                        for k in range(KB):
                            mm = nc.tensor.matmul(ps[2 * i + m][:, 0:CB * IMG], w[:, k, m * P:(m + 1) * P],
                                                  px[:, k, i * CB * IMG:(i + 1) * CB * IMG], start=(k == 0), stop=(k == KB - 1))
                        mm.then_inc(mm_done, 1)

            @block.scalar
            def _(act):
                act.dma_start(h[:, :, :], h_text).then_inc(text_in, 16)
                nc.scalar.preload_act_table_set(EXP_LN)
                act.wait_ge(text_in, 16)
                act.wait_ge(w_in, 32)
                for i in range(B // CB):
                    for m in range(DK):
                        act.wait_ge(mm_done, 2 * i + m + 1)
                        dst = h[:, m, :].rearrange("p (b n) -> p b n", n=N)[:, i * CB:(i + 1) * CB, 0:IMG]
                        nc.scalar.activation(dst, ps[2 * i + m][:, 0:CB * IMG].rearrange("p (b n) -> p b n", n=IMG),
                                             ACT.Identity, bias=b[:, m:m + 1]).then_inc(tok_done, 1)
        st.clear()


def l0_attn(nc, h, c, wq, wq_rot, wk, wk_rot, wv, wo, biases, cos, sin, even):
    H, HD = 16, 16
    UNITS = GB * 4
    with Stage(nc, "at0") as st:
        W = {x: st.sbuf(x, [P, DK, D]) for x in ("wq", "wqr", "wk", "wkr", "wv", "wo")}
        bs = st.sbuf("bs", [P, 6, DK])
        cs = st.sbuf("cos", [P, DK, N])
        sn = st.sbuf("sin", [P, DK, N])
        ev = st.sbuf("even", [P, 2])
        ps = [st.psum(f"ps{i}") for i in range(8)]
        N_BANK = 7
        norm = Norm(st, ps[N_BANK], ps[N_BANK])
        rot_a = st.sbuf("rot_a", [P, 4, GT])
        rot_b = st.sbuf("rot_b", [P, 4, GT])
        q = st.sbuf("q", [P, DK, GT])
        kk = st.sbuf("k", [P, DK, GT])
        kpar = [st.sbuf("k_even", [P, DK, GT]), st.sbuf("k_odd", [P, DK, GT])]
        v = st.sbuf("v", [N, GB, H // 2, 2, 2, HD])
        NE = 4
        low = st.sbuf("shifted", [N, NE, 4 * N])
        ex = st.sbuf("ex", [N, NE, 4 * N])
        exT = st.sbuf("exT", [N, NE, 4 * N])
        mx = st.sbuf("mx", [N, UNITS, 4])
        sm = st.sbuf("sm", [N, UNITS, 4])
        rs = st.sbuf("rs", [N, UNITS, 4])
        ctxT = st.sbuf("ctxT", [P, DK, GT])
        (w_in, ones_set, proj_done, a_done, b_done, q_done, k_done, kpar_done, v_mm, v_done, s_done, mx_done, low_done,
         ex_done, sm_done, rs_done, pn_done, t_done, exT_done, av_done, ctx_done, o_done, res_done) = (
            st.sem(x) for x in ("w_in", "ones_set", "proj_done", "a_done", "b_done", "q_done", "k_done", "kpar_done", "v_mm",
                                "v_done", "s_done", "mx_done", "low_done", "ex_done", "sm_done", "rs_done", "pn_done", "t_done",
                                "exT_done", "av_done", "ctx_done", "o_done", "res_done"))
        with nc.Block() as block:
            @block.sync
            def _(sp):
                for x, src in (("wq", wq), ("wqr", wq_rot), ("wk", wk), ("wkr", wk_rot), ("wv", wv), ("wo", wo)):
                    sp.dma_start(W[x][:, :, :], src.rearrange("(k p) n -> p k n", p=P)).then_inc(w_in, 16)
                sp.dma_start(bs[:, :, :], biases).then_inc(w_in, 16)
                sp.dma_start(cs[:, :, :], cos).then_inc(w_in, 16)
                sp.dma_start(sn[:, :, :], sin).then_inc(w_in, 16)
                sp.dma_start(ev[:, :], even).then_inc(w_in, 16)
                sp.wait_ge(w_in, 160)

            @block.gpsimd
            def _(pool):
                nc.gpsimd.memset(v[:, :, :, :, :, :], 0.0).then_inc(ones_set, 1)

            @block.scalar
            def _(act):
                nc.scalar.preload_act_table_set(EXP_LN)
        st.clear()
        S_BANK, T_BANK, C_BANK = (0, 1, 2), (3, 4), (5, 6)

        def head(r, j):
            return 8 * (j // 2) + 2 * r + j % 2

        def prepare(front):
            with nc.Block(no_gpsimd_drain=True) as block:
                @block.tensor
                def _(pe):
                    norm.tensor_mean(nc, pe, c["ones"], lambda k: h[:, k, front])
                    norm.tensor_var(nc, pe, c["ones"])

                @block.scalar
                def _(act):
                    norm.scalar(nc, act, c["eps"])

                @block.vector
                def _(dve):
                    norm.vector(nc, dve, h[:, :, front])
            st.clear()

        MEAN, CENTRE, SQUARE, VAR, RSTD, SCALE = 1, 3, 5, 6, 9, 10

        def step(front, back):
            with nc.Block(no_gpsimd_drain=True) as block:
                @block.tensor
                def _(pe):
                    for i, x in enumerate(("wq", "wqr", "wk", "wkr")):
                        for m in range(DK):
                            for k in range(DK):
                                mm = nc.tensor.matmul(ps[2 * i + m][:, 0:GT], W[x][:, k, m * P:(m + 1) * P],
                                                      norm.out[:, k, :], start=(k == 0), stop=(k == DK - 1))
                            mm.then_inc(proj_done, 1)
                    for b in range(GB):
                        if b % 2 == 0:
                            pe.wait_ge(b_done if b else a_done, 2)
                        bank = ps[2 * (b // 2)]
                        for k in range(DK):
                            mm = nc.tensor.matmul(bank[0:N, (b % 2) * D:(b % 2 + 1) * D], norm.out[:, k, b * N:(b + 1) * N],
                                                  W["wv"][:, k, :], start=(k == 0), stop=(k == DK - 1))
                        if b % 2:
                            mm.then_inc(v_mm, 1)

                    def scores(u):
                        b, r = u // 4, u % 4
                        if u < 3:
                            pe.wait_ge(v_done, GB)
                            pe.wait_ge(b_done, 4)
                            pe.wait_ge(q_done, 2)
                            pe.wait_ge(kpar_done, 4)
                        else:
                            pe.wait_ge(low_done, u - 2)
                        for j in range(4):
                            m = j // 2
                            mm = nc.tensor.matmul(ps[S_BANK[u % 3]][0:N, j * N:(j + 1) * N],
                                                  q[32 * r:32 * r + 32, m, b * N:(b + 1) * N],
                                                  kpar[j % 2][32 * r:32 * r + 32, m, b * N:(b + 1) * N], start=True, stop=True)
                        mm.then_inc(s_done, 1)

                    def turn(u):
                        pe.wait_ge(pn_done, u + 1)
                        if u >= 2:
                            pe.wait_ge(exT_done, u - 1)
                        for j in range(4):
                            mm = nc.tensor.transpose(ps[T_BANK[u % 2]][0:N, j * N:(j + 1) * N],
                                                     ex[:, u % NE, j * N:(j + 1) * N], c["ident"][0:N, 0:N])
                        mm.then_inc(t_done, 1)

                    def values(u):
                        b, r = u // 4, u % 4
                        pe.wait_ge(exT_done, u + 1)
                        for j in range(4):
                            m, odd = j // 2, j % 2
                            mm = nc.tensor.matmul(ps[C_BANK[m]][32 * r:32 * r + 32, b * N:(b + 1) * N],
                                                  v[:, b, 4 * m + r, odd, :, :].rearrange("p a e -> p (a e)"),
                                                  exT[:, u % NE, j * N:(j + 1) * N], start=(odd == 0), stop=(odd == 1),
                                                  skip_group_check=True)
                        mm.then_inc(av_done, 1)

                    for u in range(UNITS + 3):
                        if u < UNITS:
                            scores(u)
                        if 2 <= u <= UNITS + 1:
                            turn(u - 2)
                        if u >= 3:
                            values(u - 3)
                        if front is not None and u == MEAN:
                            norm.tensor_mean(nc, pe, c["ones"], lambda k: h[:, k, front])
                        if front is not None and u == VAR:
                            norm.tensor_var(nc, pe, c["ones"])
                    pe.wait_ge(low_done, UNITS)
                    for m in range(DK):
                        for k in range(DK):
                            if m == 0:
                                pe.wait_ge(ctx_done, k + 1)
                            mm = nc.tensor.matmul(ps[m][:, 0:GT], W["wo"][:, k, m * P:(m + 1) * P], ctxT[:, k, :],
                                                  start=(k == 0), stop=(k == DK - 1))
                        mm.then_inc(o_done, 1)

                @block.scalar
                def _(act):
                    for b in range(0, GB, 2):
                        act.wait_ge(v_mm, b // 2 + 1)
                        for odd in range(2):
                            nc.scalar.activation(v[:, b:b + 2, :, odd, odd, :],
                                                 ps[b][0:N, :].rearrange("p (b h o e) -> p b h o e", b=2, o=2, e=HD)[:, :, :, odd, :],
                                                 ACT.Copy).then_inc(v_done, 1)
                    for u in range(UNITS + 2):
                        if u < UNITS:
                            act.wait_ge(low_done, u + 1)
                            if u >= NE:
                                act.wait_ge(t_done, u - NE + 1)
                            nc.scalar.activation(ex[:, u % NE, :], low[:, u % NE, :], ACT.Exp, scale=HD ** -0.5)\
                                .then_inc(ex_done, 1)
                        if u >= 2:
                            act.wait_ge(t_done, u - 1)
                            if u - 2 >= NE:
                                act.wait_ge(av_done, u - NE - 1)
                            nc.scalar.activation(exT[:, (u - 2) % NE, :], ps[T_BANK[(u - 2) % 2]][0:N, 0:4 * N], ACT.Copy)\
                                .then_inc(exT_done, 1)
                        if front is not None and u == SQUARE:
                            act.wait_ge(norm.centred_ready, 1)
                            nc.scalar.activation(norm.square[:, :, :], norm.centred[:, :, :], ACT.Square)\
                                .then_inc(norm.square_ready, 1)
                        if front is not None and u == RSTD:
                            norm.scalar_root(nc, act, c["eps"])
                    for m in range(DK):
                        act.wait_ge(av_done, UNITS)
                        nc.scalar.activation(ctxT[:, m, :], ps[C_BANK[m]][:, 0:GT], ACT.Identity, bias=bs[:, 4, m:m + 1])\
                            .then_inc(ctx_done, 1)

                @block.gpsimd
                def _(pool):
                    for u in range(UNITS):
                        pool.wait_ge(rs_done, u + 1)
                        e = ex[:, u % NE, :].rearrange("p (j n) -> p j n", n=N)
                        nc.gpsimd.tensor_tensor(e, e, rs[:, u, :].unsqueeze(2).to_broadcast([N, 4, N]), ALU.mult).then_inc(pn_done, 1)

                @block.vector
                def _(dve):
                    def table(t, m):
                        return t[:, m, :].unsqueeze(1).to_broadcast([P, GB, N])

                    def rows(ap):
                        return ap.rearrange("p (b n) -> p b n", n=N)

                    for i in range(2):
                        for m in range(DK):
                            j = 2 * i + m
                            dve.wait_ge(proj_done, 4 * i + m + 1)
                            nc.vector.scalar_tensor_tensor(out=rows(rot_a[:, j, :]), in0=rows(ps[4 * i + m][:, 0:GT]),
                                                           scalar=bs[:, 2 * i, m:m + 1], in1=table(cs, m),
                                                           op0=ALU.add, op1=ALU.mult).then_inc(a_done, 1)
                        for m in range(DK):
                            j = 2 * i + m
                            dve.wait_ge(proj_done, 4 * i + 2 + m + 1)
                            nc.vector.scalar_tensor_tensor(out=rows(rot_b[:, j, :]), in0=rows(ps[4 * i + 2 + m][:, 0:GT]),
                                                           scalar=bs[:, 2 * i + 1, m:m + 1], in1=table(sn, m),
                                                           op0=ALU.add, op1=ALU.mult).then_inc(b_done, 1)
                        for m in range(DK):
                            j = 2 * i + m
                            dve.wait_ge(b_done, j + 1)
                            dve.wait_ge(a_done, j + 1)
                            dst, done = ((q, q_done), (kk, k_done))[i]
                            nc.vector.tensor_tensor(dst[:, m, :], rot_a[:, j, :], rot_b[:, j, :], ALU.add).then_inc(done, 1)
                    dve.wait_ge(k_done, 2)
                    for par in range(2):
                        for m in range(DK):
                            nc.vector.tensor_scalar(kpar[par][:, m, :], kk[:, m, :], ev[:, par:par + 1], None, ALU.mult)\
                                .then_inc(kpar_done, 1)

                    def shift(u):
                        s = ps[S_BANK[u % 3]][0:N, 0:4 * N].rearrange("p (j n) -> p j n", n=N)
                        dve.wait_ge(s_done, u + 1)
                        nc.vector.tensor_reduce(mx[:, u, :], s, AX.X, ALU.max).then_inc(mx_done, 1)
                        dve.wait_ge(mx_done, u + 1)
                        if u >= NE:
                            dve.wait_ge(ex_done, u - NE + 1)
                        nc.vector.tensor_tensor(low[:, u % NE, :].rearrange("p (j n) -> p j n", n=N), s,
                                                mx[:, u, :].unsqueeze(2).to_broadcast([N, 4, N]), ALU.subtract)\
                            .then_inc(low_done, 1)

                    def total(u):
                        dve.wait_ge(ex_done, u + 1)
                        nc.vector.tensor_reduce(sm[:, u, :], ex[:, u % NE, :].rearrange("p (j n) -> p j n", n=N), AX.X, ALU.add)\
                            .then_inc(sm_done, 1)
                        dve.wait_ge(sm_done, u + 1)
                        nc.vector.reciprocal(rs[:, u, :], sm[:, u, :]).then_inc(rs_done, 1)

                    for u in range(UNITS + 1):
                        if u < UNITS:
                            shift(u)
                        if u >= 1:
                            total(u - 1)
                        if front is not None and u == CENTRE:
                            norm.vector_centre(nc, dve, h[:, :, front])
                        if front is not None and u == SCALE:
                            norm.vector_scale(nc, dve)
                    for m in range(DK):
                        dve.wait_ge(o_done, m + 1)
                        nc.vector.scalar_tensor_tensor(out=h[:, m, back], in0=ps[m][:, 0:GT],
                                                       scalar=bs[:, 5, m:m + 1], in1=h[:, m, back],
                                                       op0=ALU.add, op1=ALU.add).then_inc(res_done, 1)
            st.clear()

        prepare(group_cols(0))
        with nc.Fori(0, GROUPS - 1) as g:
            step(group_cols(g + 1), group_cols(g))
        step(None, group_cols(GROUPS - 1))


def l2_attn(nc, h, c, wq, wk, wv):
    MASKED = -1e30
    with Stage(nc, "at2") as st:
        W = {x: st.sbuf(x, [P, DK, D]) for x in ("wq", "wk", "wv")}
        mask = st.sbuf("mask", [N, N])
        ps = [st.psum(f"ps{i}") for i in range(8)]
        S_BANK, N_BANK, Q_BANK, V_BANK = 0, 1, (2, 3, 4, 5), (6, 7)
        norm = Norm(st, ps[N_BANK], ps[N_BANK])
        q = st.sbuf("q", [P, DK, GT])
        kk = st.sbuf("k", [P, DK, GT])
        v = st.sbuf("v", [N, GB, D])
        sc = st.sbuf("sc", [N, GB, N])
        low = st.sbuf("low", [N, GB, N])
        ex = st.sbuf("ex", [N, GB, N])
        pr = st.sbuf("pr", [N, GB, N])
        prT = st.sbuf("prT", [N, GB, N])
        mx, sm, rs = (st.sbuf(x, [N, GB]) for x in ("mx", "sm", "rs"))
        (w_in, zero, masked, proj_done, qk_done, v_mm, v_done, s_done, sc_done, mx_done, low_done, ex_done, sm_done, rs_done,
         pr_done, t_done, prT_done, o_done, res_done) = (
            st.sem(x) for x in ("w_in", "zero", "masked", "proj_done", "qk_done", "v_mm", "v_done", "s_done", "sc_done",
                                "mx_done", "low_done", "ex_done", "sm_done", "rs_done", "pr_done", "t_done", "prT_done",
                                "o_done", "res_done"))
        with nc.Block() as block:
            @block.sync
            def _(sp):
                for x, src in (("wq", wq), ("wk", wk), ("wv", wv)):
                    sp.dma_start(W[x][:, :, :], src.rearrange("(k p) n -> p k n", p=P)).then_inc(w_in, 16)
                sp.wait_ge(w_in, 48)

            @block.gpsimd
            def _(pool):
                nc.gpsimd.memset(mask[:, :], 0.0).then_inc(zero, 1)
                pool.wait_ge(zero, 1)
                nc.gpsimd.affine_select(out=mask[:, :], in_=mask[:, :], compare_op=ALU.is_ge, fill=MASKED,
                                        base=0, pattern=[[-1, N]], channel_multiplier=1).then_inc(masked, 1)

            @block.scalar
            def _(act):
                nc.scalar.preload_act_table_set(EXP_LN)
        st.clear()
        def step(front, back):
            with nc.Block(no_gpsimd_drain=True) as block:
                @block.tensor
                def _(pe):
                    if front is not None:
                        norm.tensor_mean(nc, pe, c["ones"], lambda k: h[:, k, front])
                    if back is not None:
                        for b in range(GB):
                            for k in range(DK):
                                mm = nc.tensor.matmul(ps[S_BANK][0:N, b * N:(b + 1) * N], q[:, k, b * N:(b + 1) * N],
                                                      kk[:, k, b * N:(b + 1) * N], start=(k == 0), stop=(k == DK - 1))
                        mm.then_inc(s_done, 1)
                    if front is not None:
                        norm.tensor_var(nc, pe, c["ones"])
                        pe.wait_ge(norm.ready, 1)
                        for i, x in enumerate(("wq", "wk")):
                            for m in range(DK):
                                for k in range(DK):
                                    mm = nc.tensor.matmul(ps[Q_BANK[2 * i + m]][:, 0:GT], W[x][:, k, m * P:(m + 1) * P],
                                                          norm.out[:, k, :], start=(k == 0), stop=(k == DK - 1))
                                mm.then_inc(proj_done, 1)
                    if back is not None:
                        pe.wait_ge(pr_done, 1)
                        for b in range(GB):
                            mm = nc.tensor.transpose(ps[S_BANK][0:N, b * N:(b + 1) * N], pr[:, b, :], c["ident"][0:N, 0:N])
                        mm.then_inc(t_done, 1)
                    if front is not None:
                        for b in range(GB):
                            for k in range(DK):
                                mm = nc.tensor.matmul(ps[V_BANK[b // 2]][0:N, (b % 2) * D:(b % 2 + 1) * D],
                                                      norm.out[:, k, b * N:(b + 1) * N], W["wv"][:, k, :],
                                                      start=(k == 0), stop=(k == DK - 1))
                            if b % 2:
                                mm.then_inc(v_mm, 1)
                    if back is not None:
                        pe.wait_ge(prT_done, 1)
                        for m in range(DK):
                            if front is not None:
                                pe.wait_ge(qk_done, m + 1)
                            for b in range(GB):
                                mm = nc.tensor.matmul(ps[Q_BANK[m]][:, b * N:(b + 1) * N], v[:, b, m * P:(m + 1) * P], prT[:, b, :],
                                                      start=True, stop=True)
                            mm.then_inc(o_done, 1)

                @block.scalar
                def _(act):
                    if front is not None:
                        act.wait_ge(norm.centred_ready, 1)
                        nc.scalar.activation(norm.square[:, :, :], norm.centred[:, :, :], ACT.Square).then_inc(norm.square_ready, 1)
                        norm.scalar_root(nc, act, c["eps"])
                    if back is not None:
                        act.wait_ge(low_done, 1)
                        nc.scalar.activation(ex[:, :, :], low[:, :, :], ACT.Exp).then_inc(ex_done, 1)
                    if front is not None:
                        if back is not None:
                            act.wait_ge(s_done, 1)
                        for i in range(4):
                            act.wait_ge(proj_done, i + 1)
                            dst = (q, kk)[i // 2]
                            nc.scalar.activation(dst[:, i % 2, :], ps[Q_BANK[i]][:, 0:GT], ACT.Copy).then_inc(qk_done, 1)
                    if back is not None:
                        act.wait_ge(t_done, 1)
                        nc.scalar.activation(prT[:, :, :], ps[S_BANK][0:N, 0:GT].rearrange("p (b n) -> p b n", n=N), ACT.Copy)\
                            .then_inc(prT_done, 1)
                    if front is not None:
                        if back is not None:
                            act.wait_ge(o_done, DK)
                        for b in range(0, GB, 2):
                            act.wait_ge(v_mm, b // 2 + 1)
                            nc.scalar.activation(v[:, b:b + 2, :], ps[V_BANK[b // 2]][0:N, :].rearrange("p (b d) -> p b d", b=2),
                                                 ACT.Copy).then_inc(v_done, 1)

                @block.vector
                def _(dve):
                    if front is not None:
                        norm.vector_centre(nc, dve, h[:, :, front])
                    if back is not None:
                        dve.wait_ge(s_done, 1)
                        nc.vector.scalar_tensor_tensor(out=sc[:, :, :], in0=ps[S_BANK][0:N, 0:GT].rearrange("p (b n) -> p b n", n=N),
                                                       scalar=D ** -0.5, in1=mask[:, :].unsqueeze(1).to_broadcast([N, GB, N]),
                                                       op0=ALU.mult, op1=ALU.add).then_inc(sc_done, 1)
                        dve.wait_ge(sc_done, 1)
                        nc.vector.tensor_reduce(mx[:, :], sc[:, :, :], AX.X, ALU.max).then_inc(mx_done, 1)
                        dve.wait_ge(mx_done, 1)
                        nc.vector.tensor_tensor(low[:, :, :], sc[:, :, :], mx[:, :].unsqueeze(2).to_broadcast([N, GB, N]),
                                                ALU.subtract).then_inc(low_done, 1)
                    if front is not None:
                        norm.vector_scale(nc, dve)
                    if back is not None:
                        dve.wait_ge(ex_done, 1)
                        nc.vector.tensor_reduce(sm[:, :], ex[:, :, :], AX.X, ALU.add).then_inc(sm_done, 1)
                        dve.wait_ge(sm_done, 1)
                        nc.vector.reciprocal(rs[:, :], sm[:, :]).then_inc(rs_done, 1)
                        dve.wait_ge(rs_done, 1)
                        nc.vector.tensor_tensor(pr[:, :, :], ex[:, :, :], rs[:, :].unsqueeze(2).to_broadcast([N, GB, N]),
                                                ALU.mult).then_inc(pr_done, 1)
                        for m in range(DK):
                            dve.wait_ge(o_done, m + 1)
                            nc.vector.tensor_tensor(h[:, m, back], ps[Q_BANK[m]][:, 0:GT], h[:, m, back], ALU.add).then_inc(res_done, 1)
            st.clear()

        step(group_cols(0), None)
        with nc.Fori(0, GROUPS - 1) as g:
            step(group_cols(g + 1), group_cols(g))
        step(None, group_cols(GROUPS - 1))


def moe(nc, h, c, router_w, router_b, gate_up, down, slots_in, slots_out):
    E = router_w.shape[1]
    TOPK = 2
    F = gate_up.shape[4]
    FB = [(f, min(P, F - f)) for f in range(0, F, P)]
    C = -(-5 * T * TOPK // (4 * E))
    STRIDE = slots_in.shape[0] // (E + 1)
    TILES = [(t, min(P, C - t)) for t in range(0, C, P)]
    HALVES = [(0, (C + 1) // 2), ((C + 1) // 2, C // 2)]
    NOWHERE = 1 << 20
    NT = len(TILES)
    with Stage(nc, "moe") as st:
        ps = [st.psum(f"ps{i}") for i in range(8)]
        normed = st.sbuf("normed", [P, DK, T])
        share = st.sbuf("share", [N, B, TOPK])
        to_slot = st.sbuf("to_slot", [P, B, TOPK], U32)
        from_slot = st.sbuf("from_slot", [P, B, TOPK], U32)

        shared_gu = st.sbuf("shared_gu", [P, DK, 2, F])
        shared_dn = st.sbuf("shared_dn", [P, len(FB), D])
        shared_hid = st.sbuf("shared_hid", [P, len(FB), T])

        with Stage(nc, "rt") as sr:
            token_rows = sr.sbuf("token_rows", [P, B, D])
            logits = sr.sbuf("logits", [N, B, E])
            w_r = sr.sbuf("w_r", [P, DK, E])
            b_r = sr.sbuf("b_r", [N, E])
            zeros = sr.sbuf("zeros", [P, STRIDE // P, D])
            scattered = sr.sem("scattered")
            shared_in = sr.sem("shared_in")
            filled = sr.sem("filled")
            with Stage(nc, "rn") as sn:
                norm = Norm(sn, ps[0], ps[1])
                loaded, zeroed, kept, score_mm, score_done, turned, rows_done = (
                    sn.sem(x) for x in ("loaded", "zeroed", "kept", "score_mm", "score_done", "turned", "rows_done"))
                with nc.Block() as block:
                    @block.sync
                    def _(sp):
                        sp.dma_start(w_r[:, :, :], router_w.rearrange("(k p) e -> p k e", p=P)).then_inc(loaded, 16)
                        sp.dma_start(b_r[:, :], router_b.to_broadcast([N, E])).then_inc(loaded, 16)
                        sp.dma_start(shared_gu[:, :, :, :], gate_up[E:E + 1, :, :, :, :].rearrange("e p k g f -> (e p) k g f"))\
                            .then_inc(shared_in, 16)
                        sp.dma_start(shared_dn[:, :, :], down[E:E + 1, :, :, :].rearrange("e p k n -> (e p) k n")).then_inc(shared_in, 16)
                        sp.wait_ge(loaded, 32)
                        sp.wait_ge(zeroed, 1)
                        for e in range(E + 1):
                            sp.dma_start(slots_in[e * STRIDE:(e + 1) * STRIDE, :].rearrange("(a p) d -> p a d", p=P),
                                         zeros[:, :, :]).then_inc(filled, 16)

                    @block.gpsimd
                    def _(pool):
                        nc.gpsimd.memset(zeros[:, :, :], 0.0).then_inc(zeroed, 1)
                        nc.gpsimd.memset(token_rows[:, :, :], 0.0)

                    @block.scalar
                    def _(act):
                        nc.scalar.preload_act_table_set(EXP_LN)
                sn.clear()

                def route(front, back, row):
                    with nc.Block(no_gpsimd_drain=True) as block:
                        @block.tensor
                        def _(pe):
                            if front is not None:
                                norm.tensor_mean(nc, pe, c["ones"], lambda k: h[:, k, front])
                            if back is not None:
                                for b in range(GB):
                                    for k in range(DK):
                                        mm = nc.tensor.matmul(ps[2][0:N, b * E:(b + 1) * E], norm.out[:, k, b * N:(b + 1) * N],
                                                              w_r[:, k, :], start=(k == 0), stop=(k == DK - 1))
                                mm.then_inc(score_mm, 1)
                                for b in range(GB):
                                    for k in range(DK):
                                        mm = nc.tensor.transpose(ps[3 + b // 2][0:N, (b % 2 * DK + k) * P:(b % 2 * DK + k + 1) * P],
                                                                 norm.out[:, k, b * N:(b + 1) * N], c["ident"][:, :])
                                    if b % 2:
                                        mm.then_inc(turned, 1)
                            if front is not None:
                                norm.tensor_var(nc, pe, c["ones"])

                        @block.scalar
                        def _(act):
                            if back is not None:
                                nc.scalar.activation(normed[:, :, back], norm.out[:, :, :], ACT.Copy).then_inc(kept, 1)
                            if front is not None:
                                norm.scalar(nc, act, c["eps"])
                            if back is not None:
                                for i in range(GB // 2):
                                    act.wait_ge(turned, i + 1)
                                    nc.scalar.activation(token_rows[0:N, bass.ds(row + 2 * i, 2), :],
                                                         ps[3 + i][0:N, :].rearrange("p (b d) -> p b d", b=2), ACT.Copy)\
                                        .then_inc(rows_done, 1)

                        @block.vector
                        def _(dve):
                            if front is not None:
                                norm.vector_centre(nc, dve, h[:, :, front])
                            if back is not None:
                                dve.wait_ge(score_mm, 1)
                                nc.vector.tensor_tensor(logits[:, bass.ds(row, GB), :],
                                                        ps[2][0:N, 0:GB * E].rearrange("p (b e) -> p b e", e=E),
                                                        b_r[:, :].unsqueeze(1).to_broadcast([N, GB, E]), ALU.add)\
                                    .then_inc(score_done, 1)
                                dve.wait_ge(kept, 1)
                                dve.wait_ge(turned, GB // 2)
                            if front is not None:
                                norm.vector_scale(nc, dve)
                    sn.clear()

                route(group_cols(0), None, 0)
                with nc.Fori(0, GROUPS - 1) as g:
                    route(group_cols(g + 1), group_cols(g), g * GB)
                route(None, group_cols(GROUPS - 1), (GROUPS - 1) * GB)

            with Stage(nc, "ch") as sc:
                tile = lambda x, shape=(N, B, E), dt=F32: sc.sbuf(x, list(shape), dt)
                small = lambda x: sc.sbuf(x, [N, B])
                ramp, shifted, ex, probs = tile("ramp", (N, E)), tile("shifted"), tile("ex"), tile("probs")
                top, idx = tile("top", (N, B, 8)), tile("idx", (N, B, 8), U32)
                hot = [tile("hot0"), tile("hot1")]
                both_hot, totals = tile("both_hot"), tile("totals", (N, E, B))
                fresh, upto, before = tile("fresh", (N, E, B)), tile("upto", (N, E, B)), tile("before", (N, E, B))
                place, hit = tile("place"), [tile("hit0"), tile("hit1")]
                earlier, every = sc.sbuf("earlier", [N, N]), sc.sbuf("every", [N, N])
                mx, sm, rs, wsum, wr_ = small("mx"), small("sm"), small("rs"), small("wsum"), small("wr")
                pos, base, inside, low, gat, far, sca, wk_ = ([small(f"{x}{k}") for k in range(TOPK)] for x in
                                                             ("pos", "base", "inside", "low", "gat", "far", "sca", "wk"))
                silu = sc.sbuf("silu", [P, 2, GT])
                made, step, counted, spread_ready, gate_mm, up_mm, silu_done, hid_done = (
                    sc.sem(x) for x in ("made", "step", "counted", "spread_ready", "gate_mm", "up_mm", "silu_done", "hid_done"))
                UNITS = [(g, f) for g in range(GROUPS) for f in range(len(FB))]
                with nc.Block() as block:
                    @block.gpsimd
                    def _(pool):
                        nc.gpsimd.iota(ramp[:, :], pattern=[[1, E]], base=0, channel_multiplier=0,
                                       allow_small_or_imprecise_dtypes=True)
                        nc.gpsimd.memset(every[:, :], 1.0)
                        nc.gpsimd.memset(fresh[:, :, :], 1.0)
                        nc.gpsimd.memset(to_slot[:, :, :], NOWHERE)
                        nc.gpsimd.memset(from_slot[:, :, :], NOWHERE)
                        nc.gpsimd.memset(earlier[:, :], 1.0).then_inc(made, 1)
                        pool.wait_ge(made, 1)
                        nc.gpsimd.memset(fresh[:, :, 0:1], 0.0)
                        nc.gpsimd.affine_select(out=earlier[:, :], in_=earlier[:, :], compare_op=ALU.is_gt, fill=0.0,
                                                base=0, pattern=[[1, N]], channel_multiplier=-1).then_inc(made, 1)
                        pool.wait_ge(spread_ready, TOPK)
                        pool.wait_ge(filled, 16 * (E + 1))
                        for b in range(B):
                            for k in range(TOPK):
                                nc.gpsimd.indirect_dma_start(
                                    out=slots_in[:, :], out_offset=bass.IndirectOffsetOnAxis(ap=to_slot[:, b, k:k + 1], axis=0),
                                    in_=token_rows[:, b, :], in_offset=None, bounds_check=(E + 1) * STRIDE - 1,
                                    oob_is_err=False).then_inc(scattered, 16)
                        pool.wait_ge(scattered, 16 * B * TOPK)

                    @block.scalar
                    def _(act):
                        act.wait_ge(step, 2)
                        nc.scalar.activation(ex[:, :, :], shifted[:, :, :], ACT.Exp).then_inc(counted, 1)
                        for u, (g, f) in enumerate(UNITS):
                            fn = FB[f][1]
                            act.wait_ge(gate_mm, u + 1)
                            if u >= 2:
                                act.wait_ge(hid_done, u - 1)
                            nc.scalar.activation(silu[0:fn, u % 2, :], ps[2 + u % 3][0:fn, 0:GT], ACT.Silu).then_inc(silu_done, 1)

                    @block.tensor
                    def _(pe):
                        pe.wait_ge(made, 2)
                        pe.wait_ge(step, 11 + 2 * B)
                        flat = both_hot[:, :, :].rearrange("p b e -> p (b e)")
                        nc.tensor.matmul(ps[0][0:N, :], earlier[:, :], flat, start=True, stop=True).then_inc(counted, 1)
                        nc.tensor.matmul(ps[1][0:N, :], every[:, :], flat, start=True, stop=True).then_inc(counted, 1)
                        pe.wait_ge(shared_in, 32)
                        for u, (g, f) in enumerate(UNITS):
                            f0, fn = FB[f]
                            if u >= 3:
                                pe.wait_ge(silu_done, u - 2)
                                pe.wait_ge(hid_done, u - 2)
                            for half, bank, done in ((0, ps[2 + u % 3], gate_mm), (1, ps[5 + u % 3], up_mm)):
                                for k in range(DK):
                                    mm = nc.tensor.matmul(bank[0:fn, 0:GT], shared_gu[:, k, half, f0:f0 + fn],
                                                          normed[:, k, g * GT:(g + 1) * GT], start=(k == 0), stop=(k == DK - 1))
                                mm.then_inc(done, 1)

                    @block.vector
                    def _(dve):
                        n = [0]

                        def count(ins):
                            n[0] += 1
                            ins.then_inc(step, 1)

                        def after(ins):
                            count(ins)
                            dve.wait_ge(step, n[0])

                        def wide(x):
                            return x[:, :].unsqueeze(2).to_broadcast([N, B, E])

                        V = nc.vector
                        after(V.tensor_reduce(mx[:, :], logits[:, :, :], AX.X, ALU.max))
                        after(V.tensor_tensor(shifted[:, :, :], logits[:, :, :], wide(mx), ALU.subtract))
                        dve.wait_ge(counted, 1)
                        after(V.tensor_reduce(sm[:, :], ex[:, :, :], AX.X, ALU.add))
                        after(V.reciprocal(rs[:, :], sm[:, :]))
                        after(V.tensor_tensor(probs[:, :, :], ex[:, :, :], wide(rs), ALU.mult))
                        for b in range(B):
                            count(V.max(top[:, b, :], probs[:, b, :]))
                        dve.wait_ge(step, n[0])
                        for b in range(B):
                            count(V.max_index(idx[:, b, :], top[:, b, :], probs[:, b, :]))
                        dve.wait_ge(step, n[0])
                        dve.wait_ge(made, 2)
                        after(V.tensor_tensor(wsum[:, :], top[:, :, 0], top[:, :, 1], ALU.add))
                        after(V.tensor_scalar(wsum[:, :], wsum[:, :], 1e-9, None, ALU.add))
                        after(V.reciprocal(wr_[:, :], wsum[:, :]))
                        for k in range(TOPK):
                            after(V.tensor_tensor(hot[k][:, :, :], ramp[:, :].unsqueeze(1).to_broadcast([N, B, E]),
                                                  idx[:, :, k:k + 1].to_broadcast([N, B, E]), ALU.is_equal))
                        after(V.tensor_tensor(both_hot[:, :, :], hot[0][:, :, :], hot[1][:, :, :], ALU.add))
                        dve.wait_ge(counted, 3)
                        after(V.tensor_copy(totals[:, :, :], ps[1][0:N, :].rearrange("p (b e) -> p e b", e=E)))
                        line = lambda x: x[:, :, :].rearrange("p e b -> p (e b)")
                        after(V.tensor_tensor_scan(line(upto), line(fresh), line(totals), 0.0, ALU.mult, ALU.add))
                        after(V.tensor_tensor(before[:, :, :], upto[:, :, :], totals[:, :, :], ALU.subtract))
                        after(V.tensor_tensor(place[:, :, :], ps[0][0:N, :].rearrange("p (b e) -> p b e", e=E),
                                              before[:, :, :].rearrange("p e b -> p b e"), ALU.add))
                        for k in range(TOPK):
                            after(V.tensor_tensor(hit[k][:, :, :], hot[k][:, :, :], place[:, :, :], ALU.mult))
                            after(V.tensor_reduce(pos[k][:, :], hit[k][:, :, :], AX.X, ALU.add))
                            after(V.tensor_scalar(base[k][:, :], idx[:, :, k], float(STRIDE), None, ALU.mult))
                            after(V.tensor_scalar(inside[k][:, :], pos[k][:, :], float(C), None, ALU.is_lt))
                            after(V.tensor_scalar(low[k][:, :], pos[k][:, :], float(C - 1), None, ALU.min))
                            after(V.scalar_tensor_tensor(out=gat[k][:, :], in0=idx[:, :, k], scalar=float(C), in1=low[k][:, :],
                                                         op0=ALU.mult, op1=ALU.add))
                            after(V.tensor_copy(from_slot[0:N, :, k], gat[k][:, :]))
                            after(V.tensor_tensor(low[k][:, :], low[k][:, :], base[k][:, :], ALU.add))
                            after(V.tensor_scalar(far[k][:, :], inside[k][:, :], -float(NOWHERE), float(NOWHERE), ALU.mult, ALU.add))
                            after(V.tensor_tensor(sca[k][:, :], far[k][:, :], low[k][:, :], ALU.add))
                            after(V.tensor_copy(to_slot[0:N, :, k], sca[k][:, :]))
                            after(V.tensor_tensor(wk_[k][:, :], top[:, :, k], wr_[:, :], ALU.mult))
                            V.tensor_tensor(share[:, :, k], wk_[k][:, :], inside[k][:, :], ALU.mult).then_inc(spread_ready, 1)
                        for u, (g, f) in enumerate(UNITS):
                            fn = FB[f][1]
                            dve.wait_ge(silu_done, u + 1)
                            dve.wait_ge(up_mm, u + 1)
                            nc.vector.tensor_tensor(shared_hid[0:fn, f, g * GT:(g + 1) * GT], silu[0:fn, u % 2, :],
                                                    ps[5 + u % 3][0:fn, 0:GT], ALU.mult).then_inc(hid_done, 1)
                sr.clear(pool_dmas=True)
                sc.clear()

        w_gu = [st.sbuf(f"w_gu{i}", [P, DK, 2, F]) for i in range(2)]
        w_dn = [st.sbuf(f"w_dn{i}", [P, len(FB), D]) for i in range(2)]

        def fetch_weights(sp, e, i, done):
            sp.dma_start(w_gu[i][:, :, :, :], gate_up[bass.ds(e, 1), :, :, :, :].rearrange("e p k g f -> (e p) k g f"))\
                .then_inc(done, 16)
            sp.dma_start(w_dn[i][:, :, :], down[bass.ds(e, 1), :, :, :].rearrange("e p k n -> (e p) k n")).then_inc(done, 16)

        with Stage(nc, "xp") as sx:
            rows_in = [sx.sbuf(f"rows_in{i}", [P, NT, D]) for i in range(2)]
            xT = [sx.sbuf(f"xT{i}", [P, DK, C]) for i in range(2)]
            silu = sx.sbuf("silu", [P, 2, HALVES[0][1]])
            hid = [sx.sbuf(f"hid{i}", [P, len(FB), C]) for i in range(2)]
            rows_out = [sx.sbuf(f"rows_out{i}", [P, NT, D]) for i in range(2)]
            landed = [sx.sem(f"landed{i}") for i in range(2)]
            stored = [sx.sem(f"stored{i}") for i in range(2)]
            turned, xT_done, gate_mm, up_mm, silu_done, hid_done, down_mm, out_done = (
                sx.sem(x) for x in ("turned", "xT_done", "gate_mm", "up_mm", "silu_done", "hid_done", "down_mm", "out_done"))
            NF = len(FB)
            FULL = NT - 1
            LAST = TILES[-1][1]
            EI = 4
            O_BANK = (7, 5, 7)
            OUTS = len(O_BANK)

            def fetch(sp, e, i):
                fetch_weights(sp, e, i, landed[i])
                sp.dma_start(rows_in[i][:, 0:FULL, :], slots_in[bass.ds(e * STRIDE, FULL * P), :].rearrange("(a p) d -> p a d", p=P))\
                    .then_inc(landed[i], 16)
                sp.dma_start(rows_in[i][0:LAST, FULL, :], slots_in[bass.ds(e * STRIDE + FULL * P, LAST), :]).then_inc(landed[i], 16)

            with nc.Block() as block:
                @block.sync
                def _(sp):
                    fetch(sp, 0, 0)
                    sp.wait_ge(landed[0], 64)
            sx.clear()
            with nc.Fori(0, E // EI) as g:
                with nc.Block(no_gpsimd_drain=True) as block:
                    @block.sync
                    def _(sp):
                        fetch(sp, g * EI + 1, 1)
                        for i in range(EI):
                            if i + 2 <= EI:
                                sp.wait_ge(down_mm, OUTS * (i + 1))
                                fetch(sp, g * EI + i + 2, i % 2)
                            sp.wait_ge(out_done, OUTS * (i + 1))
                            e = g * EI + i
                            sp.dma_start(slots_out[bass.ds(e * C, FULL * P), :].rearrange("(a p) d -> p a d", p=P),
                                         rows_out[i % 2][:, 0:FULL, :]).then_inc(stored[i % 2], 16)
                            sp.dma_start(slots_out[bass.ds(e * C + FULL * P, LAST), :], rows_out[i % 2][0:LAST, FULL, :])\
                                .then_inc(stored[i % 2], 16)
                        sp.wait_ge(landed[0], 64 * EI // 2)
                        for i in range(2):
                            sp.wait_ge(stored[i], 32 * EI // 2)

                    @block.tensor
                    def _(pe):
                        def turn(i):
                            if i:
                                pe.wait_ge(landed[i % 2], 64 * ((i + 1) // 2))
                                pe.wait_ge(xT_done, 3 * i)
                            for t in range(NT):
                                for k in range(DK):
                                    r = TILES[t][1]
                                    dst = ps[k][:, t * P:(t + 1) * P] if t < FULL else ps[2][:, k * LAST:(k + 1) * LAST]
                                    mm = nc.tensor.transpose(dst, rows_in[i % 2][0:r, t, k * P:(k + 1) * P], c["ident"][0:r, 0:r])
                            mm.then_inc(turned, 1)

                        turn(0)
                        for i in range(EI):
                            pe.wait_ge(xT_done, 3 * i + 3)
                            for hf, (c0, cn) in enumerate(HALVES):
                                for f, (f0, fn) in enumerate(FB):
                                    u = (i * 2 + hf) * NF + f
                                    if u >= 2:
                                        pe.wait_ge(silu_done, u - 1)
                                    for k in range(DK):
                                        mm = nc.tensor.matmul(ps[3 + u % 2][0:fn, 0:cn], w_gu[i % 2][:, k, 0, f0:f0 + fn],
                                                              xT[i % 2][:, k, c0:c0 + cn], start=(k == 0), stop=(k == DK - 1))
                                    mm.then_inc(gate_mm, 1)
                                    if u >= 2:
                                        pe.wait_ge(hid_done, u - 1)
                                    if i and u % 2 == 0:
                                        pe.wait_ge(out_done, OUTS * i - 1)
                                    for k in range(DK):
                                        mm = nc.tensor.matmul(ps[5 + u % 2][0:fn, 0:cn], w_gu[i % 2][:, k, 1, f0:f0 + fn],
                                                              xT[i % 2][:, k, c0:c0 + cn], start=(k == 0), stop=(k == DK - 1))
                                    mm.then_inc(up_mm, 1)
                            if i + 1 < EI:
                                turn(i + 1)
                            pe.wait_ge(hid_done, (i + 1) * 2 * NF)
                            for t, (t0, r) in enumerate(TILES):
                                o = t // 2
                                if t % 2 == 0 and (i or o == 2):
                                    pe.wait_ge(out_done, OUTS * i + (0, 0, 1)[o])
                                for f, (f0, fn) in enumerate(FB):
                                    mm = nc.tensor.matmul(ps[O_BANK[o]][0:r, (t % 2) * D:(t % 2 + 1) * D], hid[i % 2][0:fn, f, t0:t0 + r],
                                                          w_dn[i % 2][0:fn, f, :], start=(f == 0), stop=(f == NF - 1))
                                if t % 2 or t == NT - 1:
                                    mm.then_inc(down_mm, 1)

                    @block.scalar
                    def _(act):
                        for i in range(EI):
                            act.wait_ge(turned, i + 1)
                            for k in range(DK):
                                nc.scalar.activation(xT[i % 2][:, k, 0:FULL * P], ps[k][:, :], ACT.Copy).then_inc(xT_done, 1)
                            nc.scalar.activation(xT[i % 2][:, :, FULL * P:C], ps[2][:, 0:DK * LAST].rearrange("p (k r) -> p k r", k=DK),
                                                 ACT.Copy).then_inc(xT_done, 1)
                            for u in range(2 * NF * i, 2 * NF * (i + 1)):
                                hf, f = u // NF % 2, u % NF
                                cn, fn = HALVES[hf][1], FB[f][1]
                                act.wait_ge(gate_mm, u + 1)
                                if u >= 2:
                                    act.wait_ge(hid_done, u - 1)
                                nc.scalar.activation(silu[0:fn, u % 2, 0:cn], ps[3 + u % 2][0:fn, 0:cn], ACT.Silu).then_inc(silu_done, 1)

                    @block.vector
                    def _(dve):
                        for i in range(EI):
                            for u in range(2 * NF * i, 2 * NF * (i + 1)):
                                hf, f = u // NF % 2, u % NF
                                (c0, cn), fn = HALVES[hf], FB[f][1]
                                dve.wait_ge(silu_done, u + 1)
                                dve.wait_ge(up_mm, u + 1)
                                nc.vector.tensor_tensor(hid[i % 2][0:fn, f, c0:c0 + cn], silu[0:fn, u % 2, 0:cn],
                                                        ps[5 + u % 2][0:fn, 0:cn], ALU.mult).then_inc(hid_done, 1)
                            if i >= 2:
                                dve.wait_ge(stored[i % 2], 32 * (i // 2))
                            for q in range(OUTS):
                                r = P if q < OUTS - 1 else LAST
                                tiles = 2 if q < OUTS - 1 else 1
                                dve.wait_ge(down_mm, OUTS * i + q + 1)
                                nc.vector.tensor_copy(rows_out[i % 2][0:r, 2 * q:2 * q + tiles, :],
                                                      ps[O_BANK[q]][0:r, 0:tiles * D].rearrange("p (t d) -> p t d", d=D)).then_inc(out_done, 1)
                sx.clear()

        with Stage(nc, "sh") as ss:
            now_slot = ss.sbuf("now_slot", [P, GB * TOPK], U32)
            now_share = ss.sbuf("now_share", [N, GB * TOPK])
            got = [[ss.sbuf(f"got{b}{k}", [P, D]) for k in range(TOPK)] for b in range(GB)]
            part = ss.sbuf("part", [N, GB, D])
            mixed = ss.sbuf("mixed", [N, GB, D])
            hn = ss.sbuf("hn", [P, DK, GT])
            NF = len(FB)
            gathered = [ss.sem(f"gathered{b}") for b in range(GB)]
            slot_done, share_done, part_done, mixed_done, sum_mm, hn_done, res_done = (
                ss.sem(x) for x in ("slot_done", "share_done", "part_done", "mixed_done", "sum_mm", "hn_done", "res_done"))
            with nc.Fori(0, GROUPS) as g:
                with nc.Block(no_gpsimd_drain=True) as block:
                    @block.gpsimd
                    def _(pool):
                        pool.wait_ge(slot_done, 1)
                        for b in range(GB):
                            for k in range(TOPK):
                                nc.gpsimd.indirect_dma_start(
                                    out=got[b][k][:, :], out_offset=None, in_=slots_out[:, :],
                                    in_offset=bass.IndirectOffsetOnAxis(ap=now_slot[:, b * TOPK + k:b * TOPK + k + 1], axis=0),
                                    bounds_check=E * C - 1, oob_is_err=False).then_inc(gathered[b], 16)
                        for b in range(GB):
                            pool.wait_ge(gathered[b], 16 * TOPK)

                    @block.tensor
                    def _(pe):
                        for m in range(DK):
                            for f, (f0, fn) in enumerate(FB):
                                nc.tensor.matmul(ps[6 + m][:, 0:GT], shared_dn[0:fn, f, m * P:(m + 1) * P],
                                                 shared_hid[0:fn, f, group_cols(g)], start=(f == 0), stop=False, skip_group_check=True)
                        for b in range(GB):
                            pe.wait_ge(mixed_done, b + 1)
                            for m in range(DK):
                                mm = nc.tensor.matmul(ps[6 + m][:, b * N:(b + 1) * N], mixed[:, b, m * P:(m + 1) * P],
                                                      c["ident"][0:N, 0:N], start=False, stop=(b == GB - 1), skip_group_check=True)
                        mm.then_inc(sum_mm, 1)

                    @block.vector
                    def _(dve):
                        nc.vector.tensor_copy(now_slot[:, :], from_slot[:, bass.ds(g * GB, GB), :].rearrange("p b k -> p (b k)"))\
                            .then_inc(slot_done, 1)
                        nc.vector.tensor_copy(now_share[:, :], share[:, bass.ds(g * GB, GB), :].rearrange("p b k -> p (b k)"))\
                            .then_inc(share_done, 1)
                        nc.vector.tensor_tensor(hn[:, :, :], h[:, :, group_cols(g)], normed[:, :, group_cols(g)], ALU.add)\
                            .then_inc(hn_done, 1)
                        dve.wait_ge(share_done, 1)
                        for b in range(GB):
                            dve.wait_ge(gathered[b], 16 * TOPK)
                            nc.vector.tensor_scalar(part[:, b, :], got[b][0][0:N, :], now_share[:, 2 * b:2 * b + 1], None, ALU.mult)\
                                .then_inc(part_done, 1)
                            dve.wait_ge(part_done, b + 1)
                            nc.vector.scalar_tensor_tensor(out=mixed[:, b, :], in0=got[b][1][0:N, :],
                                                           scalar=now_share[:, 2 * b + 1:2 * b + 2], in1=part[:, b, :],
                                                           op0=ALU.mult, op1=ALU.add).then_inc(mixed_done, 1)
                        dve.wait_ge(sum_mm, 1)
                        dve.wait_ge(hn_done, 1)
                        for m in range(DK):
                            nc.vector.tensor_tensor(h[:, m, group_cols(g)], ps[6 + m][:, 0:GT], hn[:, m, :], ALU.add)\
                                .then_inc(res_done, 1)
                ss.clear(pool_dmas=True)


def mamba(nc, h, c, params):
    INNER = params[0]["in_t"].shape[1] // 2
    IB = INNER // P
    S = params[0]["a_log"].shape[2]
    R = params[0]["dt_t"].shape[0]
    TAPS = params[0]["conv_w"].shape[2]
    BC = 2 * S
    PARTS = 3
    DT0 = PARTS * BC
    JS = 2
    STEPS = S * IB
    NB = 4
    CB = 4

    with Stage(nc, "ssm_late") as sl, Stage(nc, "ssm") as st:
        late = sl.sem("late")
        w_in = [st.sbuf(f"w_in{d}", [P, DK, 2 * INNER]) for d in range(2)]
        w_xp = [st.sbuf(f"w_xp{d}", [P, IB, DT0 + R]) for d in range(2)]
        w_dt = [st.sbuf(f"w_dt{d}", [R + 1, INNER]) for d in range(2)]
        w_out = [st.sbuf(f"w_out{d}", [P, IB, D]) for d in range(2)]
        conv_w = [st.sbuf(f"conv_w{d}", [P, IB, TAPS]) for d in range(2)]
        conv_b, skip = ([st.sbuf(f"{x}{d}", [P, IB]) for d in range(2)] for x in ("conv_b", "skip"))
        decay = [st.sbuf(f"decay{d}", [P, IB, S]) for d in range(2)]
        pick = st.sbuf("pick", [DT0, BC, P], BF16)
        dA = [st.sbuf(f"dA{d}", [P, NB, GT]) for d in range(2)]
        one = st.sbuf("one", [P, 1])
        ps = [st.psum(f"ps{i}") for i in range(8)]
        Y_BANK, B_BANK, C_BANK, X_BANK, Z_BANK = ps[0:2], ps[2:4], ps[4:6], ps[6], ps[7]
        norm = Norm(st, X_BANK, X_BANK)
        conv = st.sbuf("conv", [P, IB, GT])
        y = st.sbuf("y", [P, JS, GT])
        xc, z, step, du = ([st.sbuf(f"{x}{d}", [P, IB, GT]) for d in range(2)] for x in ("xc", "z", "step", "du"))
        parts = [st.sbuf(f"parts{d}", [DT0, GT], BF16) for d in range(2)]
        rest = st.sbuf("rest", [DT0, GT])
        dt_in = st.sbuf("dt_in", [R + 1, GT])
        mag = norm.square
        bc = st.sbuf("bc", [P, CB, GT])
        dBu = st.sbuf("dBu", [P, NB, GT])
        hs = st.sbuf("hs", [P, NB, GT])
        hc = st.sbuf("hc", [P, NB, GT])
        yz = st.sbuf("yz", [P, IB, GT])
        names = ("w_loaded", "zeros", "picked", "expd", "decay_done",
                 "x_mm", "z_mm", "conv_step", "z_raw", "xc_done", "z_done", "xp_done", "hi_done", "dt_in_done", "rest_done",
                 "mid_done", "lo_done", "dt_mm", "mag_done", "ea_done", "sp_done", "step_done", "du_done",
                 "b_mm", "c_mm", "bc_done", "dA_done", "dbu_dve", "dbu_pool",
                 "scan_done", "hc_done", "y_mm", "y_done", "yz_pool", "yz_done", "o_mm", "res_done")
        s = {x: st.sem(x) for x in names}
        with nc.Block() as block:
            @block.sync
            def _(sp):
                for d in range(2):
                    sp.dma_start(decay[d][:, :, :], params[d]["a_log"]).then_inc(s["w_loaded"], 16)
                for d in range(2):
                    done = (s["w_loaded"], late)[d]
                    xproj = params[d]["xproj_t"].rearrange("(k p) n -> p k n", p=P)
                    sp.dma_start(w_in[d][:, :, :], params[d]["in_t"].rearrange("(k p) n -> p k n", p=P)).then_inc(done, 16)
                    sp.dma_start(conv_w[d][:, :, :], params[d]["conv_w"]).then_inc(done, 16)
                    sp.dma_start(conv_b[d][:, :], params[d]["conv_b"]).then_inc(done, 16)
                    for r in range(PARTS):
                        sp.dma_start(w_xp[d][:, :, r * BC:(r + 1) * BC], xproj[:, :, R:R + BC]).then_inc(done, 16)
                    sp.dma_start(w_xp[d][:, :, DT0:DT0 + R], xproj[:, :, 0:R]).then_inc(done, 16)
                    sp.dma_start(w_dt[d][0:R, :], params[d]["dt_t"]).then_inc(done, 16)
                    sp.dma_start(w_dt[d][R:R + 1, :], params[d]["dt_b"]).then_inc(done, 16)
                    sp.dma_start(skip[d][:, :], params[d]["d"]).then_inc(done, 16)
                for d in range(2):
                    sp.dma_start(w_out[d][:, :, :], params[d]["out_t"].rearrange("(k p) n -> p k n", p=P)).then_inc(late, 16)
                sp.wait_ge(s["w_loaded"], (2 + 7 + PARTS) * 16)

            @block.gpsimd
            def _(pool):
                nc.gpsimd.memset(dA[0][:, :, :], 0.0)
                nc.gpsimd.memset(dA[1][:, :, :], 0.0)
                nc.gpsimd.memset(one[:, :], 1.0)
                nc.gpsimd.memset(dt_in[:, :], 1.0)
                nc.gpsimd.memset(pick[:, :, :], 0.0).then_inc(s["zeros"], 1)
                for r in range(PARTS):
                    pool.wait_ge(s["zeros"], r + 1)
                    nc.gpsimd.affine_select(out=pick[:, :, :], in_=pick[:, :, :], compare_op=ALU.not_equal, fill=1.0,
                                            base=-r * BC, pattern=[[-1, BC], [0, P]], channel_multiplier=1).then_inc(s["zeros"], 1)

            @block.scalar
            def _(act):
                nc.scalar.preload_act_table_set(EXP_LN)
                act.wait_ge(s["w_loaded"], (2 + 7 + PARTS) * 16)
                for d in range(2):
                    nc.scalar.activation(decay[d][:, :, :], decay[d][:, :, :], ACT.Exp).then_inc(s["expd"], 1)

            @block.vector
            def _(dve):
                dve.wait_ge(s["expd"], 2)
                for d in range(2):
                    nc.vector.tensor_scalar(decay[d][:, :, :], decay[d][:, :, :], -1.0, None, ALU.mult)\
                        .then_inc(s["decay_done"], 1)
        st.clear()

        def rows(ap):
            return ap.rearrange("p (b n) -> p b n", n=N)

        def flow(ap, d):
            return ap if d == 0 else ap[:, ::-1]

        def recurrence(i):
            q = i // JS
            return q, q % S, q // S * JS + i % JS

        def by_pool(i):
            return i % 4 != 0

        pool_upto = [sum(by_pool(j) for j in range(i + 1)) for i in range(STEPS)]
        dve_upto = [i + 1 - pool_upto[i] for i in range(STEPS)]

        MEAN, CENTRE, SQUARE, VAR, RSTD, SCALE = -1, 1, 4, 4, 9, 10
        OUT_MM, RES = (2, 7), (6, 13)
        X_MM = [12 + 6 * m for m in range(IB)]
        Z_MM = [15 + 6 * m for m in range(IB)]
        TAP = [17 + 6 * m for m in range(IB)]
        CONV = [15 + 6 * m for m in range(IB)]
        Z_RAW = [20 + 6 * m for m in range(IB)]
        XC = (29, 40)
        XP_MM, HI, REST, MID, LO = 41, 47, 48, 52, 53
        DT_MM = (49, 50, 55, 57)
        SOFTPLUS = (53, 55, 59, 61)
        STEP = (54, 56, 60, 62)
        DU = (59, 61, 63, 63)
        GATE = (STEPS // 2 + 6, STEPS // 2 + 8)
        Z_SILU = STEPS - 1

        def half(d, rec, front, norm_in, out_cols):
            f = 1 - d
            with nc.Block(no_gpsimd_drain=True) as block:
                @block.sync
                def _(sp):
                    if front and not rec:
                        sp.wait_ge(late, (7 + PARTS + 2) * 16)

                @block.tensor
                def _(pe):
                    def spread_b(q):
                        if q >= 2:
                            pe.wait_ge(s["bc_done"], q - 1)
                        nc.tensor.matmul(B_BANK[q % 2][:, 0:GT], pick[:, q % S, :], parts[d][:, :], start=True, stop=True)\
                            .then_inc(s["b_mm"], 1)

                    def spread_c(q):
                        if q >= 2:
                            pe.wait_ge(s["hc_done"], JS * (q - 1))
                        nc.tensor.matmul(C_BANK[q % 2][:, 0:GT], pick[:, S + q % S, :], parts[d][:, :], start=True, stop=True)\
                            .then_inc(s["c_mm"], 1)

                    def beside(i):
                        if norm_in is not None and i == MEAN:
                            norm.tensor_mean(nc, pe, c["ones"], lambda k: h[:, k, norm_in])
                        if norm_in is not None and i == VAR:
                            norm.tensor_var(nc, pe, c["ones"])
                        if out_cols is not None and i in OUT_MM:
                            m = OUT_MM.index(i)
                            if m:
                                pe.wait_ge(s["res_done"], m)
                            for k in range(IB):
                                mm = nc.tensor.matmul(Z_BANK[:, 0:GT], w_out[f][:, k, m * P:(m + 1) * P], yz[:, k, :],
                                                      start=(k == 0), stop=(k == IB - 1))
                            mm.then_inc(s["o_mm"], 1)
                        if not front:
                            return
                        if i in X_MM:
                            m = X_MM.index(i)
                            if m:
                                pe.wait_ge(s["conv_step"], TAPS * m)
                            elif norm_in is not None:
                                pe.wait_ge(norm.ready, 1)
                            for k in range(DK):
                                mm = nc.tensor.matmul(X_BANK[:, 0:GT], w_in[f][:, k, m * P:(m + 1) * P], norm.out[:, k, :],
                                                      start=(k == 0), stop=(k == DK - 1))
                            mm.then_inc(s["x_mm"], 1)
                        if i in Z_MM:
                            m = Z_MM.index(i)
                            if m:
                                pe.wait_ge(s["z_raw"], m)
                            elif out_cols is not None:
                                pe.wait_ge(s["res_done"], DK)
                            for k in range(DK):
                                mm = nc.tensor.matmul(Z_BANK[:, 0:GT], w_in[f][:, k, INNER + m * P:INNER + (m + 1) * P],
                                                      norm.out[:, k, :], start=(k == 0), stop=(k == DK - 1))
                            mm.then_inc(s["z_mm"], 1)
                        if i == XP_MM:
                            pe.wait_ge(s["xc_done"], IB)
                            pe.wait_ge(s["conv_step"], TAPS * IB)
                            for k in range(IB):
                                mm = nc.tensor.matmul(X_BANK[0:DT0 + R, 0:GT], w_xp[f][:, k, :], xc[f][:, k, :],
                                                      start=(k == 0), stop=(k == IB - 1))
                            mm.then_inc(s["xp_done"], 1)
                        if i in DT_MM:
                            m = DT_MM.index(i)
                            if m == 0:
                                pe.wait_ge(s["dt_in_done"], 1)
                                pe.wait_ge(s["z_raw"], IB)
                            elif m == 1:
                                pe.wait_ge(s["rest_done"], 1)
                            else:
                                pe.wait_ge(s["step_done"], m - 1)
                            nc.tensor.matmul((Z_BANK, X_BANK)[m % 2][:, 0:GT], w_dt[f][:, m * P:(m + 1) * P], dt_in[:, :],
                                             start=True, stop=True).then_inc(s["dt_mm"], 1)

                    if rec:
                        spread_b(0)
                        spread_b(1)
                        spread_c(0)
                        spread_c(1)
                    beside(-1)
                    for i in range(STEPS):
                        q, n, j = recurrence(i)
                        if rec:
                            if q == 0:
                                spread_b(2 + i)
                            pe.wait_ge(s["hc_done"], i + 1)
                            if n == 0 and j >= JS:
                                pe.wait_ge(s["y_done"], j - JS + 1)
                            nc.tensor.matmul(Y_BANK[j % JS][:, 0:GT], c["ident"][:, :], hc[:, i % NB, :],
                                             start=(n == 0), stop=(n == S - 1)).then_inc(s["y_mm"], 1)
                            if i % JS == JS - 1:
                                if q + 4 < STEPS // JS:
                                    spread_b(q + 4)
                                if q + 2 < STEPS // JS:
                                    spread_c(q + 2)
                        beside(i)

                @block.scalar
                def _(act):
                    def input_row(q):
                        act.wait_ge(s["b_mm"], q + 1)
                        if q >= CB:
                            act.wait_ge(s["dbu_pool"], pool_upto[JS * (q - CB + 1) - 1])
                            act.wait_ge(s["dbu_dve"], dve_upto[JS * (q - CB + 1) - 1])
                        nc.scalar.activation(bc[:, q % CB, :], B_BANK[q % 2][:, 0:GT], ACT.Copy).then_inc(s["bc_done"], 1)

                    def beside(i):
                        if norm_in is not None and i == SQUARE:
                            act.wait_ge(norm.centred_ready, 1)
                            nc.scalar.activation(norm.square[:, :, :], norm.centred[:, :, :], ACT.Square)\
                                .then_inc(norm.square_ready, 1)
                        if norm_in is not None and i == RSTD:
                            act.wait_ge(norm.var_ready, 1)
                            nc.scalar.activation(norm.log_var[:, :], norm.var_ps[:, 0:GT], ACT.Ln, bias=c["eps"][:, 0:1])\
                                .then_inc(norm.log_ready, 1)
                            act.wait_ge(norm.log_ready, 1)
                            nc.scalar.activation(norm.rstd[:, :], norm.log_var[:, :], ACT.Exp, scale=-0.5)\
                                .then_inc(norm.rstd_ready, 1)
                        if not front:
                            return
                        if i in TAP:
                            m = TAP.index(i)
                            act.wait_ge(s["x_mm"], m + 1)
                            nc.scalar.activation(conv[:, m, :], X_BANK[:, 0:GT], ACT.Identity, bias=conv_b[f][:, m:m + 1],
                                                 scale=conv_w[f][:, m, TAPS - 1:TAPS]).then_inc(s["conv_step"], 1)
                        if i in Z_RAW:
                            m = Z_RAW.index(i)
                            act.wait_ge(s["z_mm"], m + 1)
                            nc.scalar.activation(z[f][:, m, :], Z_BANK[:, 0:GT], ACT.Copy).then_inc(s["z_raw"], 1)
                        if i in XC:
                            m0 = XC.index(i) * IB // 2
                            act.wait_ge(s["conv_step"], TAPS * (m0 + IB // 2))
                            nc.scalar.activation(xc[f][:, m0:m0 + IB // 2, :], conv[:, m0:m0 + IB // 2, :], ACT.Silu)\
                                .then_inc(s["xc_done"], IB // 2)
                            nc.scalar.preload_act_table_set(EXP_LN)
                        if i == Z_SILU:
                            act.wait_ge(s["z_raw"], IB)
                            nc.scalar.activation(z[f][:, :, :], z[f][:, :, :], ACT.Silu).then_inc(s["z_done"], IB)
                            nc.scalar.preload_act_table_set(EXP_LN)
                        if i == HI:
                            act.wait_ge(s["xp_done"], 1)
                            nc.scalar.activation(dt_in[0:R, :], X_BANK[DT0:DT0 + R, 0:GT], ACT.Copy).then_inc(s["dt_in_done"], 1)
                            nc.scalar.activation(parts[f][:, :], X_BANK[0:DT0, 0:GT], ACT.Copy).then_inc(s["hi_done"], 1)
                        if i == MID:
                            act.wait_ge(s["rest_done"], 1)
                            nc.scalar.activation(parts[f][0:2 * BC, :], rest[0:2 * BC, :], ACT.Copy).then_inc(s["mid_done"], 1)
                        if i in SOFTPLUS:
                            m = SOFTPLUS.index(i)
                            act.wait_ge(s["dt_mm"], m + 1)
                            nc.scalar.activation(mag[:, m % 2, :], (Z_BANK, X_BANK)[m % 2][:, 0:GT], ACT.Abs).then_inc(s["mag_done"], 1)
                            act.wait_ge(s["mag_done"], m + 1)
                            nc.scalar.activation(mag[:, m % 2, :], mag[:, m % 2, :], ACT.Exp, scale=-1.0).then_inc(s["ea_done"], 1)
                            act.wait_ge(s["ea_done"], m + 1)
                            nc.scalar.activation(step[f][:, m, :], mag[:, m % 2, :], ACT.Ln, bias=one[:, 0:1]).then_inc(s["sp_done"], 1)

                    for i in range(STEPS):
                        q, n, j = recurrence(i)
                        if rec:
                            if i == 0:
                                input_row(0)
                            if i % JS == 0 and i // JS + 1 < STEPS // JS:
                                input_row(i // JS + 1)
                            if i >= NB:
                                act.wait_ge(s["scan_done"], i - NB + 1)
                            lo = 1 if d == 0 else 0
                            nc.scalar.activation(rows(dA[d][:, i % NB, :])[:, :, lo:lo + N - 1],
                                                 rows(step[d][:, j, :])[:, :, lo:lo + N - 1], ACT.Exp,
                                                 scale=decay[d][:, j, n:n + 1]).then_inc(s["dA_done"], 1)
                        beside(i)

                @block.gpsimd
                def _(pool):
                    for i in range(STEPS):
                        q, n, j = recurrence(i)
                        if rec and by_pool(i):
                            pool.wait_ge(s["bc_done"], q + 1)
                            if i >= NB:
                                pool.wait_ge(s["scan_done"], i - NB + 1)
                            nc.gpsimd.tensor_tensor(dBu[:, i % NB, :], du[d][:, j, :], bc[:, q % CB, :], ALU.mult)\
                                .then_inc(s["dbu_pool"], 1)
                        for j in range(JS):
                            if rec and i == GATE[j]:
                                pool.wait_ge(s["y_done"], j + 1)
                                if j == 0 and out_cols is not None:
                                    pool.wait_ge(s["o_mm"], DK)
                                nc.gpsimd.tensor_tensor(yz[:, j, :], y[:, j, :], z[d][:, j, :], ALU.mult).then_inc(s["yz_pool"], 1)
                        for m in range(IB):
                            if front and i == DU[m]:
                                pool.wait_ge(s["step_done"], m + 1)
                                pool.wait_ge(s["xc_done"], IB)
                                nc.gpsimd.tensor_tensor(du[f][:, m, :], step[f][:, m, :], xc[f][:, m, :], ALU.mult)\
                                    .then_inc(s["du_done"], 1)
                    if front:
                        pool.wait_ge(s["du_done"], IB)

                @block.vector
                def _(dve):
                    def input_term(i):
                        q, n, j = recurrence(i)
                        dve.wait_ge(s["bc_done"], q + 1)
                        if i >= NB:
                            dve.wait_ge(s["scan_done"], i - NB + 1)
                        nc.vector.tensor_tensor(dBu[:, i % NB, :], du[d][:, j, :], bc[:, q % CB, :], ALU.mult)\
                            .then_inc(s["dbu_dve"], 1)

                    def recur(i):
                        if not by_pool(i):
                            dve.wait_ge(s["dbu_dve"], dve_upto[i])
                        else:
                            dve.wait_ge(s["dbu_pool"], pool_upto[i])
                        dve.wait_ge(s["dA_done"], i + 1)
                        if i >= NB:
                            dve.wait_ge(s["hc_done"], i - NB + 1)
                        nc.vector.tensor_tensor_scan(flow(hs[:, i % NB, :], d), flow(dA[d][:, i % NB, :], d),
                                                     flow(dBu[:, i % NB, :], d), 0.0, ALU.mult, ALU.add).then_inc(s["scan_done"], 1)

                    def output_term(i):
                        q, n, j = recurrence(i)
                        dve.wait_ge(s["scan_done"], i + 1)
                        dve.wait_ge(s["c_mm"], q + 1)
                        if i >= NB:
                            dve.wait_ge(s["y_mm"], i - NB + 1)
                        nc.vector.tensor_tensor(hc[:, i % NB, :], hs[:, i % NB, :], C_BANK[q % 2][:, 0:GT], ALU.mult)\
                            .then_inc(s["hc_done"], 1)

                    def tap(m, t):
                        src, dst = rows(X_BANK[:, 0:GT]), rows(conv[:, m, :])
                        src, dst = ((src[:, :, 0:N - t], dst[:, :, t:N]) if f == 0 else
                                    (src[:, :, t:N], dst[:, :, 0:N - t]))
                        dve.wait_ge(s["conv_step"], TAPS * m + t)
                        nc.vector.scalar_tensor_tensor(out=dst, in0=src, scalar=conv_w[f][:, m, TAPS - 1 - t:TAPS - t],
                                                       in1=dst, op0=ALU.mult, op1=ALU.add).then_inc(s["conv_step"], 1)

                    def beside(i):
                        if norm_in is not None and i == CENTRE:
                            dve.wait_ge(norm.mean_ready, 1)
                            nc.vector.tensor_tensor(norm.centred[:, :, :], h[:, :, norm_in],
                                                    norm.mean_ps[:, 0:GT].unsqueeze(1).to_broadcast([P, DK, GT]),
                                                    ALU.subtract).then_inc(norm.centred_ready, 1)
                        if norm_in is not None and i == SCALE:
                            dve.wait_ge(norm.rstd_ready, 1)
                            dve.wait_ge(norm.centred_ready, 1)
                            nc.vector.tensor_tensor(norm.out[:, :, :], norm.centred[:, :, :],
                                                    norm.rstd[:, :].unsqueeze(1).to_broadcast([P, DK, GT]),
                                                    ALU.mult).then_inc(norm.ready, 1)
                        if out_cols is not None and i in RES:
                            m = RES.index(i)
                            dve.wait_ge(s["o_mm"], m + 1)
                            nc.vector.tensor_tensor(h[:, m, out_cols], Z_BANK[:, 0:GT], h[:, m, out_cols], ALU.add)\
                                .then_inc(s["res_done"], 1)
                        if not front:
                            return
                        for m in range(IB):
                            if CONV[m] < i < CONV[m] + TAPS:
                                tap(m, i - CONV[m])
                        if i == REST:
                            dve.wait_ge(s["hi_done"], 1)
                            nc.vector.tensor_tensor(rest[:, :], X_BANK[0:DT0, 0:GT], parts[f][:, :], ALU.subtract)\
                                .then_inc(s["rest_done"], 1)
                        if i == LO:
                            dve.wait_ge(s["mid_done"], 1)
                            nc.vector.tensor_tensor(parts[f][0:BC, :], rest[0:BC, :], parts[f][0:BC, :], ALU.subtract)\
                                .then_inc(s["lo_done"], 1)
                        if i in STEP:
                            m = STEP.index(i)
                            dve.wait_ge(s["sp_done"], m + 1)
                            nc.vector.scalar_tensor_tensor(out=step[f][:, m, :], in0=(Z_BANK, X_BANK)[m % 2][:, 0:GT], scalar=0.0,
                                                           in1=step[f][:, m, :], op0=ALU.max, op1=ALU.add).then_inc(s["step_done"], 1)

                    def collect(j):
                        dve.wait_ge(s["y_mm"], STEPS // IB * JS * (j // JS + 1) - JS + j % JS + 1)
                        if j >= JS:
                            dve.wait_ge(s["yz_pool"], j - JS + 1)
                        nc.vector.scalar_tensor_tensor(out=y[:, j % JS, :], in0=xc[d][:, j, :], scalar=skip[d][:, j:j + 1],
                                                       in1=Y_BANK[j % JS][:, 0:GT], op0=ALU.mult, op1=ALU.add).then_inc(s["y_done"], 1)

                    def gate(j):
                        dve.wait_ge(s["y_done"], j + 1)
                        nc.vector.tensor_tensor(yz[:, j, :], y[:, j % JS, :], z[d][:, j, :], ALU.mult).then_inc(s["yz_done"], 1)

                    if rec:
                        input_term(0)
                    for i in range(STEPS):
                        if rec:
                            recur(i)
                            if i + 1 < STEPS and not by_pool(i + 1):
                                input_term(i + 1)
                            if i:
                                output_term(i - 1)
                            for j in range(JS):
                                if i == STEPS // 2 + 1 + j:
                                    collect(j)
                        beside(i)
                    if rec:
                        output_term(STEPS - 1)
                        for j in range(JS, IB):
                            collect(j)
                        for j in range(JS, IB):
                            gate(j)

            st.clear()

        def both(g, before, after):
            half(0, True, True, None, group_cols(g - 1) if before else None)
            half(1, True, after, group_cols(g + 1) if after else None, group_cols(g))

        half(1, False, True, group_cols(0), None)
        both(0, False, True)
        with nc.Fori(1, GROUPS - 1) as g:
            both(g, True, True)
        both(GROUPS - 1, True, False)
        half(0, False, False, None, group_cols(GROUPS - 1))
        sl.clear()


def l1_ffn(nc, h, c, w_fc, w_proj, u_t, v, fast_b, gate):
    HID, RANK = w_fc.shape[0], v.shape[0]
    HB = HID // P
    with Stage(nc, "l1f") as st:
        ps = [st.psum(f"ps{i}") for i in range(8)]
        wfcT = st.sbuf("wfcT", [P, DK, HID])
        wprojT = st.sbuf("wprojT", [P, HB, D])
        with Stage(nc, "l1w") as sw:
            raw = {"fc": sw.sbuf("raw_fc", [P, HB, D]), "proj": sw.sbuf("raw_proj", [P, DK, HID])}
            mag = {"fc": sw.sbuf("mag_fc", [P, HB]), "proj": sw.sbuf("mag_proj", [P, DK])}
            pos = sw.sbuf("pos", [P, HB * D])
            neg = sw.sbuf("neg", [P, HB * D])
            uT = sw.sbuf("uT", [RANK, HID])
            vs = sw.sbuf("vs", [RANK, D])
            fb = sw.sbuf("fb", [RANK, RANK])
            gt = sw.sbuf("gt", [RANK, 1])
            low = sw.sbuf("low", [RANK, HID])
            thr = {"fc": sw.sbuf("thr_fc", [P, HB]), "proj": sw.sbuf("thr_proj", [P, DK])}
            loaded, step, low_mm, low_ready, tern, turned, copied = (
                sw.sem(x) for x in ("loaded", "step", "low_mm", "low_ready", "tern", "turned", "copied"))
            with nc.Block() as block:
                @block.sync
                def _(sp):
                    sp.dma_start(raw["fc"][:, :, :], w_fc.rearrange("(m p) d -> p m d", p=P)).then_inc(loaded, 16)
                    sp.dma_start(raw["proj"][:, :, :], w_proj.rearrange("(m p) d -> p m d", p=P)).then_inc(loaded, 16)
                    sp.dma_start(uT[:, :], u_t).then_inc(loaded, 16)
                    sp.dma_start(vs[:, :], v).then_inc(loaded, 16)
                    sp.dma_start(fb[:, :], fast_b).then_inc(loaded, 16)
                    sp.dma_start(gt[:, :], gate.to_broadcast([RANK, 1])).then_inc(loaded, 16)

                @block.vector
                def _(dve):
                    dve.wait_ge(loaded, 96)
                    n = 0
                    for w, rows, cols in (("fc", HB, D), ("proj", DK, HID)):
                        W, pv = raw[w], pos[:, 0:rows * cols].rearrange("p (m d) -> p m d", m=rows)
                        nv = neg[:, 0:rows * cols].rearrange("p (m d) -> p m d", m=rows)
                        nc.vector.scalar_tensor_tensor(out=pv, in0=W[:, :, :], scalar=-1.0, in1=W[:, :, :],
                                                       op0=ALU.mult, op1=ALU.max).then_inc(step, 1)
                        dve.wait_ge(step, n + 1)
                        nc.vector.tensor_reduce(thr[w][:, :], pv, AX.X, ALU.add).then_inc(step, 1)
                        dve.wait_ge(step, n + 2)
                        nc.vector.tensor_scalar(mag[w][:, :], thr[w][:, :], 1.0 / cols, 1e-5, ALU.mult, ALU.max)\
                            .then_inc(step, 1)
                        dve.wait_ge(step, n + 3)
                        nc.vector.tensor_scalar(thr[w][:, :], mag[w][:, :], 0.5, None, ALU.mult).then_inc(step, 1)
                        dve.wait_ge(step, n + 4)
                        wide = thr[w][:, :].unsqueeze(2).to_broadcast([P, rows, cols])
                        nc.vector.tensor_tensor(pv, W[:, :, :], wide, ALU.is_gt).then_inc(step, 1)
                        nc.vector.scalar_tensor_tensor(out=nv, in0=W[:, :, :], scalar=-1.0, in1=wide,
                                                       op0=ALU.mult, op1=ALU.is_gt).then_inc(step, 1)
                        dve.wait_ge(step, n + 6)
                        nc.vector.tensor_tensor(pv, pv, nv, ALU.subtract).then_inc(step, 1)
                        dve.wait_ge(step, n + 7)
                        nc.vector.tensor_tensor(nv, pv, W[:, :, :], ALU.subtract).then_inc(step, 1)
                        dve.wait_ge(step, n + 8)
                        nc.vector.tensor_tensor(nv, W[:, :, :], nv, ALU.add).then_inc(step, 1)
                        dve.wait_ge(step, n + 9)
                        nc.vector.tensor_tensor(W[:, :, :], nv, mag[w][:, :].unsqueeze(2).to_broadcast([P, rows, cols]),
                                                ALU.mult).then_inc(tern, 1)
                        dve.wait_ge(tern, 1 if w == "fc" else 2)
                        n += 9

                @block.scalar
                def _(act):
                    nc.scalar.preload_act_table_set(EXP_LN)
                    act.wait_ge(loaded, 96)
                    for j in range(2):
                        act.wait_ge(low_mm, j + 1)
                        nc.scalar.activation(low[:, j * 512:(j + 1) * 512], ps[j][0:RANK, :], ACT.Copy, scale=gt[:, 0:1])\
                            .then_inc(low_ready, 1)
                    for i in range(HB + DK * HB // 4):
                        act.wait_ge(turned, i + 1)
                        bank = ps[2 + i % 6]
                        if i < HB:
                            dst = wfcT[:, i // 4, (i % 4) * 256:(i % 4) * 256 + 256]
                            nc.scalar.activation(dst, bank[:, 0:256], ACT.Copy).then_inc(copied, 1)
                        else:
                            m = i - HB
                            nc.scalar.activation(wprojT[:, 2 * m:2 * m + 2, :].rearrange("p a d -> p (a d)"),
                                                 bank[:, :], ACT.Copy).then_inc(copied, 1)

                @block.tensor
                def _(pe):
                    pe.wait_ge(loaded, 96)
                    for j in range(2):
                        nc.tensor.matmul(ps[j][0:RANK, :], fb[:, :], uT[:, j * 512:(j + 1) * 512],
                                         start=True, stop=True).then_inc(low_mm, 1)
                    pe.wait_ge(low_ready, 2)
                    pe.wait_ge(tern, 1)
                    for i in range(HB):
                        if i >= 6:
                            pe.wait_ge(copied, i - 5)
                        k, q = i // 4, i % 4
                        for j in range(2):
                            m = 2 * q + j
                            out = ps[2 + i % 6][:, j * P:(j + 1) * P]
                            nc.tensor.matmul(out, raw["fc"][:, m, k * P:(k + 1) * P], c["ident"][:, :], start=True, stop=False)
                            mm = nc.tensor.matmul(out, vs[:, k * P:(k + 1) * P], low[:, m * P:(m + 1) * P],
                                                  start=False, stop=True)
                        mm.then_inc(turned, 1)
                    pe.wait_ge(tern, 2)
                    for i in range(HB, HB + DK * HB // 4):
                        pe.wait_ge(copied, i - 5)
                        for j in range(4):
                            kb, m = 2 * (i - HB) + j // 2, j % 2
                            mm = nc.tensor.matmul(ps[2 + i % 6][:, j * P:(j + 1) * P], raw["proj"][:, m, kb * P:(kb + 1) * P],
                                                  c["ident"][:, :], start=True, stop=True)
                        mm.then_inc(turned, 1)
            sw.clear()

        norm = Norm(st, ps[0], ps[1])
        relu = st.sbuf("relu", [P, 2, GT])
        act2 = st.sbuf("act2", [P, HB, GT])
        fc_done, relu_done, sq_done, proj_done, res_done = (
            st.sem(x) for x in ("fc_done", "relu_done", "sq_done", "proj_done", "res_done"))

        def step(front, back):
            with nc.Block(no_gpsimd_drain=True) as block:
                @block.tensor
                def _(pe):
                    def up(m):
                        if back is None:
                            return
                        if m >= 4:
                            pe.wait_ge(relu_done, m - 3)
                        for k in range(DK):
                            mm = nc.tensor.matmul(ps[2 + m % 4][:, 0:GT], wfcT[:, k, m * P:(m + 1) * P], norm.out[:, k, :],
                                                  start=(k == 0), stop=(k == DK - 1))
                        mm.then_inc(fc_done, 1)

                    if front is not None:
                        norm.tensor_mean(nc, pe, c["ones"], lambda k: h[:, k, front])
                    for m in range(4):
                        up(m)
                    if front is not None:
                        norm.tensor_var(nc, pe, c["ones"])
                    for m in range(4, HB):
                        up(m)
                    if back is not None:
                        for j in range(DK):
                            for m in range(HB):
                                if j == 0:
                                    pe.wait_ge(sq_done, m + 1)
                                mm = nc.tensor.matmul(ps[6 + j][:, 0:GT], wprojT[:, m, j * P:(j + 1) * P], act2[:, m, :],
                                                      start=(m == 0), stop=(m == HB - 1))
                            mm.then_inc(proj_done, 1)

                @block.scalar
                def _(act):
                    nc.scalar.preload_act_table_set(EXP_LN)

                    def rectify(m):
                        act.wait_ge(fc_done, m + 1)
                        if m >= 2:
                            act.wait_ge(sq_done, m - 1)
                        nc.scalar.activation(relu[:, m % 2, :], ps[2 + m % 4][:, 0:GT], ACT.Relu).then_inc(relu_done, 1)

                    if front is not None:
                        act.wait_ge(norm.centred_ready, 1)
                        nc.scalar.activation(norm.square[:, :, :], norm.centred[:, :, :], ACT.Square).then_inc(norm.square_ready, 1)
                    for m in range(HB):
                        if back is not None:
                            rectify(m)
                        if m == 5 and front is not None:
                            norm.scalar_root(nc, act, c["eps"])

                @block.vector
                def _(dve):
                    if front is not None:
                        norm.vector_centre(nc, dve, h[:, :, front])
                    if back is not None:
                        for m in range(HB):
                            dve.wait_ge(relu_done, m + 1)
                            nc.vector.tensor_tensor(act2[:, m, :], relu[:, m % 2, :], relu[:, m % 2, :], ALU.mult).then_inc(sq_done, 1)
                        dve.wait_ge(fc_done, HB)
                    if front is not None:
                        norm.vector_scale(nc, dve)
                    if back is not None:
                        for j in range(DK):
                            dve.wait_ge(proj_done, j + 1)
                            nc.vector.tensor_tensor(h[:, j, back], h[:, j, back], ps[6 + j][:, 0:GT], ALU.add).then_inc(res_done, 1)
            st.clear()

        step(group_cols(0), None)
        with nc.Fori(0, GROUPS - 1) as g:
            step(group_cols(g + 1), group_cols(g))
        step(None, group_cols(GROUPS - 1))


def l2_ffn(nc, h, c, wr, br, w1, b1, w2, b2, row_expert):
    E = wr.shape[1]
    HID = w1.shape[3]
    HB = HID // P
    with Stage(nc, "ex2") as st:
        ps = [st.psum(f"ps{i}") for i in range(8)]
        normed = st.sbuf("normed", [P, DK, T])
        means = st.sbuf("means", [P, DK, B])
        with Stage(nc, "rt2") as sr:
            NW = 2
            norms = [Norm(sr, ps[2 * i], ps[2 * i + 1], f"ln{i}") for i in range(NW)]
            kept, summed = sr.sem("kept"), sr.sem("summed")
            with nc.Fori(0, GROUPS // NW) as g:
                with nc.Block(no_gpsimd_drain=True) as block:
                    @block.tensor
                    def _(pe):
                        for i, norm in enumerate(norms):
                            norm.tensor_mean(nc, pe, c["ones"], lambda k: h[:, k, group_cols(g * NW + i)])
                        for norm in norms:
                            norm.tensor_var(nc, pe, c["ones"])

                    @block.scalar
                    def _(act):
                        nc.scalar.preload_act_table_set(EXP_LN)
                        for norm in norms:
                            act.wait_ge(norm.centred_ready, 1)
                            nc.scalar.activation(norm.square[:, :, :], norm.centred[:, :, :], ACT.Square)\
                                .then_inc(norm.square_ready, 1)
                        for norm in norms:
                            norm.scalar_root(nc, act, c["eps"])
                        for i, norm in enumerate(norms):
                            act.wait_ge(norm.ready, 1)
                            nc.scalar.activation(normed[:, :, group_cols(g * NW + i)], norm.out[:, :, :], ACT.Copy).then_inc(kept, 1)

                    @block.vector
                    def _(dve):
                        for i, norm in enumerate(norms):
                            norm.vector_centre(nc, dve, h[:, :, group_cols(g * NW + i)])
                        for norm in norms:
                            norm.vector_scale(nc, dve)
                        for i, norm in enumerate(norms):
                            dve.wait_ge(norm.ready, 1)
                            nc.vector.tensor_reduce(means[:, :, bass.ds((g * NW + i) * GB, GB)],
                                                    norm.out[:, :, :].rearrange("p k (b n) -> p k b n", n=N), AX.X, ALU.add)\
                                .then_inc(summed, 1)
                sr.clear()
            w_r = sr.sbuf("w_r", [P, DK, E])
            b_r = sr.sbuf("b_r", [B, E])
            score = sr.sbuf("score", [B, E])
            top = sr.sbuf("top", [B, 8])
            best = sr.sbuf("best", [B, 8], U32)
            loaded, mean_ready, score_mm, score_done, top_done, best_done, sent = (
                sr.sem(x) for x in ("loaded", "mean_ready", "score_mm", "score_done", "top_done", "best_done", "sent"))
            with nc.Block() as block:
                @block.sync
                def _(sp):
                    sp.dma_start(w_r[:, :, :], wr.rearrange("(k p) e -> p k e", p=P)).then_inc(loaded, 16)
                    sp.dma_start(b_r[:, :], br.to_broadcast([B, E])).then_inc(loaded, 16)
                    sp.wait_ge(best_done, 1)
                    sp.dma_start(row_expert, best[:, 0:1]).then_inc(sent, 16)
                    sp.wait_ge(sent, 16)

                @block.vector
                def _(dve):
                    nc.vector.tensor_scalar(means[:, :, :], means[:, :, :], 1.0 / N, None, ALU.mult).then_inc(mean_ready, 1)
                    dve.wait_ge(score_mm, 1)
                    dve.wait_ge(loaded, 32)
                    nc.vector.tensor_tensor(score[:, :], ps[0][0:B, 0:E], b_r[:, :], ALU.add).then_inc(score_done, 1)
                    dve.wait_ge(score_done, 1)
                    nc.vector.max(top[:, :], score[:, :]).then_inc(top_done, 1)
                    dve.wait_ge(top_done, 1)
                    nc.vector.max_index(best[:, :], top[:, :], score[:, :]).then_inc(best_done, 1)

                @block.tensor
                def _(pe):
                    pe.wait_ge(loaded, 32)
                    pe.wait_ge(mean_ready, 1)
                    for k in range(DK):
                        mm = nc.tensor.matmul(ps[0][0:B, 0:E], means[:, k, :], w_r[:, k, :], start=(k == 0), stop=(k == DK - 1))
                    mm.then_inc(score_mm, 1)
            sr.clear()

        WB = GB
        W1 = [st.sbuf(f"w1_{i}", [P, DK, HID]) for i in range(WB)]
        W2 = [st.sbuf(f"w2_{i}", [P, HB, D]) for i in range(WB)]
        B1 = [st.sbuf(f"b1_{i}", [P, HB]) for i in range(WB)]
        B2 = [st.sbuf(f"b2_{i}", [P, DK]) for i in range(WB)]
        ids = st.sbuf("ids", [1, B + 1], U32)
        hid = st.sbuf("hid", [P, 2, HB, N])
        x_in = st.sbuf("x_in", [P, DK, GT])
        id_in = st.sem("id_in")
        landed = [st.sem(f"landed{i}") for i in range(WB)]
        x_done, up_done, relu_done, down_done, res_done = (
            st.sem(x) for x in ("x_done", "up_done", "relu_done", "down_done", "res_done"))

        def fetch(sp, row, i):
            e = nc.sync.value_load(ids[0:1, bass.ds(row, 1)], min_val=0, max_val=E - 1)
            for dst, src in ((W1[i][:, :, :], w1[bass.ds(e, 1), :, :, :]), (W2[i][:, :, :], w2[bass.ds(e, 1), :, :, :]),
                             (B1[i][:, :], b1[bass.ds(e, 1), :, :]), (B2[i][:, :], b2[bass.ds(e, 1), :, :])):
                names = "e p k n -> (e p) k n" if len(src.shape) == 4 else "e p n -> (e p) n"
                sp.dma_start(dst, src.rearrange(names)).then_inc(landed[i], 16)

        with nc.Block() as block:
            @block.sync
            def _(sp):
                sp.dma_start(ids[0:1, 0:B], row_expert.rearrange("b a -> a b")).then_inc(id_in, 16)
                sp.dma_start(ids[0:1, B:B + 1], row_expert[0:1, :]).then_inc(id_in, 16)
                sp.wait_ge(id_in, 32)
                fetch(sp, 0, 0)
                sp.wait_ge(landed[0], 64)
        st.clear()
        with nc.Fori(0, GROUPS) as g:
            with nc.Block(no_gpsimd_drain=True) as block:
                @block.sync
                def _(sp):
                    for i in range(1, WB):
                        fetch(sp, g * GB + i, i)
                    sp.wait_ge(down_done, DK)
                    sp.wait_ge(res_done, DK)
                    fetch(sp, g * GB + GB, 0)
                    sp.wait_ge(landed[0], 64)

                @block.tensor
                def _(pe):
                    pe.wait_ge(x_done, 1)
                    for i in range(GB):
                        if i:
                            pe.wait_ge(landed[i], 64)
                        for m in range(HB):
                            bank = ps[2 * (i % 2) + m // 4]
                            if m % 4 == 0 and i >= 2:
                                pe.wait_ge(relu_done, HB * (i - 2) + m + 4)
                            for k in range(DK):
                                mm = nc.tensor.matmul(bank[:, (m % 4) * N:(m % 4 + 1) * N], W1[i][:, k, m * P:(m + 1) * P],
                                                      x_in[:, k, i * N:(i + 1) * N], start=(k == 0), stop=(k == DK - 1))
                            if m % 4 == 3:
                                mm.then_inc(up_done, 1)
                        for j in range(DK):
                            if i >= 2:
                                pe.wait_ge(res_done, DK * (i - 2) + j + 1)
                            for m in range(HB):
                                if j == 0:
                                    pe.wait_ge(relu_done, HB * i + m + 1)
                                mm = nc.tensor.matmul(ps[4 + 2 * (i % 2) + j][:, 0:N], W2[i][:, m, j * P:(j + 1) * P],
                                                      hid[:, i % 2, m, :], start=(m == 0), stop=(m == HB - 1))
                            mm.then_inc(down_done, 1)

                @block.scalar
                def _(act):
                    nc.scalar.activation(x_in[:, :, :], normed[:, :, group_cols(g)], ACT.Copy).then_inc(x_done, 1)
                    for i in range(GB):
                        if i:
                            act.wait_ge(landed[i], 64)
                        if i >= 2:
                            act.wait_ge(down_done, DK * (i - 1))
                        for m in range(HB):
                            act.wait_ge(up_done, 2 * i + m // 4 + 1)
                            nc.scalar.activation(hid[:, i % 2, m, :], ps[2 * (i % 2) + m // 4][:, (m % 4) * N:(m % 4 + 1) * N],
                                                 ACT.Relu, bias=B1[i][:, m:m + 1]).then_inc(relu_done, 1)

                @block.vector
                def _(dve):
                    for i in range(GB):
                        if i:
                            dve.wait_ge(landed[i], 64)
                        for j in range(DK):
                            at = h[:, j, bass.ds(g * GT + i * N, N)]
                            dve.wait_ge(down_done, DK * i + j + 1)
                            nc.vector.scalar_tensor_tensor(out=at, in0=ps[4 + 2 * (i % 2) + j][:, 0:N], scalar=B2[i][:, j:j + 1],
                                                           in1=at, op0=ALU.add, op1=ALU.add).then_inc(res_done, 1)
            st.clear()


FAR = -1e38


def rwkv(nc, h, c, wk, wv, wr, ck, cv, cr, cols):
    HID = ck.shape[1]
    HB = HID // P
    NC = 11
    DECAY, FIRST, G1, B1, G2, B2, MK, MV, MR, CK, CR = range(NC)
    MIXES = (MK, MV, MR, CK, CR)
    with Stage(nc, "rw_late") as sl, Stage(nc, "rw") as st:
        late = sl.sem("late")
        W = {x: st.sbuf(x, [P, DK, D]) for x in ("wk", "wv", "wr", "cr")}
        w_ck = st.sbuf("ck", [P, DK, HID])
        w_cv = st.sbuf("cv", [P, HB, D])
        col = st.sbuf("cols", [P, NC, DK])
        rest = st.sbuf("rest", [P, NC, DK])
        first_neg = st.sbuf("first_neg", [P, DK])
        ps = [st.psum(f"ps{i}") for i in range(8)]
        norms = [Norm(st, ps[0], ps[0], f"ln{i}") for i in range(3)]
        T_BANK = ((1, 2), (3, 1), (2, 3))
        C_BANK, O_BANK = (4, 5), (6, 7)
        h1 = st.sbuf("h1", [P, DK, GT])
        back = st.sbuf("back", [P, 5, DK, GT])
        mixed = st.sbuf("mixed", [P, 5, DK, GT])
        drift = st.sbuf("drift", [P, DK, GB, N + 1])
        kp = st.sbuf("kp", [P, DK, GB, N + 1])
        v = st.sbuf("v", [P, DK, GT])
        Mp = st.sbuf("Mp", [P, DK, GB, N + 1])
        PPp = st.sbuf("PPp", [P, DK, GB, N + 1])
        AAp = st.sbuf("AAp", [P, DK, GB, N + 1])
        d1 = st.sbuf("d1", [P, DK, GT])
        d2 = st.sbuf("d2", [P, DK, GT])
        s_ = st.sbuf("s", [P, DK, GT])
        gate = st.sbuf("gate", [P, DK, GT])
        rg = st.sbuf("rg", [P, DK, GT])
        aa = st.sbuf("aa", [P, DK, GT])
        x2 = st.sbuf("x2", [P, DK, GT])
        relu = st.sbuf("relu", [P, 2, GT])
        cg = st.sbuf("cg", [P, DK, GT])
        act2 = st.sbuf("act2", [P, HB, GT])
        names = ("loaded", "set", "rested", "h1_done", "back_done", "mix_done", "k_mm", "v_mm", "r_mm", "k_done", "v_done",
                 "M_done", "d1_done", "d2_done", "a_done", "s_done", "ln_done", "pp_done", "dl_done", "min_done", "e_done",
                 "ev_done", "aa_done", "aap_done", "diff_done", "gate_done", "rg_done", "gd_done", "y_done", "ry_done", "x2_done", "h2_done",
                 "c_mm", "relu_done", "sq_done", "cr_mm", "cg_raw", "cg_done", "cv_mm", "sk_done", "x3_done", "res_done")
        s = {x: st.sem(x) for x in names}
        with nc.Block() as block:
            @block.sync
            def _(sp):
                sp.dma_start(col[:, :, :], cols).then_inc(s["loaded"], 16)
                for dst, src in ((W["wk"], wk), (W["wv"], wv), (W["wr"], wr)):
                    sp.dma_start(dst[:, :, :], src.rearrange("(k p) n -> p k n", p=P)).then_inc(s["loaded"], 16)
                for dst, src in ((W["cr"], cr), (w_ck, ck), (w_cv, cv)):
                    sp.dma_start(dst[:, :, :], src.rearrange("(k p) n -> p k n", p=P)).then_inc(late, 16)
                sp.wait_ge(s["loaded"], 64)

            @block.gpsimd
            def _(pool):
                nc.gpsimd.memset(back[:, :, :, :], 0.0)
                nc.gpsimd.memset(kp[:, :, :, :], 0.0)
                nc.gpsimd.memset(PPp[:, :, :, :], FAR)
                nc.gpsimd.memset(AAp[:, :, :, :], 0.0)
                nc.gpsimd.memset(drift[:, :, :, :], 0.0).then_inc(s["set"], 1)

            @block.vector
            def _(dve):
                dve.wait_ge(s["loaded"], 64)
                nc.vector.tensor_scalar(rest[:, :, :], col[:, :, :], -1.0, 1.0, ALU.mult, ALU.add).then_inc(s["rested"], 1)
                nc.vector.tensor_scalar(first_neg[:, :], col[:, FIRST, :], -1.0, None, ALU.mult).then_inc(s["rested"], 1)
                dve.wait_ge(s["set"], 1)
                for k in range(DK):
                    nc.vector.tensor_scalar(drift[:, k, :, 1:N + 1], drift[:, k, :, 1:N + 1], col[:, DECAY, k:k + 1], None,
                                            ALU.add).then_inc(s["rested"], 1)
                nc.vector.memset(drift[:, :, :, 0:1], FAR).then_inc(s["rested"], 1)

            @block.scalar
            def _(act):
                nc.scalar.preload_act_table_set(EXP_LN)
        st.clear()

        def rows(ap):
            return ap.rearrange("p (b n) -> p b n", n=N)

        def both(ap):
            return ap.rearrange("p k (b n) -> p k b n", n=N)

        def step(front, back_cols):
            with nc.Block(no_gpsimd_drain=True) as block:
                @block.sync
                def _(sp):
                    if back_cols is None:
                        sp.wait_ge(late, 48)

                @block.tensor
                def _(pe):
                    def hidden(m):
                        if back_cols is None:
                            return
                        if m >= 2:
                            pe.wait_ge(s["relu_done"], m - 1)
                        for k in range(DK):
                            mm = nc.tensor.matmul(ps[C_BANK[m % 2]][:, 0:GT], w_ck[:, k, m * P:(m + 1) * P], mixed[:, 3, k, :],
                                                  start=(k == 0), stop=(k == DK - 1))
                        mm.then_inc(s["c_mm"], 1)

                    def channel_gate():
                        if back_cols is None:
                            return
                        for m in range(DK):
                            for k in range(DK):
                                mm = nc.tensor.matmul(ps[O_BANK[m]][:, 0:GT], W["cr"][:, k, m * P:(m + 1) * P], mixed[:, 4, k, :],
                                                      start=(k == 0), stop=(k == DK - 1))
                            mm.then_inc(s["cr_mm"], 1)

                    def channel_out():
                        if back_cols is None:
                            return
                        pe.wait_ge(s["cg_raw"], DK)
                        for j in range(DK):
                            for m in range(HB):
                                pe.wait_ge(s["sq_done"], m + 1)
                                mm = nc.tensor.matmul(ps[O_BANK[j]][:, 0:GT], w_cv[:, m, j * P:(j + 1) * P], act2[:, m, :],
                                                      start=(m == 0), stop=(m == HB - 1))
                            mm.then_inc(s["cv_mm"], 1)

                    def project(i, x, done):
                        pe.wait_ge(s["mix_done"], DK * (i + 1))
                        for m in range(DK):
                            if i == 1 and m == 1:
                                pe.wait_ge(s["k_done"], 1)
                            if i == 2:
                                pe.wait_ge(*((s["k_done"], 2), (s["v_done"], 1))[m])
                            for k in range(DK):
                                mm = nc.tensor.matmul(ps[T_BANK[i][m]][:, 0:GT], W[x][:, k, m * P:(m + 1) * P],
                                                      mixed[:, i, k, :], start=(k == 0), stop=(k == DK - 1))
                            mm.then_inc(done, 1)

                    if front is not None:
                        norms[0].tensor_mean(nc, pe, c["ones"], lambda k: h[:, k, front])
                    channel_gate()
                    if front is not None:
                        norms[0].tensor_var(nc, pe, c["ones"])
                    hidden(0)
                    hidden(1)
                    if front is not None:
                        pe.wait_ge(norms[0].ready, 1)
                        norms[1].tensor_mean(nc, pe, c["ones"], lambda k: norms[0].out[:, k, :])
                    hidden(2)
                    hidden(3)
                    if front is not None:
                        norms[1].tensor_var(nc, pe, c["ones"])
                    hidden(4)
                    hidden(5)
                    hidden(6)
                    if front is not None:
                        project(0, "wk", s["k_mm"])
                    hidden(7)
                    if front is not None:
                        project(1, "wv", s["v_mm"])
                        project(2, "wr", s["r_mm"])
                    channel_out()
                    if front is not None:
                        pe.wait_ge(s["x2_done"], 1)
                        norms[2].tensor_mean(nc, pe, c["ones"], lambda k: x2[:, k, :])
                        norms[2].tensor_var(nc, pe, c["ones"])

                @block.scalar
                def _(act):
                    def rectify(m):
                        if back_cols is None:
                            return
                        act.wait_ge(s["c_mm"], m + 1)
                        if m >= 2:
                            act.wait_ge(s["sq_done"], m - 1)
                        nc.scalar.activation(relu[:, m % 2, :], ps[C_BANK[m % 2]][:, 0:GT], ACT.Relu).then_inc(s["relu_done"], 1)

                    def raw_gate():
                        if back_cols is not None:
                            for k in range(DK):
                                act.wait_ge(s["cr_mm"], k + 1)
                                nc.scalar.activation(cg[:, k, :], ps[O_BANK[k]][:, 0:GT], ACT.Copy).then_inc(s["cg_raw"], 1)

                    def sigmoid_gate():
                        if back_cols is not None:
                            act.wait_ge(s["cg_raw"], DK)
                            nc.scalar.activation(cg[:, :, :], cg[:, :, :], ACT.Sigmoid).then_inc(s["cg_done"], DK)

                    if front is None:
                        raw_gate()
                        for m in range(HB):
                            rectify(m)
                        sigmoid_gate()
                        return
                    nc.scalar.preload_act_table_set(EXP_LN)
                    norms[0].scalar(nc, act, c["eps"])
                    raw_gate()
                    rectify(0)
                    rectify(1)
                    act.wait_ge(norms[1].centred_ready, 1)
                    nc.scalar.activation(norms[1].square[:, :, :], norms[1].centred[:, :, :], ACT.Square)\
                        .then_inc(norms[1].square_ready, 1)
                    rectify(2)
                    rectify(3)
                    norms[1].scalar_root(nc, act, c["eps"])

                    def shifted(i, mix, ready):
                        act.wait_ge(s["h1_done"] if i < 3 else s["h2_done"], ready)
                        for k in range(DK):
                            nc.scalar.activation(rows(back[:, i, k, :])[:, :, 1:N], rows(h1[:, k, :])[:, :, 0:N - 1],
                                                 ACT.Copy, scale=rest[:, mix, k:k + 1]).then_inc(s["back_done"], 1)

                    shifted(0, MIXES[0], DK)
                    rectify(4)
                    shifted(1, MIXES[1], DK)
                    rectify(5)
                    shifted(2, MIXES[2], DK)
                    rectify(6)
                    rectify(7)
                    for k in range(DK):
                        act.wait_ge(s["k_mm"], k + 1)
                        nc.scalar.activation(kp[:, k, :, 1:N + 1], rows(ps[T_BANK[0][k]][:, 0:GT]), ACT.Copy).then_inc(s["k_done"], 1)
                    for k in range(DK):
                        act.wait_ge(s["v_mm"], k + 1)
                        nc.scalar.activation(v[:, k, :], ps[T_BANK[1][k]][:, 0:GT], ACT.Copy).then_inc(s["v_done"], 1)
                    for k in range(DK):
                        act.wait_ge(s["d1_done"], k + 1)
                        nc.scalar.activation(d1[:, k, :], d1[:, k, :], ACT.Exp).then_inc(s["a_done"], 1)
                        act.wait_ge(s["d2_done"], k + 1)
                        nc.scalar.activation(d2[:, k, :], d2[:, k, :], ACT.Exp).then_inc(s["a_done"], 1)
                    for k in range(DK):
                        act.wait_ge(s["s_done"], k + 1)
                        nc.scalar.activation(aa[:, k, :], s_[:, k, :], ACT.Ln).then_inc(s["ln_done"], 1)
                    for k in range(DK):
                        act.wait_ge(s["min_done"], 2 * k + 1)
                        nc.scalar.activation(d1[:, k, :], d1[:, k, :], ACT.Exp).then_inc(s["e_done"], 1)
                        act.wait_ge(s["min_done"], 2 * k + 2)
                        nc.scalar.activation(d2[:, k, :], d2[:, k, :], ACT.Exp).then_inc(s["e_done"], 1)
                    for k in range(DK):
                        act.wait_ge(s["r_mm"], k + 1)
                        nc.scalar.activation(rg[:, k, :], ps[T_BANK[2][k]][:, 0:GT], ACT.Sigmoid).then_inc(s["rg_done"], 1)
                    for k in range(DK):
                        nc.scalar.activation(gate[:, k, :], s_[:, k, :], ACT.Sigmoid, bias=first_neg[:, k:k + 1])\
                            .then_inc(s["gate_done"], 1)
                    sigmoid_gate()
                    nc.scalar.preload_act_table_set(EXP_LN)
                    norms[2].scalar(nc, act, c["eps"])
                    for i in range(3, 5):
                        shifted(i, MIXES[i], DK)

                @block.vector
                def _(dve):
                    def square(m):
                        if back_cols is None:
                            return
                        dve.wait_ge(s["relu_done"], m + 1)
                        nc.vector.tensor_tensor(act2[:, m, :], relu[:, m % 2, :], relu[:, m % 2, :], ALU.mult)\
                            .then_inc(s["sq_done"], 1)

                    def output(k):
                        if back_cols is None:
                            return
                        dve.wait_ge(s["cg_done"], DK)
                        dve.wait_ge(s["cv_mm"], k + 1)
                        nc.vector.tensor_tensor(cg[:, k, :], cg[:, k, :], ps[O_BANK[k]][:, 0:GT], ALU.mult).then_inc(s["sk_done"], 1)
                        dve.wait_ge(s["sk_done"], k + 1)
                        dve.wait_ge(s["x3_done"], 1)
                        nc.vector.tensor_tensor(h[:, k, back_cols], h[:, k, back_cols], cg[:, k, :], ALU.add).then_inc(s["res_done"], 1)

                    if back_cols is not None:
                        nc.vector.tensor_tensor(h[:, :, back_cols], x2[:, :, :], h[:, :, back_cols], ALU.add).then_inc(s["x3_done"], 1)
                    if front is None:
                        for m in range(HB):
                            square(m)
                        for k in range(DK):
                            output(k)
                        return
                    x = norms[0].out
                    norms[0].vector(nc, dve, h[:, :, front])
                    square(0)
                    square(1)
                    dve.wait_ge(norms[0].ready, 1)
                    norms[1].vector(nc, dve, x[:, :, :])
                    square(2)
                    square(3)
                    def scaled(norm, gain, bias, done):
                        dve.wait_ge(norm.ready, 1)
                        for k in range(DK):
                            nc.vector.tensor_scalar(h1[:, k, :], norm.out[:, k, :], col[:, gain, k:k + 1],
                                                    col[:, bias, k:k + 1], ALU.mult, ALU.add).then_inc(done, 1)
                        dve.wait_ge(done, DK)

                    def mix(i):
                        for k in range(DK):
                            dve.wait_ge(s["back_done"], DK * i + k + 1)
                            nc.vector.scalar_tensor_tensor(out=mixed[:, i, k, :], in0=h1[:, k, :],
                                                           scalar=col[:, MIXES[i], k:k + 1], in1=back[:, i, k, :],
                                                           op0=ALU.mult, op1=ALU.add).then_inc(s["mix_done"], 1)

                    scaled(norms[1], G1, B1, s["h1_done"])
                    mix(0)
                    square(4)
                    mix(1)
                    square(5)
                    mix(2)
                    square(6)
                    square(7)
                    for k in range(DK):
                        dve.wait_ge(s["k_done"], k + 1)
                        nc.vector.tensor_tensor_scan(Mp[:, k, :, :].rearrange("p b n -> p (b n)"),
                                                     kp[:, k, :, :].rearrange("p b n -> p (b n)"),
                                                     drift[:, k, :, :].rearrange("p b n -> p (b n)"), FAR, ALU.max, ALU.add)\
                            .then_inc(s["M_done"], 1)
                    for k in range(DK):
                        dve.wait_ge(s["M_done"], k + 1)
                        nc.vector.scalar_tensor_tensor(out=rows(d1[:, k, :]), in0=Mp[:, k, :, 0:N], scalar=col[:, DECAY, k:k + 1],
                                                       in1=Mp[:, k, :, 1:N + 1], op0=ALU.add, op1=ALU.subtract)\
                            .then_inc(s["d1_done"], 1)
                        nc.vector.scalar_tensor_tensor(out=rows(d2[:, k, :]), in0=kp[:, k, :, 1:N + 1],
                                                       scalar=col[:, DECAY, k:k + 1],
                                                       in1=Mp[:, k, :, 1:N + 1], op0=ALU.add, op1=ALU.subtract)\
                            .then_inc(s["d2_done"], 1)
                    for k in range(DK):
                        dve.wait_ge(s["a_done"], 2 * k + 2)
                        nc.vector.tensor_tensor_scan(s_[:, k, :], d1[:, k, :], d2[:, k, :], 0.0, ALU.mult, ALU.add)\
                            .then_inc(s["s_done"], 1)
                    for k in range(DK):
                        dve.wait_ge(s["ln_done"], k + 1)
                        nc.vector.tensor_tensor(PPp[:, k, :, 1:N + 1], Mp[:, k, :, 1:N + 1], rows(aa[:, k, :]), ALU.add)\
                            .then_inc(s["pp_done"], 1)
                        dve.wait_ge(s["pp_done"], k + 1)
                        nc.vector.tensor_tensor(rows(s_[:, k, :]), PPp[:, k, :, 0:N], kp[:, k, :, 1:N + 1], ALU.subtract)\
                            .then_inc(s["dl_done"], 1)
                        dve.wait_ge(s["dl_done"], k + 1)
                        nc.vector.tensor_scalar(d1[:, k, :], s_[:, k, :], 0.0, None, ALU.min).then_inc(s["min_done"], 1)
                        nc.vector.tensor_scalar(d2[:, k, :], s_[:, k, :], -1.0, 0.0, ALU.mult, ALU.min).then_inc(s["min_done"], 1)
                    dve.wait_ge(s["v_done"], DK)
                    for k in range(DK):
                        dve.wait_ge(s["e_done"], 2 * k + 2)
                        nc.vector.tensor_tensor(d2[:, k, :], d2[:, k, :], v[:, k, :], ALU.mult).then_inc(s["ev_done"], 1)
                        dve.wait_ge(s["ev_done"], k + 1)
                        nc.vector.tensor_tensor_scan(aa[:, k, :], d1[:, k, :], d2[:, k, :], 0.0, ALU.mult, ALU.add)\
                            .then_inc(s["aa_done"], 1)
                    for k in range(DK):
                        dve.wait_ge(s["aa_done"], k + 1)
                        nc.vector.tensor_copy(AAp[:, k, :, 1:N + 1], rows(aa[:, k, :])).then_inc(s["aap_done"], 1)
                    for k in range(DK):
                        dve.wait_ge(s["aap_done"], k + 1)
                        dve.wait_ge(s["aa_done"], DK)
                        nc.vector.tensor_tensor(rows(d1[:, k, :]), AAp[:, k, :, 0:N], rows(v[:, k, :]), ALU.subtract)\
                            .then_inc(s["diff_done"], 1)
                    dve.wait_ge(s["diff_done"], DK)
                    dve.wait_ge(s["gate_done"], DK)
                    nc.vector.tensor_tensor(d1[:, :, :], d1[:, :, :], gate[:, :, :], ALU.mult).then_inc(s["gd_done"], 1)
                    dve.wait_ge(s["gd_done"], 1)
                    nc.vector.tensor_tensor(d1[:, :, :], d1[:, :, :], v[:, :, :], ALU.add).then_inc(s["y_done"], 1)
                    dve.wait_ge(s["y_done"], 1)
                    dve.wait_ge(s["rg_done"], DK)
                    nc.vector.tensor_tensor(d1[:, :, :], d1[:, :, :], rg[:, :, :], ALU.mult).then_inc(s["ry_done"], 1)
                    dve.wait_ge(s["ry_done"], 1)
                    nc.vector.tensor_tensor(x2[:, :, :], d1[:, :, :], x[:, :, :], ALU.add).then_inc(s["x2_done"], 1)
                    dve.wait_ge(s["x2_done"], 1)
                    norms[2].vector(nc, dve, x2[:, :, :])
                    output(0)
                    output(1)
                    scaled(norms[2], G2, B2, s["h2_done"])
                    if back_cols is not None:
                        dve.wait_ge(s["c_mm"], HB)
                        dve.wait_ge(s["cr_mm"], DK)
                    mix(3)
                    mix(4)
            st.clear()

        step(group_cols(0), None)
        with nc.Fori(0, GROUPS - 1) as g:
            step(group_cols(g + 1), group_cols(g))
        step(None, group_cols(GROUPS - 1))
        sl.clear()


def peer(nc, h, c, wq, keys_t, down_t, up, norm_w, out):
    HEADS, KEYS, TOP = keys_t.shape[1] // 2, keys_t.shape[2], 8
    CH = HEADS * TOP
    EB = KEYS // 2
    PB = 2
    PT = PB * N
    CHUNK = 512 // (PB * EB)
    CHUNKS = [(t, min(CHUNK, N - t)) for t in range(0, N, CHUNK)]
    SETS = 2 * HEADS
    STEPS = B // PB
    with Stage(nc, "peer_out") as so, Stage(nc, "peer") as st:
        out_sent = so.sem("out_sent")
        big_in = so.sem("big_in")
        ps = [st.psum(f"ps{i}") for i in range(8)]
        kq = st.sbuf("kq", [P, DK, SETS * KEYS])
        down = st.sbuf("down", [P, DK, EB, P])
        w_up = st.sbuf("up", [P, EB, D])
        nw = st.sbuf("nw", [P, DK])
        ramp = st.sbuf("ramp", [P, P])
        eps6 = st.sbuf("eps6", [P, 1])
        with Stage(nc, "pkq") as sk:
            w_q = sk.sbuf("w_q", [P, SETS, D])
            keys = sk.sbuf("keys", [P, SETS, KEYS])
            loaded, set_, kq_mm, kq_done = (sk.sem(x) for x in ("loaded", "set", "kq_mm", "kq_done"))
            with nc.Block() as block:
                @block.sync
                def _(sp):
                    sp.dma_start(w_q[:, :, :], wq.rearrange("(s p) d -> p s d", p=P)).then_inc(loaded, 16)
                    sp.dma_start(keys[:, :, :], keys_t).then_inc(loaded, 16)
                    sp.dma_start(nw[:, :], norm_w).then_inc(loaded, 16)
                    sp.dma_start(down[:, :, :, :], down_t).then_inc(big_in, 16)
                    sp.dma_start(w_up[:, :, :], up).then_inc(big_in, 16)

                @block.gpsimd
                def _(pool):
                    nc.gpsimd.iota(ramp[:, :], pattern=[[1, P]], base=0, channel_multiplier=0,
                                   allow_small_or_imprecise_dtypes=True).then_inc(set_, 1)
                    nc.gpsimd.memset(eps6[:, :], 1e-6).then_inc(set_, 1)

                @block.tensor
                def _(pe):
                    pe.wait_ge(loaded, 48)
                    for m in range(DK):
                        for half in range(2):
                            for j in range(SETS // 2):
                                i = half * SETS // 2 + j
                                mm = nc.tensor.matmul(ps[2 * m + half][:, j * KEYS:(j + 1) * KEYS],
                                                      w_q[:, i, m * P:(m + 1) * P], keys[:, i, :], start=True, stop=True)
                            mm.then_inc(kq_mm, 1)

                @block.vector
                def _(dve):
                    for m in range(DK):
                        for half in range(2):
                            dve.wait_ge(kq_mm, 2 * m + half + 1)
                            nc.vector.tensor_copy(kq[:, m, half * 512:(half + 1) * 512], ps[2 * m + half][:, :])\
                                .then_inc(kq_done, 1)
            sk.clear()

        norm = Norm(st, ps[0], ps[0], "ln", PT)
        log2, rms = norm.log_var, norm.rstd
        xn = st.sbuf("xn", [P, DK, PT])
        hid = st.sbuf("hid", [P, EB, PT])
        weight = st.sbuf("weight", [P, EB, PB, N])
        top = st.sbuf("top", [N, PB, SETS, TOP])
        idx = st.sbuf("idx", [N, PB, SETS, TOP], U32)
        pair = st.sbuf("pair", [N, PB, HEADS, TOP, TOP])
        best = st.sbuf("best", [N, PB, HEADS, TOP])
        at = st.sbuf("at", [N, PB, HEADS, TOP], U32)
        at_hi = st.sbuf("at_hi", [N, PB * HEADS, TOP], U32)
        at_lo = st.sbuf("at_lo", [N, PB * HEADS, TOP], U32)
        hit1 = st.sbuf("hit1", [N, PB * HEADS, TOP, TOP])
        hit2 = st.sbuf("hit2", [N, PB * HEADS, TOP, TOP])
        i1 = st.sbuf("i1", [N, PB * HEADS, TOP])
        i2 = st.sbuf("i2", [N, PB * HEADS, TOP])
        i2u, odd = (st.sbuf(x, [N, PB * CH], U32) for x in ("i2u", "odd"))
        half_ = st.sbuf("half", [N, PB * CH], U32)
        codes = st.sbuf("codes", [N, 3, PB * CH])
        codesT = st.sbuf("codesT", [P, 3, N])
        HB = 3
        hot_rows = st.sbuf("hot_rows", [P, HB, CHUNK, P])
        hot_cols = st.sbuf("hot_cols", [P, HB, CHUNK, PB * EB])
        names = ("sq2", "ms_mm", "log2_done", "rms_done", "xn_done", "sim_mm", "top_done", "idx_done", "pair_done", "best_done", "at_done",
                 "split_done", "hit_done", "mul_done", "sel_done", "u_done", "bits_done", "code_done", "t_done", "ct_done",
                 "hid_mm", "gelu_done", "rows_done", "hot_done", "cols_done", "g_mm", "evac_done", "wgt_done", "up_mm", "res_done")
        s = {x: st.sem(x) for x in names}
        J = 2
        HU = EB // J
        NC = len(CHUNKS)

        def best_experts(dve):
            for b in range(PB):
                for i in range(SETS):
                    if i % HEADS == 0:
                        dve.wait_ge(s["sim_mm"], 2 * b + i // HEADS + 1)
                    nc.vector.max(top[:, b, i, :], ps[1 + 2 * b + i // HEADS][0:N, (i % HEADS) * KEYS:(i % HEADS + 1) * KEYS])\
                        .then_inc(s["top_done"], 1)
                for i in range(SETS):
                    dve.wait_ge(s["top_done"], SETS * b + i + 1)
                    nc.vector.max_index(idx[:, b, i, :], top[:, b, i, :],
                                        ps[1 + 2 * b + i // HEADS][0:N, (i % HEADS) * KEYS:(i % HEADS + 1) * KEYS])\
                        .then_inc(s["idx_done"], 1)
                sets = top[:, b, :, :].rearrange("p (h s) k -> p h s k", s=2)
                nc.vector.tensor_tensor(pair[:, b, :, :, :], sets[:, :, 0, :].unsqueeze(3).to_broadcast([N, HEADS, TOP, TOP]),
                                        sets[:, :, 1, :].unsqueeze(2).to_broadcast([N, HEADS, TOP, TOP]), ALU.add)\
                    .then_inc(s["pair_done"], 1)
                dve.wait_ge(s["pair_done"], b + 1)
                for i in range(HEADS):
                    nc.vector.max(best[:, b, i, :], pair[:, b, i, :, :].rearrange("p a k -> p (a k)")).then_inc(s["best_done"], 1)
                for i in range(HEADS):
                    dve.wait_ge(s["best_done"], HEADS * b + i + 1)
                    nc.vector.max_index(at[:, b, i, :], best[:, b, i, :], pair[:, b, i, :, :].rearrange("p a k -> p (a k)"))\
                        .then_inc(s["at_done"], 1)
            dve.wait_ge(s["at_done"], PB * HEADS)
            dve.wait_ge(s["idx_done"], PB * SETS)
            flat = at[:, :, :, :].rearrange("p b h k -> p (b h) k")
            nc.vector.tensor_scalar(at_hi[:, :, :], flat, 3, None, ALU.logical_shift_right).then_inc(s["split_done"], 1)
            nc.vector.tensor_scalar(at_lo[:, :, :], flat, 7, None, ALU.bitwise_and).then_inc(s["split_done"], 1)
            dve.wait_ge(s["split_done"], 2)
            shape = [N, PB * HEADS, TOP, TOP]
            ids = idx[:, :, :, :].rearrange("p b (h s) k -> p (b h) s k", s=2)
            steps = ramp[0:N, 0:TOP].unsqueeze(1).unsqueeze(1).to_broadcast(shape)
            for i, (hit, place) in enumerate(((hit1, at_hi), (hit2, at_lo))):
                nc.vector.tensor_tensor(hit[:, :, :, :], steps, place[:, :, :].unsqueeze(3).to_broadcast(shape), ALU.is_equal)\
                    .then_inc(s["hit_done"], 1)
            for i, hit in enumerate((hit1, hit2)):
                dve.wait_ge(s["hit_done"], i + 1)
                nc.vector.tensor_tensor(hit[:, :, :, :], hit[:, :, :, :], ids[:, :, i, :].unsqueeze(2).to_broadcast(shape),
                                        ALU.mult).then_inc(s["mul_done"], 1)
            for i, (hit, sel) in enumerate(((hit1, i1), (hit2, i2))):
                dve.wait_ge(s["mul_done"], i + 1)
                nc.vector.tensor_reduce(sel[:, :, :], hit[:, :, :, :], AX.X, ALU.add).then_inc(s["sel_done"], 1)
            dve.wait_ge(s["sel_done"], 2)
            nc.vector.tensor_copy(i2u[:, :], i2[:, :, :].rearrange("p h k -> p (h k)")).then_inc(s["u_done"], 1)
            dve.wait_ge(s["u_done"], 1)
            nc.vector.tensor_scalar(odd[:, :], i2u[:, :], 1, None, ALU.bitwise_and).then_inc(s["bits_done"], 1)
            nc.vector.tensor_scalar(half_[:, :], i2u[:, :], 1, None, ALU.logical_shift_right).then_inc(s["bits_done"], 1)
            dve.wait_ge(s["bits_done"], 2)
            nc.vector.scalar_tensor_tensor(out=codes[:, 0, :], in0=odd[:, :], scalar=float(KEYS),
                                           in1=i1[:, :, :].rearrange("p h k -> p (h k)"), op0=ALU.mult, op1=ALU.add)\
                .then_inc(s["code_done"], 1)
            for b in range(PB):
                nc.vector.tensor_scalar(codes[:, 1, b * CH:(b + 1) * CH], half_[:, b * CH:(b + 1) * CH], float(b * EB), None, ALU.add)\
                    .then_inc(s["code_done"], 1)
            nc.vector.tensor_scalar(codes[:, 2, :], best[:, :, :, :].rearrange("p b h k -> p (b h k)"), 0.0, None, ALU.max)\
                .then_inc(s["code_done"], 1)

        def step(front, back):
            with nc.Block(no_gpsimd_drain=True) as block:
                @block.sync
                def _(sp):
                    if back is None:
                        sp.wait_ge(big_in, 32)
                    else:
                        sp.wait_ge(s["res_done"], DK)
                        sp.dma_start(out[:, :, back], h[:, :, back]).then_inc(out_sent, 16)

                @block.tensor
                def _(pe):
                    def hidden(i):
                        if i >= 3:
                            pe.wait_ge(s["gelu_done"], i - 2)
                        for jj in range(J):
                            for k in range(DK):
                                mm = nc.tensor.matmul(ps[1 + i % 3][:, jj * PT:(jj + 1) * PT], down[:, k, i * J + jj, :],
                                                      xn[:, k, :], start=(k == 0), stop=(k == DK - 1))
                        mm.then_inc(s["hid_mm"], 1)

                    def weights(ch):
                        pe.wait_ge(s["rows_done"], ch + 1)
                        pe.wait_ge(s["cols_done"], ch + 1)
                        if ch >= HB:
                            pe.wait_ge(s["evac_done"], ch - HB + 1)
                        for t in range(CHUNKS[ch][1]):
                            mm = nc.tensor.matmul(ps[4 + ch % HB][:, t * PB * EB:(t + 1) * PB * EB], hot_rows[:, ch % HB, t, :],
                                                  hot_cols[:, ch % HB, t, :], start=True, stop=True)
                        mm.then_inc(s["g_mm"], 1)

                    if front is not None:
                        norm.tensor_mean(nc, pe, c["ones"], lambda k: h[:, k, front])
                    if back is not None:
                        hidden(0)
                    if front is not None:
                        norm.tensor_var(nc, pe, c["ones"])
                    if back is not None:
                        hidden(1)
                        weights(0)
                    if front is not None:
                        pe.wait_ge(s["sq2"], 1)
                        for k in range(DK):
                            mm = nc.tensor.matmul(ps[0][:, 0:PT], c["ones"][:, :], norm.square[:, k, :],
                                                  start=(k == 0), stop=(k == DK - 1))
                        mm.then_inc(s["ms_mm"], 1)
                    if back is not None:
                        for i in range(2, HU):
                            hidden(i)
                            if i - 1 < NC:
                                weights(i - 1)
                        for ch in range(HU - 1, NC):
                            weights(ch)
                        pe.wait_ge(s["gelu_done"], HU)
                        pe.wait_ge(s["evac_done"], NC)
                    if front is not None:
                        pe.wait_ge(s["xn_done"], DK)
                        for b in range(PB):
                            for half in range(2):
                                for k in range(DK):
                                    mm = nc.tensor.matmul(ps[1 + 2 * b + half][0:N, :], xn[:, k, b * N:(b + 1) * N],
                                                          kq[:, k, half * 512:(half + 1) * 512], start=(k == 0), stop=(k == DK - 1))
                                mm.then_inc(s["sim_mm"], 1)
                    if back is not None:
                        for m in range(DK):
                            for j in range(EB):
                                if m == 0 and j % J == 0:
                                    pe.wait_ge(s["wgt_done"], j // J + 1)
                                mm = nc.tensor.matmul(ps[5 + m][:, 0:PT], w_up[:, j, m * P:(m + 1) * P], hid[:, j, :],
                                                      start=(j == 0), stop=(j == EB - 1))
                            mm.then_inc(s["up_mm"], 1)
                    if front is not None:
                        pe.wait_ge(s["code_done"], 4)
                        for i in range(3):
                            mm = nc.tensor.transpose(ps[7][:, i * N:(i + 1) * N], codes[:, i, :], c["ident"][0:N, 0:N])
                        mm.then_inc(s["t_done"], 1)

                @block.scalar
                def _(act):
                    if front is not None:
                        nc.scalar.preload_act_table_set(EXP_LN)
                        norm.scalar(nc, act, c["eps"])
                        act.wait_ge(norm.ready, 1)
                        nc.scalar.activation(norm.square[:, :, :], norm.out[:, :, :], ACT.Square).then_inc(s["sq2"], 1)
                        act.wait_ge(s["ms_mm"], 1)
                        nc.scalar.activation(log2[:, :], ps[0][:, 0:PT], ACT.Ln, bias=eps6[:, 0:1]).then_inc(s["log2_done"], 1)
                        act.wait_ge(s["log2_done"], 1)
                        nc.scalar.activation(rms[:, :], log2[:, :], ACT.Exp, scale=-0.5).then_inc(s["rms_done"], 1)
                    if back is not None:
                        for i in range(max(HU, NC)):
                            if i < HU:
                                act.wait_ge(s["hid_mm"], i + 1)
                                nc.scalar.activation(hid[:, i * J:(i + 1) * J, :].rearrange("p j n -> p (j n)"),
                                                     ps[1 + i % 3][:, 0:J * PT], ACT.Gelu).then_inc(s["gelu_done"], 1)
                            if i < NC:
                                t0, n = CHUNKS[i]
                                act.wait_ge(s["g_mm"], i + 1)
                                nc.scalar.activation(weight[:, :, :, t0:t0 + n],
                                                     ps[4 + i % HB][:, 0:n * PB * EB].rearrange("p (t b j) -> p j b t", b=PB, j=EB),
                                                     ACT.Copy).then_inc(s["evac_done"], 1)
                    if front is not None:
                        act.wait_ge(s["t_done"], 1)
                        if back is not None:
                            act.wait_ge(s["rows_done"], NC)
                            act.wait_ge(s["cols_done"], NC)
                        nc.scalar.activation(codesT[:, :, :].rearrange("p a n -> p (a n)"), ps[7][:, 0:3 * N], ACT.Copy)\
                            .then_inc(s["ct_done"], 1)

                @block.gpsimd
                def _(pool):
                    if back is not None:
                        for ch, (t0, n) in enumerate(CHUNKS):
                            shape = [P, n, PB * EB]
                            pool.wait_ge(s["hot_done"], ch + 1)
                            nc.gpsimd.tensor_tensor(hot_cols[:, ch % HB, 0:n, :], hot_cols[:, ch % HB, 0:n, :],
                                                    codesT[:, 2, t0:t0 + n].unsqueeze(2).to_broadcast(shape), ALU.mult)\
                                .then_inc(s["cols_done"], 1)

                @block.vector
                def _(dve):
                    def one_hot(ch):
                        t0, n = CHUNKS[ch]
                        if ch >= HB:
                            dve.wait_ge(s["g_mm"], ch - HB + 1)
                        nc.vector.tensor_tensor(hot_rows[:, ch % HB, 0:n, :], ramp[:, :].unsqueeze(1).to_broadcast([P, n, P]),
                                                codesT[:, 0, t0:t0 + n].unsqueeze(2).to_broadcast([P, n, P]), ALU.is_equal)\
                            .then_inc(s["rows_done"], 1)
                        nc.vector.tensor_tensor(hot_cols[:, ch % HB, 0:n, :], ramp[:, 0:PB * EB].unsqueeze(1).to_broadcast([P, n, PB * EB]),
                                                codesT[:, 1, t0:t0 + n].unsqueeze(2).to_broadcast([P, n, PB * EB]), ALU.is_equal)\
                            .then_inc(s["hot_done"], 1)

                    if back is not None:
                        one_hot(0)
                    if front is not None:
                        norm.vector(nc, dve, h[:, :, front])
                    if back is not None:
                        for ch in range(1, NC):
                            one_hot(ch)
                    if front is not None:
                        dve.wait_ge(norm.ready, 1)
                        dve.wait_ge(s["rms_done"], 1)
                        if back is not None:
                            dve.wait_ge(s["hid_mm"], HU)
                        for k in range(DK):
                            nc.vector.scalar_tensor_tensor(out=xn[:, k, :], in0=norm.out[:, k, :], scalar=nw[:, k:k + 1],
                                                           in1=rms[:, :], op0=ALU.mult, op1=ALU.mult).then_inc(s["xn_done"], 1)
                    if back is not None:
                        dve.wait_ge(s["gelu_done"], HU)
                        dve.wait_ge(s["evac_done"], NC)
                        for i in range(HU):
                            block_ = hid[:, i * J:(i + 1) * J, :]
                            nc.vector.tensor_tensor(block_, block_, weight[:, i * J:(i + 1) * J, :, :].rearrange("p j b n -> p j (b n)"),
                                                    ALU.mult).then_inc(s["wgt_done"], 1)
                    if front is not None:
                        best_experts(dve)
                    if back is not None:
                        for m in range(DK):
                            dve.wait_ge(s["up_mm"], m + 1)
                            nc.vector.tensor_tensor(h[:, m, back], h[:, m, back], ps[5 + m][:, 0:PT], ALU.add).then_inc(s["res_done"], 1)
            st.clear()

        def pair_cols(g):
            return bass.ds(g * PT, PT)

        step(pair_cols(0), None)
        with nc.Fori(0, STEPS - 1) as g:
            step(pair_cols(g + 1), pair_cols(g))
        step(None, pair_cols(STEPS - 1))
        with nc.Block() as block:
            @block.sync
            def _(sp):
                sp.wait_ge(out_sent, 16 * STEPS)
        so.clear()


def early_fusion(nc, a, out):
    with Stage(nc, "net") as st:
        h = st.sbuf("h", [P, DK, T])
        c = dict(ones=st.sbuf("ones", [P, P]), ident=st.sbuf("ident", [P, P]), eps=st.sbuf("eps", [P, 1]))
        slots_in = nc.dram_tensor("slots_in", [17 * 640, D], F32).ap()
        slots_out = nc.dram_tensor("slots_out", [16 * 565, D], F32).ap()
        row_expert = nc.dram_tensor("row_expert", [B, 1], U32).ap()
        constants(nc, c)
        tok(nc, h, c, **a["tok"])
        l0_attn(nc, h, c, **a["l0_attn"])
        moe(nc, h, c, slots_in=slots_in, slots_out=slots_out, **a["moe"])
        mamba(nc, h, c, [a["mamba_f"], a["mamba_b"]])
        l1_ffn(nc, h, c, **a["l1_ffn"])
        l2_attn(nc, h, c, **a["l2_attn"])
        l2_ffn(nc, h, c, row_expert=row_expert, **a["l2_ffn"])
        rwkv(nc, h, c, **a["rwkv"])
        peer(nc, h, c, out=out, **a["peer"])



def feature_cols(v):
    return v.reshape(-1, P).T


def feature_blocks(w):
    return w.reshape(-1, P, w.shape[1]).transpose(1, 0, 2)


def rope_tables():
    n = np.arange(N)
    places = (n // 256, n % 256 // 16, n % 16)
    rate = (1.0 / 10000.0 ** (np.arange(2, dtype=np.float32) / 2.0)).astype(np.float32)
    cos, sin = np.ones((D, N), np.float32), np.zeros((D, N), np.float32)
    for i in range(D):
        f = i % 16
        if f < 12:
            angle = (places[f // 4].astype(np.float32) * rate[f % 2]).astype(np.float32)
            cos[i] = np.cos(angle)
            sin[i] = np.sin(angle) * (-1 if f % 2 == 0 else 1)
    head = np.arange(P) // 16 % 2
    even = np.stack([head == 0, head == 1], 1).astype(np.float32)
    table = lambda t: t.reshape(DK, P, N).transpose(1, 0, 2)
    return table(cos), table(sin), even


def layout(I):
    out = {}
    x = I["x"]
    text = np.zeros((B, N, D), np.float32)
    text[:, IMG:] = I["txt"]
    px = x.reshape(B, 3, GRID, 16, GRID, 16).transpose(1, 3, 5, 0, 2, 4).reshape(6, P, B * IMG).transpose(1, 0, 2)
    out["tok"] = dict(h_text=text.reshape(T, DK, P).transpose(2, 1, 0), patches=px, w_t=feature_blocks(I["L0_tok_W"].T),
                      bias=feature_cols(I["L0_tok_b"]))

    w = lambda n: I[f"L0_attn_{n}"]
    turn = np.arange(D) ^ 1
    cos, sin, even = rope_tables()
    biases = np.stack([feature_cols(v) for v in (w("bq"), w("bq")[turn], w("bk"), w("bk")[turn], w("bv"), w("bo"))], 1)
    out["l0_attn"] = dict(wq=w("Wq"), wq_rot=w("Wq")[:, turn], wk=w("Wk"), wk_rot=w("Wk")[:, turn], wv=w("Wv"), wo=w("Wo"),
                          biases=biases, cos=cos, sin=sin, even=even)

    w = lambda n: I[f"L0_ffn_{n}"]
    gate = np.concatenate([w("w_gate"), w("sw_gate")[None]])
    up = np.concatenate([w("w_up"), w("sw_up")[None]])
    down = np.concatenate([w("w_down"), w("sw_down")[None]])
    gate_up = np.stack([gate, up], 2).reshape(17, DK, P, 2, 352).transpose(0, 2, 1, 3, 4)
    padded = np.zeros((17, 3 * P, D), np.float32)
    padded[:, :352] = down
    out["moe"] = dict(router_w=w("router_w"), router_b=w("router_b").reshape(1, 16), gate_up=gate_up,
                      down=padded.reshape(17, 3, P, D).transpose(0, 2, 1, 3))

    for p in "fb":
        w = lambda n: I[f"L1_attn_{p}_{n}"]
        out[f"mamba_{p}"] = dict(in_t=w("in_w").T, xproj_t=w("xproj_w").T, dt_t=w("dt_w").T, out_t=w("out_w").T,
                                 conv_w=feature_blocks(w("conv_w")), conv_b=feature_cols(w("conv_b")),
                                 dt_b=w("dt_b").reshape(1, -1), a_log=feature_blocks(w("A_log")), d=feature_cols(w("D")))

    w = lambda n: I[f"L1_ffn_{n}"]
    out["l1_ffn"] = dict(w_fc=w("w_fc"), w_proj=w("w_proj"), u_t=w("u").T, v=w("v"), fast_b=w("fast_b"),
                         gate=np.asarray(w("gate")).reshape(1, 1))
    w = lambda n: I[f"L2_attn_{n}"]
    out["l2_attn"] = dict(wq=w("W_Q"), wk=w("W_K"), wv=w("W_V"))

    w = lambda n: I[f"L2_ffn_{n}"]
    out["l2_ffn"] = dict(wr=w("Wr"), br=w("br").reshape(1, 8), w1=w("W1").reshape(8, DK, P, 1024).transpose(0, 2, 1, 3),
                         b1=w("b1").reshape(8, 8, P).transpose(0, 2, 1), w2=w("W2").reshape(8, 8, P, D).transpose(0, 2, 1, 3),
                         b2=w("b2").reshape(8, DK, P).transpose(0, 2, 1))

    w = lambda n: I[f"L3_attn_{n}"]
    cols = np.stack([feature_cols(w(n).reshape(-1)) for n in
                     ("time_decay", "time_first", "ln1_g", "ln1_b", "ln2_g", "ln2_b", "mix_k", "mix_v", "mix_r", "cmix_k",
                      "cmix_r")], 1)
    out["rwkv"] = dict(wk=w("w_tk"), wv=w("w_tv"), wr=w("w_tr"), ck=w("w_ck"), cv=w("w_cv"), cr=w("w_cr"), cols=cols)

    w = lambda n: I[f"L3_ffn_{n}"]
    keys = w("keys").transpose(3, 0, 2, 1).reshape(P, 16, 64)
    order = np.arange(4096).reshape(64, 32, 2).transpose(1, 2, 0).reshape(32, P)
    out["peer"] = dict(wq=w("w_q"), keys_t=keys,
                       down_t=w("expert_down")[order].transpose(2, 0, 1).reshape(DK, P, 32, P).transpose(1, 0, 2, 3),
                       up=w("expert_up")[order].transpose(1, 0, 2), norm_w=feature_cols(w("norm_w")))
    return out


def kernel(**inputs):
    import concourse.bacc as _bacc
    from concourse.bass_utils import run_bass_kernel_spmd as _run

    nc = _bacc.Bacc("TRN2", target_bir_lowering=False, num_devices=1)
    arrays, aps = {}, {}
    for stage, parts in layout({k: np.asarray(v) for k, v in inputs.items()}).items():
        aps[stage] = {}
        for name, value in parts.items():
            value = np.ascontiguousarray(value)
            arrays[f"in_{stage}_{name}"] = value
            aps[stage][name] = nc.dram_tensor(f"in_{stage}_{name}", value.shape, mybir.dt.from_np(value.dtype),
                                              kind="ExternalInput").ap()
    out = nc.dram_tensor("out", [P, DK, T], F32, kind="ExternalOutput").ap()
    early_fusion(nc, aps, out)
    result = _run(nc, [arrays], core_ids=[0]).results[0]["out"]
    return np.ascontiguousarray(result.transpose(2, 1, 0).reshape(B, N, D))
```
